# Optimizing a Trainium2 kernel written in Bass

```python
import numpy as np
import jax
import jax.numpy as jnp

def _softmax(x, axis=-1):
    return jax.nn.softmax(x, axis=axis)

def _gelu(x):
    return jax.nn.gelu(x, approximate=True)

def _silu(x):
    return jax.nn.silu(x)

def _sigmoid(x):
    return jax.nn.sigmoid(x)

def _layernorm(x, axis=-1, eps=1e-05):
    m = jnp.mean(x, axis=axis, keepdims=True)
    v = jnp.var(x, axis=axis, keepdims=True)
    return (x - m) / jnp.sqrt(v + eps)

def _scatter_add(tgt, idx, src, axis=0):
    return tgt.at[idx].add(src)

def _segment_sum(src, seg, n):
    return jax.ops.segment_sum(src, seg, n)
kernel_name = 'mk_decoder_preln_d2_seqx_r4_2be16e'

def setup_inputs(seed: int=0):
    np.random.seed(seed)
    _w = jnp.asarray

    def _rec_inputs():
        import jax
        import jax.numpy as jnp
        _rk = jax.random.key(seed)
        x = -0.0002928 + 1 * jax.random.normal(jax.random.fold_in(_rk, 1), (2, 1024, 256), jnp.float32)
        _lenS = 1024 - jax.random.randint(jax.random.fold_in(_rk, 7), (2,), 0, max(1, 1024 // 4) + 1, jnp.int32)
        _lenS2 = 154 - jax.random.randint(jax.random.fold_in(_rk, 8), (2,), 0, max(1, 154 // 4) + 1, jnp.int32)
        _ctx_768P = jax.random.normal(jax.random.fold_in(_rk, 11), (2, 16, 192), jnp.float32)
        _ctx_768c = jax.random.dirichlet(jax.random.fold_in(_rk, 511), 0.3 * jnp.ones((16,), jnp.float32), (2, 154))
        _ctx_768t = jnp.einsum('bsk,bkd->bsd', _ctx_768c, _ctx_768P)
        _ctx_768t = _ctx_768t * jax.lax.rsqrt(jnp.mean(jnp.square(_ctx_768t)) + 1e-12) * 0.953939
        ctx_768 = 2.09791e-05 + 1.00001 * (_ctx_768t + 0.3 * jax.random.normal(jax.random.fold_in(_rk, 611), (2, 154, 192), jnp.float32))
        _validS = jnp.arange(1024)[None, :] < _lenS[:, None]
        _validS2 = jnp.arange(154)[None, :] < _lenS2[:, None]
        _causal = jnp.tril(jnp.ones((1024, 1024), dtype=bool))
        mask_BxS_bf1 = jnp.ones((2, 1024), dtype=bool)
        mask_BxS2_bf1 = jnp.ones((2, 154), dtype=bool)
        return (x, ctx_768, mask_BxS_bf1, mask_BxS2_bf1)
    x, ctx_768, mask_BxS_bf1, mask_BxS2_bf1 = _rec_inputs()

    def _L0_attn_setup():
        import jax, jax.numpy as jnp
        import numpy as np
        import math
        N_EMBD = 256
        N_HEAD = 16
        HEAD_DIM = N_EMBD // N_HEAD
        B, T = (2, 512)
        LORA_RANK = 16
        LORA_SCALE = 32.0 / 16.0
        QMIN, QMAX = (0.0, 255.0)

        def round_ste(x):
            return x + jax.lax.stop_gradient(jnp.round(x) - x)

        def fake_quant(x, scale, zero_point):
            q = jnp.clip(round_ste(x / scale + zero_point), QMIN, QMAX)
            return (q - zero_point) * scale

        def lora_linear(x, w, b, la, lb):
            return x @ w + b + LORA_SCALE * (x @ la @ lb)
        key = jax.random.key(seed)
        ks = jax.random.split(key, 10)
        std = 0.02
        hidden_states = jax.random.normal(ks[0], (B, T, N_EMBD), dtype=jnp.float32)
        w_attn = jax.random.normal(ks[1], (N_EMBD, 3 * N_EMBD), dtype=jnp.float32) * std
        b_attn = jnp.zeros((3 * N_EMBD,), dtype=jnp.float32)
        la_attn = jax.random.normal(ks[2], (N_EMBD, LORA_RANK), dtype=jnp.float32) * std
        lb_attn = jnp.zeros((LORA_RANK, 3 * N_EMBD), dtype=jnp.float32)
        w_proj = jax.random.normal(ks[3], (N_EMBD, N_EMBD), dtype=jnp.float32) * std
        b_proj = jnp.zeros((N_EMBD,), dtype=jnp.float32)
        la_proj = jax.random.normal(ks[4], (N_EMBD, LORA_RANK), dtype=jnp.float32) * std
        lb_proj = jnp.zeros((LORA_RANK, N_EMBD), dtype=jnp.float32)
        kv_scale = jnp.asarray(0.05, dtype=jnp.float32)
        kv_zero_point = jnp.asarray(128.0, dtype=jnp.float32)
        return {'hidden_states': hidden_states, 'w_attn': w_attn, 'b_attn': b_attn, 'la_attn': la_attn, 'lb_attn': lb_attn, 'w_proj': w_proj, 'b_proj': b_proj, 'la_proj': la_proj, 'lb_proj': lb_proj, 'kv_scale': kv_scale, 'kv_zero_point': kv_zero_point}
    _L0_attn_all = _L0_attn_setup()
    _L0_attn_in = {k: v for k, v in _L0_attn_all.items() if k in ('w_attn', 'b_attn', 'la_attn', 'lb_attn', 'w_proj', 'b_proj', 'la_proj', 'lb_proj', 'kv_scale', 'kv_zero_point')}
    del _L0_attn_all

    def _L0_xattn_setup():
        import jax, jax.numpy as jnp
        import numpy as np
        H = 8
        D = 64
        SCALE = D ** (-0.5)
        key = jax.random.key(seed)
        ks = jax.random.split(key, 7)
        B, Nq, Nkv = (2, 512, 512)
        Cq, Ck, I = (256, 192, H * D)
        return {'x': jax.random.normal(ks[0], (B, Nq, Cq), jnp.float32), 'context': jax.random.normal(ks[1], (B, Nkv, Ck), jnp.float32), 'Wq': jax.random.normal(ks[2], (Cq, I), jnp.float32) * Cq ** (-0.5), 'Wk': jax.random.normal(ks[3], (Ck, I), jnp.float32) * Ck ** (-0.5), 'Wv': jax.random.normal(ks[4], (Ck, I), jnp.float32) * Ck ** (-0.5), 'Wo': jax.random.normal(ks[5], (I, Cq), jnp.float32) * I ** (-0.5), 'bo': jnp.zeros((Cq,), jnp.float32)}
    _L0_xattn_all = _L0_xattn_setup()
    _L0_xattn_in = {k: v for k, v in _L0_xattn_all.items() if k in ('Wq', 'Wk', 'Wv', 'Wo', 'bo')}
    del _L0_xattn_all

    def _L0_ffn_setup():
        import jax, jax.numpy as jnp
        import numpy as np
        N_HEAD = 16
        N_ACTIVE = 4
        D_MODEL = 256
        D_ATTN = 64
        B = 4
        S = 512
        key = jax.random.key(seed)
        ks = jax.random.split(key, 6)
        sc = 1.0 / np.sqrt(D_MODEL).astype(np.float32)
        return {'x': jax.random.normal(ks[0], (B, S, D_MODEL), jnp.float32), 'Wq': jax.random.normal(ks[1], (D_MODEL, N_HEAD * D_ATTN), jnp.float32) * sc, 'bq': jnp.zeros((N_HEAD * D_ATTN,), jnp.float32), 'Wk': jax.random.normal(ks[2], (D_MODEL, N_HEAD * D_ATTN), jnp.float32) * sc, 'bk': jnp.zeros((N_HEAD * D_ATTN,), jnp.float32), 'Wv': jax.random.normal(ks[3], (D_MODEL, N_HEAD * D_ATTN), jnp.float32) * sc, 'bv': jnp.zeros((N_HEAD * D_ATTN,), jnp.float32), 'Wr': jax.random.normal(ks[4], (D_MODEL, N_HEAD), jnp.float32) * sc, 'br': jnp.zeros((N_HEAD,), jnp.float32), 'Wo': jax.random.normal(ks[5], (N_ACTIVE * D_ATTN, D_MODEL), jnp.float32) * (1.0 / np.sqrt(N_ACTIVE * D_ATTN).astype(np.float32)), 'bo': jnp.zeros((D_MODEL,), jnp.float32)}
    _L0_ffn_all = _L0_ffn_setup()
    _L0_ffn_in = {k: v for k, v in _L0_ffn_all.items() if k in ('Wq', 'bq', 'Wk', 'bk', 'Wv', 'bv', 'Wr', 'br', 'Wo', 'bo')}
    del _L0_ffn_all

    def _L1_attn_setup():
        import jax, jax.numpy as jnp
        import numpy as np
        LN_EPS = 1e-05
        key = jax.random.key(seed)
        ks = jax.random.split(key, 5)
        B, S, E, H = (4, 256, 256, 16)
        sd = E ** (-0.5)
        return {'x': jax.random.normal(ks[0], (B, S, E), jnp.float32), 'Wq': jax.random.normal(ks[1], (E, E), jnp.float32) * sd, 'Wk': jax.random.normal(ks[2], (E, E), jnp.float32) * sd, 'Wv': jax.random.normal(ks[3], (E, E), jnp.float32) * sd, 'bias_table': jax.random.normal(ks[4], (2 * S - 1, H), jnp.float32) * 0.02, 'ln_gamma': jnp.ones((E,), jnp.float32), 'ln_beta': jnp.zeros((E,), jnp.float32)}
    _L1_attn_all = _L1_attn_setup()
    _L1_attn_in = {k: v for k, v in _L1_attn_all.items() if k in ('Wq', 'Wk', 'Wv', 'bias_table', 'ln_gamma', 'ln_beta')}
    del _L1_attn_all

    def _L1_xattn_setup():
        import jax, jax.numpy as jnp
        import numpy as np
        B, T, DT, G, DV = (16, 128, 256, 144, 192)
        H, DH = (4, 32)
        INNER = H * DH
        HID = 4 * DT
        N_STATE = 64
        K_TOP = 32

        def layernorm(x, g, b, eps=1e-05):
            m = x.mean(-1, keepdims=True)
            v = x.var(-1, keepdims=True)
            return (x - m) * jax.lax.rsqrt(v + eps) * g + b

        def s4d(x, log_dt, A_re, A_im, C_re, C_im, D_skip):
            Bb, L, D = x.shape
            dt = jnp.exp(log_dt)
            A = A_re + 1j * A_im
            C = C_re + 1j * C_im
            dtA = dt[:, None] * A
            dC = C * (jnp.exp(dtA) - 1.0) / A
            powers = jnp.exp(dtA[:, :, None] * jnp.arange(L))
            K = 2.0 * jnp.einsum('dn,dnl->dl', dC, powers).real
            n = 2 * L
            Kf = jnp.fft.rfft(K, n=n, axis=-1)
            xf = jnp.fft.rfft(x, n=n, axis=1)
            y = jnp.fft.irfft(xf * Kf.T[None], n=n, axis=1)[:, :L]
            return y + x * D_skip
        key = jax.random.key(seed)
        ks = jax.random.split(key, 16)
        s = 0.02
        inp = {'x_text': jax.random.normal(ks[0], (B, T, DT), jnp.float32), 'x_vision': jax.random.normal(ks[1], (B, G, DV), jnp.float32), 'text_mask': jnp.ones((B, T), bool), 'vision_mask': jnp.ones((B, G), bool), 'Wq': jax.random.normal(ks[2], (DT, INNER), jnp.float32) * s, 'Wk': jax.random.normal(ks[3], (DV, INNER), jnp.float32) * s, 'Wv': jax.random.normal(ks[4], (DV, DT), jnp.float32) * s, 'W_film_in': jax.random.normal(ks[5], (DT, 2 * DT), jnp.float32) * s, 'b_film_in': jnp.zeros((2 * DT,), jnp.float32), 'W_film_out': jax.random.normal(ks[6], (DT, 2 * DT), jnp.float32) * s, 'b_film_out': jnp.zeros((2 * DT,), jnp.float32), 'g_norm_in': jnp.ones((DT,), jnp.float32), 'b_norm_in': jnp.zeros((DT,), jnp.float32), 'g_norm_out': jnp.ones((DT,), jnp.float32), 'b_norm_out': jnp.zeros((DT,), jnp.float32), 'g_ffn': jnp.ones((DT,), jnp.float32), 'b_ffn': jnp.zeros((DT,), jnp.float32), 'W1': jax.random.normal(ks[7], (DT, HID), jnp.float32) * s, 'b1': jnp.zeros((HID,), jnp.float32), 'W2': jax.random.normal(ks[8], (HID, DT), jnp.float32) * s, 'b2': jnp.zeros((DT,), jnp.float32), 'log_dt': jnp.log(0.001) + jax.random.uniform(ks[9], (DT,), jnp.float32) * (jnp.log(0.1) - jnp.log(0.001)), 'A_re': -0.5 * jnp.ones((DT, N_STATE), jnp.float32), 'A_im': jnp.tile(jnp.pi * jnp.arange(N_STATE, dtype=jnp.float32), (DT, 1)), 'C_re': jax.random.normal(ks[10], (DT, N_STATE), jnp.float32) * 0.5 ** 0.5, 'C_im': jax.random.normal(ks[11], (DT, N_STATE), jnp.float32) * 0.5 ** 0.5, 'D_skip': jax.random.normal(ks[12], (DT,), jnp.float32), 'mod_gate': jnp.array(0.5, jnp.float32)}
        return inp
    _L1_xattn_all = _L1_xattn_setup()
    _L1_xattn_in = {k: v for k, v in _L1_xattn_all.items() if k in ('Wq', 'Wk', 'Wv', 'W_film_in', 'b_film_in', 'W_film_out', 'b_film_out', 'g_norm_in', 'b_norm_in', 'g_norm_out', 'b_norm_out', 'g_ffn', 'b_ffn', 'W1', 'b1', 'W2', 'b2', 'log_dt', 'A_re', 'A_im', 'C_re', 'C_im', 'D_skip', 'mod_gate')}
    del _L1_xattn_all

    def _L1_ffn_setup():
        import jax, jax.numpy as jnp
        import numpy as np
        E = 8
        K = 2
        D = 256
        P = 1024
        key = jax.random.key(seed)
        ks = jax.random.split(key, 8)
        s = lambda fan_in: 1.0 / np.sqrt(fan_in)
        x = jax.random.normal(ks[0], (2, 512, D), dtype=jnp.float32)
        W1 = jax.random.normal(ks[1], (E, D, P), dtype=jnp.float32) * s(D)
        b1 = jax.random.normal(ks[2], (E, P), dtype=jnp.float32) * 0.01
        W2 = jax.random.normal(ks[3], (E, P, D), dtype=jnp.float32) * s(P)
        b2 = jax.random.normal(ks[4], (E, D), dtype=jnp.float32) * 0.01
        Wr = jax.random.normal(ks[5], (D, E), dtype=jnp.float32) * s(D)
        br = jax.random.normal(ks[6], (E,), dtype=jnp.float32) * 0.01
        return {'x': x, 'W1': W1, 'b1': b1, 'W2': W2, 'b2': b2, 'Wr': Wr, 'br': br}
    _L1_ffn_all = _L1_ffn_setup()
    _L1_ffn_in = {k: v for k, v in _L1_ffn_all.items() if k in ('W1', 'b1', 'W2', 'b2', 'Wr', 'br')}
    del _L1_ffn_all
    return {'x': x, 'ctx_768': ctx_768, 'mask_BxS_bf1': mask_BxS_bf1, 'mask_BxS2_bf1': mask_BxS2_bf1, 'L0_attn_w_attn': _L0_attn_in['w_attn'], 'L0_attn_b_attn': _L0_attn_in['b_attn'], 'L0_attn_la_attn': _L0_attn_in['la_attn'], 'L0_attn_lb_attn': _L0_attn_in['lb_attn'], 'L0_attn_w_proj': _L0_attn_in['w_proj'], 'L0_attn_b_proj': _L0_attn_in['b_proj'], 'L0_attn_la_proj': _L0_attn_in['la_proj'], 'L0_attn_lb_proj': _L0_attn_in['lb_proj'], 'L0_attn_kv_scale': _L0_attn_in['kv_scale'], 'L0_attn_kv_zero_point': _L0_attn_in['kv_zero_point'], 'L0_xattn_Wq': _L0_xattn_in['Wq'], 'L0_xattn_Wk': _L0_xattn_in['Wk'], 'L0_xattn_Wv': _L0_xattn_in['Wv'], 'L0_xattn_Wo': _L0_xattn_in['Wo'], 'L0_xattn_bo': _L0_xattn_in['bo'], 'L0_ffn_Wq': _L0_ffn_in['Wq'], 'L0_ffn_bq': _L0_ffn_in['bq'], 'L0_ffn_Wk': _L0_ffn_in['Wk'], 'L0_ffn_bk': _L0_ffn_in['bk'], 'L0_ffn_Wv': _L0_ffn_in['Wv'], 'L0_ffn_bv': _L0_ffn_in['bv'], 'L0_ffn_Wr': _L0_ffn_in['Wr'], 'L0_ffn_br': _L0_ffn_in['br'], 'L0_ffn_Wo': _L0_ffn_in['Wo'], 'L0_ffn_bo': _L0_ffn_in['bo'], 'L1_attn_Wq': _L1_attn_in['Wq'], 'L1_attn_Wk': _L1_attn_in['Wk'], 'L1_attn_Wv': _L1_attn_in['Wv'], 'L1_attn_bias_table': _L1_attn_in['bias_table'], 'L1_attn_ln_gamma': _L1_attn_in['ln_gamma'], 'L1_attn_ln_beta': _L1_attn_in['ln_beta'], 'L1_xattn_Wq': _L1_xattn_in['Wq'], 'L1_xattn_Wk': _L1_xattn_in['Wk'], 'L1_xattn_Wv': _L1_xattn_in['Wv'], 'L1_xattn_W_film_in': _L1_xattn_in['W_film_in'], 'L1_xattn_b_film_in': _L1_xattn_in['b_film_in'], 'L1_xattn_W_film_out': _L1_xattn_in['W_film_out'], 'L1_xattn_b_film_out': _L1_xattn_in['b_film_out'], 'L1_xattn_g_norm_in': _L1_xattn_in['g_norm_in'], 'L1_xattn_b_norm_in': _L1_xattn_in['b_norm_in'], 'L1_xattn_g_norm_out': _L1_xattn_in['g_norm_out'], 'L1_xattn_b_norm_out': _L1_xattn_in['b_norm_out'], 'L1_xattn_g_ffn': _L1_xattn_in['g_ffn'], 'L1_xattn_b_ffn': _L1_xattn_in['b_ffn'], 'L1_xattn_W1': _L1_xattn_in['W1'], 'L1_xattn_b1': _L1_xattn_in['b1'], 'L1_xattn_W2': _L1_xattn_in['W2'], 'L1_xattn_b2': _L1_xattn_in['b2'], 'L1_xattn_log_dt': _L1_xattn_in['log_dt'], 'L1_xattn_A_re': _L1_xattn_in['A_re'], 'L1_xattn_A_im': _L1_xattn_in['A_im'], 'L1_xattn_C_re': _L1_xattn_in['C_re'], 'L1_xattn_C_im': _L1_xattn_in['C_im'], 'L1_xattn_D_skip': _L1_xattn_in['D_skip'], 'L1_xattn_mod_gate': _L1_xattn_in['mod_gate'], 'L1_ffn_W1': _L1_ffn_in['W1'], 'L1_ffn_b1': _L1_ffn_in['b1'], 'L1_ffn_W2': _L1_ffn_in['W2'], 'L1_ffn_b2': _L1_ffn_in['b2'], 'L1_ffn_Wr': _L1_ffn_in['Wr'], 'L1_ffn_br': _L1_ffn_in['br']}

def reference(x, ctx_768, mask_BxS_bf1, mask_BxS2_bf1, L0_attn_w_attn, L0_attn_b_attn, L0_attn_la_attn, L0_attn_lb_attn, L0_attn_w_proj, L0_attn_b_proj, L0_attn_la_proj, L0_attn_lb_proj, L0_attn_kv_scale, L0_attn_kv_zero_point, L0_xattn_Wq, L0_xattn_Wk, L0_xattn_Wv, L0_xattn_Wo, L0_xattn_bo, L0_ffn_Wq, L0_ffn_bq, L0_ffn_Wk, L0_ffn_bk, L0_ffn_Wv, L0_ffn_bv, L0_ffn_Wr, L0_ffn_br, L0_ffn_Wo, L0_ffn_bo, L1_attn_Wq, L1_attn_Wk, L1_attn_Wv, L1_attn_bias_table, L1_attn_ln_gamma, L1_attn_ln_beta, L1_xattn_Wq, L1_xattn_Wk, L1_xattn_Wv, L1_xattn_W_film_in, L1_xattn_b_film_in, L1_xattn_W_film_out, L1_xattn_b_film_out, L1_xattn_g_norm_in, L1_xattn_b_norm_in, L1_xattn_g_norm_out, L1_xattn_b_norm_out, L1_xattn_g_ffn, L1_xattn_b_ffn, L1_xattn_W1, L1_xattn_b1, L1_xattn_W2, L1_xattn_b2, L1_xattn_log_dt, L1_xattn_A_re, L1_xattn_A_im, L1_xattn_C_re, L1_xattn_C_im, L1_xattn_D_skip, L1_xattn_mod_gate, L1_ffn_W1, L1_ffn_b1, L1_ffn_W2, L1_ffn_b2, L1_ffn_Wr, L1_ffn_br):
    import jax
    import jax.numpy as jnp

    def _L0_attn_ref(hidden_states, w_attn, b_attn, la_attn, lb_attn, w_proj, b_proj, la_proj, lb_proj, kv_scale, kv_zero_point):
        import jax, jax.numpy as jnp
        import numpy as np
        import math
        N_EMBD = 256
        N_HEAD = 16
        HEAD_DIM = N_EMBD // N_HEAD
        B, T = (2, 512)
        LORA_RANK = 16
        LORA_SCALE = 32.0 / 16.0
        QMIN, QMAX = (0.0, 255.0)

        def round_ste(x):
            return x + jax.lax.stop_gradient(jnp.round(x) - x)

        def fake_quant(x, scale, zero_point):
            q = jnp.clip(round_ste(x / scale + zero_point), QMIN, QMAX)
            return (q - zero_point) * scale

        def lora_linear(x, w, b, la, lb):
            return x @ w + b + LORA_SCALE * (x @ la @ lb)
        Bn, Tn, C = hidden_states.shape
        qkv = lora_linear(hidden_states, w_attn, b_attn, la_attn, lb_attn)
        q, k, v = jnp.split(qkv, 3, axis=2)

        def to_heads(x):
            return x.reshape(Bn, Tn, N_HEAD, HEAD_DIM).transpose(0, 2, 1, 3)
        q, k, v = (to_heads(q), to_heads(k), to_heads(v))
        k = fake_quant(k, kv_scale, kv_zero_point)
        v = fake_quant(v, kv_scale, kv_zero_point)
        scores = jnp.einsum('bhqd,bhkd->bhqk', q, k) / math.sqrt(HEAD_DIM)
        causal = jnp.tril(jnp.ones((Tn, Tn), dtype=bool))
        scores = jnp.where(causal, scores, -jnp.inf)
        attn = jax.nn.softmax(scores, axis=-1)
        out = jnp.einsum('bhqk,bhkd->bhqd', attn, v)
        out = out.transpose(0, 2, 1, 3).reshape(Bn, Tn, C)
        return lora_linear(out, w_proj, b_proj, la_proj, lb_proj)

    def _L0_xattn_ref(x, context, Wq, Wk, Wv, Wo, bo):
        import jax, jax.numpy as jnp
        import numpy as np
        H = 8
        D = 64
        SCALE = D ** (-0.5)
        B, Nq, _ = x.shape
        Nkv = context.shape[1]
        q = (x @ Wq).reshape(B, Nq, H, D)
        k = (context @ Wk).reshape(B, Nkv, H, D)
        v = (context @ Wv).reshape(B, Nkv, H, D)
        sim = jnp.einsum('bihd,bjhd->bhij', q, k) * SCALE
        attn = jax.nn.softmax(sim, axis=-1)
        out = jnp.einsum('bhij,bjhd->bihd', attn, v).reshape(B, Nq, H * D)
        return out @ Wo + bo

    def _L0_ffn_ref(x, Wq, bq, Wk, bk, Wv, bv, Wr, br, Wo, bo):
        import jax, jax.numpy as jnp
        import numpy as np
        N_HEAD = 16
        N_ACTIVE = 4
        D_MODEL = 256
        D_ATTN = 64
        B = 4
        S = 512
        b, s, _ = x.shape
        dist = jax.nn.softmax(jnp.mean(x @ Wr + br, axis=1), axis=-1)
        _, idx = jax.lax.top_k(dist, N_ACTIVE)
        idx = jnp.sort(idx, axis=-1)

        def proj(W, bias):
            return (x @ W + bias).reshape(b, s, N_HEAD, D_ATTN).transpose(0, 2, 1, 3)
        Q = proj(Wq, bq)
        K = proj(Wk, bk)
        V = proj(Wv, bv)
        gather = lambda t: jnp.take_along_axis(t, idx[:, :, None, None], axis=1)
        Qs, Ks, Vs = (gather(Q), gather(K), gather(V))
        scale = 1.0 / jnp.sqrt(jnp.asarray(D_ATTN, x.dtype))
        score = jax.nn.softmax(jnp.einsum('bhqd,bhkd->bhqk', Qs, Ks) * scale, axis=-1)
        O = jnp.einsum('bhqk,bhkd->bhqd', score, Vs)
        O = O.transpose(0, 2, 1, 3).reshape(b, s, N_ACTIVE * D_ATTN)
        return O @ Wo + bo

    def _L1_attn_ref(x, Wq, Wk, Wv, bias_table, ln_gamma, ln_beta):
        import jax, jax.numpy as jnp
        import numpy as np
        LN_EPS = 1e-05
        B, S, E = x.shape
        H = bias_table.shape[1]
        d = E // H
        scale = E ** (-0.5)
        q = (x @ Wq.T).reshape(B, S, H, d).transpose(0, 2, 1, 3)
        k = (x @ Wk.T).reshape(B, S, H, d).transpose(0, 2, 1, 3)
        v = (x @ Wv.T).reshape(B, S, H, d).transpose(0, 2, 1, 3)
        attn = jax.nn.softmax(jnp.einsum('bhsd,bhtd->bhst', q, k) * scale, axis=-1)
        rel_idx = jnp.arange(S)[:, None] - jnp.arange(S)[None, :] + (S - 1)
        rel_bias = bias_table[rel_idx].transpose(2, 0, 1)
        attn = attn + rel_bias[None]
        out = jnp.einsum('bhst,bhtd->bhsd', attn, v)
        out = out.transpose(0, 2, 1, 3).reshape(B, S, E)
        mu = out.mean(-1, keepdims=True)
        var = out.var(-1, keepdims=True)
        out = (out - mu) * jax.lax.rsqrt(var + LN_EPS) * ln_gamma + ln_beta
        return out

    def _L1_xattn_ref(x_text, x_vision, text_mask, vision_mask, Wq, Wk, Wv, W_film_in, b_film_in, W_film_out, b_film_out, g_norm_in, b_norm_in, g_norm_out, b_norm_out, g_ffn, b_ffn, W1, b1, W2, b2, log_dt, A_re, A_im, C_re, C_im, D_skip, mod_gate):
        import jax, jax.numpy as jnp
        import numpy as np
        B, T, DT, G, DV = (16, 128, 256, 144, 192)
        H, DH = (4, 32)
        INNER = H * DH
        HID = 4 * DT
        N_STATE = 64
        K_TOP = 32

        def layernorm(x, g, b, eps=1e-05):
            m = x.mean(-1, keepdims=True)
            v = x.var(-1, keepdims=True)
            return (x - m) * jax.lax.rsqrt(v + eps) * g + b

        def s4d(x, log_dt, A_re, A_im, C_re, C_im, D_skip):
            Bb, L, D = x.shape
            dt = jnp.exp(log_dt)
            A = A_re + 1j * A_im
            C = C_re + 1j * C_im
            dtA = dt[:, None] * A
            dC = C * (jnp.exp(dtA) - 1.0) / A
            powers = jnp.exp(dtA[:, :, None] * jnp.arange(L))
            K = 2.0 * jnp.einsum('dn,dnl->dl', dC, powers).real
            n = 2 * L
            Kf = jnp.fft.rfft(K, n=n, axis=-1)
            xf = jnp.fft.rfft(x, n=n, axis=1)
            y = jnp.fft.irfft(xf * Kf.T[None], n=n, axis=1)[:, :L]
            return y + x * D_skip
        Bb, Tt, D = x_text.shape
        Gg = x_vision.shape[1]
        Q = (x_text @ Wq).reshape(Bb, Tt, H, DH)
        K = (x_vision @ Wk).reshape(Bb, Gg, H, DH)
        scores = jnp.einsum('bthd,bghd->bhtg', Q, K) / np.sqrt(DH).astype(np.float32)
        scores = jnp.where(vision_mask[:, None, None, :], scores, -jnp.inf)
        topv, topi = jax.lax.top_k(scores, K_TOP)
        probs = jax.nn.softmax(topv, axis=-1)
        bi = jnp.arange(Bb)[:, None, None, None]
        hi = jnp.arange(H)[None, :, None, None]
        ti = jnp.arange(Tt)[None, None, :, None]
        attn = jnp.zeros_like(scores).at[bi, hi, ti, topi].set(probs)
        attn_mean = attn.mean(axis=1)
        V = x_vision @ Wv
        c_t = jnp.einsum('btg,bgd->btd', attn_mean, V)
        c_t = c_t * text_mask[..., None]
        x = layernorm(x_text, g_norm_in, b_norm_in)
        scale_in, shift_in = jnp.split(c_t @ W_film_in + b_film_in, 2, axis=-1)
        x = x * (1.0 + mod_gate * scale_in) + mod_gate * shift_in
        y = s4d(x, log_dt, A_re, A_im, C_re, C_im, D_skip)
        scale_out, shift_out = jnp.split(c_t @ W_film_out + b_film_out, 2, axis=-1)
        y = y * (1.0 + mod_gate * scale_out) + mod_gate * shift_out
        xt = x_text + y
        h = layernorm(xt, g_ffn, b_ffn)
        h = jax.nn.gelu(h @ W1 + b1, approximate=False) @ W2 + b2
        xt = xt + h
        return layernorm(xt, g_norm_out, b_norm_out)

    def _L1_ffn_ref(x, W1, b1, W2, b2, Wr, br):
        import jax, jax.numpy as jnp
        import numpy as np
        E = 8
        K = 2
        D = 256
        P = 1024
        B, S, _ = x.shape
        xf = x.reshape(B * S, D)
        scores = xf @ Wr + br
        _, top_idx = jax.lax.top_k(scores, K)
        mask = jax.nn.one_hot(top_idx, E, dtype=scores.dtype).sum(-2) > 0
        router_weights = jax.nn.softmax(jnp.where(mask, scores, -jnp.inf), axis=-1)
        h = jax.nn.gelu(jnp.einsum('td,edp->etp', xf, W1) + b1[:, None, :])
        y = jnp.einsum('etp,epd->etd', h, W2) + b2[:, None, :]
        out = jnp.einsum('te,etd->td', router_weights, y)
        return out.reshape(B, S, D)
    x = x + _L0_attn_ref(_layernorm(x, axis=-1), L0_attn_w_attn, L0_attn_b_attn, L0_attn_la_attn, L0_attn_lb_attn, L0_attn_w_proj, L0_attn_b_proj, L0_attn_la_proj, L0_attn_lb_proj, L0_attn_kv_scale, L0_attn_kv_zero_point)
    x = x + _L0_xattn_ref(_layernorm(x, axis=-1), ctx_768, L0_xattn_Wq, L0_xattn_Wk, L0_xattn_Wv, L0_xattn_Wo, L0_xattn_bo)
    x = x + _L0_ffn_ref(_layernorm(x, axis=-1), L0_ffn_Wq, L0_ffn_bq, L0_ffn_Wk, L0_ffn_bk, L0_ffn_Wv, L0_ffn_bv, L0_ffn_Wr, L0_ffn_br, L0_ffn_Wo, L0_ffn_bo)
    x = x + _L1_attn_ref(_layernorm(x, axis=-1), L1_attn_Wq, L1_attn_Wk, L1_attn_Wv, L1_attn_bias_table, L1_attn_ln_gamma, L1_attn_ln_beta)
    x = x + _L1_xattn_ref(_layernorm(x, axis=-1), ctx_768, mask_BxS_bf1, mask_BxS2_bf1, L1_xattn_Wq, L1_xattn_Wk, L1_xattn_Wv, L1_xattn_W_film_in, L1_xattn_b_film_in, L1_xattn_W_film_out, L1_xattn_b_film_out, L1_xattn_g_norm_in, L1_xattn_b_norm_in, L1_xattn_g_norm_out, L1_xattn_b_norm_out, L1_xattn_g_ffn, L1_xattn_b_ffn, L1_xattn_W1, L1_xattn_b1, L1_xattn_W2, L1_xattn_b2, L1_xattn_log_dt, L1_xattn_A_re, L1_xattn_A_im, L1_xattn_C_re, L1_xattn_C_im, L1_xattn_D_skip, L1_xattn_mod_gate)
    x = x + _L1_ffn_ref(_layernorm(x, axis=-1), L1_ffn_W1, L1_ffn_b1, L1_ffn_W2, L1_ffn_b2, L1_ffn_Wr, L1_ffn_br)
    return x

_drawn_inputs = setup_inputs


def setup_inputs(seed=0):
    import zlib

    import numpy as np

    out = dict(_drawn_inputs(seed))
    spreads = {'L0_attn_b_attn': (0.0, 0.1),
     'L0_attn_lb_attn': (0.0, 0.402),
     'L0_attn_b_proj': (0.0, 0.1),
     'L0_attn_lb_proj': (0.0, 0.1),
     'L0_xattn_bo': (0.0, 0.1),
     'L0_ffn_bq': (0.0, 0.686),
     'L0_ffn_bk': (0.0, 2.0),
     'L0_ffn_bv': (0.0, 0.1),
     'L0_ffn_br': (0.0, 0.1),
     'L0_ffn_bo': (0.0, 0.1),
     'L1_attn_ln_gamma': (1.0, 0.2),
     'L1_attn_ln_beta': (0.0, 0.1),
     'L1_xattn_b_film_in': (0.0, 0.1),
     'L1_xattn_b_film_out': (0.0, 0.328),
     'L1_xattn_g_norm_in': (1.0, 0.2),
     'L1_xattn_b_norm_in': (0.0, 0.1),
     'L1_xattn_g_norm_out': (1.0, 0.2),
     'L1_xattn_b_norm_out': (0.0, 0.1),
     'L1_xattn_g_ffn': (1.0, 0.6),
     'L1_xattn_b_ffn': (0.0, 2.0),
     'L1_xattn_b1': (0.0, 0.527),
     'L1_xattn_b2': (0.0, 0.32),
     'L1_xattn_A_re': (-0.5, 0.2)}
    factors = {'L0_attn_w_attn': 2.777,
     'L0_attn_la_attn': 3.535,
     'L1_attn_Wq': 8.0,
     'L1_attn_Wk': 8.0,
     'L1_xattn_Wq': 12.898,
     'L1_xattn_Wk': 10.895,
     'L1_xattn_W_film_out': 3.128,
     'L1_ffn_b1': 31.057,
     'L1_ffn_b2': 8.0,
     'L1_ffn_br': 4.716,
     'L1_xattn_W_film_in': 3.277}
    for name, (base, spread) in spreads.items():
        noise = np.random.default_rng([zlib.crc32(name.encode()), seed]).standard_normal(out[name].shape)
        drawn = base * np.exp(spread * noise) if base else spread * noise
        out[name] = jnp.asarray(drawn.astype(out[name].dtype))
    for name, factor in factors.items():
        out[name] = (out[name] * factor).astype(out[name].dtype)
    return out
```

```python
from contextlib import ExitStack

import numpy as np
import concourse.bass as bass
from concourse import mybir

F32 = mybir.dt.float32
BF16 = mybir.dt.bfloat16
I32 = mybir.dt.int32
ALU = mybir.AluOpType
ACT = mybir.ActivationFunctionType
AX = mybir.AxisListType

P = 128
B, S, D = 2, 1024, 256
DC = D // P
TT = B * S // P
TB = S // P
N = 512
NQ = S // N
ROUND = 12582912.0
LN_EPS = 1e-5
NEG = -1.0e30


class Link:

    def __init__(self, eng, sem):
        self.eng, self.sem, self.n = eng, sem, 0

    def __call__(self, ins):
        self.n += 1
        ins.then_inc(self.sem, 1)
        self.eng.wait_ge(self.sem, self.n)


class Stage:

    spent = []
    KEEP = 110

    def __init__(self, nc, name):
        self.nc, self.name, self.ctx, self.sems = nc, name, ExitStack(), []

    def __enter__(self):
        self.ctx.__enter__()
        if len(Stage.spent) > Stage.KEEP:
            self.nc.clear_and_free_semaphores(Stage.spent)
            Stage.spent = []
            self.nc.all_engine_barrier()
        return self

    def __exit__(self, *a):
        Stage.spent += self.sems
        return self.ctx.__exit__(*a)

    def sb(self, name, shape, dt=F32):
        return self.ctx.enter_context(self.nc.sbuf_tensor(f"{self.name}_{name}", shape, dt))

    def ps(self, name, shape, dt=F32):
        return self.ctx.enter_context(self.nc.psum_tensor(f"{self.name}_{name}", shape, dt))

    def sem(self, name):
        self.sems.append(self.nc.alloc_semaphore(f"{self.name}_{name}"))
        return self.sems[-1]

    def block(self):
        return self.nc.Block()


def row(ap, n=P):
    return ap.rearrange("(a n) -> a n", a=1).to_broadcast([n, ap.shape[0]])


def setup(nc, K, x):
    with Stage(nc, "setup") as st:
        loaded, made, zeroed = st.sem("loaded"), st.sem("made"), st.sem("zeroed")
        with st.block() as block:
            @block.sync
            def _(sp):
                for b in range(B):
                    sp.dma_start(K.X[:, b * TB:(b + 1) * TB, :],
                                 x[b].rearrange("(t p) d -> p t d", p=P)).then_inc(loaded, 16)
                sp.wait_ge(loaded, 16 * B)

            @block.gpsimd
            def _(pool):
                pool.memset(K.ident[:], 0.0).then_inc(zeroed, 1)
                pool.memset(K.cmask[:], 0.0).then_inc(zeroed, 1)
                pool.memset(K.cmaskT[:], 0.0).then_inc(zeroed, 1)
                pool.memset(K.ones[:], 1.0).then_inc(zeroed, 1)
                pool.wait_ge(zeroed, 4)
                pool.affine_select(out=K.ident[:], in_=K.ident[:], compare_op=ALU.not_equal, fill=1.0,
                                   base=0, pattern=[[-1, P]], channel_multiplier=1).then_inc(made, 1)
                pool.affine_select(out=K.cmask[:], in_=K.cmask[:], compare_op=ALU.is_ge, fill=NEG,
                                   base=0, pattern=[[-1, P]], channel_multiplier=1).then_inc(made, 1)
                pool.affine_select(out=K.cmaskT[:], in_=K.cmaskT[:], compare_op=ALU.is_ge, fill=NEG,
                                   base=0, pattern=[[-P, N // P], [1, N]], channel_multiplier=-1).then_inc(made, 1)

            @block.vector
            def _(dve):
                dve.wait_ge(made, 1)
                dve.tensor_copy(K.identb[:], K.ident[:]).then_inc(zeroed, 1)
                dve.memset(K.eps[:], LN_EPS).then_inc(zeroed, 1)
                dve.memset(K.onesb[:], 1.0).then_inc(zeroed, 1)


def norm_stats(st, block, K, src, mean_rstd, ready):
    stats = st.sb("stats", [P, TT, 6])
    aggr = st.sb("aggr", [P, TT, 2])
    std = st.sb("std", [P, TT])
    stats_done, aggr_done, std_done = st.sem("stats_done"), st.sem("aggr_done"), st.sem("std_done")

    def on_vector(dve):
        for t in range(TT):
            dve.bn_stats(stats[:, t, :], src[:, t, :]).then_inc(stats_done, 1)
        dve.wait_ge(stats_done, TT)
        for t in range(TT):
            dve.bn_aggr(aggr[:, t, :], stats[:, t, :]).then_inc(aggr_done, 1)
        dve.wait_ge(aggr_done, TT)
        dve.tensor_copy(mean_rstd[:, :, 0], aggr[:, :, 0]).then_inc(ready, 1)
        dve.wait_ge(std_done, 1)
        dve.reciprocal(mean_rstd[:, :, 1], std[:]).then_inc(ready, 1)
        dve.wait_ge(ready, 2)

    def on_scalar(act):
        act.wait_ge(aggr_done, TT)
        act.activation(std[:], aggr[:, :, 1], ACT.Sqrt, bias=K.eps[:, 0:1]).then_inc(std_done, 1)

    return on_vector, on_scalar


def transposer(st, src, dst, width, ident, src_ready):
    pt = st.ps("turned", [P, 4, N])
    turned, moved = st.sem("turned"), st.sem("moved")
    jobs = [(g, c) for g in range(TT // 4) for c in range(width // P)]

    def on_tensor(pe):
        for n, (g, c) in enumerate(jobs):
            src_ready(pe, 4 * g + 3)
            if n >= 4:
                pe.wait_ge(moved, n - 3)
            for k in range(4):
                last = pe.transpose(pt[:, n % 4, k * P:(k + 1) * P], src[:, 4 * g + k, c * P:(c + 1) * P], ident[:])
            last.then_inc(turned, 1)

    def on_scalar(act):
        for n, (g, c) in enumerate(jobs):
            act.wait_ge(turned, n + 1)
            act.copy(dst[:, c, g * N:(g + 1) * N], pt[:, n % 4, :]).then_inc(moved, 1)

    return on_tensor, on_scalar, moved


def layernorm(nc, K, name, src, dst, dstT=None, gamma=None, beta=None):
    with Stage(nc, name) as st:
        mr = st.sb("mean_rstd", [P, TT, 2])
        ready, normed, loaded = st.sem("ready"), st.sem("normed"), st.sem("loaded")
        if gamma is not None:
            gb = st.sb("gb", [P, 2, D])
        with st.block() as block:
            stats_v, stats_s = norm_stats(st, block, K, src, mr, ready)
            passes = 1 if gamma is None else 3
            if dstT is not None:
                turn_t, turn_s, _ = transposer(st, dst, dstT, D, K.ident,
                                               lambda e, t: e.wait_ge(normed, passes * (t + 1)))

            @block.sync
            def _(sp):
                if gamma is not None:
                    sp.dma_start(gb[:, 0, :], row(gamma)).then_inc(loaded, 16)
                    sp.dma_start(gb[:, 1, :], row(beta)).then_inc(loaded, 16)

            @block.vector
            def _(dve):
                stats_v(dve)
                if gamma is not None:
                    dve.wait_ge(loaded, 32)
                for t in range(TT):
                    dve.tensor_scalar(dst[:, t, :], src[:, t, :], mr[:, t, 0:1], mr[:, t, 1:2],
                                      ALU.subtract, ALU.mult).then_inc(normed, 1)
                    if gamma is not None:
                        dve.wait_ge(normed, 3 * t + 1)
                        dve.tensor_tensor(dst[:, t, :], dst[:, t, :], gb[:, 0, :], ALU.mult).then_inc(normed, 1)
                        dve.wait_ge(normed, 3 * t + 2)
                        dve.tensor_tensor(dst[:, t, :], dst[:, t, :], gb[:, 1, :], ALU.add).then_inc(normed, 1)

            @block.scalar
            def _(act):
                stats_s(act)
                if dstT is not None:
                    turn_s(act)

            @block.tensor
            def _(pe):
                if dstT is not None:
                    turn_t(pe)


def split_store(st, K, src, name):
    return [st.sb(f"{name}_{x}", list(src.shape), BF16) for x in ("hi", "mid", "lo")]


def split(link, eng, src, parts):
    hi, mid, lo = parts
    link(eng.tensor_copy(hi, src))
    link(eng.tensor_tensor(src, src, hi, ALU.subtract))
    link(eng.tensor_copy(mid, src))
    link(eng.tensor_tensor(lo, src, mid, ALU.subtract))


HD = 16
NH = D // HD
QBLOCKS = (0, 1, 2, 0, 1, 0)
KBLOCKS = (0, 0, 0, 1, 1, 2)
ROWS = HD * len(QBLOCKS)


def qkv16(nc, K, name, W, XNT, QS, KS, V, weights, bias=None, lora=None, quant=None, transposed=False):
    with Stage(nc, name) as st:
        Wt = st.sb("W", [P, DC, 3 * D])
        QF, KF = st.sb("QF", [P, DC, B * S]), st.sb("KF", [P, DC, B * S])
        qparts, kparts = split_store(st, K, QF, "q"), split_store(st, K, KF, "k")
        pm = st.ps("mm", [P, 6, N])
        pw = st.ps("w", [P, 2, N])
        loaded, wmm, wready = st.sem("loaded"), st.sem("wmm"), st.sem("wready")
        mm, evq, evk, evv = st.sem("mm"), st.sem("evq"), st.sem("evk"), st.sem("evv")
        vlink, plink, stored = st.sem("vlink"), st.sem("plink"), st.sem("stored")
        qsplit, ksplit, inv = st.sem("qsplit"), st.sem("ksplit"), st.sem("inv")
        if transposed:
            Wraw = st.sb("Wraw", [P, 3, DC, D])
        if lora is not None:
            la, lb = st.sb("la", [P, DC, HD]), st.sb("lb", [HD, 3 * D])
            laT = st.sb("laT", [HD, DC, P])
        if bias is not None:
            bqk, bv = st.sb("bqk", [P, 2, DC]), st.sb("bv", [P, D])
        if quant is not None:
            qs = st.sb("quant", [P, 3])
        nload = (3 if transposed else 1) + (2 if lora is not None else 0) + (2 if bias is not None else 0) \
            + (2 if quant is not None else 0)
        qk = [(w, c, t) for w in (0, 1) for c in range(DC) for t in range(B * S // N)]
        vt = list(range(TT // 2))
        jobs = [("qk", j) for j in qk] + [("v", j) for j in vt]
        evac = {"q": 0, "k": 0, "v": 0}
        seen = []
        for kind, j in jobs:
            k = "v" if kind == "v" else "qk"[j[0]]
            evac[k] += 1
            seen.append((k, evac[k]))
        sem_of = {"q": evq, "k": evk, "v": evv}
        with st.block() as block:
            @block.sync
            def _(sp):
                if transposed:
                    for w in range(3):
                        sp.dma_start(Wraw[:, w, :, :], weights[w].rearrange("(c p) n -> p c n", p=P)).then_inc(loaded, 16)
                else:
                    sp.dma_start(Wt[:], weights.rearrange("(c p) n -> p c n", p=P)).then_inc(loaded, 16)
                if lora is not None:
                    sp.dma_start(la[:], lora[0].rearrange("(c p) n -> p c n", p=P)).then_inc(loaded, 16)
                    sp.dma_start(lb[:], lora[1]).then_inc(loaded, 16)
                if bias is not None:
                    sp.dma_start(bqk[:].rearrange("p w c -> p (w c)"),
                                 bias[0:2 * D].rearrange("(w p) -> p w", p=P),
                                 allow_slow_non_contiguous=True).then_inc(loaded, 16)
                    sp.dma_start(bv[:], row(bias[2 * D:3 * D])).then_inc(loaded, 16)
                if quant is not None:
                    sp.dma_start(qs[:, 0:1], row(quant[0])).then_inc(loaded, 16)
                    sp.dma_start(qs[:, 1:2], row(quant[1])).then_inc(loaded, 16)
                stores = 0
                for done, parts, blocks, out in ((qsplit, qparts, QBLOCKS, QS), (ksplit, kparts, KBLOCKS, KS)):
                    sp.wait_ge(done, 4)
                    for j, part in enumerate(blocks):
                        for c in range(DC):
                            sp.dma_start(out[c * P // HD:(c + 1) * P // HD, j * HD:(j + 1) * HD, :],
                                         parts[part][:, c, :]).then_inc(stored, 16)
                            stores += 1
                sp.wait_ge(stored, 16 * stores)

            @block.tensor
            def _(pe):
                pe.wait_ge(loaded, 16 * nload)
                n = 0
                if transposed:
                    for w in range(3):
                        if n >= 2:
                            pe.wait_ge(wready, n - 1)
                        for ci in range(DC):
                            for co in range(DC):
                                last = pe.transpose(pw[:, n % 2, ci * D + co * P:ci * D + (co + 1) * P],
                                                    Wraw[:, w, co, ci * P:(ci + 1) * P], K.ident[:])
                        last.then_inc(wmm, 1)
                        n += 1
                if lora is not None:
                    for c in range(DC):
                        last = pe.transpose(pw[0:HD, 0, c * P:(c + 1) * P], la[:, c, :], K.ident[:])
                    last.then_inc(wmm, 1)
                    for c in range(DC):
                        for h in range(2):
                            n += 1
                            pe.wait_ge(wready, n)
                            pe.matmul(pw[:, n % 2, 0:3 * D // 2], laT[:, c, :], lb[:, h * 3 * D // 2:(h + 1) * 3 * D // 2],
                                      start=True, stop=True).then_inc(wmm, 1)
                    n += 1
                pe.wait_ge(wready, n)
                for m, (kind, j) in enumerate(jobs):
                    if m >= 6:
                        pe.wait_ge(sem_of[seen[m - 6][0]], seen[m - 6][1])
                    if kind == "qk":
                        w, c, t = j
                        for ci in range(DC):
                            last = pe.matmul(pm[:, m % 6, :], Wt[:, ci, w * D + c * P:w * D + (c + 1) * P],
                                             XNT[:, ci, t * N:(t + 1) * N], start=ci == 0, stop=ci == DC - 1)
                    else:
                        for k in range(2):
                            for ci in range(DC):
                                last = pe.matmul(pm[:, m % 6, k * D:(k + 1) * D],
                                                 XNT[:, ci, (2 * j + k) * P:(2 * j + k + 1) * P],
                                                 Wt[:, ci, 2 * D:3 * D], start=ci == 0, stop=ci == DC - 1)
                    last.then_inc(mm, 1)

            @block.scalar
            def _(act):
                if lora is not None:
                    act.wait_ge(wmm, 1)
                    act.mul(laT[:], pw[0:HD, 0, 0:D].rearrange("p (c n) -> p c n", c=DC), 2.0).then_inc(wready, 1)
                if bias is not None:
                    act.wait_ge(loaded, 16 * nload)
                for m, (kind, j) in enumerate(jobs):
                    if kind == "qk" and j[0] == 0:
                        _, c, t = j
                        act.wait_ge(mm, m + 1)
                        dst = QF[:, c, t * N:(t + 1) * N]
                        if bias is not None:
                            act.activation(dst, pm[:, m % 6, :], ACT.Identity, bias=bqk[:, 0, c:c + 1]).then_inc(evq, 1)
                        else:
                            act.copy(dst, pm[:, m % 6, :]).then_inc(evq, 1)

            @block.gpsimd
            def _(pool):
                pool.wait_ge(evq, len(qk) // 2)
                split(Link(pool, qsplit), pool, QF[:], [x[:] for x in qparts])

            @block.vector
            def _(dve):
                if transposed:
                    for w in range(3):
                        dve.wait_ge(wmm, w + 1)
                        dve.tensor_copy(Wt[:, :, w * D:(w + 1) * D],
                                        pw[:, w % 2, :].rearrange("p (c n) -> p c n", c=DC)).then_inc(wready, 1)
                if lora is not None:
                    n = 1
                    for c in range(DC):
                        for h in range(2):
                            cols = slice(h * 3 * D // 2, (h + 1) * 3 * D // 2)
                            dve.wait_ge(wmm, n + 1)
                            dve.tensor_tensor(Wt[:, c, cols], Wt[:, c, cols], pw[:, n % 2, 0:3 * D // 2],
                                              ALU.add).then_inc(wready, 1)
                            n += 1
                if quant is not None:
                    dve.wait_ge(loaded, 16 * nload)
                    dve.reciprocal(qs[:, 2:3], qs[:, 0:1]).then_inc(inv, 1)
                    dve.wait_ge(inv, 1)
                for m, (kind, j) in enumerate(jobs):
                    if kind == "qk" and j[0] == 1:
                        _, c, t = j
                        dve.wait_ge(mm, m + 1)
                        dst = KF[:, c, t * N:(t + 1) * N]
                        if bias is not None:
                            dve.tensor_scalar(dst, pm[:, m % 6, :], bqk[:, 1, c:c + 1], None, ALU.add).then_inc(evk, 1)
                        else:
                            dve.tensor_copy(dst, pm[:, m % 6, :]).then_inc(evk, 1)
                    if kind == "v":
                        dve.wait_ge(mm, m + 1)
                        dst = V[:, 2 * j:2 * j + 2, :]
                        src = pm[:, m % 6, :].rearrange("p (k n) -> p k n", k=2)
                        if bias is not None:
                            dve.tensor_tensor(dst, src, bv[:].rearrange("p (a n) -> p a n", a=1).to_broadcast([P, 2, D]),
                                              ALU.add).then_inc(evv, 1)
                        else:
                            dve.tensor_copy(dst, src).then_inc(evv, 1)
                dve.wait_ge(evk, len(qk) // 2)
                dve.wait_ge(evv, len(vt))
                link = Link(dve, vlink)
                if quant is not None:
                    for y in (KF[:], V[:]):
                        link(dve.tensor_scalar(y, y, qs[:, 2:3], qs[:, 1:2], ALU.mult, ALU.add))
                        link(dve.tensor_scalar(y, y, ROUND, ROUND, ALU.add, ALU.subtract))
                        link(dve.tensor_scalar(y, y, 0.0, 255.0, ALU.max, ALU.min))
                        link(dve.tensor_scalar(y, y, qs[:, 1:2], qs[:, 0:1], ALU.subtract, ALU.mult))
                split(Link(dve, ksplit), dve, KF[:], [x[:] for x in kparts])


def attention(nc, K, name, heads, scale, dv, kp, kt, causal, qsrc, ksrc, pairs, V, Y, staged):
    nk = kp * kt
    narrow = dv == HD
    vw = 32 if narrow else dv + 1
    chunks = []
    for qt in range(TB):
        end = (qt + 1) * P if causal else nk
        chunks += [(qt, k0, min(N, end - k0)) for k0 in range(0, end, N)]
    nm = len(chunks)
    steps = []
    for qh in range(NQ):
        last = (qh + 1) * (N // P) if causal else kt
        steps += [(qh, (a, a + 1)) for a in range(0, last, 2)]
    ns = len(steps)
    per = 2 if kt > 2 else 1
    ng = ns // per
    first_of = [min(n for n, s in enumerate(steps) if s[0] == qh) for qh in range(NQ)]
    last_of = [max(n for n, s in enumerate(steps) if s[0] == qh) for qh in range(NQ)]
    UB = 4
    NI = heads // 2
    nq, nkk = len(qsrc), len(ksrc)
    kr = qsrc[0][1]
    with Stage(nc, name) as st:
        if staged:
            Qs = [st.sb(f"Q{j}", [P, UB, S], BF16) for j in range(nq)]
            Ks = [st.sb(f"K{j}", [P, UB, nk], BF16) for j in range(nkk)]

        def operand(staging, source, length, i, u, c0, c1):
            if staged:
                return staging[0:kr, u, c0:c1]
            start = (u % 2) * length
            return source[:, bass.ds(i * 2 + u // 2, 1), start + c0:start + c1].rearrange("p a n -> p (a n)")

        def q_of(j, i, u, c0, c1):
            return operand(Qs[j] if staged else None, qsrc[j][0], S, i, u, c0, c1)

        def k_of(j, i, u, c0, c1):
            return operand(Ks[j] if staged else None, ksrc[j][0], nk, i, u, c0, c1)
        Vs = st.sb("V", [kp, UB, kt, vw])
        Pr = st.sb("P", [kp, 2, 2 * per, N])
        MD = st.sb("MD", [P, 2, S], BF16)
        mxc = st.sb("mxc", [P, TB, 2])
        mneg = st.sb("mneg", [P, TB])
        OT = st.sb("OT", [P, NQ, N])
        rc = st.sb("rc", [P, NQ, N // P])
        sel = st.sb("sel", [P, dv + 1])
        SM, ST = st.ps("SM", [P, 2, N]), st.ps("ST", [P, 2, 2, N])
        OP, OUT = st.ps("OP", [P, N]), st.ps("OUT", [P, N // P, P])
        ld = [st.sem(f"operands{j}") for j in range(2)]
        mx_ready, mx_read, md_ready = st.sem("mx_ready"), st.sem("mx_read"), st.sem("md_ready")
        comb, st_ready, exp_done, pv_done = st.sem("comb"), st.sem("st_ready"), st.sem("exp_done"), st.sem("pv_done")
        ot_done, out_ready, rc_done, y_done = st.sem("ot_done"), st.sem("out_ready"), st.sem("rc_done"), st.sem("y_done")
        v_ready, fixed, sel_done = st.sem("v_ready"), st.sem("fixed"), st.sem("sel_done")
        comb_init = st.sem("comb_init")
        nd = nq + nkk

        def following(i, u):
            return (i, u + 1) if u < UB - 1 else (i + 1, 0)

        with st.block() as block:
            @block.sync
            def _(sp):
                def load(i, hp):
                    head = i * 2 + hp
                    for j in range(nq):
                        sp.dma_start(Qs[j][0:kr, 2 * hp:2 * hp + 2, :], qsrc[j][0](head)).then_inc(ld[hp], 16)
                    for j in range(nkk):
                        sp.dma_start(Ks[j][0:kr, 2 * hp:2 * hp + 2, :], ksrc[j][0](head)).then_inc(ld[hp], 16)

                if not staged:
                    return
                for hp in range(2):
                    load(0, hp)
                with sp.Fori(1, NI, 1) as i:
                    for hp in range(2):
                        sp.wait_ge(st_ready, (i * UB + 2 * hp + 2 - UB) * ns)
                        load(i, hp)

            @block.gpsimd
            def _(pool):
                if narrow:
                    pool.memset(sel[:], 0.0).then_inc(sel_done, 1)
                    pool.wait_ge(sel_done, 1)
                    for j in range(4):
                        pool.affine_select(out=sel[:], in_=sel[:], compare_op=ALU.not_equal, fill=1.0,
                                           base=-32 * j, pattern=[[-1, dv + 1]], channel_multiplier=1).then_inc(sel_done, 1)
                        pool.wait_ge(sel_done, j + 2)
                    pool.memset(Vs[:], 0.0).then_inc(fixed, 1)
                    pool.wait_ge(fixed, 1)
                    pool.memset(Vs[:, :, :, dv:dv + 1], 1.0).then_inc(fixed, 1)
                else:
                    pool.memset(Vs[:, :, :, dv:dv + 1], 1.0).then_inc(fixed, 2)
                    pool.tensor_copy(sel[:], K.ident[:, 0:dv + 1]).then_inc(sel_done, 5)
                pool.wait_ge(fixed, 2)

                def copy_v(i, hp):
                    head = i * 2 + hp
                    for b in range(B):
                        pool.tensor_copy(Vs[:, 2 * hp + b, :, 0:dv], V(b, head)).then_inc(v_ready, 1)

                for hp in range(2):
                    copy_v(0, hp)
                with pool.Fori(1, NI, 1) as i:
                    for hp in range(2):
                        pool.wait_ge(pv_done, (i * UB + 2 * hp + 2 - UB) * ng + 2)
                        copy_v(i, hp)

            @block.tensor
            def _(pe):
                def maxima(i, u, some):
                    U = i * UB + u
                    for c in some:
                        qt, k0, kn = chunks[c]
                        if c == 0 and staged:
                            pe.wait_ge(ld[u // 2], (i + 1) * (16 * nd))
                        pe.wait_ge(mx_read, U * nm + c + 1)
                        diag = causal and k0 + kn == (qt + 1) * P
                        parts = [(0, kn, False)] if not diag else [(0, kn - P, False)] * (kn > P) + [(kn - P, kn, True)]
                        for c0, c1, masked in parts:
                            out = SM[:, (u * nm + c) % 2, c0:c1]
                            for n, (a, b_) in enumerate(pairs):
                                last = pe.matmul(out, q_of(a, i, u, qt * P, (qt + 1) * P),
                                                 k_of(b_, i, u, k0 + c0, k0 + c1),
                                                 start=n == 0, stop=n == len(pairs) - 1 and not masked)
                            if masked:
                                last = pe.matmul(out, K.identb[:], K.cmask[:], start=False, stop=True)
                        last.then_inc(mx_ready, 1)

                def scores(i, u, n):
                    U = i * UB + u
                    qh, kts = steps[n]
                    if n == 0:
                        pe.wait_ge(md_ready, U + 1)
                    pe.wait_ge(exp_done, U * ns + n + 1)
                    for j, k in enumerate(kts):
                        out = ST[0:kp, (u * ns + n) % 2, j, :]
                        for m, (a, b_) in enumerate(pairs):
                            pe.matmul(out, k_of(b_, i, u, k * kp, (k + 1) * kp), q_of(a, i, u, qh * N, (qh + 1) * N),
                                      start=m == 0, stop=False)
                        if causal and k >= qh * (N // P):
                            pe.matmul(out, K.identb[:], K.cmaskT[:, k - qh * (N // P), :], start=False, stop=False)
                        last = pe.matmul(out, K.onesb[:, 0:kp], MD[:, u % 2, qh * N:(qh + 1) * N], start=False, stop=True)
                    last.then_inc(st_ready, 1)

                def values(i, u, g):
                    U = i * UB + u
                    mine = steps[g * per:(g + 1) * per]
                    qh = mine[0][0]
                    if g == 0:
                        pe.wait_ge(v_ready, U + 1)
                    if g * per == first_of[qh]:
                        pe.wait_ge(ot_done, 2 * U + qh)
                    pe.wait_ge(exp_done, U * ns + (g + 1) * per + 2)
                    for m, (_, kts) in enumerate(mine):
                        for j, k in enumerate(kts):
                            p = Pr[:, (u * ng + g) % 2, 2 * m + j, :]
                            lastg = (g + 1) * per - 1 == last_of[qh]
                            if narrow:
                                out = OP[32 * (k % 4):32 * (k % 4) + 32, :]
                                last = pe.matmul(out, Vs[:, u, k, :], p, start=k < 4, stop=lastg)
                            else:
                                last = pe.matmul(OP[0:vw, :], Vs[:, u, k, :], p, start=k == 0,
                                                 stop=lastg and k == kts[-1] and m == per - 1)
                    last.then_inc(pv_done, 1)

                def outputs(i, u, qh):
                    U = i * UB + u
                    rows = P if narrow else vw
                    pe.wait_ge(ot_done, 2 * U + qh + 1)
                    pe.wait_ge(y_done, 2 * U + qh)
                    for t in range(N // P):
                        last = pe.matmul(OUT[:, t, 0:dv + 1], OT[0:rows, qh, t * P:(t + 1) * P], sel[0:rows, :],
                                         start=True, stop=True)
                    last.then_inc(out_ready, 1)

                def unit(i, u, last):
                    more = chunks and not last
                    ni, nu = following(i, u)
                    done = 0
                    for n in range(ns):
                        scores(i, u, n)
                        if more:
                            upto = nm * (n + 1) // ns
                            maxima(ni, nu, range(done, upto))
                            done = upto
                        if (n + 1) % per == 0 and n >= per:
                            values(i, u, (n + 1) // per - 2)
                        if n == last_of[0] + 1 + per:
                            outputs(i, u, 0)
                    values(i, u, ng - 1)
                    if last_of[1] < last_of[0] + 1 + per:
                        outputs(i, u, 0)
                    outputs(i, u, 1)

                pe.wait_ge(fixed, 2)
                pe.wait_ge(sel_done, 5)
                maxima(0, 0, range(nm))
                with pe.Fori(0, NI - 1, 1) as i:
                    for u in range(UB):
                        unit(i, u, False)
                for u in range(UB):
                    unit(NI - 1, u, u == UB - 1)

            @block.scalar
            def _(act):
                act.sem_inc(exp_done, 2)
                act.sem_inc(pv_done, 2)

                def turned(i, u, qh):
                    U = i * UB + u
                    rows = P if narrow else vw
                    act.wait_ge(pv_done, U * ng + (last_of[qh] + 1) // per + 2)
                    act.wait_ge(y_done, 2 * U)
                    act.copy(OT[0:rows, qh, :], OP[0:rows, :]).then_inc(ot_done, 1)

                def unit(i, u):
                    U = i * UB + u
                    for n in range(ns):
                        g = n // per
                        act.wait_ge(st_ready, U * ns + n + 1)
                        act.wait_ge(pv_done, U * ng + g + 1)
                        act.activation(Pr[:, (u * ng + g) % 2, 2 * (n % per):2 * (n % per) + 2, :],
                                       ST[0:kp, (u * ns + n) % 2, :, :], ACT.Exp, scale=scale).then_inc(exp_done, 1)
                        if n == last_of[0] + per:
                            turned(i, u, 0)
                    if last_of[1] < last_of[0] + per:
                        turned(i, u, 0)
                    turned(i, u, 1)

                with act.Fori(0, NI, 1) as i:
                    for u in range(UB):
                        unit(i, u)

            @block.vector
            def _(dve):
                dve.sem_inc(mx_read, 2)

                def maxima(i, u, some):
                    U = i * UB + u
                    for c in some:
                        qt, k0, kn = chunks[c]
                        dve.wait_ge(mx_ready, U * nm + c + 1)
                        dve.tensor_reduce(mxc[:, qt, k0 // N:k0 // N + 1], SM[:, (u * nm + c) % 2, 0:kn],
                                          AX.X, ALU.max).then_inc(mx_read, 1)

                def diagonal(i, u, first=False):
                    U = i * UB + u
                    dve.wait_ge(mx_read, (U + 1) * nm + 2)
                    dve.wait_ge(md_ready, U)
                    dve.tensor_reduce(mneg[:], mxc[:], AX.X, ALU.max, negate=True).then_inc(comb, 1)
                    dve.wait_ge(comb, U + 1)
                    if not first:
                        dve.wait_ge(st_ready, (U - 1) * ns)
                    for t in range(TB):
                        last = dve.tensor_scalar(MD[:, u % 2, t * P:(t + 1) * P], K.identb[:], mneg[:, t:t + 1],
                                                 None, ALU.mult)
                    last.then_inc(md_ready, 1)

                def result(i, u, qh):
                    U = i * UB + u
                    head = i * 2 + u // 2
                    dve.wait_ge(out_ready, 2 * U + qh + 1)
                    dve.reciprocal(rc[:, qh, :], OUT[:, :, dv]).then_inc(rc_done, 1)
                    dve.wait_ge(rc_done, 2 * U + qh + 1)
                    t0 = (u % 2) * TB + qh * (N // P)
                    dve.tensor_tensor(Y[:, t0:t0 + N // P, bass.ds(head * dv, dv)], OUT[:, :, 0:dv],
                                      rc[:, qh, :].rearrange("p (t a) -> p t a", a=1).to_broadcast([P, N // P, dv]),
                                      ALU.mult).then_inc(y_done, 1)

                def unit(i, u, last):
                    ni, nu = following(i, u)
                    split_at = nm * min(last_of[0] + 2 + per, ns) // ns
                    if not last:
                        maxima(ni, nu, range(split_at))
                        if split_at < nm:
                            result(i, u, 0)
                        maxima(ni, nu, range(split_at, nm))
                        diagonal(ni, nu)
                        if split_at == nm:
                            result(i, u, 0)
                    else:
                        result(i, u, 0)
                    result(i, u, 1)

                dve.memset(mxc[:], -3.0e38).then_inc(comb_init, 1)
                dve.wait_ge(comb_init, 1)
                maxima(0, 0, range(nm))
                diagonal(0, 0, True)
                with dve.Fori(0, NI - 1, 1) as i:
                    for u in range(UB):
                        unit(i, u, False)
                for u in range(UB):
                    unit(NI - 1, u, u == UB - 1)
                dve.wait_ge(y_done, 2 * UB * NI)




def project(nc, K, name, Y, width, weight, bias, lora=None):
    WC = width // P
    with Stage(nc, name) as st:
        YT = st.sb("YT", [P, WC, B * S])
        Wt = st.sb("W", [P, WC, D])
        brow = st.sb("bias", [P, D])
        pm, pw = st.ps("mm", [P, 3, 2, D]), st.ps("w", [P, D])
        loaded, wmm, wready, biased = st.sem("loaded"), st.sem("wmm"), st.sem("wready"), st.sem("biased")
        mm, added = st.sem("mm"), st.sem("added")
        if lora is not None:
            la, lb, laT = st.sb("la", [P, DC, HD]), st.sb("lb", [HD, D]), st.sb("laT", [HD, D])
        nload = 2 + (2 if lora is not None else 0)
        with st.block() as block:
            turn_t, turn_s, moved = transposer(st, Y, YT, width, K.ident, lambda e, t: None)
            turns = TT // 4 * WC

            @block.sync
            def _(sp):
                sp.dma_start(Wt[:], weight.rearrange("(c p) n -> p c n", p=P)).then_inc(loaded, 16)
                sp.dma_start(brow[:], row(bias)).then_inc(loaded, 16)
                if lora is not None:
                    sp.dma_start(la[:], lora[0].rearrange("(c p) n -> p c n", p=P)).then_inc(loaded, 16)
                    sp.dma_start(lb[:], lora[1]).then_inc(loaded, 16)

            @block.tensor
            def _(pe):
                pe.wait_ge(loaded, 16 * nload)
                if lora is not None:
                    for c in range(DC):
                        last = pe.transpose(pw[0:HD, c * P:(c + 1) * P], la[:, c, :], K.ident[:])
                    last.then_inc(wmm, 1)
                    for c in range(DC):
                        pe.wait_ge(wready, c + 1)
                        pe.matmul(pw[:], laT[:, c * P:(c + 1) * P], lb[:], start=True, stop=True).then_inc(wmm, 1)
                turn_t(pe)
                pe.wait_ge(moved, turns)
                if lora is not None:
                    pe.wait_ge(wready, 1 + DC)
                for j in range(TT // 2):
                    if j >= 3:
                        pe.wait_ge(added, j - 2)
                    for k in range(2):
                        for c in range(WC):
                            t = 2 * j + k
                            last = pe.matmul(pm[:, j % 3, k, :], YT[:, c, t * P:(t + 1) * P], Wt[:, c, :],
                                             start=c == 0, stop=c == WC - 1)
                    last.then_inc(mm, 1)

            @block.scalar
            def _(act):
                if lora is not None:
                    act.wait_ge(wmm, 1)
                    act.mul(laT[:], pw[0:HD, :], 2.0).then_inc(wready, 1)
                turn_s(act)

            @block.vector
            def _(dve):
                dve.wait_ge(loaded, 16 * nload)
                if lora is not None:
                    for c in range(DC):
                        dve.wait_ge(wmm, c + 2)
                        dve.tensor_tensor(Wt[:, c, :], Wt[:, c, :], pw[:], ALU.add).then_inc(wready, 1)
                dve.tensor_tensor(K.X[:], K.X[:], brow[:].rearrange("p (a n) -> p a n", a=1).to_broadcast([P, TT, D]),
                                  ALU.add).then_inc(biased, 1)
                dve.wait_ge(biased, 1)
                for j in range(TT // 2):
                    dve.wait_ge(mm, j + 1)
                    dve.tensor_tensor(K.X[:, 2 * j:2 * j + 2, :], K.X[:, 2 * j:2 * j + 2, :], pm[:, j % 3, :, :],
                                      ALU.add).then_inc(added, 1)


WD = 64
CT_P, CT_N = 77, 2
CL = CT_P * CT_N
CW, CW_P, CW_N = 192, 96, 2


def context(nc, K, ctx):
    with Stage(nc, "context") as st:
        raw = st.sb("raw", [CT_P, B * CT_N, CW])
        pt = st.ps("turned", [CW_P, CW_N, N])
        loaded, turned, moved = st.sem("loaded"), st.sem("turned"), st.sem("moved")
        with st.block() as block:
            @block.sync
            def _(sp):
                sp.dma_start(raw[:], ctx.rearrange("b (t p) w -> p (b t) w", p=CT_P)).then_inc(loaded, 16)

            @block.tensor
            def _(pe):
                pe.wait_ge(loaded, 16)
                for c in range(CW_N):
                    for t in range(B * CT_N):
                        last = pe.transpose(pt[:, c, t * CT_P:(t + 1) * CT_P], raw[:, t, c * CW_P:(c + 1) * CW_P],
                                            K.ident[0:CT_P, 0:CT_P])
                last.then_inc(turned, 1)

            @block.vector
            def _(dve):
                dve.wait_ge(turned, 1)
                dve.tensor_copy(K.CT[:], pt[:, :, 0:B * CL]).then_inc(moved, 1)


def stacks64(nc, K, name, kind, W, kp, src, jobs, out, bias=None):
    H = WD
    w0 = max(n for _, _, n, _, _ in jobs)
    with Stage(nc, name) as st:
        R = st.sb("R", [P, 4, w0])
        pm = st.ps("mm", [P, 4, N])
        mm, ev, done, rdone, q1, q2 = (st.sem(x) for x in ("mm", "ev", "done", "rdone", "q1", "q2"))
        with st.block() as block:
            @block.tensor
            def _(pe):
                for m, (w, c0, n, dh, d0) in enumerate(jobs):
                    if m >= 4:
                        pe.wait_ge(ev, m - 3)
                    nc_ = W.shape[1]
                    for c in range(nc_):
                        last = pe.matmul(pm[:, m % 4, 0:n], W[0:kp, c, w, :], src[0:kp, c, c0:c0 + n],
                                         start=c == 0, stop=c == nc_ - 1)
                    last.then_inc(mm, 1)

            @block.scalar
            def _(act):
                for m, (w, c0, n, dh, d0) in enumerate(jobs):
                    act.wait_ge(mm, m + 1)
                    if m >= 4:
                        act.wait_ge(done, m - 3)
                        act.wait_ge(q2, m - 3)
                    if bias is None:
                        act.copy(R[:, m % 4, 0:n], pm[:, m % 4, 0:n]).then_inc(ev, 1)
                    else:
                        act.activation(R[:, m % 4, 0:n], pm[:, m % 4, 0:n], ACT.Identity,
                                       bias=bias[:, w:w + 1]).then_inc(ev, 1)

            @block.vector
            def _(dve):
                for m, (w, c0, n, dh, d0) in enumerate(jobs):
                    o = [x[:, dh, d0:d0 + n] for x in out]
                    r = R[:, m % 4, 0:n]
                    dve.wait_ge(ev, m + 1)
                    dve.tensor_copy(o[0], r).then_inc(q1, 1)
                    dve.wait_ge(q1, m + 1)
                    dve.tensor_tensor(r, r, o[0], ALU.subtract).then_inc(rdone, 1)
                    dve.wait_ge(rdone, m + 1)
                    if kind == "q":
                        dve.tensor_copy(o[0][H:P], r[H:P]).then_inc(done, 1)
                    else:
                        dve.tensor_copy(o[1], r).then_inc(done, 1)

            @block.gpsimd
            def _(pool):
                for m, (w, c0, n, dh, d0) in enumerate(jobs):
                    o = [x[:, dh, d0:d0 + n] for x in out]
                    r = R[:, m % 4, 0:n]
                    if kind == "q":
                        pool.wait_ge(q1, m + 1)
                        pool.tensor_copy(o[1][0:H], o[0][0:H])
                        pool.wait_ge(done, m + 1)
                        pool.tensor_tensor(o[1][H:P], r[H:P], o[0][H:P], ALU.subtract).then_inc(q2, 1)
                    else:
                        pool.wait_ge(q1, m + 1)
                        pool.tensor_copy(o[2][H:P], o[0][H:P])
                        pool.wait_ge(done, m + 1)
                        pool.tensor_tensor(o[2][0:H], r[0:H], o[1][0:H], ALU.subtract).then_inc(q2, 1)


def cross_values(nc, K, name, Wv, width, V):
    with Stage(nc, name) as st:
        Wt = st.sb("W", [CW_P, CW_N, width])
        pm = st.ps("mm", [CT_P, 4, N])
        loaded, mm, ev = st.sem("loaded"), st.sem("mm"), st.sem("ev")
        with st.block() as block:
            @block.sync
            def _(sp):
                sp.dma_start(Wt[:], Wv.rearrange("(c p) n -> p c n", p=CW_P)).then_inc(loaded, 16)

            @block.tensor
            def _(pe):
                pe.wait_ge(loaded, 16)
                for t in range(B * CT_N):
                    for c in range(CW_N):
                        last = pe.matmul(pm[:, t, 0:width], K.CT[:, c, t * CT_P:(t + 1) * CT_P], Wt[:, c, :],
                                         start=c == 0, stop=c == CW_N - 1)
                    last.then_inc(mm, 1)

            @block.vector
            def _(dve):
                for t in range(B * CT_N):
                    dve.wait_ge(mm, t + 1)
                    dve.tensor_copy(V[:, t, :], pm[:, t, 0:width]).then_inc(ev, 1)


def load_twice(nc, K, name, pairs):
    with Stage(nc, name) as st:
        loaded = st.sem("loaded")
        with st.block() as block:
            @block.sync
            def _(sp):
                n = 0
                for dst, src, p in pairs:
                    for c in range(dst.shape[1]):
                        for twice in range(2):
                            sp.dma_start(dst[:, c, :, twice * WD:(twice + 1) * WD],
                                         src[c * p:(c + 1) * p, :].rearrange("p (h n) -> p h n", n=WD)).then_inc(loaded, 16)
                            n += 1
                sp.wait_ge(loaded, 16 * n)


def cross_attention(nc, K, a):
    H = 8
    with ExitStack() as ctx:
        def sb(name, shape, dt=F32):
            return ctx.enter_context(nc.sbuf_tensor(name, shape, dt))
        QA, QB = sb("c0_QA", [P, H, B * S], BF16), sb("c0_QB", [P, H, B * S], BF16)
        KK = [sb(f"c0_K{x}", [P, H, B * CL], BF16) for x in "ABC"]
        V = sb("c0_values", [CT_P, B * CT_N, H * WD])
        with nc.sbuf_tensor("c0_Wq", [P, DC, H, P], F32) as Wq, nc.sbuf_tensor("c0_Wk", [CW_P, CW_N, H, P], F32) as Wk:
            load_twice(nc, K, "c0_w", [(Wq, a["L0_xattn_Wq"], P), (Wk, a["L0_xattn_Wk"], CW_P)])
            cross_values(nc, K, "c0_v", a["L0_xattn_Wv"], H * WD, V)
            stacks64(nc, K, "c0_q", "q", Wq, P, K.XNT,
                     [(h, t * N, N, h, t * N) for h in range(H) for t in range(B * S // N)], [QA, QB])
            stacks64(nc, K, "c0_k", "k", Wk, CW_P, K.CT, [(h, 0, B * CL, h, 0) for h in range(H)], KK)
        Y = K.wide

        attention(nc, K, "c0", H, WD ** -0.5, WD, CT_P, CT_N, False, [(QA, P), (QB, P)],
                  [(x, P) for x in KK], [(0, 0), (0, 1), (1, 2)],
                  lambda b, h: V[:, b * CT_N:(b + 1) * CT_N, bass.ds(h * WD, WD)], Y, False)
    project(nc, K, "c0_out", Y, H * WD, a["L0_xattn_Wo"], a["L0_xattn_bo"])


def ranks(link, dve, scores, others, earlier, greater, equal, rank):
    link(dve.tensor_tensor(greater, others, scores, ALU.is_gt))
    link(dve.tensor_tensor(equal, others, scores, ALU.is_equal))
    link(dve.tensor_tensor(equal, equal, earlier, ALU.mult))
    link(dve.tensor_tensor(greater, greater, equal, ALU.add))
    link(dve.tensor_reduce(rank, greater, AX.X, ALU.add))


def choose_heads(nc, K, Wr, br, chosen, active):
    H = Wr.shape[1]
    with Stage(nc, "choose") as st:
        total = st.sb("total", [P, DC, B])
        W, brow = st.sb("W", [P, DC, H]), st.sb("br", [1, H])
        lg, rank, sel = st.sb("logits", [1, B, H]), st.sb("rank", [1, B, H]), st.sb("sel", [1, B, H])
        g, e = st.sb("g", [1, B * H, H]), st.sb("e", [1, B * H, H])
        earlier, place = st.sb("earlier", [1, B * H, H]), st.sb("place", [1, B, H])
        index, idx = st.sb("index", [1, B, H]), st.sb("idx", [1, B, active])
        hit = st.sb("hit", [1, B, H])
        pm = st.ps("mm", [1, B, H])
        loaded, summed, mm, chain, made = (st.sem(x) for x in ("loaded", "summed", "mm", "chain", "made"))
        with st.block() as block:
            @block.sync
            def _(sp):
                sp.dma_start(W[:], Wr.rearrange("(c p) n -> p c n", p=P)).then_inc(loaded, 16)
                sp.dma_start(brow[:], br.rearrange("(a n) -> a n", a=1)).then_inc(loaded, 16)

            @block.gpsimd
            def _(pool):
                pool.memset(earlier[:], 1.0).then_inc(made, 1)
                pool.wait_ge(made, 1)
                for b in range(B):
                    v = earlier[:, b * H:(b + 1) * H, :]
                    pool.affine_select(out=v, in_=v, compare_op=ALU.is_gt, fill=0.0, base=0,
                                       pattern=[[1, H], [-1, H]], channel_multiplier=0).then_inc(made, 1)
                pool.iota(index[:], pattern=[[0, B], [1, H]], base=0, channel_multiplier=0,
                          allow_small_or_imprecise_dtypes=True).then_inc(made, 1)

            @block.vector
            def _(dve):
                dve.tensor_reduce(total[:], K.XNT[:].rearrange("p c (b n) -> p c b n", b=B), AX.X,
                                  ALU.add).then_inc(summed, 1)
                dve.wait_ge(mm, 1)
                dve.wait_ge(made, 2 + B)
                link = Link(dve, chain)
                link(dve.tensor_scalar(lg[:], pm[:], 1.0 / S, None, ALU.mult))
                link(dve.tensor_tensor(lg[:], lg[:], brow[:].rearrange("p (a h) -> p a h", a=1).to_broadcast([1, B, H]),
                                       ALU.add))
                for b in range(B):
                    v = slice(b * H, (b + 1) * H)
                    mine = lg[:, b, :].rearrange("p (h a) -> p h a", a=1).to_broadcast([1, H, H])
                    others = lg[:, b:b + 1, :].to_broadcast([1, H, H])
                    ranks(link, dve, mine, others, earlier[:, v, :], g[:, v, :], e[:, v, :], rank[:, b, :])
                link(dve.tensor_scalar(sel[:], rank[:], float(active), None, ALU.is_lt))
                for b in range(B):
                    v = slice(b * H, (b + 1) * H)
                    link(dve.tensor_tensor(e[:, v, :], sel[:, b:b + 1, :].to_broadcast([1, H, H]), earlier[:, v, :],
                                           ALU.mult))
                    link(dve.tensor_reduce(place[:, b, :], e[:, v, :], AX.X, ALU.add))
                link(dve.tensor_tensor(index[:], index[:], sel[:], ALU.mult))
                for k in range(active):
                    link(dve.tensor_scalar(hit[:], place[:], float(k), None, ALU.is_equal))
                    link(dve.tensor_tensor(hit[:], hit[:], index[:], ALU.mult))
                    link(dve.tensor_reduce(idx[:, :, k], hit[:], AX.X, ALU.add))
                link(dve.tensor_copy(chosen[:], idx[:]))

            @block.tensor
            def _(pe):
                pe.wait_ge(loaded, 32)
                pe.wait_ge(summed, 1)
                for b in range(B):
                    for c in range(DC):
                        last = pe.matmul(pm[0:1, b, :], total[:, c, b:b + 1], W[:, c, :], start=c == 0, stop=c == DC - 1)
                last.then_inc(mm, 1)


def routed_attention(nc, K, a):
    A = 4
    with ExitStack() as ctx:
        def sb(name, shape, dt=F32):
            return ctx.enter_context(nc.sbuf_tensor(name, shape, dt))
        QA, QB = sb("m0_QA", [P, A, B * S], BF16), sb("m0_QB", [P, A, B * S], BF16)
        KK = [sb(f"m0_K{x}", [P, A, B * S], BF16) for x in "ABC"]
        V = sb("m0_values", [P, TT, A * WD])
        chosen = sb("m0_chosen", [1, B, A], I32)
        choose_heads(nc, K, a["L0_ffn_Wr"], a["L0_ffn_br"], chosen, A)
        with Stage(nc, "m0_w") as st:
            W = [st.sb(f"W{x}", [P, DC, B * A, P]) for x in "qk"]
            bias = [st.sb(f"b{x}", [P, B * A]) for x in "qk"]
            Wv, bv = st.sb("Wv", [P, DC, B, A * WD]), st.sb("bv", [P, B, A * WD])
            with Stage(nc, "m0_load") as ld:
                loaded, loaded2 = ld.sem("loaded"), ld.sem("loaded2")
                with ld.block() as block:
                    def fetch(eng, loaded, Wx, bx, wsrc, bsrc, n):
                        for b in range(B):
                            for k in range(A):
                                w = b * A + k
                                h = eng.value_load(chosen[0:1, b, k:k + 1], min_val=0, max_val=15)
                                src = wsrc.rearrange("(c p) n -> p c n", p=P)[:, :, bass.ds(h * WD, WD)]
                                bcol = bsrc[bass.ds(h * WD, WD)].rearrange("(p a) -> p a", a=1)
                                for twice in range(2):
                                    eng.dma_start(Wx[:, :, w, twice * WD:(twice + 1) * WD], src).then_inc(loaded, 16)
                                    eng.dma_start(bx[twice * WD:(twice + 1) * WD, w:w + 1], bcol,
                                                  allow_slow_non_contiguous=True).then_inc(loaded, 16)
                                    n += 2
                        return n

                    @block.sync
                    def _(sp):
                        n = fetch(sp, loaded, W[0], bias[0], a["L0_ffn_Wq"], a["L0_ffn_bq"], 0)
                        sp.wait_ge(loaded, 16 * n)

                    @block.scalar
                    def _(act):
                        n = fetch(act, loaded2, W[1], bias[1], a["L0_ffn_Wk"], a["L0_ffn_bk"], 0)
                        for b in range(B):
                            for k in range(A):
                                h = act.value_load(chosen[0:1, b, k:k + 1], min_val=0, max_val=15)
                                src = a["L0_ffn_Wv"].rearrange("(c p) n -> p c n", p=P)[:, :, bass.ds(h * WD, WD)]
                                act.dma_start(Wv[:, :, b, k * WD:(k + 1) * WD], src).then_inc(loaded2, 16)
                                act.dma_start(bv[:, b, k * WD:(k + 1) * WD],
                                              row(a["L0_ffn_bv"][bass.ds(h * WD, WD)])).then_inc(loaded2, 16)
                                n += 2
                        act.wait_ge(loaded2, 16 * n)
            jobs = [(b * A + k, b * S + t * N, N, k, b * S + t * N)
                    for b in range(B) for k in range(A) for t in range(S // N)]
            stacks64(nc, K, "m0_q", "q", W[0], P, K.XNT, jobs, [QA, QB], bias=bias[0])
            stacks64(nc, K, "m0_k", "k", W[1], P, K.XNT, jobs, KK, bias=bias[1])
            with Stage(nc, "m0_v") as vs:
                pm = vs.ps("mm", [P, 4, N])
                mm, ev = vs.sem("mm"), vs.sem("ev")
                with vs.block() as block:
                    @block.tensor
                    def _(pe):
                        for t in range(TT):
                            if t >= 4:
                                pe.wait_ge(ev, t - 3)
                            for c in range(DC):
                                last = pe.matmul(pm[:, t % 4, 0:A * WD], K.XNT[:, c, t * P:(t + 1) * P], Wv[:, c, t // TB, :],
                                                 start=c == 0, stop=c == DC - 1)
                            last.then_inc(mm, 1)

                    @block.vector
                    def _(dve):
                        for t in range(TT):
                            dve.wait_ge(mm, t + 1)
                            dve.tensor_tensor(V[:, t, :], pm[:, t % 4, 0:A * WD], bv[:, t // TB, :], ALU.add).then_inc(ev, 1)

        attention(nc, K, "m0", A, WD ** -0.5, WD, P, TB, False, [(QA, P), (QB, P)],
                  [(x, P) for x in KK], [(0, 0), (0, 1), (1, 2)],
                  lambda b, h: V[:, b * TB:(b + 1) * TB, bass.ds(h * WD, WD)], K.XN, False)
    project(nc, K, "m0_out", K.XN, A * WD, a["L0_ffn_Wo"], a["L0_ffn_bo"])


def relative_bias(nc, K, V, table, Y, G):
    R = table.shape[0]
    assert R < N and S - 1 - R >= N and S == 2 * N
    KT = N // P
    U = 2 * N
    HW = N + (KT - 1) * P
    with Stage(nc, "bias") as st:
        tb, gt = st.sb("table", [P, R // P + 1, NH]), st.sb("gt", [NH, U])
        crow = st.sb("crow", [P, NH])
        flip, sel = st.sb("flip", [P, P]), st.sb("sel", [P, 32])
        vr = st.sb("vr", [P, B, KT, D])
        slot, hk = st.sb("slot", [P, 2, KT, B, HD]), st.sb("hankel", [P, 2, HW])
        ot = st.sb("ot", [P, 2, N])
        cs = st.sb("cs", [P, B, D])
        ps_r, ps_s = st.ps("rev", [P, 2, 2, D]), st.ps("sum", [P, B, D])
        ps_t, ps_o, ps_f = st.ps("turn", [NH, N]), st.ps("o", [P, 2, N]), st.ps("f", [P, 2, N])
        loaded, made, turned, gdone, stored = (st.sem(x) for x in ("loaded", "made", "turned", "gdone", "stored"))
        rev, revc, sums, chain = (st.sem(x) for x in ("rev", "revc", "sums", "chain"))
        hl = [st.sem(f"hankel{j}") for j in range(2)]
        vs, od, oc, fd, yd = (st.sem(x) for x in ("vslot", "o", "ocopied", "final", "y"))
        with st.block() as block:
            @block.sync
            def _(sp):
                full = R // P * P
                sp.dma_start(tb[:, 0:R // P, :], table[0:full, :].rearrange("(t p) h -> p t h", p=P)).then_inc(loaded, 16)
                sp.dma_start(tb[0:R - full, R // P, :], table[full:R, :]).then_inc(loaded, 16)
                sp.dma_start(crow[:], row(table[R - 1, :])).then_inc(loaded, 16)
                sp.wait_ge(gdone, 3)
                sp.dma_start(G, gt[:]).then_inc(stored, 16)
                sp.wait_ge(stored, 16)

                def load(i, j):
                    src = bass.AP(G.tensor, (i * 2 + j) * U, [[1, P], [1, HW]])
                    sp.dma_start(hk[:, j, :], src).then_inc(hl[j], 16)

                for j in range(2):
                    load(0, j)
                with sp.Fori(1, NH // 2, 1) as i:
                    for j in range(2):
                        sp.wait_ge(od, i * 2 + j - 1)
                        load(i, j)

            @block.gpsimd
            def _(pool):
                pool.memset(flip[:], 0.0).then_inc(made, 1)
                pool.memset(sel[:], 0.0).then_inc(made, 1)
                pool.wait_ge(made, 2)
                pool.affine_select(out=flip[:], in_=flip[:], compare_op=ALU.not_equal, fill=1.0, base=-(P - 1),
                                   pattern=[[1, P]], channel_multiplier=1).then_inc(made, 1)
                for j in range(4):
                    pool.affine_select(out=sel[:], in_=sel[:], compare_op=ALU.not_equal, fill=1.0, base=-32 * j,
                                       pattern=[[-1, 32]], channel_multiplier=1).then_inc(made, 1)
                    pool.wait_ge(made, 4 + j)
                pool.wait_ge(revc, B * KT // 2)

                def copy_v(i, j):
                    for b in range(B):
                        last = pool.tensor_copy(slot[:, j, :, b, :], vr[:, b, :, bass.ds((i * 2 + j) * HD, HD)])
                    last.then_inc(vs, 1)

                for j in range(2):
                    copy_v(0, j)
                with pool.Fori(1, NH // 2, 1) as i:
                    for j in range(2):
                        pool.wait_ge(od, i * 2 + j - 1)
                        copy_v(i, j)

            @block.tensor
            def _(pe):
                pe.wait_ge(loaded, 48)
                for t in range(R // P + 1):
                    n = min(P, R - t * P)
                    last = pe.transpose(ps_t[:, t * P:t * P + n], tb[0:n, t, :], K.ident[0:n, 0:n])
                last.then_inc(turned, 1)
                for b in range(B):
                    for t in range(TB):
                        last = pe.matmul(ps_s[:, b, :], K.ones[:], V[:, b * TB + t, :], start=t == 0, stop=t == TB - 1)
                last.then_inc(sums, 1)
                pe.wait_ge(made, 7)
                for n in range(B * KT // 2):
                    if n >= 2:
                        pe.wait_ge(revc, n - 1)
                    for k in range(2):
                        b, t = divmod(2 * n + k, KT)
                        last = pe.matmul(ps_r[:, n % 2, k, :], flip[:], V[:, b * TB + N // P + t, :], start=True, stop=True)
                    last.then_inc(rev, 1)

                def head(i, j):
                    h = i * 2 + j
                    pe.wait_ge(hl[j], (i + 1) * 16)
                    pe.wait_ge(vs, h + 1)
                    pe.wait_ge(oc, h + 1)
                    for k in range(KT):
                        last = pe.matmul(ps_o[32 * k:32 * k + 32, j, :], slot[:, j, k, :, :].rearrange("p b d -> p (b d)"),
                                         hk[:, j, (KT - 1 - k) * P:(KT - 1 - k) * P + N], start=True, stop=True)
                    last.then_inc(od, 1)
                    pe.wait_ge(oc, h + 3)
                    pe.wait_ge(yd, h + 1)
                    for t in range(KT):
                        last = pe.matmul(ps_f[:, j, t * B * HD:(t + 1) * B * HD], ot[:, j, t * P:(t + 1) * P],
                                         sel[:], start=True, stop=True)
                    last.then_inc(fd, 1)

                with pe.Fori(0, NH // 2, 1) as i:
                    for j in range(2):
                        head(i, j)

            @block.scalar
            def _(act):
                act.sem_inc(oc, 2)
                for n in range(B * KT // 2):
                    act.wait_ge(rev, n + 1)
                    b, t = divmod(2 * n, KT)
                    act.copy(vr[:, b, t:t + 2, :], ps_r[:, n % 2, :, :]).then_inc(revc, 1)
                with act.Fori(0, NH // 2, 1) as i:
                    for j in range(2):
                        act.wait_ge(od, i * 2 + j + 1)
                        act.wait_ge(fd, i * 2 + j + 1)
                        act.copy(ot[:, j, :], ps_o[:, j, :]).then_inc(oc, 1)

            @block.vector
            def _(dve):
                dve.sem_inc(yd, 2)
                dve.sem_inc(fd, 2)
                dve.memset(gt[:], 0.0).then_inc(gdone, 1)
                dve.wait_ge(turned, 1)
                dve.wait_ge(gdone, 1)
                dve.tensor_copy(gt[:, 0:R], ps_t[:, 0:R]).then_inc(gdone, 1)
                dve.wait_ge(gdone, 2)
                dve.tensor_scalar(gt[:, 0:R], ps_t[:, 0:R], gt[:, R - 1:R], None, ALU.subtract).then_inc(gdone, 1)
                dve.wait_ge(sums, 1)
                dve.wait_ge(loaded, 48)
                link = Link(dve, chain)
                for b in range(B):
                    link(dve.tensor_tensor(cs[:, b, :].rearrange("p (h d) -> p h d", d=HD),
                                           ps_s[:, b, :].rearrange("p (h d) -> p h d", d=HD),
                                           crow[:].rearrange("p (h a) -> p h a", a=1).to_broadcast([P, NH, HD]), ALU.mult))
                    y = Y[:, b * TB:(b + 1) * TB, :]
                    link(dve.tensor_tensor(y, y, cs[:, b:b + 1, :].to_broadcast([P, TB, D]), ALU.add))
                with dve.Fori(0, NH // 2, 1) as i:
                    for j in range(2):
                        h = i * 2 + j
                        dve.wait_ge(fd, h + 3)
                        for b in range(B):
                            y = Y[:, b * TB:b * TB + KT, bass.ds(h * HD, HD)]
                            f = ps_f[:, j, 0:KT * B * HD].rearrange("p (t b d) -> p t b d", t=KT, b=B)
                            last = dve.tensor_tensor(y, y, f[:, :, b, :], ALU.add)
                        last.then_inc(yd, 1)


XH, XD, TOP = 4, 32, 32


def sparse_cross(nc, K, a, text_mask, ctx_mask, CTT):
    Wq, Wk, Wv = (a[f"L1_xattn_W{x}"] for x in "qkv")
    with Stage(nc, "e_att") as st:
        wq, wk = st.sb("wq", [P, DC, P]), st.sb("wk", [CW_P, CW_N, P])
        wv, V = st.sb("wv", [CW_P, CW_N, D]), st.sb("V", [CT_P, B * CT_N, D])
        QT, KT = st.sb("QT", [P, B * S]), st.sb("KT", [P, B * CL])
        AT = st.sb("AT", [CT_P, CT_N, B * S])
        mraw, mrow = st.sb("mraw", [P, B, CL], mybir.dt.uint8), st.sb("mrow", [P, B, CL])
        traw, tmask = st.sb("traw", [P, TT], mybir.dt.uint8), st.sb("tmask", [P, TT])
        sc = st.sb("sc", [P, 2, XH, CL])
        left, ex, mk = st.sb("left", [P, XH, CL]), st.sb("ex", [P, 2, XH, CL]), st.sb("mk", [P, XH, CL])
        top, neg = st.sb("top", [P, XH, TOP // 8, 8]), st.sb("neg", [P, 2, XH])
        den, r = st.sb("den", [P, XH]), st.sb("r", [P, XH])
        mean = st.sb("mean", [P, 2, CL])
        ps, pt, pc = st.ps("s", [P, XH, N]), st.ps("t", [CT_P, 2, N]), st.ps("c", [P, 2, N])
        loaded, mm, ev, maskd = (st.sem(x) for x in ("loaded", "mm", "ev", "maskd"))
        s_ready, s_read, chain, e_go, e_done = (st.sem(x) for x in ("s_ready", "s_read", "chain", "e_go", "e_done"))
        m_ready, t_ready, t_done, c_ready, c_done = (st.sem(x) for x in ("m_ready", "t_ready", "t_done", "c_ready", "c_done"))
        nload = 5
        jobs = [("q", t) for t in range(B * S // N)] + [("k", 0)] + [("v", t) for t in range(B * CT_N)]
        with st.block() as block:
            @block.sync
            def _(sp):
                sp.dma_start(wq[:], Wq.rearrange("(c p) n -> p c n", p=P)).then_inc(loaded, 16)
                sp.dma_start(wk[:], Wk.rearrange("(c p) n -> p c n", p=CW_P)).then_inc(loaded, 16)
                sp.dma_start(wv[:], Wv.rearrange("(c p) n -> p c n", p=CW_P)).then_inc(loaded, 16)
                sp.dma_start(mraw[:].rearrange("p b n -> p (b n)"), row(ctx_mask.rearrange("b n -> (b n)"))).then_inc(loaded, 16)
                sp.dma_start(traw[:], text_mask.rearrange("b (t p) -> p (b t)", p=P),
                             allow_slow_non_contiguous=True).then_inc(loaded, 16)

            @block.tensor
            def _(pe):
                pe.wait_ge(loaded, 16 * nload)
                for m, (kind, t) in enumerate(jobs):
                    if m >= 2:
                        pe.wait_ge(ev, m - 1)
                    out = pc[:, m % 2, :]
                    for c in range(DC):
                        kw = dict(start=c == 0, stop=c == DC - 1)
                        if kind == "q":
                            last = pe.matmul(out, wq[:, c, :], K.XNT[:, c, t * N:(t + 1) * N], **kw)
                        elif kind == "k":
                            last = pe.matmul(out[:, 0:B * CL], wk[:, c, :], K.CT[:, c, :], **kw)
                        else:
                            last = pe.matmul(out[0:CT_P, 0:D], K.CT[:, c, t * CT_P:(t + 1) * CT_P], wv[:, c, :], **kw)
                    last.then_inc(mm, 1)
                pe.wait_ge(ev, len(jobs))

                def turn(t):
                    pe.wait_ge(m_ready, t + 1)
                    if t >= 2:
                        pe.wait_ge(t_done, t - 1)
                    for j in range(CT_N):
                        last = pe.transpose(pt[:, t % 2, j * P:(j + 1) * P], mean[:, t % 2, j * CT_P:(j + 1) * CT_P],
                                            K.ident[:])
                    last.then_inc(t_ready, 1)

                for t in range(TT):
                    b = t // TB
                    if t:
                        pe.wait_ge(s_read, t)
                    for h in range(XH):
                        last = pe.matmul(ps[:, h, 0:CL], QT[h * XD:(h + 1) * XD, t * P:(t + 1) * P],
                                         KT[h * XD:(h + 1) * XD, b * CL:(b + 1) * CL], start=True, stop=True)
                    last.then_inc(s_ready, 1)
                    if t:
                        turn(t - 1)
                turn(TT - 1)
                pe.wait_ge(t_done, TT)
                for m in range(DC * B * S // N):
                    c, t = divmod(m, B * S // N)
                    b = t // (S // N)
                    if m >= 2:
                        pe.wait_ge(c_done, m - 1)
                    for j in range(CT_N):
                        last = pe.matmul(pc[:, m % 2, :], V[:, b * CT_N + j, c * P:(c + 1) * P],
                                         AT[:, j, t * N:(t + 1) * N], start=j == 0, stop=j == CT_N - 1)
                    last.then_inc(c_ready, 1)

            @block.scalar
            def _(act):
                for m, (kind, t) in enumerate(jobs):
                    act.wait_ge(mm, m + 1)
                    src = pc[:, m % 2, :]
                    if kind == "q":
                        act.copy(QT[:, t * N:(t + 1) * N], src).then_inc(ev, 1)
                    elif kind == "k":
                        act.copy(KT[:], src[:, 0:B * CL]).then_inc(ev, 1)
                    else:
                        act.copy(V[:, t, :], src[0:CT_P, 0:D]).then_inc(ev, 1)
                for t in range(TT):
                    act.wait_ge(e_go, t + 1)
                    for h in range(XH):
                        last = act.activation(ex[:, t % 2, h, :], sc[:, t % 2, h, :], ACT.Exp, bias=neg[:, t % 2, h:h + 1])
                    last.then_inc(e_done, 1)
                    if t:
                        act.wait_ge(t_ready, t)
                        act.copy(AT[:, :, (t - 1) * P:t * P],
                                 pt[:, (t - 1) % 2, 0:CT_N * P].rearrange("p (j n) -> p j n", j=CT_N)).then_inc(t_done, 1)
                act.wait_ge(t_ready, TT)
                act.copy(AT[:, :, (TT - 1) * P:TT * P],
                         pt[:, (TT - 1) % 2, 0:CT_N * P].rearrange("p (j n) -> p j n", j=CT_N)).then_inc(t_done, 1)
                for m in range(DC * B * S // N):
                    c, t = divmod(m, B * S // N)
                    act.wait_ge(c_ready, m + 1)
                    act.copy(CTT[:, c, t * N:(t + 1) * N], pc[:, m % 2, :]).then_inc(c_done, 1)

            @block.vector
            def _(dve):
                link = Link(dve, chain)
                dve.wait_ge(loaded, 16 * nload)
                link(dve.tensor_copy(mrow[:], mraw[:]))
                link(dve.tensor_scalar(mrow[:], mrow[:], 1.0, -NEG, ALU.subtract, ALU.mult))
                link(dve.tensor_copy(tmask[:], traw[:]))
                link(dve.tensor_scalar(tmask[:], tmask[:], 1.0 / XH, None, ALU.mult))
                for t in range(TT):
                    b, s2 = t // TB, sc[:, t % 2, :, :]
                    dve.wait_ge(s_ready, t + 1)
                    if t >= 2:
                        dve.wait_ge(e_done, t - 1)
                    dve.scalar_tensor_tensor(out=s2, in0=ps[:, :, 0:CL], scalar=XD ** -0.5,
                                             in1=mrow[:, b:b + 1, :].to_broadcast([P, XH, CL]),
                                             op0=ALU.mult, op1=ALU.add).then_inc(s_read, 1)
                    dve.wait_ge(s_read, t + 1)
                    for n in range(TOP // 8):
                        for h in range(XH):
                            last = dve.max(top[:, h, n, :], s2[:, h, :] if n == 0 else left[:, h, :])
                        link(last)
                        if n == 0:
                            dve.tensor_scalar(neg[:, t % 2, :], top[:, :, 0, 0], -1.0, None, ALU.mult).then_inc(e_go, 1)
                        for h in range(XH):
                            last = dve.match_replace(left[:, h, :], top[:, h, n, :], s2[:, h, :] if n == 0 else left[:, h, :],
                                                     -3.0e38)
                        link(last)
                    link(dve.tensor_tensor(mk[:], left[:], s2, ALU.not_equal))
                    dve.wait_ge(e_done, t + 1)
                    link(dve.tensor_tensor(mk[:], mk[:], ex[:, t % 2, :, :], ALU.mult))
                    link(dve.tensor_reduce(den[:], mk[:], AX.X, ALU.add))
                    link(dve.reciprocal(r[:], den[:]))
                    link(dve.tensor_scalar(r[:], r[:], tmask[:, t:t + 1], None, ALU.mult))
                    if t >= 2:
                        dve.wait_ge(t_ready, t - 1)
                    m2 = mean[:, t % 2, :]
                    link(dve.tensor_scalar(m2, mk[:, 0, :], r[:, 0:1], None, ALU.mult))
                    for h in range(1, XH):
                        last = dve.scalar_tensor_tensor(out=m2, in0=mk[:, h, :], scalar=r[:, h:h + 1], in1=m2,
                                                        op0=ALU.mult, op1=ALU.add)
                        if h < XH - 1:
                            link(last)
                    last.then_inc(m_ready, 1)


def film(nc, K, name, CTT, W, bias, gate, dst):
    with Stage(nc, name) as st:
        Wt, brow, g = st.sb("W", [P, DC, 2 * D]), st.sb("bias", [P, 2 * D]), st.sb("gate", [P, 1])
        f = st.sb("f", [P, 2, 2 * D])
        pm = st.ps("mm", [P, 3, N])
        loaded, mm, fd, d1, d2, d3 = (st.sem(x) for x in ("loaded", "mm", "fd", "d1", "d2", "d3"))
        with st.block() as block:
            @block.sync
            def _(sp):
                sp.dma_start(Wt[:], W.rearrange("(c p) n -> p c n", p=P)).then_inc(loaded, 16)
                sp.dma_start(brow[:], row(bias)).then_inc(loaded, 16)
                sp.dma_start(g[:], row(gate)).then_inc(loaded, 16)

            @block.tensor
            def _(pe):
                pe.wait_ge(loaded, 48)
                for t in range(TT):
                    if t >= 3:
                        pe.wait_ge(fd, t - 2)
                    for c in range(DC):
                        last = pe.matmul(pm[:, t % 3, :], CTT[:, c, t * P:(t + 1) * P], Wt[:, c, :],
                                         start=c == 0, stop=c == DC - 1)
                    last.then_inc(mm, 1)

            @block.vector
            def _(dve):
                dve.wait_ge(loaded, 48)
                for t in range(TT):
                    ft = f[:, t % 2, :]
                    dve.wait_ge(mm, t + 1)
                    if t >= 2:
                        dve.wait_ge(d3, t - 1)
                    dve.tensor_tensor(ft, pm[:, t % 3, :], brow[:], ALU.add).then_inc(fd, 1)
                    dve.wait_ge(fd, t + 1)
                    dve.tensor_scalar(ft, ft, g[:, 0:1], None, ALU.mult).then_inc(d1, 1)
                    dve.wait_ge(d1, t + 1)
                    dve.scalar_tensor_tensor(out=dst[:, t, :], in0=ft[:, 0:D], scalar=1.0, in1=dst[:, t, :],
                                             op0=ALU.add, op1=ALU.mult).then_inc(d2, 1)

            @block.gpsimd
            def _(pool):
                for t in range(TT):
                    pool.wait_ge(d2, t + 1)
                    pool.tensor_tensor(dst[:, t, :], dst[:, t, :], f[:, t % 2, D:], ALU.add).then_inc(d3, 1)


TWO_PI = 6.283185307179586
FACT = [1.0, 1.0, 1 / 2, 1 / 6, 1 / 24, 1 / 120, 1 / 720, 1 / 5040]
LN2_HI, LN2_LO = 0.693359375, -2.12194440e-4
PI2_HI, PI2_LO = 6.28125, 6.283185307179586 - 6.28125
NS = 64
LB = S // P


def accurate_exp(link, eng, out, x, k, r, pw):
    link(eng.tensor_scalar(k, x, 1.4426950408889634, ROUND, ALU.mult, ALU.add))
    link(eng.tensor_scalar(k, k, ROUND, -126.0, ALU.subtract, ALU.max))
    link(eng.tensor_scalar(k, k, 127.0, None, ALU.min))
    link(eng.scalar_tensor_tensor(out=r, in0=k, scalar=-LN2_HI, in1=x, op0=ALU.mult, op1=ALU.add))
    link(eng.scalar_tensor_tensor(out=r, in0=k, scalar=-LN2_LO, in1=r, op0=ALU.mult, op1=ALU.add))
    link(eng.tensor_scalar(k, k, 127.0, 8388608.0, ALU.add, ALU.mult))
    link(eng.tensor_copy(pw, k))
    link(eng.tensor_scalar(out, r, FACT[7], None, ALU.mult))
    for n in range(6, 0, -1):
        link(eng.scalar_tensor_tensor(out=out, in0=out, scalar=FACT[n], in1=r, op0=ALU.add, op1=ALU.mult))
    link(eng.scalar_tensor_tensor(out=out, in0=out, scalar=1.0, in1=pw.bitcast(F32), op0=ALU.add, op1=ALU.mult))


def ssm_kernel(nc, K, a, KN):
    CH = 32
    with Stage(nc, "ssm") as st:
        raw = st.sb("raw", [P, 4, DC, 2, NS])
        V = [st.sb(f"v{n}", [P, D]) for n in range(4)]
        Ar, Ai, Cr, Ci = V
        dt, ar, tw = st.sb("dt", [P, D]), st.sb("ar", [P, D]), st.sb("tw", [P, D])
        T = [st.sb(f"t{n}", [P, D]) for n in range(8)]
        pw = st.sb("pw", [P, D], I32)
        R, Rk = st.sb("R", [P, D, LB]), [st.sb(f"Rk{n}", [P, D, LB]) for n in range(3)]
        posn, blk = st.sb("pos", [P, P]), st.sb("blk", [P, LB])
        ph = st.sb("ph", [P, 8])
        F, G = st.sb("F", [P, 2, CH, P]), st.sb("G", [P, 2, CH, P])
        W2 = st.sb("W2", [P, CH, P])
        pv, pk = st.ps("turned", [P, 4, N]), st.ps("k", [P, 2, N])
        loaded, chain, turned, made, actd, coef = (st.sem(x) for x in ("loaded", "chain", "turned", "made", "actd", "coef"))
        f1, f2, f3, f4, g1, sn, wd, kd, kc = (st.sem(x) for x in ("f1", "f2", "f3", "f4", "g1", "sn", "wd", "kd", "kc"))
        e1, ask, ans = st.sem("e1"), st.sem("ask"), st.sem("ans")
        names = ("A_re", "A_im", "C_re", "C_im")
        EPS = 1e-5
        NCH = D // CH
        def asked(T, Rk):
            return [(T[5][:], T[3][:], 0.5, None, ACT.Sin), (T[6][:], T[3][:], 1.0, None, ACT.Sin),
                    (Rk[0][:], Rk[0][:], -6.283185, 2, ACT.Sin), (Rk[1][:], Rk[1][:], -6.283185, None, ACT.Sin),
                    (Rk[2][:], Rk[2][:], 1.0, None, ACT.Exp)]

        with st.block() as block:
            @block.sync
            def _(sp):
                for j, x in enumerate(names):
                    for twice in range(2):
                        sp.dma_start(raw[:, j, :, twice, :],
                                     a["L1_xattn_" + x].rearrange("(c p) n -> p c n", p=P)).then_inc(loaded, 16)
                sp.dma_start(dt[:], row(a["L1_xattn_log_dt"])).then_inc(loaded, 16)

            @block.tensor
            def _(pe):
                pe.wait_ge(loaded, 16 * 9)
                for j in range(4):
                    for c in range(DC):
                        last = pe.transpose(pv[:, j, c * P:(c + 1) * P], raw[:, j, c, :, :].rearrange("p t n -> p (t n)"),
                                            K.ident[:])
                last.then_inc(turned, 1)
                pe.wait_ge(coef, 1)

                def slot(i, j):
                    q = i * 2 + j
                    pe.wait_ge(wd, q + 1)
                    pe.wait_ge(kc, q + 1)
                    for c in range(CH):
                        last = pe.matmul(pk[:, j, c * LB:(c + 1) * LB], F[:, j, c, :],
                                         R[:, bass.ds(q * CH + c, 1), :].rearrange("p a n -> p (a n)"),
                                         start=True, stop=True)
                    last.then_inc(kd, 1)

                with pe.Fori(0, NCH // 2, 1) as i:
                    for j in range(2):
                        slot(i, j)

            @block.gpsimd
            def _(pool):
                pool.iota(posn[:], pattern=[[1, P]], base=0, channel_multiplier=0,
                          allow_small_or_imprecise_dtypes=True).then_inc(made, 1)
                pool.iota(blk[:], pattern=[[1, LB]], base=0, channel_multiplier=0,
                          allow_small_or_imprecise_dtypes=True).then_inc(made, 1)
                pool.wait_ge(coef, 1)

                def slot(i, j):
                    q = i * 2 + j
                    pool.tensor_tensor(G[:, j, :, :], ar[:, bass.ds(q * CH, CH)].rearrange("p (c a) -> p c a", a=1)
                                       .to_broadcast([P, CH, P]),
                                       posn[:].rearrange("p (a n) -> p a n", a=1).to_broadcast([P, CH, P]),
                                       ALU.mult).then_inc(g1, 1)
                    pool.wait_ge(sn, q + 1)
                    pool.wait_ge(e1, q + 1)
                    pool.tensor_tensor(F[:, j, :, :], F[:, j, :, :], G[:, j, :, :], ALU.mult).then_inc(wd, 1)

                with pool.Fori(0, NCH // 2, 1) as i:
                    for j in range(2):
                        slot(i, j)

            @block.scalar
            def _(act):
                act.sem_inc(kc, 2)
                for n, (o, x, s, bcol, fn) in enumerate(asked(T, Rk)):
                    act.wait_ge(ask, n + 1)
                    act.activation(o, x, fn, scale=s, **({} if bcol is None else {"bias": ph[:, bcol:bcol + 1]})).then_inc(ans, 1)
                with act.Fori(0, NCH // 2, 1) as i:
                    for j in range(2):
                        q = i * 2 + j
                        act.wait_ge(f4, q + 1)
                        act.activation(F[:, j, :, :], F[:, j, :, :], ACT.Sin, scale=-6.283185,
                                       bias=ph[:, 1:2]).then_inc(sn, 1)
                    for j in range(2):
                        q = i * 2 + j
                        act.wait_ge(g1, q + 1)
                        act.activation(G[:, j, :, :], G[:, j, :, :], ACT.Exp).then_inc(e1, 1)
                    for j in range(2):
                        q = i * 2 + j
                        act.wait_ge(kd, q + 1)
                        act.copy(KN[:, :, bass.ds(q * CH, CH)],
                                 pk[:, j, 0:CH * LB].rearrange("p (c l) -> p l c", l=LB)).then_inc(kc, 1)

            @block.vector
            def _(dve):
                link = Link(dve, chain)
                tt, ts, stt = dve.tensor_tensor, dve.tensor_scalar, dve.scalar_tensor_tensor
                top, bot = slice(0, NS), slice(NS, P)
                for rows, phase in ((top, 0.25), (bot, 0.0)):
                    link(dve.memset(ph[rows, 0:1], phase))
                    link(dve.memset(ph[rows, 1:2], phase * TWO_PI))
                    link(dve.memset(ph[rows, 3:4], phase + 0.5 - 1e-7))
                    link(dve.memset(ph[rows, 4:5], phase - 0.5 + 1e-7))
                link(dve.memset(ph[:, 2:3], 0.25 * TWO_PI))
                dve.wait_ge(turned, 1)
                for j in range(4):
                    link(dve.tensor_copy(V[j][:], pv[:, j, 0:D]))
                t = [x[:] for x in T]
                link(dve.tensor_copy(t[7], dt[:]))
                accurate_exp(link, dve, dt[:], t[7], t[0], t[1], pw[:])
                link(tt(ar[:], dt[:], Ar[:], ALU.mult))
                link(tt(t[2], dt[:], Ai[:], ALU.mult))
                link(ts(t[3], t[2], 1 / TWO_PI, ROUND, ALU.mult, ALU.add))
                link(ts(t[4], t[3], ROUND, None, ALU.subtract))
                link(stt(out=t[3], in0=t[4], scalar=-PI2_HI, in1=t[2], op0=ALU.mult, op1=ALU.add))
                link(stt(out=t[3], in0=t[4], scalar=-PI2_LO, in1=t[3], op0=ALU.mult, op1=ALU.add))
                link(ts(t[3], t[3], 3.1415925, -3.1415925, ALU.min, ALU.max))
                link(ts(tw[:], t[3], 1 / TWO_PI, None, ALU.mult))
                dve.sem_inc(ask, 2)
                accurate_exp(link, dve, t[7], ar[:], t[0], t[1], pw[:])
                dve.wait_ge(ans, 2)
                link(tt(t[5], t[5], t[5], ALU.mult))
                link(tt(t[5], t[5], t[7], ALU.mult))
                link(ts(t[0], t[7], 1.0, None, ALU.subtract))
                link(stt(out=t[0], in0=t[5], scalar=-2.0, in1=t[0], op0=ALU.mult, op1=ALU.add))
                link(tt(t[1], t[7], t[6], ALU.mult))
                link(tt(t[2], Ar[:], Ar[:], ALU.mult))
                link(tt(t[4], Ai[:], Ai[:], ALU.mult))
                link(tt(t[2], t[2], t[4], ALU.add))
                link(dve.reciprocal(t[2], t[2]))
                link(tt(t[4], t[0], Ar[:], ALU.mult))
                link(tt(t[5], t[1], Ai[:], ALU.mult))
                link(tt(t[4], t[4], t[5], ALU.add))
                link(tt(t[5], t[1], Ar[:], ALU.mult))
                link(tt(t[6], t[0], Ai[:], ALU.mult))
                link(tt(t[5], t[5], t[6], ALU.subtract))
                link(tt(t[4], t[4], t[2], ALU.mult))
                link(tt(t[5], t[5], t[2], ALU.mult))
                link(tt(t[0], Cr[:], t[4], ALU.mult))
                link(tt(t[6], Ci[:], t[5], ALU.mult))
                link(tt(t[0], t[0], t[6], ALU.subtract))
                link(tt(t[1], Cr[:], t[5], ALU.mult))
                link(tt(t[6], Ci[:], t[4], ALU.mult))
                link(tt(t[1], t[1], t[6], ALU.add))
                link(ts(t[4][top], t[0][top], 2.0, None, ALU.mult))
                link(ts(t[4][bot], t[1][bot], -2.0, None, ALU.mult))
                link(ts(t[5][top], t[1][top], 2.0, None, ALU.mult))
                link(ts(t[5][bot], t[0][bot], 2.0, None, ALU.mult))
                link(ts(t[2], tw[:], float(P), None, ALU.mult))
                link(ts(t[6], t[2], ROUND, ROUND, ALU.add, ALU.subtract))
                link(tt(t[2], t[2], t[6], ALU.subtract))
                dve.wait_ge(made, 2)

                def by_d(x):
                    return x.rearrange("p (d a) -> p d a", a=1).to_broadcast([P, D, LB])

                lb = blk[:].rearrange("p (a n) -> p a n", a=1).to_broadcast([P, D, LB])
                link(tt(R[:], by_d(t[2]), lb, ALU.mult))
                for n, phase in ((0, 0.25), (1, 0.0)):
                    link(ts(Rk[n][:], R[:], phase, ROUND, ALU.add, ALU.add))
                    link(stt(out=Rk[n][:], in0=Rk[n][:], scalar=ROUND, in1=R[:], op0=ALU.subtract, op1=ALU.subtract))
                    link(ts(Rk[n][:], Rk[n][:], phase + 0.5 - 1e-7, phase - 0.5 + 1e-7, ALU.min, ALU.max))
                link(ts(t[3], ar[:], float(P), None, ALU.mult))
                link(tt(Rk[2][:], by_d(t[3]), lb, ALU.mult))
                dve.sem_inc(ask, 3)
                dve.wait_ge(ans, 5)
                link(tt(Rk[0][:], Rk[0][:], by_d(t[4]), ALU.mult))
                link(tt(Rk[1][:], Rk[1][:], by_d(t[5]), ALU.mult))
                link(tt(Rk[0][:], Rk[0][:], Rk[1][:], ALU.subtract))
                link(tt(R[:], Rk[0][:], Rk[2][:], ALU.mult))
                dve.sem_inc(coef, 1)

                def slot(i, j):
                    q = i * 2 + j
                    f, k = F[:, j, :, :], W2[:]
                    dve.wait_ge(kc, q + 1)
                    tt(f, tw[:, bass.ds(q * CH, CH)].rearrange("p (c a) -> p c a", a=1).to_broadcast([P, CH, P]),
                       posn[:].rearrange("p (a n) -> p a n", a=1).to_broadcast([P, CH, P]), ALU.mult).then_inc(f1, 1)
                    dve.wait_ge(f1, q + 1)
                    ts(k, f, ph[:, 0:1], ROUND, ALU.add, ALU.add).then_inc(f2, 1)
                    dve.wait_ge(f2, q + 1)
                    stt(out=f, in0=k, scalar=ROUND, in1=f, op0=ALU.subtract, op1=ALU.subtract).then_inc(f3, 1)
                    dve.wait_ge(f3, q + 1)
                    ts(f, f, ph[:, 3:4], ph[:, 4:5], ALU.min, ALU.max).then_inc(f4, 1)

                with dve.Fori(0, NCH // 2, 1) as i:
                    for j in range(2):
                        slot(i, j)


def convolution(nc, K, KN, U, Dskip, tables):
    FB = S // P
    with Stage(nc, "conv") as st:
        YR, YI = st.sb("YR", [P, FB, B * D]), st.sb("YI", [P, FB, B * D])
        tab = st.sb("tab", [P, 2, 2, FB, P])
        kk = st.sb("kk", [P, 2, 2, D])
        tmp = st.sb("tmp", [P, 2, 4, B * D])
        drow = st.sb("drow", [P, D])
        px, pk, py = st.ps("x", [P, 2, 2, N]), st.ps("k", [P, 2, N]), st.ps("y", [P, 2, N])
        tl = [st.sem(f"table{j}") for j in range(2)]
        loaded, xd, kc, m1, m4, yd, ydi = (st.sem(x) for x in ("loaded", "xd", "kc", "m1", "m4", "yd", "ydi"))
        bd, ba, du = st.sem("bd"), st.sem("ba"), st.sem("du")
        NB = FB // 2
        with st.block() as block:
            @block.sync
            def _(sp):
                sp.dma_start(drow[:], row(Dskip)).then_inc(loaded, 16)

                def load(way, i, j):
                    for x in range(2):
                        sp.dma_start(tab[:, j, x, :, :],
                                     tables[way * 2 + x, bass.ds(i * 2 + j, 1)].rearrange("a p c n -> (a p) c n")).then_inc(tl[j], 16)

                for j in range(2):
                    load(0, 0, j)
                with sp.Fori(1, NB, 1) as i:
                    for j in range(2):
                        sp.wait_ge(xd, i * 2 + j - 1)
                        load(0, i, j)
                for j in range(2):
                    sp.wait_ge(xd, FB - 1 + j)
                    load(1, 0, j)
                with sp.Fori(1, NB, 1) as i:
                    for j in range(2):
                        sp.wait_ge(bd, i * 2 + j - 1)
                        load(1, i, j)

            @block.tensor
            def _(pe):
                with pe.Fori(0, NB, 1) as i:
                    for j in range(2):
                        q = i * 2 + j
                        pe.wait_ge(tl[j], (i + 1) * 32)
                        pe.wait_ge(m4, q + 1)
                        for x in range(2):
                            for t in range(FB):
                                kw = dict(start=t == 0, stop=t == FB - 1)
                                pe.matmul(px[:, j, x, :], tab[:, j, x, t, :],
                                          U[:].rearrange("p (b t) d -> p t b d", b=B)[:, t, :, :], **kw)
                            for t in range(FB):
                                kw = dict(start=t == 0, stop=t == FB - 1)
                                last = pe.matmul(pk[:, j, x * D:(x + 1) * D], tab[:, j, x, t, :], KN[:, t, :], **kw)
                        last.then_inc(xd, 1)
                pe.wait_ge(yd, FB)
                pe.wait_ge(ydi, FB + 2)
                with pe.Fori(0, NB, 1) as i:
                    for j in range(2):
                        q = i * 2 + j
                        pe.wait_ge(tl[j], (i + 1) * 32 + 32 * NB)
                        pe.wait_ge(ba, q + 1)
                        for x, y in ((0, YR), (1, YI)):
                            for f in range(FB):
                                last = pe.matmul(py[:, j, :], tab[:, j, x, f, :], y[:, f, :],
                                                 start=x == 0 and f == 0, stop=x == 1 and f == FB - 1)
                        last.then_inc(bd, 1)

            @block.scalar
            def _(act):
                with act.Fori(0, NB, 1) as i:
                    for j in range(2):
                        act.wait_ge(xd, i * 2 + j + 1)
                        act.wait_ge(m4, i * 2 + j + 1)
                        act.copy(kk[:, j, :, :].rearrange("p x d -> p (x d)"), pk[:, j, :]).then_inc(kc, 1)

            @block.gpsimd
            def _(pool):
                pool.sem_inc(ydi, 2)
                with pool.Fori(0, NB, 1) as i:
                    for j in range(2):
                        q = i * 2 + j
                        pool.wait_ge(m4, q + 3)
                        for y, x in ((YR, 0), (YI, 2)):
                            pool.tensor_tensor(y[:, bass.ds(q, 1), :].rearrange("p a n -> p (a n)"), tmp[:, j, x, :],
                                               tmp[:, j, x + 1, :], ALU.subtract if x == 0 else ALU.add
                                               ).then_inc(yd if x == 0 else ydi, 1)
                pool.wait_ge(xd, FB)
                pool.wait_ge(loaded, 16)
                pool.tensor_tensor(U[:], U[:], drow[:].rearrange("p (a d) -> p a d", a=1).to_broadcast([P, TT, D]),
                                   ALU.mult).then_inc(du, 1)

            @block.vector
            def _(dve):
                dve.sem_inc(m4, 2)
                dve.sem_inc(ba, 2)
                with dve.Fori(0, NB, 1) as i:
                    for j in range(2):
                        q = i * 2 + j
                        dve.wait_ge(kc, q + 1)
                        dve.wait_ge(ydi, q + 1)
                        for n, (x, k) in enumerate(((0, 0), (1, 1), (0, 1), (1, 0))):
                            last = dve.tensor_tensor(tmp[:, j, n, :].rearrange("p (b d) -> p b d", b=B),
                                                     px[:, j, x, :].rearrange("p (b d) -> p b d", b=B),
                                                     kk[:, j, k:k + 1, :].to_broadcast([P, B, D]), ALU.mult)
                        last.then_inc(m4, 1)
                dve.wait_ge(du, 1)
                with dve.Fori(0, NB, 1) as i:
                    for j in range(2):
                        q = i * 2 + j
                        dve.wait_ge(bd, q + 1)
                        u = U[:].rearrange("p (b t) d -> p t b d", b=B)[:, bass.ds(q, 1), :, :].rearrange("p a b d -> p (a b) d")
                        dve.tensor_tensor(u, u, py[:, j, :].rearrange("p (b d) -> p b d", b=B), ALU.add).then_inc(ba, 1)


HID = 1024


def add_into(nc, K, name, dst, src):
    with Stage(nc, name) as st:
        added = st.sem("added")
        with st.block() as block:
            @block.vector
            def _(dve):
                dve.tensor_tensor(dst, dst, src, ALU.add).then_inc(added, 1)


def feed_forward(nc, K, name, HT, W1, b1, W2, fn, acc, weights=None):
    E = W1.shape[0]
    PT = HID // P
    TC = B * S // N
    TN = N // P
    par = 2 if E > 1 else 1
    NI = E // par
    with Stage(nc, name) as st:
        w1, w2 = st.sb("w1", [P, par, DC, HID]), st.sb("w2", [P, par, PT, D])
        bias = st.sb("b1", [P, par, PT])
        hg = st.sb("hg", [P, 2, PT, N])
        ph, py = st.ps("h", [P, 4, N]), st.ps("y", [P, 4, N])
        ld = [st.sem(f"weights{j}") for j in range(par)]
        h_ready, h_done, y_ready, y_done = (st.sem(x) for x in ("h_ready", "h_done", "y_ready", "y_done"))
        used = st.sem("used")
        YP = TN // 2

        def loop(eng, lo, body):
            if NI == 1:
                return body(0) if lo == 0 else None
            with eng.Fori(lo, NI, 1) as i:
                body(i)

        with st.block() as block:
            @block.sync
            def _(sp):
                def load(i, j):
                    e = bass.ds(i * par + j, 1)
                    sp.dma_start(w1[:, j, :, :], W1[e].rearrange("a (c p) n -> p (a c) n", p=P)).then_inc(ld[j], 16)
                    sp.dma_start(bias[:, j, :], b1[e].rearrange("a (t p) -> p (a t)", p=P),
                                 allow_slow_non_contiguous=True).then_inc(ld[j], 16)
                    sp.dma_start(w2[:, j, :, :], W2[e].rearrange("a (c p) n -> p (a c) n", p=P)).then_inc(ld[j], 16)

                for j in range(par):
                    load(0, j)

                def body(i):
                    for j in range(par):
                        sp.wait_ge(y_ready, (i * par + j + 1 - par) * (TC * YP))
                        load(i, j)
                if NI > 1:
                    loop(sp, 1, body)

            @block.tensor
            def _(pe):
                def body(i):
                    for j in range(par):
                        q = i * par + j
                        pe.wait_ge(ld[j], (i + 1) * 48)

                        def up(t):
                            for m in range(PT):
                                pe.wait_ge(h_done, q * (TC * PT) + t * PT + m + 1)
                                for c in range(DC):
                                    last = pe.matmul(ph[:, m % 4, :], w1[:, j, c, m * P:(m + 1) * P],
                                                     HT[:, c, t * N:(t + 1) * N], start=c == 0, stop=c == DC - 1)
                                last.then_inc(h_ready, 1)

                        def down(t):
                            for y in range(YP):
                                pe.wait_ge(h_done, q * (TC * PT) + (t + 1) * PT + 4)
                                pe.wait_ge(y_done, q * (TC * YP) + t * YP + y + 1)
                                for k in range(2):
                                    c0 = (2 * y + k) * P
                                    for m in range(PT):
                                        last = pe.matmul(py[:, (t * YP + y) % 4, k * D:(k + 1) * D],
                                                         hg[:, t % 2, m, c0:c0 + P], w2[:, j, m, :],
                                                         start=m == 0, stop=m == PT - 1)
                                last.then_inc(y_ready, 1)

                        up(0)
                        for t in range(1, TC):
                            up(t)
                            down(t - 1)
                        down(TC - 1)
                loop(pe, 0, body)

            @block.scalar
            def _(act):
                act.sem_inc(h_done, 4)
                act.sem_inc(used, 2)

                def body(i):
                    for j in range(par):
                        q = i * par + j
                        for t in range(TC):
                            for m in range(PT):
                                act.wait_ge(h_ready, q * (TC * PT) + t * PT + m + 1)
                                if m == 0:
                                    act.wait_ge(used, q * TC + t + 1)
                                act.activation(hg[:, t % 2, m, :], ph[:, m % 4, :], fn,
                                               bias=bias[:, j, m:m + 1]).then_inc(h_done, 1)
                loop(act, 0, body)

            @block.vector
            def _(dve):
                dve.sem_inc(y_done, 4)

                def body(i):
                    for j in range(par):
                        q = i * par + j
                        for t in range(TC):
                            for y in range(YP):
                                dve.wait_ge(y_ready, q * (TC * YP) + t * YP + y + 1)
                                tt = t * TN + 2 * y
                                if weights is None:
                                    last = dve.tensor_tensor(acc[:, tt:tt + 2, :], acc[:, tt:tt + 2, :],
                                                             py[:, (t * YP + y) % 4, :].rearrange("p (k d) -> p k d", k=2), ALU.add)
                                else:
                                    dve.wait_ge(y_done, q * (TC * YP) + t * YP + y + 4)
                                    for k in range(2):
                                        last = dve.scalar_tensor_tensor(
                                            out=acc[:, tt + k, :], in0=py[:, (t * YP + y) % 4, k * D:(k + 1) * D],
                                            scalar=weights[:, tt + k, bass.ds(q, 1)], in1=acc[:, tt + k, :],
                                            op0=ALU.mult, op1=ALU.add)
                                last.then_inc(y_done, 1)
                            dve.sem_inc(used, 1)
                loop(dve, 0, body)


def state_space(nc, K, a):
    g = lambda x: a["L1_xattn_" + x]
    with ExitStack() as ctx:
        def sb(name, shape, dt=F32):
            return ctx.enter_context(nc.sbuf_tensor(name, shape, dt))
        KN = sb("e_KN", [P, LB, D])
        ssm_kernel(nc, K, a, KN)
        U = sb("e_U", [P, TT, D])
        with nc.sbuf_tensor("e_CTT", [P, DC, B * S], F32) as CTT:
            sparse_cross(nc, K, a, a["mask_BxS_bf1"], a["mask_BxS2_bf1"], CTT)
            layernorm(nc, K, "e_n1", K.XN, U, gamma=g("g_norm_in"), beta=g("b_norm_in"))
            film(nc, K, "e_f1", CTT, g("W_film_in"), g("b_film_in"), g("mod_gate"), U)
            convolution(nc, K, KN, U, g("D_skip"), a["dft_tables"])
            film(nc, K, "e_f2", CTT, g("W_film_out"), g("b_film_out"), g("mod_gate"), U)
        add_into(nc, K, "e_a1", U[:], K.XN)
        layernorm(nc, K, "e_n2", U, K.XN, K.XNT, gamma=g("g_ffn"), beta=g("b_ffn"))
        with Stage(nc, "e_b2") as st:
            b2 = st.sb("b2", [P, D])
            loaded, added = st.sem("loaded"), st.sem("added")
            with st.block() as block:
                @block.sync
                def _(sp):
                    sp.dma_start(b2[:], row(g("b2"))).then_inc(loaded, 16)

                @block.vector
                def _(dve):
                    dve.wait_ge(loaded, 16)
                    dve.tensor_tensor(U[:], U[:], b2[:].rearrange("p (a d) -> p a d", a=1).to_broadcast([P, TT, D]),
                                      ALU.add).then_inc(added, 1)
        feed_forward(nc, K, "e_ff", K.XNT, g("W1").rearrange("(a k) n -> a k n", a=1),
                     g("b1").rearrange("(a n) -> a n", a=1), g("W2").rearrange("(a k) n -> a k n", a=1), ACT.Gelu, U)
        layernorm(nc, K, "e_n3", U, U, gamma=g("g_norm_out"), beta=g("b_norm_out"))
        add_into(nc, K, "e_a2", K.X[:], U[:])


def route_tokens(nc, K, Wr, br, b2, weights, E, TOPK):
    with Stage(nc, "route") as st:
        W, brow, b2t = st.sb("W", [P, DC, E]), st.sb("br", [P, E]), st.sb("b2", [E, D])
        lg, rank = st.sb("lg", [P, TT, E]), st.sb("rank", [P, TT, E])
        gr, eq, earlier = st.sb("gr", [P, TT * E, E]), st.sb("eq", [P, TT * E, E]), st.sb("earlier", [P, E, E])
        mx, sm, ex = st.sb("mx", [P, TT]), st.sb("sm", [P, TT]), st.sb("ex", [P, TT, E])
        wT = st.sb("wT", [E, B * S])
        pl, pt, pb = st.ps("l", [P, TT, E]), st.ps("t", [E, 4, N]), st.ps("b", [P, 2, N])
        loaded, made, mm, chain, ask, ans, turned, moved, bd, ba = (
            st.sem(x) for x in ("loaded", "made", "mm", "chain", "ask", "ans", "turned", "moved", "bd", "ba"))
        with st.block() as block:
            @block.sync
            def _(sp):
                sp.dma_start(W[:], Wr.rearrange("(c p) n -> p c n", p=P)).then_inc(loaded, 16)
                sp.dma_start(brow[:], row(br)).then_inc(loaded, 16)
                sp.dma_start(b2t[:], b2).then_inc(loaded, 16)

            @block.gpsimd
            def _(pool):
                pool.memset(earlier[:], 1.0).then_inc(made, 1)
                pool.wait_ge(made, 1)
                pool.affine_select(out=earlier[:], in_=earlier[:], compare_op=ALU.is_gt, fill=0.0, base=0,
                                   pattern=[[1, E], [-1, E]], channel_multiplier=0).then_inc(made, 1)

            @block.tensor
            def _(pe):
                pe.wait_ge(loaded, 48)
                for t in range(TT):
                    for c in range(DC):
                        last = pe.matmul(pl[:, t, :], K.XNT[:, c, t * P:(t + 1) * P], W[:, c, :],
                                         start=c == 0, stop=c == DC - 1)
                last.then_inc(mm, 1)
                pe.wait_ge(ask, 2)
                for t in range(TT):
                    last = pe.transpose(pt[:, t // 4, (t % 4) * P:(t % 4 + 1) * P], weights[:, t, :], K.ident[:])
                last.then_inc(turned, 1)
                pe.wait_ge(moved, 1)
                for n in range(TT // 2):
                    if n >= 2:
                        pe.wait_ge(ba, n - 1)
                    for k in range(2):
                        t = 2 * n + k
                        last = pe.matmul(pb[:, n % 2, k * D:(k + 1) * D], wT[:, t * P:(t + 1) * P], b2t[:],
                                         start=True, stop=True)
                    last.then_inc(bd, 1)

            @block.scalar
            def _(act):
                act.wait_ge(ask, 1)
                act.activation(ex[:], lg[:], ACT.Exp).then_inc(ans, 1)
                act.wait_ge(turned, 1)
                act.copy(wT[:], pt[:].rearrange("p a n -> p (a n)")).then_inc(moved, 1)

            @block.vector
            def _(dve):
                link = Link(dve, chain)
                dve.wait_ge(mm, 1)
                dve.wait_ge(made, 2)
                link(dve.tensor_tensor(lg[:], pl[:], brow[:].rearrange("p (a e) -> p a e", a=1).to_broadcast([P, TT, E]),
                                       ALU.add))
                for t in range(TT):
                    v = slice(t * E, (t + 1) * E)
                    mine = lg[:, t, :].rearrange("p (h a) -> p h a", a=1).to_broadcast([P, E, E])
                    link(dve.tensor_tensor(gr[:, v, :], lg[:, t:t + 1, :].to_broadcast([P, E, E]), mine, ALU.is_gt))
                    link(dve.tensor_tensor(eq[:, v, :], lg[:, t:t + 1, :].to_broadcast([P, E, E]), mine, ALU.is_equal))
                    link(dve.tensor_tensor(eq[:, v, :], eq[:, v, :], earlier[:], ALU.mult))
                link(dve.tensor_tensor(gr[:], gr[:], eq[:], ALU.add))
                link(dve.tensor_reduce(rank[:].rearrange("p t e -> p (t e)"), gr[:], AX.X, ALU.add))
                link(dve.tensor_reduce(mx[:], lg[:], AX.X, ALU.max))

                def by_t(x):
                    return x.rearrange("p (t a) -> p t a", a=1).to_broadcast([P, TT, E])
                link(dve.tensor_tensor(lg[:], lg[:], by_t(mx[:]), ALU.subtract))
                dve.sem_inc(ask, 1)
                link(dve.tensor_scalar(rank[:], rank[:], float(TOPK), None, ALU.is_lt))
                dve.wait_ge(ans, 1)
                link(dve.tensor_tensor(ex[:], ex[:], rank[:], ALU.mult))
                link(dve.tensor_reduce(sm[:], ex[:], AX.X, ALU.add))
                link(dve.reciprocal(mx[:], sm[:]))
                link(dve.tensor_tensor(weights[:], ex[:], by_t(mx[:]), ALU.mult))
                dve.sem_inc(ask, 1)
                for n in range(TT // 2):
                    dve.wait_ge(bd, n + 1)
                    x = K.X[:, 2 * n:2 * n + 2, :]
                    dve.tensor_tensor(x, x, pb[:, n % 2, :].rearrange("p (k d) -> p k d", k=2), ALU.add).then_inc(ba, 1)


def finish(nc, K, out):
    with Stage(nc, "finish") as st:
        stored = st.sem("stored")
        with st.block() as block:
            @block.sync
            def _(sp):
                for b in range(B):
                    sp.dma_start(out[b].rearrange("(t p) d -> p t d", p=P),
                                 K.X[:, b * TB:(b + 1) * TB, :]).then_inc(stored, 16)
                sp.wait_ge(stored, 16 * B)


class Shared:
    pass


def decoder(nc, a, out, upto=99):
    Stage.spent = []
    with ExitStack() as ctx:
        def sb(name, shape, dt=F32):
            return ctx.enter_context(nc.sbuf_tensor(name, shape, dt))

        K = Shared()
        K.X = sb("X", [P, TT, D])
        work = sb("work", [P, 2 * TT * D])
        K.XN = work[:, 0:TT * D].rearrange("p (t d) -> p t d", t=TT)
        K.XNT = work[:, TT * D:].rearrange("p (c n) -> p c n", c=DC)
        K.wide = work[:, :].rearrange("p (t d) -> p t d", t=TT)
        K.ident, K.identb = sb("ident", [P, P]), sb("identb", [P, P], BF16)
        K.ones, K.onesb = sb("ones", [P, P]), sb("onesb", [P, P], BF16)
        K.cmask, K.cmaskT = sb("cmask", [P, P], BF16), sb("cmaskT", [P, N // P, N], BF16)
        K.eps = sb("eps", [P, 1])
        K.CT = sb("CT", [CW_P, CW_N, B * CL])
        QS = nc.dram_tensor("q_stacks", [NH, ROWS, B * S], BF16, kind="Internal").ap()
        KS = nc.dram_tensor("k_stacks", [NH, ROWS, B * S], BF16, kind="Internal").ap()
        G = nc.dram_tensor("bias_rows", [NH, 2 * N], F32, kind="Internal").ap()

        def stack_of(src):
            return lambda head: src[bass.ds(head, 1)].rearrange("a r (b n) -> (a r) b n", b=B)

        setup(nc, K, a["x"])
        context(nc, K, a["ctx_768"])

        layernorm(nc, K, "n0", K.X, K.XN, K.XNT)
        with nc.sbuf_tensor("a0_values", [P, TT, D], F32) as V:
            qkv16(nc, K, "a0_qkv", None, K.XNT, QS, KS, V, a["L0_attn_w_attn"], bias=a["L0_attn_b_attn"],
                  lora=(a["L0_attn_la_attn"], a["L0_attn_lb_attn"]),
                  quant=(a["L0_attn_kv_scale"], a["L0_attn_kv_zero_point"]))
            attention(nc, K, "a0", NH, HD ** -0.5, HD, P, TB, True, [(stack_of(QS), ROWS)], [(stack_of(KS), ROWS)],
                      [(0, 0)], lambda b, h: V[:, b * TB:(b + 1) * TB, bass.ds(h * HD, HD)], K.XN, True)
        project(nc, K, "a0_out", K.XN, D, a["L0_attn_w_proj"], a["L0_attn_b_proj"],
                lora=(a["L0_attn_la_proj"], a["L0_attn_lb_proj"]))
        if upto <= 1:
            return finish(nc, K, out)
        layernorm(nc, K, "n1", K.X, K.XN, K.XNT)
        cross_attention(nc, K, a)
        if upto <= 2:
            return finish(nc, K, out)
        layernorm(nc, K, "n2", K.X, K.XN, K.XNT)
        routed_attention(nc, K, a)
        if upto <= 3:
            return finish(nc, K, out)
        layernorm(nc, K, "n3", K.X, K.XN, K.XNT)
        with nc.sbuf_tensor("a1_values", [P, TT, D], F32) as V:
            qkv16(nc, K, "a1_qkv", None, K.XNT, QS, KS, V, [a[f"L1_attn_W{x}"] for x in "qkv"], transposed=True)
            attention(nc, K, "a1", NH, D ** -0.5, HD, P, TB, False, [(stack_of(QS), ROWS)], [(stack_of(KS), ROWS)],
                      [(0, 0)], lambda b, h: V[:, b * TB:(b + 1) * TB, bass.ds(h * HD, HD)], K.XN, True)
            relative_bias(nc, K, V, a["L1_attn_bias_table"], K.XN, G)
        layernorm(nc, K, "a1_norm", K.XN, K.XN, gamma=a["L1_attn_ln_gamma"], beta=a["L1_attn_ln_beta"])
        add_into(nc, K, "a1_add", K.X[:], K.XN)
        if upto <= 4:
            return finish(nc, K, out)
        layernorm(nc, K, "n4", K.X, K.XN, K.XNT)
        state_space(nc, K, a)
        if upto <= 5:
            return finish(nc, K, out)
        layernorm(nc, K, "n5", K.X, K.XN, K.XNT)
        with nc.sbuf_tensor("f_weights", [P, TT, 8], F32) as weights:
            route_tokens(nc, K, a["L1_ffn_Wr"], a["L1_ffn_br"], a["L1_ffn_b2"], weights, 8, 2)
            feed_forward(nc, K, "f_ff", K.XNT, a["L1_ffn_W1"], a["L1_ffn_b1"], a["L1_ffn_W2"], ACT.Gelu_apprx_tanh,
                         K.X, weights)
        finish(nc, K, out)


def constants():
    n = np.arange(S)
    turns = np.outer(n, 2 * n + 1) % (4 * S)
    angle = turns * (2 * np.pi / (4 * S))
    c, s = np.cos(angle), np.sin(angle)

    def blocks(m):
        return m.reshape(S // P, P, S // P, P).transpose(2, 1, 0, 3)
    t = np.stack([blocks(c), blocks(-s), blocks(c.T / S), blocks(-s.T / S)])
    return {"dft_tables": np.ascontiguousarray(t.astype(np.float32))}


def kernel(**inputs):
    import concourse.bacc as bacc
    from concourse.bass_utils import run_bass_kernel_spmd

    nc = bacc.Bacc("TRN2", target_bir_lowering=False, num_devices=1)
    arrays = dict(constants())
    for name, value in inputs.items():
        array = np.ascontiguousarray(value)
        arrays[name] = array.view(np.uint8) if array.dtype == bool else array
    a = {name: nc.dram_tensor(name, array.shape, mybir.dt.from_np(array.dtype), kind="ExternalInput").ap()
         for name, array in arrays.items()}
    out = nc.dram_tensor("y", (B, S, D), F32, kind="ExternalOutput").ap()
    decoder(nc, a, out)
    return run_bass_kernel_spmd(nc, [arrays], core_ids=[0]).results[0]["y"]
```

```python
from contextlib import ExitStack

import numpy as np
import concourse.bass as bass
from concourse import mybir

F32 = mybir.dt.float32
BF16 = mybir.dt.bfloat16
I32 = mybir.dt.int32
ALU = mybir.AluOpType
ACT = mybir.ActivationFunctionType
AX = mybir.AxisListType

P = 128
B, S, D = 2, 1024, 256
DC = D // P
TT = B * S // P
TB = S // P
N = 512
NQ = S // N
ROUND = 12582912.0
LN_EPS = 1e-5
NEG = -1.0e30


class Link:

    def __init__(self, eng, sem):
        self.eng, self.sem, self.n = eng, sem, 0

    def __call__(self, ins):
        self.n += 1
        ins.then_inc(self.sem, 1)
        self.eng.wait_ge(self.sem, self.n)


class Stage:

    spent = []
    KEEP = 110

    def __init__(self, nc, name):
        self.nc, self.name, self.ctx, self.sems = nc, name, ExitStack(), []

    def __enter__(self):
        self.ctx.__enter__()
        if len(Stage.spent) > Stage.KEEP:
            self.nc.clear_and_free_semaphores(Stage.spent)
            Stage.spent = []
            self.nc.all_engine_barrier()
        return self

    def __exit__(self, *a):
        Stage.spent += self.sems
        return self.ctx.__exit__(*a)

    def sb(self, name, shape, dt=F32):
        return self.ctx.enter_context(self.nc.sbuf_tensor(f"{self.name}_{name}", shape, dt))

    def ps(self, name, shape, dt=F32):
        return self.ctx.enter_context(self.nc.psum_tensor(f"{self.name}_{name}", shape, dt))

    def sem(self, name):
        self.sems.append(self.nc.alloc_semaphore(f"{self.name}_{name}"))
        return self.sems[-1]

    def block(self):
        return self.nc.Block()


def row(ap, n=P):
    return ap.rearrange("(a n) -> a n", a=1).to_broadcast([n, ap.shape[0]])


def setup(nc, K, x):
    with Stage(nc, "setup") as st:
        loaded, made, zeroed = st.sem("loaded"), st.sem("made"), st.sem("zeroed")
        with st.block() as block:
            @block.sync
            def _(sp):
                for b in range(B):
                    sp.dma_start(K.X[:, b * TB:(b + 1) * TB, :],
                                 x[b].rearrange("(t p) d -> p t d", p=P)).then_inc(loaded, 16)
                sp.wait_ge(zeroed, 1)
                sp.dma_start(K.rows.rearrange("(t p) d -> p t d", p=P),
                             K.zeros[:].rearrange("p (a d) -> p a d", a=1).to_broadcast([P, NT, D])).then_inc(K.rows_zeroed, 16)
                sp.wait_ge(loaded, 16 * B)

            @block.gpsimd
            def _(pool):
                pool.memset(K.zeros[:], 0.0).then_inc(zeroed, 1)
                pool.memset(K.ident[:], 0.0).then_inc(zeroed, 1)
                pool.memset(K.cmask[:], 0.0).then_inc(zeroed, 1)
                pool.memset(K.cmaskT[:], 0.0).then_inc(zeroed, 1)
                pool.memset(K.ones[:], 1.0).then_inc(zeroed, 1)
                pool.wait_ge(zeroed, 5)
                pool.affine_select(out=K.ident[:], in_=K.ident[:], compare_op=ALU.not_equal, fill=1.0,
                                   base=0, pattern=[[-1, P]], channel_multiplier=1).then_inc(made, 1)
                pool.affine_select(out=K.cmask[:], in_=K.cmask[:], compare_op=ALU.is_ge, fill=NEG,
                                   base=0, pattern=[[-1, P]], channel_multiplier=1).then_inc(made, 1)
                pool.affine_select(out=K.cmaskT[:], in_=K.cmaskT[:], compare_op=ALU.is_ge, fill=NEG,
                                   base=0, pattern=[[-P, N // P], [1, N]], channel_multiplier=-1).then_inc(made, 1)

            @block.vector
            def _(dve):
                dve.wait_ge(made, 1)
                dve.tensor_copy(K.identb[:], K.ident[:]).then_inc(zeroed, 1)
                dve.memset(K.eps[:], LN_EPS).then_inc(zeroed, 1)
                dve.memset(K.onesb[:], 1.0).then_inc(zeroed, 1)


def norm_stats(st, block, K, src, mean_rstd, ready):
    stats = st.sb("stats", [P, TT, 6])
    aggr = st.sb("aggr", [P, TT, 2])
    std = st.sb("std", [P, TT])
    stats_done, aggr_done, std_done = st.sem("stats_done"), st.sem("aggr_done"), st.sem("std_done")

    def on_vector(dve):
        for t in range(TT):
            dve.bn_stats(stats[:, t, :], src[:, t, :]).then_inc(stats_done, 1)
        dve.wait_ge(stats_done, TT)
        for t in range(TT):
            dve.bn_aggr(aggr[:, t, :], stats[:, t, :]).then_inc(aggr_done, 1)
        dve.wait_ge(aggr_done, TT)
        dve.tensor_copy(mean_rstd[:, :, 0], aggr[:, :, 0]).then_inc(ready, 1)
        dve.wait_ge(std_done, 1)
        dve.reciprocal(mean_rstd[:, :, 1], std[:]).then_inc(ready, 1)
        dve.wait_ge(ready, 2)

    def on_scalar(act):
        act.wait_ge(aggr_done, TT)
        act.activation(std[:], aggr[:, :, 1], ACT.Sqrt, bias=K.eps[:, 0:1]).then_inc(std_done, 1)

    return on_vector, on_scalar


def transposer(st, src, dst, width, ident, src_ready):
    pt = st.ps("turned", [P, 4, N])
    turned, moved = st.sem("turned"), st.sem("moved")
    jobs = [(g, c) for g in range(TT // 4) for c in range(width // P)]

    def on_tensor(pe):
        for n, (g, c) in enumerate(jobs):
            src_ready(pe, 4 * g + 3)
            if n >= 4:
                pe.wait_ge(moved, n - 3)
            for k in range(4):
                last = pe.transpose(pt[:, n % 4, k * P:(k + 1) * P], src[:, 4 * g + k, c * P:(c + 1) * P], ident[:])
            last.then_inc(turned, 1)

    def on_scalar(act):
        for n, (g, c) in enumerate(jobs):
            act.wait_ge(turned, n + 1)
            act.copy(dst[:, c, g * N:(g + 1) * N], pt[:, n % 4, :]).then_inc(moved, 1)

    return on_tensor, on_scalar, moved


def layernorm(nc, K, name, src, dst, dstT=None, gamma=None, beta=None):
    with Stage(nc, name) as st:
        mr = st.sb("mean_rstd", [P, TT, 2])
        ready, normed, loaded = st.sem("ready"), st.sem("normed"), st.sem("loaded")
        if gamma is not None:
            gb = st.sb("gb", [P, 2, D])
        with st.block() as block:
            stats_v, stats_s = norm_stats(st, block, K, src, mr, ready)
            passes = 1 if gamma is None else 3
            if dstT is not None:
                turn_t, turn_s, _ = transposer(st, dst, dstT, D, K.ident,
                                               lambda e, t: e.wait_ge(normed, passes * (t + 1)))

            @block.sync
            def _(sp):
                if gamma is not None:
                    sp.dma_start(gb[:, 0, :], row(gamma)).then_inc(loaded, 16)
                    sp.dma_start(gb[:, 1, :], row(beta)).then_inc(loaded, 16)

            @block.vector
            def _(dve):
                stats_v(dve)
                if gamma is not None:
                    dve.wait_ge(loaded, 32)
                for t in range(TT):
                    dve.tensor_scalar(dst[:, t, :], src[:, t, :], mr[:, t, 0:1], mr[:, t, 1:2],
                                      ALU.subtract, ALU.mult).then_inc(normed, 1)
                    if gamma is not None:
                        dve.wait_ge(normed, 3 * t + 1)
                        dve.tensor_tensor(dst[:, t, :], dst[:, t, :], gb[:, 0, :], ALU.mult).then_inc(normed, 1)
                        dve.wait_ge(normed, 3 * t + 2)
                        dve.tensor_tensor(dst[:, t, :], dst[:, t, :], gb[:, 1, :], ALU.add).then_inc(normed, 1)

            @block.scalar
            def _(act):
                stats_s(act)
                if dstT is not None:
                    turn_s(act)

            @block.tensor
            def _(pe):
                if dstT is not None:
                    turn_t(pe)


def split_store(st, K, src, name):
    return [st.sb(f"{name}_{x}", list(src.shape), BF16) for x in ("hi", "mid", "lo")]


def split(link, eng, src, parts):
    hi, mid, lo = parts
    link(eng.tensor_copy(hi, src))
    link(eng.tensor_tensor(src, src, hi, ALU.subtract))
    link(eng.tensor_copy(mid, src))
    link(eng.tensor_tensor(lo, src, mid, ALU.subtract))


HD = 16
NH = D // HD
QBLOCKS = (0, 1, 2, 0, 1, 0)
KBLOCKS = (0, 0, 0, 1, 1, 2)
ROWS = HD * len(QBLOCKS)


def qkv16(nc, K, name, W, XNT, QS, KS, V, weights, bias=None, lora=None, quant=None, transposed=False):
    with Stage(nc, name) as st:
        Wt = st.sb("W", [P, DC, 3 * D])
        QF, KF = st.sb("QF", [P, DC, B * S]), st.sb("KF", [P, DC, B * S])
        qparts, kparts = split_store(st, K, QF, "q"), split_store(st, K, KF, "k")
        pm = st.ps("mm", [P, 6, N])
        pw = st.ps("w", [P, 2, N])
        loaded, wmm, wready = st.sem("loaded"), st.sem("wmm"), st.sem("wready")
        mm, evq, evk, evv = st.sem("mm"), st.sem("evq"), st.sem("evk"), st.sem("evv")
        vlink, plink, stored = st.sem("vlink"), st.sem("plink"), st.sem("stored")
        qsplit, ksplit, inv = st.sem("qsplit"), st.sem("ksplit"), st.sem("inv")
        if transposed:
            Wraw = st.sb("Wraw", [P, 3, DC, D])
        if lora is not None:
            la, lb = st.sb("la", [P, DC, HD]), st.sb("lb", [HD, 3 * D])
            laT = st.sb("laT", [HD, DC, P])
        if bias is not None:
            bqk, bv = st.sb("bqk", [P, 2, DC]), st.sb("bv", [P, D])
        if quant is not None:
            qs = st.sb("quant", [P, 3])
        nload = (3 if transposed else 1) + (2 if lora is not None else 0) + (2 if bias is not None else 0) \
            + (2 if quant is not None else 0)
        qk = [(w, c, t) for w in (0, 1) for c in range(DC) for t in range(B * S // N)]
        vt = list(range(TT // 2))
        jobs = [("qk", j) for j in qk] + [("v", j) for j in vt]
        evac = {"q": 0, "k": 0, "v": 0}
        seen = []
        for kind, j in jobs:
            k = "v" if kind == "v" else "qk"[j[0]]
            evac[k] += 1
            seen.append((k, evac[k]))
        sem_of = {"q": evq, "k": evk, "v": evv}
        with st.block() as block:
            @block.sync
            def _(sp):
                if transposed:
                    for w in range(3):
                        sp.dma_start(Wraw[:, w, :, :], weights[w].rearrange("(c p) n -> p c n", p=P)).then_inc(loaded, 16)
                else:
                    sp.dma_start(Wt[:], weights.rearrange("(c p) n -> p c n", p=P)).then_inc(loaded, 16)
                if lora is not None:
                    sp.dma_start(la[:], lora[0].rearrange("(c p) n -> p c n", p=P)).then_inc(loaded, 16)
                    sp.dma_start(lb[:], lora[1]).then_inc(loaded, 16)
                if bias is not None:
                    sp.dma_start(bqk[:].rearrange("p w c -> p (w c)"),
                                 bias[0:2 * D].rearrange("(w p) -> p w", p=P),
                                 allow_slow_non_contiguous=True).then_inc(loaded, 16)
                    sp.dma_start(bv[:], row(bias[2 * D:3 * D])).then_inc(loaded, 16)
                if quant is not None:
                    sp.dma_start(qs[:, 0:1], row(quant[0])).then_inc(loaded, 16)
                    sp.dma_start(qs[:, 1:2], row(quant[1])).then_inc(loaded, 16)
                stores = 0
                for done, parts, blocks, out in ((qsplit, qparts, QBLOCKS, QS), (ksplit, kparts, KBLOCKS, KS)):
                    sp.wait_ge(done, 4)
                    for j, part in enumerate(blocks):
                        for c in range(DC):
                            sp.dma_start(out[c * P // HD:(c + 1) * P // HD, j * HD:(j + 1) * HD, :],
                                         parts[part][:, c, :]).then_inc(stored, 16)
                            stores += 1
                sp.wait_ge(stored, 16 * stores)

            @block.tensor
            def _(pe):
                pe.wait_ge(loaded, 16 * nload)
                n = 0
                if transposed:
                    for w in range(3):
                        if n >= 2:
                            pe.wait_ge(wready, n - 1)
                        for ci in range(DC):
                            for co in range(DC):
                                last = pe.transpose(pw[:, n % 2, ci * D + co * P:ci * D + (co + 1) * P],
                                                    Wraw[:, w, co, ci * P:(ci + 1) * P], K.ident[:])
                        last.then_inc(wmm, 1)
                        n += 1
                if lora is not None:
                    for c in range(DC):
                        last = pe.transpose(pw[0:HD, 0, c * P:(c + 1) * P], la[:, c, :], K.ident[:])
                    last.then_inc(wmm, 1)
                    for c in range(DC):
                        for h in range(2):
                            n += 1
                            pe.wait_ge(wready, n)
                            pe.matmul(pw[:, n % 2, 0:3 * D // 2], laT[:, c, :], lb[:, h * 3 * D // 2:(h + 1) * 3 * D // 2],
                                      start=True, stop=True).then_inc(wmm, 1)
                    n += 1
                pe.wait_ge(wready, n)
                for m, (kind, j) in enumerate(jobs):
                    if m >= 6:
                        pe.wait_ge(sem_of[seen[m - 6][0]], seen[m - 6][1])
                    if kind == "qk":
                        w, c, t = j
                        for ci in range(DC):
                            last = pe.matmul(pm[:, m % 6, :], Wt[:, ci, w * D + c * P:w * D + (c + 1) * P],
                                             XNT[:, ci, t * N:(t + 1) * N], start=ci == 0, stop=ci == DC - 1)
                    else:
                        for k in range(2):
                            for ci in range(DC):
                                last = pe.matmul(pm[:, m % 6, k * D:(k + 1) * D],
                                                 XNT[:, ci, (2 * j + k) * P:(2 * j + k + 1) * P],
                                                 Wt[:, ci, 2 * D:3 * D], start=ci == 0, stop=ci == DC - 1)
                    last.then_inc(mm, 1)

            @block.scalar
            def _(act):
                if lora is not None:
                    act.wait_ge(wmm, 1)
                    act.mul(laT[:], pw[0:HD, 0, 0:D].rearrange("p (c n) -> p c n", c=DC), 2.0).then_inc(wready, 1)
                if bias is not None:
                    act.wait_ge(loaded, 16 * nload)
                for m, (kind, j) in enumerate(jobs):
                    if kind == "qk" and j[0] == 0:
                        _, c, t = j
                        act.wait_ge(mm, m + 1)
                        dst = QF[:, c, t * N:(t + 1) * N]
                        if bias is not None:
                            act.activation(dst, pm[:, m % 6, :], ACT.Identity, bias=bqk[:, 0, c:c + 1]).then_inc(evq, 1)
                        else:
                            act.copy(dst, pm[:, m % 6, :]).then_inc(evq, 1)

            @block.gpsimd
            def _(pool):
                pool.wait_ge(evq, len(qk) // 2)
                split(Link(pool, qsplit), pool, QF[:], [x[:] for x in qparts])

            @block.vector
            def _(dve):
                if transposed:
                    for w in range(3):
                        dve.wait_ge(wmm, w + 1)
                        dve.tensor_copy(Wt[:, :, w * D:(w + 1) * D],
                                        pw[:, w % 2, :].rearrange("p (c n) -> p c n", c=DC)).then_inc(wready, 1)
                if lora is not None:
                    n = 1
                    for c in range(DC):
                        for h in range(2):
                            cols = slice(h * 3 * D // 2, (h + 1) * 3 * D // 2)
                            dve.wait_ge(wmm, n + 1)
                            dve.tensor_tensor(Wt[:, c, cols], Wt[:, c, cols], pw[:, n % 2, 0:3 * D // 2],
                                              ALU.add).then_inc(wready, 1)
                            n += 1
                if quant is not None:
                    dve.wait_ge(loaded, 16 * nload)
                    dve.reciprocal(qs[:, 2:3], qs[:, 0:1]).then_inc(inv, 1)
                    dve.wait_ge(inv, 1)
                for m, (kind, j) in enumerate(jobs):
                    if kind == "qk" and j[0] == 1:
                        _, c, t = j
                        dve.wait_ge(mm, m + 1)
                        dst = KF[:, c, t * N:(t + 1) * N]
                        if bias is not None:
                            dve.tensor_scalar(dst, pm[:, m % 6, :], bqk[:, 1, c:c + 1], None, ALU.add).then_inc(evk, 1)
                        else:
                            dve.tensor_copy(dst, pm[:, m % 6, :]).then_inc(evk, 1)
                    if kind == "v":
                        dve.wait_ge(mm, m + 1)
                        dst = V[:, 2 * j:2 * j + 2, :]
                        src = pm[:, m % 6, :].rearrange("p (k n) -> p k n", k=2)
                        if bias is not None:
                            dve.tensor_tensor(dst, src, bv[:].rearrange("p (a n) -> p a n", a=1).to_broadcast([P, 2, D]),
                                              ALU.add).then_inc(evv, 1)
                        else:
                            dve.tensor_copy(dst, src).then_inc(evv, 1)
                dve.wait_ge(evk, len(qk) // 2)
                dve.wait_ge(evv, len(vt))
                link = Link(dve, vlink)
                if quant is not None:
                    for y in (KF[:], V[:]):
                        link(dve.tensor_scalar(y, y, qs[:, 2:3], qs[:, 1:2], ALU.mult, ALU.add))
                        link(dve.tensor_scalar(y, y, ROUND, ROUND, ALU.add, ALU.subtract))
                        link(dve.tensor_scalar(y, y, 0.0, 255.0, ALU.max, ALU.min))
                        link(dve.tensor_scalar(y, y, qs[:, 1:2], qs[:, 0:1], ALU.subtract, ALU.mult))
                split(Link(dve, ksplit), dve, KF[:], [x[:] for x in kparts])


def attention(nc, K, name, heads, scale, dv, kp, kt, causal, qsrc, ksrc, pairs, V, Y, staged):
    nk = kp * kt
    narrow = dv == HD
    vw = 32 if narrow else dv + 1
    chunks = []
    for qt in range(TB):
        end = (qt + 1) * P if causal else nk
        chunks += [(qt, k0, min(N, end - k0)) for k0 in range(0, end, N)]
    nm = len(chunks)
    nb = nm + NQ if staged else nm
    steps = []
    for qh in range(NQ):
        last = (qh + 1) * (N // P) if causal else kt
        steps += [(qh, (a, a + 1)) for a in range(0, last, 2)]
    ns = len(steps)
    early = int(ns > 3)
    per = 2 if kt > 2 else 1
    ng = ns // per
    first_of = [min(n for n, s in enumerate(steps) if s[0] == qh) for qh in range(NQ)]
    last_of = [max(n for n, s in enumerate(steps) if s[0] == qh) for qh in range(NQ)]
    UB = 4
    NI = heads // 2
    nq, nkk = len(qsrc), len(ksrc)
    kr = qsrc[0][1]
    lead = -(-nm // (ns - 1)) if early else 0
    kx = kr + 2 if staged else kr

    def maxima_by(n):
        return min(nm, lead + (nm - lead) * n // (ns - 2)) if early else nm * (n + 1) // ns

    def hidden(qh, k):
        return N // 2 if causal and k - qh * (N // P) >= N // P // 2 else 0
    with Stage(nc, name) as st:
        if staged:
            Qs = [st.sb(f"Q{j}", [P, UB, S], BF16) for j in range(nq)]
            Ks = [st.sb(f"K{j}", [P, UB, nk], BF16) for j in range(nkk)]

        def operand(staging, source, length, i, u, c0, c1, rows):
            if staged:
                return staging[0:rows, u, c0:c1]
            start = (u % 2) * length
            return source[:, bass.ds(i * 2 + u // 2, 1), start + c0:start + c1].rearrange("p a n -> p (a n)")

        def q_of(j, i, u, c0, c1, rows=kr):
            return operand(Qs[j] if staged else None, qsrc[j][0], S, i, u, c0, c1, rows)

        def k_of(j, i, u, c0, c1, rows=kr):
            return operand(Ks[j] if staged else None, ksrc[j][0], nk, i, u, c0, c1, rows)
        Vs = st.sb("V", [kp, UB, kt, vw])
        Pr = st.sb("P", [kp, 2, 2 * per, N])
        if staged:
            MR = st.sb("MR", [P, 2, TB, 2], BF16)
        else:
            MD = st.sb("MD", [P, 2, S], BF16)
        mxc = st.sb("mxc", [P, TB, 2])
        mneg = st.sb("mneg", [P, TB])
        OT = st.sb("OT", [P, NQ, N])
        rc = st.sb("rc", [P, NQ, N // P])
        sel = st.sb("sel", [P, dv + 1])
        SM, ST = st.ps("SM", [P, 2, N]), st.ps("ST", [P, 2, 2, N])
        OP, OUT = st.ps("OP", [P, N]), st.ps("OUT", [P, N // P, P])
        ld = [st.sem(f"operands{j}") for j in range(2)]
        mx_ready, mx_read, md_ready = st.sem("mx_ready"), st.sem("mx_read"), st.sem("md_ready")
        comb, st_ready, exp_done, pv_done = st.sem("comb"), st.sem("st_ready"), st.sem("exp_done"), st.sem("pv_done")
        ot_done, out_ready, rc_done, y_done = st.sem("ot_done"), st.sem("out_ready"), st.sem("rc_done"), st.sem("y_done")
        v_ready, fixed, sel_done = st.sem("v_ready"), st.sem("fixed"), st.sem("sel_done")
        comb_init, ones_done = st.sem("comb_init"), st.sem("ones_done")
        rows_ready, rows_read = st.sem("rows_ready"), st.sem("rows_read")
        nd = nq + nkk

        def following(i, u):
            return (i, u + 1) if u < UB - 1 else (i + 1, 0)

        with st.block() as block:
            @block.sync
            def _(sp):
                def load(i, hp):
                    head = i * 2 + hp
                    for j in range(nq):
                        sp.dma_start(Qs[j][0:kr, 2 * hp:2 * hp + 2, :], qsrc[j][0](head)).then_inc(ld[hp], 16)
                    for j in range(nkk):
                        sp.dma_start(Ks[j][0:kr, 2 * hp:2 * hp + 2, :], ksrc[j][0](head)).then_inc(ld[hp], 16)

                if not staged:
                    return
                for hp in range(2):
                    load(0, hp)
                with sp.Fori(1, NI, 1) as i:
                    for hp in range(2):
                        sp.wait_ge(st_ready, (i * UB + 2 * hp + 2 - UB) * ns)
                        load(i, hp)

            @block.gpsimd
            def _(pool):
                if staged:
                    pool.memset(Ks[0][kr:kx, :, :], 1.0).then_inc(ones_done, 1)
                    pool.wait_ge(ones_done, 1)
                if narrow:
                    pool.memset(sel[:], 0.0).then_inc(sel_done, 1)
                    pool.wait_ge(sel_done, 1)
                    for j in range(4):
                        pool.affine_select(out=sel[:], in_=sel[:], compare_op=ALU.not_equal, fill=1.0,
                                           base=-32 * j, pattern=[[-1, dv + 1]], channel_multiplier=1).then_inc(sel_done, 1)
                        pool.wait_ge(sel_done, j + 2)
                    pool.memset(Vs[:], 0.0).then_inc(fixed, 1)
                    pool.wait_ge(fixed, 1)
                    pool.memset(Vs[:, :, :, dv:dv + 1], 1.0).then_inc(fixed, 1)
                else:
                    pool.memset(Vs[:, :, :, dv:dv + 1], 1.0).then_inc(fixed, 2)
                    pool.tensor_copy(sel[:], K.ident[:, 0:dv + 1]).then_inc(sel_done, 5)
                pool.wait_ge(fixed, 2)

                def copy_v(i, hp):
                    head = i * 2 + hp
                    for b in range(B):
                        pool.tensor_copy(Vs[:, 2 * hp + b, :, 0:dv], V(b, head)).then_inc(v_ready, 1)

                for hp in range(2):
                    copy_v(0, hp)
                with pool.Fori(1, NI, 1) as i:
                    for hp in range(2):
                        pool.wait_ge(pv_done, (i * UB + 2 * hp + 2 - UB) * ng + 2)
                        copy_v(i, hp)

            @block.tensor
            def _(pe):
                def maxima(i, u, some):
                    U = i * UB + u
                    for c in some:
                        qt, k0, kn = chunks[c]
                        if c == 0 and staged:
                            pe.wait_ge(ld[u // 2], (i + 1) * (16 * nd))
                        if staged and c < 2:
                            pe.wait_ge(rows_read, 2 * U + c + 1)
                        else:
                            pe.wait_ge(mx_read, U * nm + c + 1)
                        diag = causal and k0 + kn == (qt + 1) * P
                        parts = [(0, kn, False)] if not diag else [(0, kn - P, False)] * (kn > P) + [(kn - P, kn, True)]
                        for c0, c1, masked in parts:
                            out = SM[:, (u * nb + c) % 2, c0:c1]
                            for n, (a, b_) in enumerate(pairs):
                                last = pe.matmul(out, q_of(a, i, u, qt * P, (qt + 1) * P),
                                                 k_of(b_, i, u, k0 + c0, k0 + c1),
                                                 start=n == 0, stop=n == len(pairs) - 1 and not masked)
                            if masked:
                                last = pe.matmul(out, K.identb[:], K.cmask[:], start=False, stop=True)
                        last.then_inc(mx_ready, 1)

                def rows(i, u):
                    U = i * UB + u
                    pe.wait_ge(md_ready, U + 1)
                    for qh in range(NQ):
                        for t in range(N // P):
                            last = pe.matmul(SM[kr:kx, (u * nb + nm + qh) % 2, t * P:(t + 1) * P],
                                             MR[:, u % 2, qh * (N // P) + t, :], K.identb[:], start=True, stop=True)
                        last.then_inc(rows_ready, 1)

                def scores(i, u, n):
                    U = i * UB + u
                    qh, kts = steps[n]
                    if n == 0 and staged:
                        pe.wait_ge(rows_read, 2 * U + 4)
                    elif n == 0:
                        pe.wait_ge(md_ready, U + 1)
                    pe.wait_ge(exp_done, U * ns + n + 1)
                    for j, k in enumerate(kts):
                        groups, jd = [(0, N, False)], k - qh * (N // P)
                        if causal and jd >= 0:
                            c0, end = hidden(qh, k), (jd + 1) * P
                            groups = [(c0, end, True)] + [(end, N, False)] * (end < N)
                        for c0, c1, masked in groups:
                            out = ST[0:kp, (u * ns + n) % 2, j, c0:c1]
                            for m, (a, b_) in enumerate(pairs):
                                last = pe.matmul(out, k_of(b_, i, u, k * kp, (k + 1) * kp, kx),
                                                 q_of(a, i, u, qh * N + c0, qh * N + c1, kx), start=m == 0,
                                                 stop=staged and not masked and m == len(pairs) - 1)
                            if masked:
                                last = pe.matmul(out, K.identb[:], K.cmaskT[:, jd, c0:c1], start=False, stop=staged)
                            if not staged:
                                last = pe.matmul(out, K.onesb[:, 0:kp], MD[:, u % 2, qh * N + c0:qh * N + c1],
                                                 start=False, stop=True)
                    last.then_inc(st_ready, 1)

                def values(i, u, g):
                    U = i * UB + u
                    mine = steps[g * per:(g + 1) * per]
                    qh = mine[0][0]
                    end = (qh + 1) * (N // P) if causal else kt
                    if g == 0:
                        pe.wait_ge(v_ready, U + 1)
                    if g * per == first_of[qh]:
                        pe.wait_ge(ot_done, 2 * U + qh)
                    pe.wait_ge(exp_done, U * ns + (g + 1) * per + 2)
                    for m, (_, kts) in enumerate(mine):
                        for j, k in enumerate(kts):
                            p = Pr[:, (u * ng + g) % 2, 2 * m + j, :]
                            if narrow:
                                c0 = hidden(qh, k)
                                cn = hidden(qh, k + 4) if k + 4 < end else N
                                out = OP[32 * (k % 4):32 * (k % 4) + 32, :]
                                for a, b_, stop in [(c0, cn, True)] * (cn > c0) + [(cn, N, False)] * (cn < N):
                                    last = pe.matmul(out[:, a:b_], Vs[:, u, k, :], p[:, a:b_], start=k < 4, stop=stop)
                            else:
                                last = pe.matmul(OP[0:vw, :], Vs[:, u, k, :], p, start=k == 0, stop=k == end - 1)
                    last.then_inc(pv_done, 1)

                def outputs(i, u, qh):
                    U = i * UB + u
                    rows = P if narrow else vw
                    pe.wait_ge(ot_done, 2 * U + qh + 1)
                    pe.wait_ge(y_done, 2 * U + qh)
                    for t in range(N // P):
                        r = rows // 2 if narrow and qh == 0 and t * P < hidden(0, 2) else rows
                        last = pe.matmul(OUT[:, t, 0:dv + 1], OT[0:r, qh, t * P:(t + 1) * P], sel[0:r, :],
                                         start=True, stop=True)
                    last.then_inc(out_ready, 1)

                def unit(i, u, last, next_last):
                    more = chunks and not last
                    ni, nu = following(i, u)
                    done = lead
                    for n in range(early, ns):
                        scores(i, u, n)
                        if more:
                            upto = maxima_by(n)
                            maxima(ni, nu, range(done, upto))
                            done = upto
                        if (n + 1) % per == 0 and n >= per:
                            values(i, u, (n + 1) // per - 2)
                        if n == last_of[0] + 1 + per:
                            outputs(i, u, 0)
                    if more and staged:
                        rows(ni, nu)
                    values(i, u, ng - 1)
                    if early and not last:
                        scores(ni, nu, 0)
                    if not (last or next_last):
                        maxima(*following(ni, nu), range(lead))
                    if last_of[1] < last_of[0] + 1 + per:
                        outputs(i, u, 0)
                    outputs(i, u, 1)

                pe.wait_ge(fixed, 2)
                pe.wait_ge(sel_done, 5)
                maxima(0, 0, range(nm))
                if staged:
                    pe.wait_ge(ones_done, 1)
                    rows(0, 0)
                if early:
                    scores(0, 0, 0)
                maxima(0, 1, range(lead))
                with pe.Fori(0, NI - 1, 1) as i:
                    for u in range(UB):
                        unit(i, u, False, False)
                for u in range(UB):
                    unit(NI - 1, u, u == UB - 1, u == UB - 2)

            @block.scalar
            def _(act):
                act.sem_inc(exp_done, 2)
                act.sem_inc(pv_done, 2)
                act.sem_inc(rows_read, 2)

                def rows(i, u):
                    U = i * UB + u
                    for qh in range(NQ):
                        act.wait_ge(rows_ready, 2 * U + qh + 1)
                        act.copy(Qs[0][kr:kx, u, qh * N:(qh + 1) * N],
                                 SM[kr:kx, (u * nb + nm + qh) % 2, :]).then_inc(rows_read, 1)

                def turned(i, u, qh):
                    U = i * UB + u
                    rows = P if narrow else vw
                    act.wait_ge(pv_done, U * ng + (last_of[qh] + 1) // per + 2)
                    act.wait_ge(y_done, 2 * U)
                    cut = hidden(0, 2) if narrow and qh == 0 else 0
                    if cut:
                        act.copy(OT[0:rows // 2, qh, 0:cut], OP[0:rows // 2, 0:cut])
                    act.copy(OT[0:rows, qh, cut:], OP[0:rows, cut:]).then_inc(ot_done, 1)

                def unit(i, u, last):
                    U = i * UB + u
                    for n in range(ns):
                        g = n // per
                        act.wait_ge(st_ready, U * ns + n + 1)
                        act.wait_ge(pv_done, U * ng + g + 1)
                        c0 = hidden(steps[n][0], steps[n][1][0])
                        act.activation(Pr[:, (u * ng + g) % 2, 2 * (n % per):2 * (n % per) + 2, c0:],
                                       ST[0:kp, (u * ns + n) % 2, :, c0:], ACT.Exp, scale=scale).then_inc(exp_done, 1)
                        if n == last_of[0] + per:
                            turned(i, u, 0)
                    if staged and not last:
                        rows(*following(i, u))
                    if last_of[1] < last_of[0] + per:
                        turned(i, u, 0)
                    turned(i, u, 1)

                if staged:
                    rows(0, 0)
                with act.Fori(0, NI - 1, 1) as i:
                    for u in range(UB):
                        unit(i, u, False)
                for u in range(UB):
                    unit(NI - 1, u, u == UB - 1)

            @block.vector
            def _(dve):
                dve.sem_inc(mx_read, 2)

                def maxima(i, u, some):
                    U = i * UB + u
                    for c in some:
                        qt, k0, kn = chunks[c]
                        dve.wait_ge(mx_ready, U * nm + c + 1)
                        dve.tensor_reduce(mxc[:, qt, k0 // N:k0 // N + 1], SM[:, (u * nb + c) % 2, 0:kn],
                                          AX.X, ALU.max).then_inc(mx_read, 1)

                def diagonal(i, u, first=False):
                    U = i * UB + u
                    dve.wait_ge(mx_read, U * nm + nm + 2)
                    if staged:
                        dve.tensor_reduce(mneg[:], mxc[:], AX.X, ALU.max, negate=True).then_inc(comb, 1)
                        dve.wait_ge(comb, 2 * U + 1)
                        dve.tensor_copy(MR[:, u % 2, :, 0], mneg[:]).then_inc(comb, 1)
                        dve.wait_ge(comb, 2 * U + 2)
                        dve.tensor_tensor(MR[:, u % 2, :, 1], mneg[:], MR[:, u % 2, :, 0], ALU.subtract).then_inc(md_ready, 1)
                        return
                    dve.wait_ge(md_ready, U)
                    dve.tensor_reduce(mneg[:], mxc[:], AX.X, ALU.max, negate=True).then_inc(comb, 1)
                    dve.wait_ge(comb, U + 1)
                    if not first:
                        dve.wait_ge(st_ready, (U - 1) * ns)
                    for t in range(TB):
                        last = dve.tensor_scalar(MD[:, u % 2, t * P:(t + 1) * P], K.identb[:], mneg[:, t:t + 1],
                                                 None, ALU.mult)
                    last.then_inc(md_ready, 1)

                def result(i, u, qh):
                    U = i * UB + u
                    head = i * 2 + u // 2
                    dve.wait_ge(out_ready, 2 * U + qh + 1)
                    dve.reciprocal(rc[:, qh, :], OUT[:, :, dv]).then_inc(rc_done, 1)
                    dve.wait_ge(rc_done, 2 * U + qh + 1)
                    t0 = (u % 2) * TB + qh * (N // P)
                    dve.tensor_tensor(Y[:, t0:t0 + N // P, bass.ds(head * dv, dv)], OUT[:, :, 0:dv],
                                      rc[:, qh, :].rearrange("p (t a) -> p t a", a=1).to_broadcast([P, N // P, dv]),
                                      ALU.mult).then_inc(y_done, 1)

                def unit(i, u, last, next_last):
                    ni, nu = following(i, u)
                    split_at = maxima_by(min(last_of[0] + 1 + per, ns - 1))
                    if not last:
                        maxima(ni, nu, range(lead, split_at))
                        if split_at < nm:
                            result(i, u, 0)
                        maxima(ni, nu, range(split_at, nm))
                        diagonal(ni, nu)
                        if split_at == nm:
                            result(i, u, 0)
                    else:
                        result(i, u, 0)
                    if not (last or next_last):
                        maxima(*following(ni, nu), range(lead))
                    result(i, u, 1)

                dve.memset(mxc[:], -3.0e38).then_inc(comb_init, 1)
                dve.wait_ge(comb_init, 1)
                maxima(0, 0, range(nm))
                diagonal(0, 0, True)
                maxima(0, 1, range(lead))
                with dve.Fori(0, NI - 1, 1) as i:
                    for u in range(UB):
                        unit(i, u, False, False)
                for u in range(UB):
                    unit(NI - 1, u, u == UB - 1, u == UB - 2)
                dve.wait_ge(y_done, 2 * UB * NI)




def project(nc, K, name, Y, width, weight, bias, lora=None):
    WC = width // P
    with Stage(nc, name) as st:
        YT = st.sb("YT", [P, WC, B * S])
        Wt = st.sb("W", [P, WC, D])
        brow = st.sb("bias", [P, D])
        pm, pw = st.ps("mm", [P, 3, 2, D]), st.ps("w", [P, D])
        loaded, wmm, wready, biased = st.sem("loaded"), st.sem("wmm"), st.sem("wready"), st.sem("biased")
        mm, added = st.sem("mm"), st.sem("added")
        if lora is not None:
            la, lb, laT = st.sb("la", [P, DC, HD]), st.sb("lb", [HD, D]), st.sb("laT", [HD, D])
        nload = 2 + (2 if lora is not None else 0)
        with st.block() as block:
            turn_t, turn_s, moved = transposer(st, Y, YT, width, K.ident, lambda e, t: None)
            turns = TT // 4 * WC

            @block.sync
            def _(sp):
                sp.dma_start(Wt[:], weight.rearrange("(c p) n -> p c n", p=P)).then_inc(loaded, 16)
                sp.dma_start(brow[:], row(bias)).then_inc(loaded, 16)
                if lora is not None:
                    sp.dma_start(la[:], lora[0].rearrange("(c p) n -> p c n", p=P)).then_inc(loaded, 16)
                    sp.dma_start(lb[:], lora[1]).then_inc(loaded, 16)

            @block.tensor
            def _(pe):
                pe.wait_ge(loaded, 16 * nload)
                if lora is not None:
                    for c in range(DC):
                        last = pe.transpose(pw[0:HD, c * P:(c + 1) * P], la[:, c, :], K.ident[:])
                    last.then_inc(wmm, 1)
                    for c in range(DC):
                        pe.wait_ge(wready, c + 1)
                        pe.matmul(pw[:], laT[:, c * P:(c + 1) * P], lb[:], start=True, stop=True).then_inc(wmm, 1)
                turn_t(pe)
                pe.wait_ge(moved, turns)
                if lora is not None:
                    pe.wait_ge(wready, 1 + DC)
                for j in range(TT // 2):
                    if j >= 3:
                        pe.wait_ge(added, j - 2)
                    for k in range(2):
                        for c in range(WC):
                            t = 2 * j + k
                            last = pe.matmul(pm[:, j % 3, k, :], YT[:, c, t * P:(t + 1) * P], Wt[:, c, :],
                                             start=c == 0, stop=c == WC - 1)
                    last.then_inc(mm, 1)

            @block.scalar
            def _(act):
                if lora is not None:
                    act.wait_ge(wmm, 1)
                    act.mul(laT[:], pw[0:HD, :], 2.0).then_inc(wready, 1)
                turn_s(act)

            @block.vector
            def _(dve):
                dve.wait_ge(loaded, 16 * nload)
                if lora is not None:
                    for c in range(DC):
                        dve.wait_ge(wmm, c + 2)
                        dve.tensor_tensor(Wt[:, c, :], Wt[:, c, :], pw[:], ALU.add).then_inc(wready, 1)
                dve.tensor_tensor(K.X[:], K.X[:], brow[:].rearrange("p (a n) -> p a n", a=1).to_broadcast([P, TT, D]),
                                  ALU.add).then_inc(biased, 1)
                dve.wait_ge(biased, 1)
                for j in range(TT // 2):
                    dve.wait_ge(mm, j + 1)
                    dve.tensor_tensor(K.X[:, 2 * j:2 * j + 2, :], K.X[:, 2 * j:2 * j + 2, :], pm[:, j % 3, :, :],
                                      ALU.add).then_inc(added, 1)


WD = 64
CT_P, CT_N = 77, 2
CL = CT_P * CT_N
CW, CW_P, CW_N = 192, 96, 2


def context(nc, K, ctx):
    with Stage(nc, "context") as st:
        raw = st.sb("raw", [CT_P, B * CT_N, CW])
        pt = st.ps("turned", [CW_P, CW_N, N])
        loaded, turned, moved = st.sem("loaded"), st.sem("turned"), st.sem("moved")
        with st.block() as block:
            @block.sync
            def _(sp):
                sp.dma_start(raw[:], ctx.rearrange("b (t p) w -> p (b t) w", p=CT_P)).then_inc(loaded, 16)

            @block.tensor
            def _(pe):
                pe.wait_ge(loaded, 16)
                for c in range(CW_N):
                    for t in range(B * CT_N):
                        last = pe.transpose(pt[:, c, t * CT_P:(t + 1) * CT_P], raw[:, t, c * CW_P:(c + 1) * CW_P],
                                            K.ident[0:CT_P, 0:CT_P])
                last.then_inc(turned, 1)

            @block.vector
            def _(dve):
                dve.wait_ge(turned, 1)
                dve.tensor_copy(K.CT[:], pt[:, :, 0:B * CL]).then_inc(moved, 1)


def stacks64(nc, K, name, kind, W, kp, src, jobs, out, bias=None):
    H = WD
    w0 = max(n for _, _, n, _, _ in jobs)
    with Stage(nc, name) as st:
        R = st.sb("R", [P, 4, w0])
        pm = st.ps("mm", [P, 4, N])
        mm, ev, done, rdone, q1, q2 = (st.sem(x) for x in ("mm", "ev", "done", "rdone", "q1", "q2"))
        with st.block() as block:
            @block.tensor
            def _(pe):
                for m, (w, c0, n, dh, d0) in enumerate(jobs):
                    if m >= 4:
                        pe.wait_ge(ev, m - 3)
                    nc_ = W.shape[1]
                    for c in range(nc_):
                        last = pe.matmul(pm[:, m % 4, 0:n], W[0:kp, c, w, :], src[0:kp, c, c0:c0 + n],
                                         start=c == 0, stop=c == nc_ - 1)
                    last.then_inc(mm, 1)

            @block.scalar
            def _(act):
                for m, (w, c0, n, dh, d0) in enumerate(jobs):
                    act.wait_ge(mm, m + 1)
                    if m >= 4:
                        act.wait_ge(done, m - 3)
                        act.wait_ge(q2, m - 3)
                    if bias is None:
                        act.copy(R[:, m % 4, 0:n], pm[:, m % 4, 0:n]).then_inc(ev, 1)
                    else:
                        act.activation(R[:, m % 4, 0:n], pm[:, m % 4, 0:n], ACT.Identity,
                                       bias=bias[:, w:w + 1]).then_inc(ev, 1)

            @block.vector
            def _(dve):
                for m, (w, c0, n, dh, d0) in enumerate(jobs):
                    o = [x[:, dh, d0:d0 + n] for x in out]
                    r = R[:, m % 4, 0:n]
                    dve.wait_ge(ev, m + 1)
                    dve.tensor_copy(o[0], r).then_inc(q1, 1)
                    dve.wait_ge(q1, m + 1)
                    dve.tensor_tensor(r, r, o[0], ALU.subtract).then_inc(rdone, 1)
                    dve.wait_ge(rdone, m + 1)
                    if kind == "q":
                        dve.tensor_copy(o[0][H:P], r[H:P]).then_inc(done, 1)
                    else:
                        dve.tensor_copy(o[1], r).then_inc(done, 1)

            @block.gpsimd
            def _(pool):
                for m, (w, c0, n, dh, d0) in enumerate(jobs):
                    o = [x[:, dh, d0:d0 + n] for x in out]
                    r = R[:, m % 4, 0:n]
                    if kind == "q":
                        pool.wait_ge(q1, m + 1)
                        pool.tensor_copy(o[1][0:H], o[0][0:H])
                        pool.wait_ge(done, m + 1)
                        pool.tensor_tensor(o[1][H:P], r[H:P], o[0][H:P], ALU.subtract).then_inc(q2, 1)
                    else:
                        pool.wait_ge(q1, m + 1)
                        pool.tensor_copy(o[2][H:P], o[0][H:P])
                        pool.wait_ge(done, m + 1)
                        pool.tensor_tensor(o[2][0:H], r[0:H], o[1][0:H], ALU.subtract).then_inc(q2, 1)


def cross_values(nc, K, name, Wv, width, V):
    with Stage(nc, name) as st:
        Wt = st.sb("W", [CW_P, CW_N, width])
        pm = st.ps("mm", [CT_P, 4, N])
        loaded, mm, ev = st.sem("loaded"), st.sem("mm"), st.sem("ev")
        with st.block() as block:
            @block.sync
            def _(sp):
                sp.dma_start(Wt[:], Wv.rearrange("(c p) n -> p c n", p=CW_P)).then_inc(loaded, 16)

            @block.tensor
            def _(pe):
                pe.wait_ge(loaded, 16)
                for t in range(B * CT_N):
                    for c in range(CW_N):
                        last = pe.matmul(pm[:, t, 0:width], K.CT[:, c, t * CT_P:(t + 1) * CT_P], Wt[:, c, :],
                                         start=c == 0, stop=c == CW_N - 1)
                    last.then_inc(mm, 1)

            @block.vector
            def _(dve):
                for t in range(B * CT_N):
                    dve.wait_ge(mm, t + 1)
                    dve.tensor_copy(V[:, t, :], pm[:, t, 0:width]).then_inc(ev, 1)


def load_twice(nc, K, name, pairs):
    with Stage(nc, name) as st:
        loaded = st.sem("loaded")
        with st.block() as block:
            @block.sync
            def _(sp):
                n = 0
                for dst, src, p in pairs:
                    for c in range(dst.shape[1]):
                        for twice in range(2):
                            sp.dma_start(dst[:, c, :, twice * WD:(twice + 1) * WD],
                                         src[c * p:(c + 1) * p, :].rearrange("p (h n) -> p h n", n=WD)).then_inc(loaded, 16)
                            n += 1
                sp.wait_ge(loaded, 16 * n)


def cross_attention(nc, K, a):
    H = 8
    with ExitStack() as ctx:
        def sb(name, shape, dt=F32):
            return ctx.enter_context(nc.sbuf_tensor(name, shape, dt))
        QA, QB = sb("c0_QA", [P, H, B * S], BF16), sb("c0_QB", [P, H, B * S], BF16)
        KK = [sb(f"c0_K{x}", [P, H, B * CL], BF16) for x in "ABC"]
        V = sb("c0_values", [CT_P, B * CT_N, H * WD])
        with nc.sbuf_tensor("c0_Wq", [P, DC, H, P], F32) as Wq, nc.sbuf_tensor("c0_Wk", [CW_P, CW_N, H, P], F32) as Wk:
            load_twice(nc, K, "c0_w", [(Wq, a["L0_xattn_Wq"], P), (Wk, a["L0_xattn_Wk"], CW_P)])
            cross_values(nc, K, "c0_v", a["L0_xattn_Wv"], H * WD, V)
            stacks64(nc, K, "c0_q", "q", Wq, P, K.XNT,
                     [(h, t * N, N, h, t * N) for h in range(H) for t in range(B * S // N)], [QA, QB])
            stacks64(nc, K, "c0_k", "k", Wk, CW_P, K.CT, [(h, 0, B * CL, h, 0) for h in range(H)], KK)
        Y = K.wide

        attention(nc, K, "c0", H, WD ** -0.5, WD, CT_P, CT_N, False, [(QA, P), (QB, P)],
                  [(x, P) for x in KK], [(0, 0), (0, 1), (1, 2)],
                  lambda b, h: V[:, b * CT_N:(b + 1) * CT_N, bass.ds(h * WD, WD)], Y, False)
    project(nc, K, "c0_out", Y, H * WD, a["L0_xattn_Wo"], a["L0_xattn_bo"])


def ranks(link, dve, scores, others, earlier, greater, equal, rank):
    link(dve.tensor_tensor(greater, others, scores, ALU.is_gt))
    link(dve.tensor_tensor(equal, others, scores, ALU.is_equal))
    link(dve.tensor_tensor(equal, equal, earlier, ALU.mult))
    link(dve.tensor_tensor(greater, greater, equal, ALU.add))
    link(dve.tensor_reduce(rank, greater, AX.X, ALU.add))


def choose_heads(nc, K, Wr, br, chosen, active):
    H = Wr.shape[1]
    with Stage(nc, "choose") as st:
        total = st.sb("total", [P, DC, B])
        W, brow = st.sb("W", [P, DC, H]), st.sb("br", [1, H])
        lg, rank, sel = st.sb("logits", [1, B, H]), st.sb("rank", [1, B, H]), st.sb("sel", [1, B, H])
        g, e = st.sb("g", [1, B * H, H]), st.sb("e", [1, B * H, H])
        earlier, place = st.sb("earlier", [1, B * H, H]), st.sb("place", [1, B, H])
        index, idx = st.sb("index", [1, B, H]), st.sb("idx", [1, B, active])
        hit = st.sb("hit", [1, B, H])
        pm = st.ps("mm", [1, B, H])
        loaded, summed, mm, chain, made = (st.sem(x) for x in ("loaded", "summed", "mm", "chain", "made"))
        with st.block() as block:
            @block.sync
            def _(sp):
                sp.dma_start(W[:], Wr.rearrange("(c p) n -> p c n", p=P)).then_inc(loaded, 16)
                sp.dma_start(brow[:], br.rearrange("(a n) -> a n", a=1)).then_inc(loaded, 16)

            @block.gpsimd
            def _(pool):
                pool.memset(earlier[:], 1.0).then_inc(made, 1)
                pool.wait_ge(made, 1)
                for b in range(B):
                    v = earlier[:, b * H:(b + 1) * H, :]
                    pool.affine_select(out=v, in_=v, compare_op=ALU.is_gt, fill=0.0, base=0,
                                       pattern=[[1, H], [-1, H]], channel_multiplier=0).then_inc(made, 1)
                pool.iota(index[:], pattern=[[0, B], [1, H]], base=0, channel_multiplier=0,
                          allow_small_or_imprecise_dtypes=True).then_inc(made, 1)

            @block.vector
            def _(dve):
                dve.tensor_reduce(total[:], K.XNT[:].rearrange("p c (b n) -> p c b n", b=B), AX.X,
                                  ALU.add).then_inc(summed, 1)
                dve.wait_ge(mm, 1)
                dve.wait_ge(made, 2 + B)
                link = Link(dve, chain)
                link(dve.tensor_scalar(lg[:], pm[:], 1.0 / S, None, ALU.mult))
                link(dve.tensor_tensor(lg[:], lg[:], brow[:].rearrange("p (a h) -> p a h", a=1).to_broadcast([1, B, H]),
                                       ALU.add))
                for b in range(B):
                    v = slice(b * H, (b + 1) * H)
                    mine = lg[:, b, :].rearrange("p (h a) -> p h a", a=1).to_broadcast([1, H, H])
                    others = lg[:, b:b + 1, :].to_broadcast([1, H, H])
                    ranks(link, dve, mine, others, earlier[:, v, :], g[:, v, :], e[:, v, :], rank[:, b, :])
                link(dve.tensor_scalar(sel[:], rank[:], float(active), None, ALU.is_lt))
                for b in range(B):
                    v = slice(b * H, (b + 1) * H)
                    link(dve.tensor_tensor(e[:, v, :], sel[:, b:b + 1, :].to_broadcast([1, H, H]), earlier[:, v, :],
                                           ALU.mult))
                    link(dve.tensor_reduce(place[:, b, :], e[:, v, :], AX.X, ALU.add))
                link(dve.tensor_tensor(index[:], index[:], sel[:], ALU.mult))
                for k in range(active):
                    link(dve.tensor_scalar(hit[:], place[:], float(k), None, ALU.is_equal))
                    link(dve.tensor_tensor(hit[:], hit[:], index[:], ALU.mult))
                    link(dve.tensor_reduce(idx[:, :, k], hit[:], AX.X, ALU.add))
                link(dve.tensor_copy(chosen[:], idx[:]))

            @block.tensor
            def _(pe):
                pe.wait_ge(loaded, 32)
                pe.wait_ge(summed, 1)
                for b in range(B):
                    for c in range(DC):
                        last = pe.matmul(pm[0:1, b, :], total[:, c, b:b + 1], W[:, c, :], start=c == 0, stop=c == DC - 1)
                last.then_inc(mm, 1)


def routed_attention(nc, K, a):
    A = 4
    with ExitStack() as ctx:
        def sb(name, shape, dt=F32):
            return ctx.enter_context(nc.sbuf_tensor(name, shape, dt))
        QA, QB = sb("m0_QA", [P, A, B * S], BF16), sb("m0_QB", [P, A, B * S], BF16)
        KK = [sb(f"m0_K{x}", [P, A, B * S], BF16) for x in "ABC"]
        V = sb("m0_values", [P, TT, A * WD])
        chosen = sb("m0_chosen", [1, B, A], I32)
        choose_heads(nc, K, a["L0_ffn_Wr"], a["L0_ffn_br"], chosen, A)
        with Stage(nc, "m0_w") as st:
            W = [st.sb(f"W{x}", [P, DC, B * A, P]) for x in "qk"]
            bias = [st.sb(f"b{x}", [P, B * A]) for x in "qk"]
            Wv, bv = st.sb("Wv", [P, DC, B, A * WD]), st.sb("bv", [P, B, A * WD])
            with Stage(nc, "m0_load") as ld:
                loaded, loaded2 = ld.sem("loaded"), ld.sem("loaded2")
                with ld.block() as block:
                    def fetch(eng, loaded, Wx, bx, wsrc, bsrc, n):
                        for b in range(B):
                            for k in range(A):
                                w = b * A + k
                                h = eng.value_load(chosen[0:1, b, k:k + 1], min_val=0, max_val=15)
                                src = wsrc.rearrange("(c p) n -> p c n", p=P)[:, :, bass.ds(h * WD, WD)]
                                bcol = bsrc[bass.ds(h * WD, WD)].rearrange("(p a) -> p a", a=1)
                                for twice in range(2):
                                    eng.dma_start(Wx[:, :, w, twice * WD:(twice + 1) * WD], src).then_inc(loaded, 16)
                                    eng.dma_start(bx[twice * WD:(twice + 1) * WD, w:w + 1], bcol,
                                                  allow_slow_non_contiguous=True).then_inc(loaded, 16)
                                    n += 2
                        return n

                    @block.sync
                    def _(sp):
                        n = fetch(sp, loaded, W[0], bias[0], a["L0_ffn_Wq"], a["L0_ffn_bq"], 0)
                        sp.wait_ge(loaded, 16 * n)

                    @block.scalar
                    def _(act):
                        n = fetch(act, loaded2, W[1], bias[1], a["L0_ffn_Wk"], a["L0_ffn_bk"], 0)
                        for b in range(B):
                            for k in range(A):
                                h = act.value_load(chosen[0:1, b, k:k + 1], min_val=0, max_val=15)
                                src = a["L0_ffn_Wv"].rearrange("(c p) n -> p c n", p=P)[:, :, bass.ds(h * WD, WD)]
                                act.dma_start(Wv[:, :, b, k * WD:(k + 1) * WD], src).then_inc(loaded2, 16)
                                act.dma_start(bv[:, b, k * WD:(k + 1) * WD],
                                              row(a["L0_ffn_bv"][bass.ds(h * WD, WD)])).then_inc(loaded2, 16)
                                n += 2
                        act.wait_ge(loaded2, 16 * n)
            jobs = [(b * A + k, b * S + t * N, N, k, b * S + t * N)
                    for b in range(B) for k in range(A) for t in range(S // N)]
            stacks64(nc, K, "m0_q", "q", W[0], P, K.XNT, jobs, [QA, QB], bias=bias[0])
            stacks64(nc, K, "m0_k", "k", W[1], P, K.XNT, jobs, KK, bias=bias[1])
            with Stage(nc, "m0_v") as vs:
                pm = vs.ps("mm", [P, 4, N])
                mm, ev = vs.sem("mm"), vs.sem("ev")
                with vs.block() as block:
                    @block.tensor
                    def _(pe):
                        for t in range(TT):
                            if t >= 4:
                                pe.wait_ge(ev, t - 3)
                            for c in range(DC):
                                last = pe.matmul(pm[:, t % 4, 0:A * WD], K.XNT[:, c, t * P:(t + 1) * P], Wv[:, c, t // TB, :],
                                                 start=c == 0, stop=c == DC - 1)
                            last.then_inc(mm, 1)

                    @block.vector
                    def _(dve):
                        for t in range(TT):
                            dve.wait_ge(mm, t + 1)
                            dve.tensor_tensor(V[:, t, :], pm[:, t % 4, 0:A * WD], bv[:, t // TB, :], ALU.add).then_inc(ev, 1)

        attention(nc, K, "m0", A, WD ** -0.5, WD, P, TB, False, [(QA, P), (QB, P)],
                  [(x, P) for x in KK], [(0, 0), (0, 1), (1, 2)],
                  lambda b, h: V[:, b * TB:(b + 1) * TB, bass.ds(h * WD, WD)], K.XN, False)
    project(nc, K, "m0_out", K.XN, A * WD, a["L0_ffn_Wo"], a["L0_ffn_bo"])


def relative_bias(nc, K, V, table, Y, G):
    R = table.shape[0]
    assert R < N and S - 1 - R >= N and S == 2 * N
    KT = N // P
    U = 2 * N
    HW = N + (KT - 1) * P
    with Stage(nc, "bias") as st:
        tb, gt = st.sb("table", [P, R // P + 1, NH]), st.sb("gt", [NH, U])
        crow = st.sb("crow", [P, NH])
        flip, sel = st.sb("flip", [P, P]), st.sb("sel", [P, 32])
        vr = st.sb("vr", [P, B, KT, D])
        slot, hk = st.sb("slot", [P, 2, KT, B, HD]), st.sb("hankel", [P, 2, HW])
        ot = st.sb("ot", [P, 2, N])
        cs = st.sb("cs", [P, B, D])
        ps_r, ps_s = st.ps("rev", [P, 2, 2, D]), st.ps("sum", [P, B, D])
        ps_t, ps_o, ps_f = st.ps("turn", [NH, N]), st.ps("o", [P, 2, N]), st.ps("f", [P, 2, N])
        loaded, made, turned, gdone, stored = (st.sem(x) for x in ("loaded", "made", "turned", "gdone", "stored"))
        rev, revc, sums, chain = (st.sem(x) for x in ("rev", "revc", "sums", "chain"))
        hl = [st.sem(f"hankel{j}") for j in range(2)]
        vs, od, oc, fd, yd = (st.sem(x) for x in ("vslot", "o", "ocopied", "final", "y"))
        with st.block() as block:
            @block.sync
            def _(sp):
                full = R // P * P
                sp.dma_start(tb[:, 0:R // P, :], table[0:full, :].rearrange("(t p) h -> p t h", p=P)).then_inc(loaded, 16)
                sp.dma_start(tb[0:R - full, R // P, :], table[full:R, :]).then_inc(loaded, 16)
                sp.dma_start(crow[:], row(table[R - 1, :])).then_inc(loaded, 16)
                sp.wait_ge(gdone, 3)
                sp.dma_start(G, gt[:]).then_inc(stored, 16)
                sp.wait_ge(stored, 16)

                def load(i, j):
                    src = bass.AP(G.tensor, (i * 2 + j) * U, [[1, P], [1, HW]])
                    sp.dma_start(hk[:, j, :], src).then_inc(hl[j], 16)

                for j in range(2):
                    load(0, j)
                with sp.Fori(1, NH // 2, 1) as i:
                    for j in range(2):
                        sp.wait_ge(od, i * 2 + j - 1)
                        load(i, j)

            @block.gpsimd
            def _(pool):
                pool.memset(flip[:], 0.0).then_inc(made, 1)
                pool.memset(sel[:], 0.0).then_inc(made, 1)
                pool.wait_ge(made, 2)
                pool.affine_select(out=flip[:], in_=flip[:], compare_op=ALU.not_equal, fill=1.0, base=-(P - 1),
                                   pattern=[[1, P]], channel_multiplier=1).then_inc(made, 1)
                for j in range(4):
                    pool.affine_select(out=sel[:], in_=sel[:], compare_op=ALU.not_equal, fill=1.0, base=-32 * j,
                                       pattern=[[-1, 32]], channel_multiplier=1).then_inc(made, 1)
                    pool.wait_ge(made, 4 + j)
                pool.wait_ge(revc, B * KT // 2)

                def copy_v(i, j):
                    for b in range(B):
                        last = pool.tensor_copy(slot[:, j, :, b, :], vr[:, b, :, bass.ds((i * 2 + j) * HD, HD)])
                    last.then_inc(vs, 1)

                for j in range(2):
                    copy_v(0, j)
                with pool.Fori(1, NH // 2, 1) as i:
                    for j in range(2):
                        pool.wait_ge(od, i * 2 + j - 1)
                        copy_v(i, j)

            @block.tensor
            def _(pe):
                pe.wait_ge(loaded, 48)
                for t in range(R // P + 1):
                    n = min(P, R - t * P)
                    last = pe.transpose(ps_t[:, t * P:t * P + n], tb[0:n, t, :], K.ident[0:n, 0:n])
                last.then_inc(turned, 1)
                for b in range(B):
                    for t in range(TB):
                        last = pe.matmul(ps_s[:, b, :], K.ones[:], V[:, b * TB + t, :], start=t == 0, stop=t == TB - 1)
                last.then_inc(sums, 1)
                pe.wait_ge(made, 7)
                for n in range(B * KT // 2):
                    if n >= 2:
                        pe.wait_ge(revc, n - 1)
                    for k in range(2):
                        b, t = divmod(2 * n + k, KT)
                        last = pe.matmul(ps_r[:, n % 2, k, :], flip[:], V[:, b * TB + N // P + t, :], start=True, stop=True)
                    last.then_inc(rev, 1)

                def head(i, j):
                    h = i * 2 + j
                    pe.wait_ge(hl[j], (i + 1) * 16)
                    pe.wait_ge(vs, h + 1)
                    pe.wait_ge(oc, h + 1)
                    for k in range(KT):
                        last = pe.matmul(ps_o[32 * k:32 * k + 32, j, :], slot[:, j, k, :, :].rearrange("p b d -> p (b d)"),
                                         hk[:, j, (KT - 1 - k) * P:(KT - 1 - k) * P + N], start=True, stop=True)
                    last.then_inc(od, 1)
                    pe.wait_ge(oc, h + 3)
                    pe.wait_ge(yd, h + 1)
                    for t in range(KT):
                        last = pe.matmul(ps_f[:, j, t * B * HD:(t + 1) * B * HD], ot[:, j, t * P:(t + 1) * P],
                                         sel[:], start=True, stop=True)
                    last.then_inc(fd, 1)

                with pe.Fori(0, NH // 2, 1) as i:
                    for j in range(2):
                        head(i, j)

            @block.scalar
            def _(act):
                act.sem_inc(oc, 2)
                for n in range(B * KT // 2):
                    act.wait_ge(rev, n + 1)
                    b, t = divmod(2 * n, KT)
                    act.copy(vr[:, b, t:t + 2, :], ps_r[:, n % 2, :, :]).then_inc(revc, 1)
                with act.Fori(0, NH // 2, 1) as i:
                    for j in range(2):
                        act.wait_ge(od, i * 2 + j + 1)
                        act.wait_ge(fd, i * 2 + j + 1)
                        act.copy(ot[:, j, :], ps_o[:, j, :]).then_inc(oc, 1)

            @block.vector
            def _(dve):
                dve.sem_inc(yd, 2)
                dve.sem_inc(fd, 2)
                dve.memset(gt[:], 0.0).then_inc(gdone, 1)
                dve.wait_ge(turned, 1)
                dve.wait_ge(gdone, 1)
                dve.tensor_copy(gt[:, 0:R], ps_t[:, 0:R]).then_inc(gdone, 1)
                dve.wait_ge(gdone, 2)
                dve.tensor_scalar(gt[:, 0:R], ps_t[:, 0:R], gt[:, R - 1:R], None, ALU.subtract).then_inc(gdone, 1)
                dve.wait_ge(sums, 1)
                dve.wait_ge(loaded, 48)
                link = Link(dve, chain)
                for b in range(B):
                    link(dve.tensor_tensor(cs[:, b, :].rearrange("p (h d) -> p h d", d=HD),
                                           ps_s[:, b, :].rearrange("p (h d) -> p h d", d=HD),
                                           crow[:].rearrange("p (h a) -> p h a", a=1).to_broadcast([P, NH, HD]), ALU.mult))
                    y = Y[:, b * TB:(b + 1) * TB, :]
                    link(dve.tensor_tensor(y, y, cs[:, b:b + 1, :].to_broadcast([P, TB, D]), ALU.add))
                with dve.Fori(0, NH // 2, 1) as i:
                    for j in range(2):
                        h = i * 2 + j
                        dve.wait_ge(fd, h + 3)
                        for b in range(B):
                            y = Y[:, b * TB:b * TB + KT, bass.ds(h * HD, HD)]
                            f = ps_f[:, j, 0:KT * B * HD].rearrange("p (t b d) -> p t b d", t=KT, b=B)
                            last = dve.tensor_tensor(y, y, f[:, :, b, :], ALU.add)
                        last.then_inc(yd, 1)


XH, XD, TOP = 4, 32, 32


def sparse_cross(nc, K, a, text_mask, ctx_mask, CTT):
    Wq, Wk, Wv = (a[f"L1_xattn_W{x}"] for x in "qkv")
    with Stage(nc, "e_att") as st:
        wq, wk = st.sb("wq", [P, DC, P]), st.sb("wk", [CW_P, CW_N, P])
        wv, V = st.sb("wv", [CW_P, CW_N, D]), st.sb("V", [CT_P, B * CT_N, D])
        QT, KT = st.sb("QT", [P, B * S]), st.sb("KT", [P, B * CL])
        AT = st.sb("AT", [CT_P, CT_N, B * S])
        mraw, mrow = st.sb("mraw", [P, B, CL], mybir.dt.uint8), st.sb("mrow", [P, B, CL])
        traw, tmask = st.sb("traw", [P, TT], mybir.dt.uint8), st.sb("tmask", [P, TT])
        sc = st.sb("sc", [P, 2, XH, CL])
        left, ex, mk = st.sb("left", [P, XH, CL]), st.sb("ex", [P, 2, XH, CL]), st.sb("mk", [P, XH, CL])
        top, neg = st.sb("top", [P, XH, TOP // 8, 8]), st.sb("neg", [P, 2, XH])
        den, r = st.sb("den", [P, XH]), st.sb("r", [P, XH])
        mean = st.sb("mean", [P, 2, CL])
        ps, pt, pc = st.ps("s", [P, XH, N]), st.ps("t", [CT_P, 2, N]), st.ps("c", [P, 2, N])
        loaded, mm, ev, maskd = (st.sem(x) for x in ("loaded", "mm", "ev", "maskd"))
        s_ready, s_read, chain, e_go, e_done = (st.sem(x) for x in ("s_ready", "s_read", "chain", "e_go", "e_done"))
        m_ready, t_ready, t_done, c_ready, c_done = (st.sem(x) for x in ("m_ready", "t_ready", "t_done", "c_ready", "c_done"))
        nload = 4 + 2 * B
        jobs = [("q", t) for t in range(B * S // N)] + [("k", 0)] + [("v", t) for t in range(B * CT_N)]
        with st.block() as block:
            @block.sync
            def _(sp):
                sp.dma_start(wq[:], Wq.rearrange("(c p) n -> p c n", p=P)).then_inc(loaded, 16)
                sp.dma_start(wk[:], Wk.rearrange("(c p) n -> p c n", p=CW_P)).then_inc(loaded, 16)
                sp.dma_start(wv[:], Wv.rearrange("(c p) n -> p c n", p=CW_P)).then_inc(loaded, 16)
                sp.dma_start(mraw[:].rearrange("p b n -> p (b n)"), row(ctx_mask.rearrange("b n -> (b n)"))).then_inc(loaded, 16)
                for b in range(B):
                    for x in range(2):
                        sp.dma_start(traw[:, b * TB + x * TB // 2:b * TB + (x + 1) * TB // 2],
                                     text_mask[b].rearrange("(m p x) -> p x m", p=P, x=2)[:, x, :],
                                     allow_slow_non_contiguous=True).then_inc(loaded, 16)

            @block.tensor
            def _(pe):
                pe.wait_ge(loaded, 16 * nload)
                for m, (kind, t) in enumerate(jobs):
                    if m >= 2:
                        pe.wait_ge(ev, m - 1)
                    out = pc[:, m % 2, :]
                    for c in range(DC):
                        kw = dict(start=c == 0, stop=c == DC - 1)
                        if kind == "q":
                            last = pe.matmul(out, wq[:, c, :], K.XNT[:, c, t * N:(t + 1) * N], **kw)
                        elif kind == "k":
                            last = pe.matmul(out[:, 0:B * CL], wk[:, c, :], K.CT[:, c, :], **kw)
                        else:
                            last = pe.matmul(out[0:CT_P, 0:D], K.CT[:, c, t * CT_P:(t + 1) * CT_P], wv[:, c, :], **kw)
                    last.then_inc(mm, 1)
                pe.wait_ge(ev, len(jobs))

                def turn(t):
                    pe.wait_ge(m_ready, t + 1)
                    if t >= 2:
                        pe.wait_ge(t_done, t - 1)
                    for j in range(CT_N):
                        last = pe.transpose(pt[:, t % 2, j * P:(j + 1) * P], mean[:, t % 2, j * CT_P:(j + 1) * CT_P],
                                            K.ident[:])
                    last.then_inc(t_ready, 1)

                for t in range(TT):
                    b = t // TB
                    if t:
                        pe.wait_ge(s_read, t)
                    for h in range(XH):
                        last = pe.matmul(ps[:, h, 0:CL], QT[h * XD:(h + 1) * XD, t * P:(t + 1) * P],
                                         KT[h * XD:(h + 1) * XD, b * CL:(b + 1) * CL], start=True, stop=True)
                    last.then_inc(s_ready, 1)
                    if t:
                        turn(t - 1)
                turn(TT - 1)
                pe.wait_ge(t_done, TT)
                for m in range(DC * B * S // N):
                    c, t = divmod(m, B * S // N)
                    b = t // (S // N)
                    if m >= 2:
                        pe.wait_ge(c_done, m - 1)
                    for j in range(CT_N):
                        last = pe.matmul(pc[:, m % 2, :], V[:, b * CT_N + j, c * P:(c + 1) * P],
                                         AT[:, j, t * N:(t + 1) * N], start=j == 0, stop=j == CT_N - 1)
                    last.then_inc(c_ready, 1)

            @block.scalar
            def _(act):
                for m, (kind, t) in enumerate(jobs):
                    act.wait_ge(mm, m + 1)
                    src = pc[:, m % 2, :]
                    if kind == "q":
                        act.copy(QT[:, t * N:(t + 1) * N], src).then_inc(ev, 1)
                    elif kind == "k":
                        act.copy(KT[:], src[:, 0:B * CL]).then_inc(ev, 1)
                    else:
                        act.copy(V[:, t, :], src[0:CT_P, 0:D]).then_inc(ev, 1)
                for t in range(TT):
                    act.wait_ge(e_go, t + 1)
                    for h in range(XH):
                        last = act.activation(ex[:, t % 2, h, :], sc[:, t % 2, h, :], ACT.Exp, bias=neg[:, t % 2, h:h + 1])
                    last.then_inc(e_done, 1)
                    if t:
                        act.wait_ge(t_ready, t)
                        act.copy(AT[:, :, (t - 1) * P:t * P],
                                 pt[:, (t - 1) % 2, 0:CT_N * P].rearrange("p (j n) -> p j n", j=CT_N)).then_inc(t_done, 1)
                act.wait_ge(t_ready, TT)
                act.copy(AT[:, :, (TT - 1) * P:TT * P],
                         pt[:, (TT - 1) % 2, 0:CT_N * P].rearrange("p (j n) -> p j n", j=CT_N)).then_inc(t_done, 1)
                for m in range(DC * B * S // N):
                    c, t = divmod(m, B * S // N)
                    act.wait_ge(c_ready, m + 1)
                    act.copy(CTT[:, c, t * N:(t + 1) * N], pc[:, m % 2, :]).then_inc(c_done, 1)

            @block.vector
            def _(dve):
                link = Link(dve, chain)
                dve.wait_ge(loaded, 16 * nload)
                link(dve.tensor_copy(mrow[:], mraw[:]))
                link(dve.tensor_scalar(mrow[:], mrow[:], 1.0, -NEG, ALU.subtract, ALU.mult))
                link(dve.tensor_copy(tmask[:], traw[:]))
                link(dve.tensor_scalar(tmask[:], tmask[:], 1.0 / XH, None, ALU.mult))
                for t in range(TT):
                    b, s2 = t // TB, sc[:, t % 2, :, :]
                    dve.wait_ge(s_ready, t + 1)
                    if t >= 2:
                        dve.wait_ge(e_done, t - 1)
                    dve.scalar_tensor_tensor(out=s2, in0=ps[:, :, 0:CL], scalar=XD ** -0.5,
                                             in1=mrow[:, b:b + 1, :].to_broadcast([P, XH, CL]),
                                             op0=ALU.mult, op1=ALU.add).then_inc(s_read, 1)
                    dve.wait_ge(s_read, t + 1)
                    for n in range(TOP // 8):
                        for h in range(XH):
                            last = dve.max(top[:, h, n, :], s2[:, h, :] if n == 0 else left[:, h, :])
                        link(last)
                        if n == 0:
                            dve.tensor_scalar(neg[:, t % 2, :], top[:, :, 0, 0], -1.0, None, ALU.mult).then_inc(e_go, 1)
                        for h in range(XH):
                            last = dve.match_replace(left[:, h, :], top[:, h, n, :], s2[:, h, :] if n == 0 else left[:, h, :],
                                                     -3.0e38)
                        link(last)
                    link(dve.tensor_tensor(mk[:], left[:], s2, ALU.not_equal))
                    dve.wait_ge(e_done, t + 1)
                    link(dve.tensor_tensor(mk[:], mk[:], ex[:, t % 2, :, :], ALU.mult))
                    link(dve.tensor_reduce(den[:], mk[:], AX.X, ALU.add))
                    link(dve.reciprocal(r[:], den[:]))
                    link(dve.tensor_scalar(r[:], r[:], tmask[:, t:t + 1], None, ALU.mult))
                    if t >= 2:
                        dve.wait_ge(t_ready, t - 1)
                    m2 = mean[:, t % 2, :]
                    link(dve.tensor_scalar(m2, mk[:, 0, :], r[:, 0:1], None, ALU.mult))
                    for h in range(1, XH):
                        last = dve.scalar_tensor_tensor(out=m2, in0=mk[:, h, :], scalar=r[:, h:h + 1], in1=m2,
                                                        op0=ALU.mult, op1=ALU.add)
                        if h < XH - 1:
                            link(last)
                    last.then_inc(m_ready, 1)


def film(nc, K, name, CTT, W, bias, gate, dst):
    with Stage(nc, name) as st:
        Wt, brow, g = st.sb("W", [P, DC, 2 * D]), st.sb("bias", [P, 2 * D]), st.sb("gate", [P, 1])
        f = st.sb("f", [P, 2, 2 * D])
        pm = st.ps("mm", [P, 3, N])
        loaded, mm, fd, d1, d2, d3 = (st.sem(x) for x in ("loaded", "mm", "fd", "d1", "d2", "d3"))
        with st.block() as block:
            @block.sync
            def _(sp):
                sp.dma_start(Wt[:], W.rearrange("(c p) n -> p c n", p=P)).then_inc(loaded, 16)
                sp.dma_start(brow[:], row(bias)).then_inc(loaded, 16)
                sp.dma_start(g[:], row(gate)).then_inc(loaded, 16)

            @block.tensor
            def _(pe):
                pe.wait_ge(loaded, 48)
                for t in range(TT):
                    if t >= 3:
                        pe.wait_ge(fd, t - 2)
                    for c in range(DC):
                        last = pe.matmul(pm[:, t % 3, :], CTT[:, c, t * P:(t + 1) * P], Wt[:, c, :],
                                         start=c == 0, stop=c == DC - 1)
                    last.then_inc(mm, 1)

            @block.vector
            def _(dve):
                dve.wait_ge(loaded, 48)
                for t in range(TT):
                    ft = f[:, t % 2, :]
                    dve.wait_ge(mm, t + 1)
                    if t >= 2:
                        dve.wait_ge(d3, t - 1)
                    dve.tensor_tensor(ft, pm[:, t % 3, :], brow[:], ALU.add).then_inc(fd, 1)
                    dve.wait_ge(fd, t + 1)
                    dve.tensor_scalar(ft, ft, g[:, 0:1], None, ALU.mult).then_inc(d1, 1)
                    dve.wait_ge(d1, t + 1)
                    dve.scalar_tensor_tensor(out=dst[:, t, :], in0=ft[:, 0:D], scalar=1.0, in1=dst[:, t, :],
                                             op0=ALU.add, op1=ALU.mult).then_inc(d2, 1)

            @block.gpsimd
            def _(pool):
                for t in range(TT):
                    pool.wait_ge(d2, t + 1)
                    pool.tensor_tensor(dst[:, t, :], dst[:, t, :], f[:, t % 2, D:], ALU.add).then_inc(d3, 1)


TWO_PI = 6.283185307179586
FACT = [1.0, 1.0, 1 / 2, 1 / 6, 1 / 24, 1 / 120, 1 / 720, 1 / 5040]
LN2_HI, LN2_LO = 0.693359375, -2.12194440e-4
PI2_HI, PI2_LO = 6.28125, 6.283185307179586 - 6.28125
NS = 64
LB = S // P


def accurate_exp(link, eng, out, x, k, r, pw):
    link(eng.tensor_scalar(k, x, 1.4426950408889634, ROUND, ALU.mult, ALU.add))
    link(eng.tensor_scalar(k, k, ROUND, -126.0, ALU.subtract, ALU.max))
    link(eng.tensor_scalar(k, k, 127.0, None, ALU.min))
    link(eng.scalar_tensor_tensor(out=r, in0=k, scalar=-LN2_HI, in1=x, op0=ALU.mult, op1=ALU.add))
    link(eng.scalar_tensor_tensor(out=r, in0=k, scalar=-LN2_LO, in1=r, op0=ALU.mult, op1=ALU.add))
    link(eng.tensor_scalar(k, k, 127.0, 8388608.0, ALU.add, ALU.mult))
    link(eng.tensor_copy(pw, k))
    link(eng.tensor_scalar(out, r, FACT[7], None, ALU.mult))
    for n in range(6, 0, -1):
        link(eng.scalar_tensor_tensor(out=out, in0=out, scalar=FACT[n], in1=r, op0=ALU.add, op1=ALU.mult))
    link(eng.scalar_tensor_tensor(out=out, in0=out, scalar=1.0, in1=pw.bitcast(F32), op0=ALU.add, op1=ALU.mult))


def by_parity(ap):
    return ap.rearrange("(m p x) d -> p x m d", p=P, x=2)


def ssm_kernel(nc, K, a, KN):
    CH, SL = 16, 4
    with Stage(nc, "ssm") as st:
        raw = st.sb("raw", [P, 4, DC, 2, NS])
        V = [st.sb(f"v{n}", [P, D]) for n in range(4)]
        Ar, Ai, Cr, Ci = V
        dt, ar, tw = st.sb("dt", [P, D]), st.sb("ar", [P, D]), st.sb("tw", [P, D])
        T = [st.sb(f"t{n}", [P, D]) for n in range(8)]
        pw = st.sb("pw", [P, D], I32)
        R, Rk = st.sb("R", [P, D, LB]), [st.sb(f"Rk{n}", [P, D, LB]) for n in range(3)]
        posn, blk, odd, start = st.sb("pos", [P, P]), st.sb("blk", [P, LB]), st.sb("odd", [P, LB]), st.sb("start", [P, LB])
        ph = st.sb("ph", [P, 8])
        F, G = st.sb("F", [P, SL, CH, P]), st.sb("G", [P, SL, CH, P])
        W2 = st.sb("W2", [P, CH, P])
        pv, pk = st.ps("turned", [P, 4, N]), st.ps("k", [P, D, LB])
        loaded, chain, turned, made, actd, coef = (st.sem(x) for x in ("loaded", "chain", "turned", "made", "actd", "coef"))
        f1, f2, f3, f4, g1, sn, wd, kd = (st.sem(x) for x in ("f1", "f2", "f3", "f4", "g1", "sn", "wd", "kd"))
        e1, ask, ans, kcopied = st.sem("e1"), st.sem("ask"), st.sem("ans"), st.sem("kcopied")
        stored, reloaded = st.sem("stored"), st.sem("reloaded")
        names = ("A_re", "A_im", "C_re", "C_im")
        EPS = 1e-5
        NCH = D // CH
        def asked(T, Rk):
            return [(T[5][:], T[3][:], 0.5, None, ACT.Sin), (T[6][:], T[3][:], 1.0, None, ACT.Sin),
                    (Rk[0][:], Rk[0][:], -6.283185, 2, ACT.Sin), (Rk[1][:], Rk[1][:], -6.283185, None, ACT.Sin),
                    (Rk[2][:], Rk[2][:], 1.0, None, ACT.Exp)]

        with st.block() as block:
            @block.sync
            def _(sp):
                for j, x in enumerate(names):
                    for twice in range(2):
                        sp.dma_start(raw[:, j, :, twice, :],
                                     a["L1_xattn_" + x].rearrange("(c p) n -> p c n", p=P)).then_inc(loaded, 16)
                sp.dma_start(dt[:], row(a["L1_xattn_log_dt"])).then_inc(loaded, 16)
                for b in range(B):
                    sp.dma_start(K.scratch[b].rearrange("(t p) d -> p t d", p=P),
                                 K.X[:, b * TB:(b + 1) * TB, :]).then_inc(stored, 16)
                sp.wait_ge(stored, 16 * B)
                for b in range(B):
                    for x in range(2):
                        sp.dma_start(K.X[:, b * TB + x * TB // 2:b * TB + (x + 1) * TB // 2, :],
                                     by_parity(K.scratch[b])[:, x, :, :]).then_inc(reloaded, 16)
                sp.wait_ge(reloaded, 16 * B * 2)

            @block.tensor
            def _(pe):
                pe.wait_ge(loaded, 16 * 9)
                for j in range(4):
                    for c in range(DC):
                        last = pe.transpose(pv[:, j, c * P:(c + 1) * P], raw[:, j, c, :, :].rearrange("p t n -> p (t n)"),
                                            K.ident[:])
                last.then_inc(turned, 1)
                pe.wait_ge(coef, 1)

                def slot(i, j):
                    q = i * SL + j
                    pe.wait_ge(wd, q + 1 + SL)
                    for c in range(CH):
                        last = pe.matmul(pk[:, bass.ds(q * CH + c, 1), :].rearrange("p a n -> p (a n)"), F[:, j, c, :],
                                         R[:, bass.ds(q * CH + c, 1), :].rearrange("p a n -> p (a n)"),
                                         start=True, stop=True)
                    last.then_inc(kd, 1)

                with pe.Fori(0, NCH // SL, 1) as i:
                    for j in range(SL):
                        slot(i, j)

            @block.gpsimd
            def _(pool):
                pool.iota(posn[:], pattern=[[2, P]], base=0, channel_multiplier=0,
                          allow_small_or_imprecise_dtypes=True).then_inc(made, 1)
                for x, steps in ((blk, (1, 0)), (odd, (0, 1)), (start, (2 * P, 1))):
                    pool.iota(x[:], pattern=[[steps[1], 2], [steps[0], LB // 2]], base=0, channel_multiplier=0,
                              allow_small_or_imprecise_dtypes=True).then_inc(made, 1)
                pool.wait_ge(coef, 1)

                def growth(q, j):
                    pool.wait_ge(wd, q + 1)
                    pool.tensor_tensor(G[:, j, :, :], ar[:, bass.ds(q * CH, CH)].rearrange("p (c a) -> p c a", a=1)
                                       .to_broadcast([P, CH, P]),
                                       posn[:].rearrange("p (a n) -> p a n", a=1).to_broadcast([P, CH, P]),
                                       ALU.mult).then_inc(g1, 1)

                def pair(i, h, more):
                    for j in (2 * h, 2 * h + 1):
                        if more:
                            growth(i * SL + j + 2, (j + 2) % SL)
                    for j in (2 * h, 2 * h + 1):
                        q = i * SL + j
                        pool.wait_ge(sn, q + 1)
                        pool.wait_ge(e1, q + 1)
                        pool.tensor_tensor(F[:, j, :, :], F[:, j, :, :], G[:, j, :, :], ALU.mult).then_inc(wd, 1)

                for j in range(2):
                    growth(j, j)
                with pool.Fori(0, NCH // SL - 1, 1) as i:
                    for h in range(2):
                        pair(i, h, True)
                for h in range(2):
                    pair(NCH // SL - 1, h, h == 0)

            @block.scalar
            def _(act):
                act.sem_inc(kd, SL)
                act.sem_inc(wd, SL)
                for n, (o, x, s, bcol, fn) in enumerate(asked(T, Rk)):
                    act.wait_ge(ask, n + 1)
                    act.activation(o, x, fn, scale=s, **({} if bcol is None else {"bias": ph[:, bcol:bcol + 1]})).then_inc(ans, 1)
                with act.Fori(0, NCH // SL, 1) as i:
                    for pair in range(0, SL, 2):
                        for j in (pair, pair + 1):
                            q = i * SL + j
                            act.wait_ge(f4, q + 1)
                            act.activation(F[:, j, :, :], F[:, j, :, :], ACT.Sin, scale=-6.283185,
                                           bias=ph[:, 1:2]).then_inc(sn, 1)
                        for j in (pair, pair + 1):
                            q = i * SL + j
                            act.wait_ge(g1, q + 1)
                            act.activation(G[:, j, :, :], G[:, j, :, :], ACT.Exp).then_inc(e1, 1)
                act.wait_ge(kd, NCH + SL)
                for b in range(LB // 2):
                    d = slice(b * D * 2 // LB, (b + 1) * D * 2 // LB)
                    act.copy(KN[:, :, d], pk[:, d, :].rearrange("p c l -> p l c")).then_inc(kcopied, 1)

            @block.vector
            def _(dve):
                link = Link(dve, chain)
                tt, ts, stt = dve.tensor_tensor, dve.tensor_scalar, dve.scalar_tensor_tensor
                top, bot = slice(0, NS), slice(NS, P)
                for rows, phase in ((top, 0.25), (bot, 0.0)):
                    link(dve.memset(ph[rows, 0:1], phase))
                    link(dve.memset(ph[rows, 1:2], phase * TWO_PI))
                    link(dve.memset(ph[rows, 3:4], phase + 0.5 - 1e-7))
                    link(dve.memset(ph[rows, 4:5], phase - 0.5 + 1e-7))
                link(dve.memset(ph[:, 2:3], 0.25 * TWO_PI))
                dve.wait_ge(turned, 1)
                for j in range(4):
                    link(dve.tensor_copy(V[j][:], pv[:, j, 0:D]))
                t = [x[:] for x in T]
                link(dve.tensor_copy(t[7], dt[:]))
                accurate_exp(link, dve, dt[:], t[7], t[0], t[1], pw[:])
                link(tt(ar[:], dt[:], Ar[:], ALU.mult))
                link(tt(t[2], dt[:], Ai[:], ALU.mult))
                link(ts(t[3], t[2], 1 / TWO_PI, ROUND, ALU.mult, ALU.add))
                link(ts(t[4], t[3], ROUND, None, ALU.subtract))
                link(stt(out=t[3], in0=t[4], scalar=-PI2_HI, in1=t[2], op0=ALU.mult, op1=ALU.add))
                link(stt(out=t[3], in0=t[4], scalar=-PI2_LO, in1=t[3], op0=ALU.mult, op1=ALU.add))
                link(ts(t[3], t[3], 3.1415925, -3.1415925, ALU.min, ALU.max))
                link(ts(tw[:], t[3], 1 / TWO_PI, None, ALU.mult))
                dve.sem_inc(ask, 2)
                accurate_exp(link, dve, t[7], ar[:], t[0], t[1], pw[:])
                dve.wait_ge(ans, 2)
                link(tt(t[5], t[5], t[5], ALU.mult))
                link(tt(t[5], t[5], t[7], ALU.mult))
                link(ts(t[0], t[7], 1.0, None, ALU.subtract))
                link(stt(out=t[0], in0=t[5], scalar=-2.0, in1=t[0], op0=ALU.mult, op1=ALU.add))
                link(tt(t[1], t[7], t[6], ALU.mult))
                link(tt(t[2], Ar[:], Ar[:], ALU.mult))
                link(tt(t[4], Ai[:], Ai[:], ALU.mult))
                link(tt(t[2], t[2], t[4], ALU.add))
                link(dve.reciprocal(t[2], t[2]))
                link(tt(t[4], t[0], Ar[:], ALU.mult))
                link(tt(t[5], t[1], Ai[:], ALU.mult))
                link(tt(t[4], t[4], t[5], ALU.add))
                link(tt(t[5], t[1], Ar[:], ALU.mult))
                link(tt(t[6], t[0], Ai[:], ALU.mult))
                link(tt(t[5], t[5], t[6], ALU.subtract))
                link(tt(t[4], t[4], t[2], ALU.mult))
                link(tt(t[5], t[5], t[2], ALU.mult))
                link(tt(t[0], Cr[:], t[4], ALU.mult))
                link(tt(t[6], Ci[:], t[5], ALU.mult))
                link(tt(t[0], t[0], t[6], ALU.subtract))
                link(tt(t[1], Cr[:], t[5], ALU.mult))
                link(tt(t[6], Ci[:], t[4], ALU.mult))
                link(tt(t[1], t[1], t[6], ALU.add))
                link(ts(t[4][top], t[0][top], 2.0, None, ALU.mult))
                link(ts(t[4][bot], t[1][bot], -2.0, None, ALU.mult))
                link(ts(t[5][top], t[1][top], 2.0, None, ALU.mult))
                link(ts(t[5][bot], t[0][bot], 2.0, None, ALU.mult))
                link(ts(t[2], tw[:], 2.0 * P, None, ALU.mult))
                link(ts(t[6], t[2], ROUND, ROUND, ALU.add, ALU.subtract))
                link(tt(t[2], t[2], t[6], ALU.subtract))
                dve.wait_ge(made, 4)

                def by_d(x):
                    return x.rearrange("p (d a) -> p d a", a=1).to_broadcast([P, D, LB])

                def by_block(x):
                    return x[:].rearrange("p (a n) -> p a n", a=1).to_broadcast([P, D, LB])

                link(tt(R[:], by_d(t[2]), by_block(blk), ALU.mult))
                link(tt(Rk[0][:], by_d(tw[:]), by_block(odd), ALU.mult))
                link(tt(R[:], R[:], Rk[0][:], ALU.add))
                for n, phase in ((0, 0.25), (1, 0.0)):
                    link(ts(Rk[n][:], R[:], phase, ROUND, ALU.add, ALU.add))
                    link(stt(out=Rk[n][:], in0=Rk[n][:], scalar=ROUND, in1=R[:], op0=ALU.subtract, op1=ALU.subtract))
                    link(ts(Rk[n][:], Rk[n][:], phase + 0.5 - 1e-7, phase - 0.5 + 1e-7, ALU.min, ALU.max))
                link(tt(Rk[2][:], by_d(ar[:]), by_block(start), ALU.mult))
                dve.sem_inc(ask, 3)
                dve.wait_ge(ans, 5)
                link(tt(Rk[0][:], Rk[0][:], by_d(t[4]), ALU.mult))
                link(tt(Rk[1][:], Rk[1][:], by_d(t[5]), ALU.mult))
                link(tt(Rk[0][:], Rk[0][:], Rk[1][:], ALU.subtract))
                link(tt(R[:], Rk[0][:], Rk[2][:], ALU.mult))
                dve.sem_inc(coef, 1)

                def slot(i, j):
                    q = i * SL + j
                    f, k = F[:, j, :, :], W2[:]
                    dve.wait_ge(kd, q + 1)
                    tt(f, tw[:, bass.ds(q * CH, CH)].rearrange("p (c a) -> p c a", a=1).to_broadcast([P, CH, P]),
                       posn[:].rearrange("p (a n) -> p a n", a=1).to_broadcast([P, CH, P]), ALU.mult).then_inc(f1, 1)
                    dve.wait_ge(f1, q + 1)
                    ts(k, f, ph[:, 0:1], ROUND, ALU.add, ALU.add).then_inc(f2, 1)
                    dve.wait_ge(f2, q + 1)
                    stt(out=f, in0=k, scalar=ROUND, in1=f, op0=ALU.subtract, op1=ALU.subtract).then_inc(f3, 1)
                    dve.wait_ge(f3, q + 1)
                    ts(f, f, ph[:, 3:4], ph[:, 4:5], ALU.min, ALU.max).then_inc(f4, 1)

                with dve.Fori(0, NCH // SL, 1) as i:
                    for j in range(SL):
                        slot(i, j)


def convolution(nc, K, KN, U, Dskip, tables):
    FB = S // P // 2
    W2 = B * D
    with Stage(nc, "conv") as st:
        uh, ul = st.sb("uh", [P, TT, D], BF16), st.sb("ul", [P, TT, D], BF16)
        kh, kl = st.sb("kh", [P, LB, D], BF16), st.sb("kl", [P, LB, D], BF16)
        H, L = st.sb("H", [P, FB, 4, W2], BF16), st.sb("L", [P, FB, 4, W2], BF16)
        tab = st.sb("tab", [P, 2, 2, 2, 2, FB, P], BF16)
        free = K.XNT.rearrange("p c n -> p (c n)")
        es = free[:, 0:4 * W2].rearrange("p (x n) -> p x n", x=4)
        su, di = (free[:, x * W2:(x + 2) * W2].rearrange("p (x n) -> p x n", x=2) for x in (4, 6))
        ks, ksu, kdi = st.sb("ks", [P, 2, 2, D]), st.sb("ksu", [P, 2, D]), st.sb("kdi", [P, 2, D])
        tp, tq, ab = (st.sb(x, [P, 4, W2]) for x in ("tp", "tq", "ab"))
        drow = st.sb("drow", [P, D])
        px, pk, py = st.ps("x", [P, 4, N]), st.ps("k", [P, 2, N]), st.ps("y", [P, 2, N])
        tl = [st.sem(f"table{j}") for j in range(2)]
        loaded, hi, lo, xd, ev, used, pd, qd = (st.sem(x) for x in ("loaded", "hi", "lo", "xd", "ev", "used", "pd", "qd"))
        abd, hd, ld, skipped, bd, ba = (st.sem(x) for x in ("abd", "hd", "ld", "skipped", "bd", "ba"))
        NBK = 6

        def spectrum(x):
            return x.rearrange("p x (b d) -> p x b d", b=1).to_broadcast([P, x.shape[1], B, D])

        def both(x):
            return x.rearrange("p x (b d) -> p x b d", b=B)

        def times(eng, out, x, k, done):
            eng.tensor_tensor(both(out[:, 0:2, :]), both(x), spectrum(k[:]), ALU.mult).then_inc(done, 1)
            for y in range(2):
                eng.tensor_tensor(both(out[:, 2 + y:3 + y, :]), both(x[:, y:y + 1, :]), spectrum(k[:, 1 - y:2 - y, :]),
                                  ALU.mult).then_inc(done, 1)

        with st.block() as block:
            @block.sync
            def _(sp):
                sp.dma_start(drow[:], row(Dskip)).then_inc(loaded, 16)
                for way in range(2):
                    for q in range(FB):
                        if way or q >= 2:
                            sem, per = (bd, 2) if way and q >= 2 else (xd, NBK)
                            sp.wait_ge(sem, per * (q - 1 if q >= 2 else FB - 1 + q))
                        sp.dma_start(tab[:, q % 2].rearrange("p a b c f n -> p (a b c f n)"),
                                     tables[way, q].rearrange("p a b c f n -> p (a b c f n)").bitcast(BF16)).then_inc(tl[q % 2], 16)

            @block.tensor
            def _(pe):
                parts = ((0, 0), (0, 1), (1, 0))
                pe.wait_ge(lo, 2)
                with pe.Fori(0, FB // 2, 1) as i:
                    for j in range(2):
                        q = i * 2 + j
                        pe.wait_ge(tl[j], (i + 1) * 16)
                        for n in range(NBK):
                            pe.wait_ge(ev, q * NBK + n + 1)
                            if n < 4:
                                odd, cs = divmod(n, 2)
                                jobs = [(px[:, n, :], cs, uh[:].rearrange("p (b t) d -> p t b d", b=B),
                                         ul[:].rearrange("p (b t) d -> p t b d", b=B))]
                            else:
                                odd = n - 4
                                jobs = [(pk[:, odd, cs * D:(cs + 1) * D], cs, kh, kl) for cs in range(2)]
                            for out, cs, *ops in jobs:
                                for m in range(FB):
                                    for x, (w, o) in enumerate(parts):
                                        last = pe.matmul(out, tab[:, j, w, odd, cs, m, :], ops[o][:, odd * FB + m],
                                                         start=m == 0 and x == 0, stop=m == FB - 1 and x == 2)
                            last.then_inc(xd, 1)
                pe.wait_ge(ld, FB)
                with pe.Fori(0, FB // 2, 1) as i:
                    for j in range(2):
                        pe.wait_ge(tl[j], (i + 1) * 16 + 16 * (FB // 2))
                        for odd in range(2):
                            pe.wait_ge(ba, (i * 2 + j) * 2 + odd + 1)
                            for f in range(FB):
                                for cs in range(2):
                                    for x, (w, o) in enumerate(parts):
                                        last = pe.matmul(py[:, odd, :], tab[:, j, w, odd, cs, f, :],
                                                         (H, L)[o][:, f, 2 * odd + cs, :], start=f == cs == x == 0,
                                                         stop=f == FB - 1 and cs == 1 and x == 2)
                            last.then_inc(bd, 1)

            @block.scalar
            def _(act):
                act.copy(uh[:], U[:]).then_inc(hi, 1)
                act.copy(kh[:], KN[:]).then_inc(hi, 1)
                act.sem_inc(ev, NBK)
                act.sem_inc(used, 2)

                def high(q):
                    act.wait_ge(abd, 2 * (q + 1))
                    act.copy(H[:, q, :, :], ab[:]).then_inc(hd, 1)

                for q in range(FB):
                    for n in range(NBK):
                        act.wait_ge(xd, q * NBK + n + 1)
                        if n == 0:
                            act.wait_ge(used, 2 * q + 2)
                        if n < 4:
                            act.copy(es[:, n, :], px[:, n, :]).then_inc(ev, 1)
                        else:
                            act.copy(ks[:, n - 4, :, :].rearrange("p x d -> p (x d)"), pk[:, n - 4, :]).then_inc(ev, 1)
                        if q and n == 3:
                            high(q - 1)
                high(FB - 1)

            @block.gpsimd
            def _(pool):
                def step(sem, n):
                    pool.wait_ge(sem, n)

                for q in range(FB):
                    step(ev, (q + 2) * NBK)
                    if q:
                        step(abd, 2 * q)
                    pool.tensor_tensor(di, es[:, 0:2, :], es[:, 2:4, :], ALU.subtract).then_inc(qd, 1)
                    pool.tensor_tensor(kdi[:], ks[:, 0, :, :], ks[:, 1, :, :], ALU.subtract).then_inc(qd, 1)
                    step(qd, 7 * q + 2)
                    pool.sem_inc(used, 1)
                    times(pool, tq, di, kdi, qd)
                    step(qd, 7 * q + 5)
                    pool.tensor_tensor(tq[:, 0, :], tq[:, 0, :], tq[:, 1, :], ALU.subtract).then_inc(qd, 1)
                    pool.tensor_tensor(tq[:, 2, :], tq[:, 2, :], tq[:, 3, :], ALU.add).then_inc(qd, 1)
                pool.wait_ge(loaded, 16)
                pool.wait_ge(lo, 2)
                pool.wait_ge(qd, 7 * FB)
                pool.tensor_tensor(U[:], U[:], drow[:].rearrange("p (a d) -> p a d", a=1).to_broadcast([P, TT, D]),
                                   ALU.mult).then_inc(skipped, 1)

            @block.vector
            def _(dve):
                dve.sem_inc(ba, 2)
                for n, (l, h, x) in enumerate(((ul, uh, U), (kl, kh, KN))):
                    dve.wait_ge(hi, n + 1)
                    dve.tensor_tensor(l[:], x[:], h[:], ALU.subtract).then_inc(lo, 1)
                for q in range(FB):
                    dve.wait_ge(ev, (q + 2) * NBK)
                    dve.tensor_tensor(su, es[:, 0:2, :], es[:, 2:4, :], ALU.add).then_inc(pd, 1)
                    dve.tensor_tensor(ksu[:], ks[:, 0, :, :], ks[:, 1, :, :], ALU.add).then_inc(pd, 1)
                    dve.wait_ge(pd, 7 * q + 2)
                    dve.sem_inc(used, 1)
                    times(dve, tp, su, ksu, pd)
                    dve.wait_ge(pd, 7 * q + 5)
                    dve.tensor_tensor(tp[:, 0, :], tp[:, 0, :], tp[:, 1, :], ALU.subtract).then_inc(pd, 1)
                    dve.tensor_tensor(tp[:, 2, :], tp[:, 2, :], tp[:, 3, :], ALU.add).then_inc(pd, 1)
                    dve.wait_ge(pd, 7 * q + 7)
                    dve.wait_ge(qd, 7 * q + 7)
                    dve.tensor_tensor(ab[:, 0:2, :], tp[:, 0:4:2, :], tq[:, 0:4:2, :], ALU.add).then_inc(abd, 1)
                    dve.tensor_tensor(ab[:, 2:4, :], tp[:, 0:4:2, :], tq[:, 0:4:2, :], ALU.subtract).then_inc(abd, 1)
                    dve.wait_ge(hd, q + 1)
                    dve.tensor_tensor(L[:, q, :, :], ab[:], H[:, q, :, :], ALU.subtract).then_inc(ld, 1)
                dve.wait_ge(skipped, 1)
                for m in range(FB):
                    for odd in range(2):
                        dve.wait_ge(bd, 2 * m + odd + 1)
                        u = U[:].rearrange("p (b t) d -> p b t d", b=B)[:, :, odd * FB + m, :]
                        dve.tensor_tensor(u, u, py[:, odd, :].rearrange("p (b d) -> p b d", b=B), ALU.add).then_inc(ba, 1)


def add_into(nc, K, name, dst, src):
    with Stage(nc, name) as st:
        added = st.sem("added")
        with st.block() as block:
            @block.vector
            def _(dve):
                dve.tensor_tensor(dst, dst, src, ALU.add).then_inc(added, 1)


def feed_forward(nc, K, name, HT, W1, b1, W2, fn, acc, weights=None):
    E = W1.shape[0]
    PT = HID // P
    TC = B * S // N
    TN = N // P
    par = 2 if E > 1 else 1
    NI = E // par
    with Stage(nc, name) as st:
        w1, w2 = st.sb("w1", [P, par, DC, HID]), st.sb("w2", [P, par, PT, D])
        bias = st.sb("b1", [P, par, PT])
        hg = st.sb("hg", [P, 2, PT, N])
        ph, py = st.ps("h", [P, 4, N]), st.ps("y", [P, 4, N])
        ld = [st.sem(f"weights{j}") for j in range(par)]
        h_ready, h_done, y_ready, y_done = (st.sem(x) for x in ("h_ready", "h_done", "y_ready", "y_done"))
        used = st.sem("used")
        YP = TN // 2

        def loop(eng, lo, body):
            if NI == 1:
                return body(0) if lo == 0 else None
            with eng.Fori(lo, NI, 1) as i:
                body(i)

        with st.block() as block:
            @block.sync
            def _(sp):
                def load(i, j):
                    e = bass.ds(i * par + j, 1)
                    sp.dma_start(w1[:, j, :, :], W1[e].rearrange("a (c p) n -> p (a c) n", p=P)).then_inc(ld[j], 16)
                    sp.dma_start(bias[:, j, :], b1[e].rearrange("a (t p) -> p (a t)", p=P),
                                 allow_slow_non_contiguous=True).then_inc(ld[j], 16)
                    sp.dma_start(w2[:, j, :, :], W2[e].rearrange("a (c p) n -> p (a c) n", p=P)).then_inc(ld[j], 16)

                for j in range(par):
                    load(0, j)

                def body(i):
                    for j in range(par):
                        sp.wait_ge(y_ready, (i * par + j + 1 - par) * (TC * YP))
                        load(i, j)
                if NI > 1:
                    loop(sp, 1, body)

            @block.tensor
            def _(pe):
                def body(i):
                    for j in range(par):
                        q = i * par + j
                        pe.wait_ge(ld[j], (i + 1) * 48)

                        def up(t):
                            for m in range(PT):
                                pe.wait_ge(h_done, q * (TC * PT) + t * PT + m + 1)
                                for c in range(DC):
                                    last = pe.matmul(ph[:, m % 4, :], w1[:, j, c, m * P:(m + 1) * P],
                                                     HT[:, c, t * N:(t + 1) * N], start=c == 0, stop=c == DC - 1)
                                last.then_inc(h_ready, 1)

                        def down(t):
                            for y in range(YP):
                                pe.wait_ge(h_done, q * (TC * PT) + (t + 1) * PT + 4)
                                pe.wait_ge(y_done, q * (TC * YP) + t * YP + y + 1)
                                for k in range(2):
                                    c0 = (2 * y + k) * P
                                    for m in range(PT):
                                        last = pe.matmul(py[:, (t * YP + y) % 4, k * D:(k + 1) * D],
                                                         hg[:, t % 2, m, c0:c0 + P], w2[:, j, m, :],
                                                         start=m == 0, stop=m == PT - 1)
                                last.then_inc(y_ready, 1)

                        up(0)
                        for t in range(1, TC):
                            up(t)
                            down(t - 1)
                        down(TC - 1)
                loop(pe, 0, body)

            @block.scalar
            def _(act):
                act.sem_inc(h_done, 4)
                act.sem_inc(used, 2)

                def body(i):
                    for j in range(par):
                        q = i * par + j
                        for t in range(TC):
                            for m in range(PT):
                                act.wait_ge(h_ready, q * (TC * PT) + t * PT + m + 1)
                                if m == 0:
                                    act.wait_ge(used, q * TC + t + 1)
                                act.activation(hg[:, t % 2, m, :], ph[:, m % 4, :], fn,
                                               bias=bias[:, j, m:m + 1]).then_inc(h_done, 1)
                loop(act, 0, body)

            @block.vector
            def _(dve):
                dve.sem_inc(y_done, 4)

                def body(i):
                    for j in range(par):
                        q = i * par + j
                        for t in range(TC):
                            for y in range(YP):
                                dve.wait_ge(y_ready, q * (TC * YP) + t * YP + y + 1)
                                tt = t * TN + 2 * y
                                if weights is None:
                                    last = dve.tensor_tensor(acc[:, tt:tt + 2, :], acc[:, tt:tt + 2, :],
                                                             py[:, (t * YP + y) % 4, :].rearrange("p (k d) -> p k d", k=2), ALU.add)
                                else:
                                    dve.wait_ge(y_done, q * (TC * YP) + t * YP + y + 4)
                                    for k in range(2):
                                        last = dve.scalar_tensor_tensor(
                                            out=acc[:, tt + k, :], in0=py[:, (t * YP + y) % 4, k * D:(k + 1) * D],
                                            scalar=weights[:, tt + k, bass.ds(q, 1)], in1=acc[:, tt + k, :],
                                            op0=ALU.mult, op1=ALU.add)
                                last.then_inc(y_done, 1)
                            dve.sem_inc(used, 1)
                loop(dve, 0, body)


def state_space(nc, K, a):
    g = lambda x: a["L1_xattn_" + x]
    with ExitStack() as ctx:
        def sb(name, shape, dt=F32):
            return ctx.enter_context(nc.sbuf_tensor(name, shape, dt))
        KN = sb("e_KN", [P, LB, D])
        ssm_kernel(nc, K, a, KN)
        layernorm(nc, K, "n4", K.X, K.XN, K.XNT)
        U = sb("e_U", [P, TT, D])
        with nc.sbuf_tensor("e_CTT", [P, DC, B * S], F32) as CTT:
            sparse_cross(nc, K, a, a["mask_BxS_bf1"], a["mask_BxS2_bf1"], CTT)
            layernorm(nc, K, "e_n1", K.XN, U, gamma=g("g_norm_in"), beta=g("b_norm_in"))
            film(nc, K, "e_f1", CTT, g("W_film_in"), g("b_film_in"), g("mod_gate"), U)
            convolution(nc, K, KN, U, g("D_skip"), a["dft_tables"])
            film(nc, K, "e_f2", CTT, g("W_film_out"), g("b_film_out"), g("mod_gate"), U)
        add_into(nc, K, "e_a1", U[:], K.XN)
        layernorm(nc, K, "e_n2", U, K.XN, K.XNT, gamma=g("g_ffn"), beta=g("b_ffn"))
        with Stage(nc, "e_b2") as st:
            b2 = st.sb("b2", [P, D])
            loaded, added = st.sem("loaded"), st.sem("added")
            with st.block() as block:
                @block.sync
                def _(sp):
                    sp.dma_start(b2[:], row(g("b2"))).then_inc(loaded, 16)

                @block.vector
                def _(dve):
                    dve.wait_ge(loaded, 16)
                    dve.tensor_tensor(U[:], U[:], b2[:].rearrange("p (a d) -> p a d", a=1).to_broadcast([P, TT, D]),
                                      ALU.add).then_inc(added, 1)
        feed_forward(nc, K, "e_ff", K.XNT, g("W1").rearrange("(a k) n -> a k n", a=1),
                     g("b1").rearrange("(a n) -> a n", a=1), g("W2").rearrange("(a k) n -> a k n", a=1), ACT.Gelu, U)
        layernorm(nc, K, "e_n3", U, U, gamma=g("g_norm_out"), beta=g("b_norm_out"))
        add_into(nc, K, "e_a2", K.X[:], U[:])


E, TOPK, HID = 8, 2, 1024
HM = HID // P
NT = B * S * TOPK // P + E - 1


def route_tokens(nc, K, a, R):
    with Stage(nc, "route") as st:
        W, brow, b2t = st.sb("W", [P, DC, E]), st.sb("br", [P, E]), st.sb("b2", [E, D])
        b1r = st.sb("b1r", [E * HM, P])
        lg, rank, ex = (st.sb(x, [P, TT, E]) for x in ("lg", "rank", "ex"))
        weights, chosen, within = (st.sb(x, [P, TT, E]) for x in ("weights", "chosen", "within"))
        gr, eq = st.sb("gr", [P, TT, E, E]), st.sb("eq", [P, TT, E, E])
        earlier, before, ones = st.sb("earlier", [P, E, E]), st.sb("before", [P, P]), st.sb("ones", [P, P])
        mx, sm = st.sb("mx", [P, TT]), st.sb("sm", [P, TT])
        total, first, tiles = (st.sb(x, [P, E]) for x in ("total", "first", "tiles"))
        tid, cmp, ef, posf = st.sb("tid", [P, NT]), st.sb("cmp", [P, NT, E]), st.sb("ef", [P, NT]), st.sb("posf", [P, TT, 2])
        wT = st.sb("wT", [E, B * S])
        pl, pt, pb = st.ps("l", [P, 4, TT, E]), st.ps("t", [E, 4, N]), st.ps("b", [P, 2, N])
        loaded, made, mm, chain, ask, ans, turned, moved, bd, ba = (
            st.sem(x) for x in ("loaded", "made", "mm", "chain", "ask", "ans", "turned", "moved", "bd", "ba"))
        counted = st.sem("counted")
        with st.block() as block:
            @block.sync
            def _(sp):
                sp.dma_start(W[:], a["L1_ffn_Wr"].rearrange("(c p) n -> p c n", p=P)).then_inc(loaded, 16)
                sp.dma_start(brow[:], row(a["L1_ffn_br"])).then_inc(loaded, 16)
                sp.dma_start(b2t[:], a["L1_ffn_b2"]).then_inc(loaded, 16)
                sp.dma_start(b1r[:], a["L1_ffn_b1"].rearrange("e (m p) -> (e m) p", p=P)).then_inc(loaded, 16)

            @block.gpsimd
            def _(pool):
                pool.memset(earlier[:], 1.0).then_inc(made, 1)
                pool.memset(before[:], 1.0).then_inc(made, 1)
                pool.memset(ones[:], 1.0).then_inc(made, 1)
                pool.iota(tid[:], pattern=[[1, NT]], base=0, channel_multiplier=0,
                          allow_small_or_imprecise_dtypes=True).then_inc(made, 1)
                pool.wait_ge(made, 4)
                pool.affine_select(out=earlier[:], in_=earlier[:], compare_op=ALU.is_gt, fill=0.0, base=0,
                                   pattern=[[1, E], [-1, E]], channel_multiplier=0).then_inc(made, 1)
                pool.affine_select(out=before[:], in_=before[:], compare_op=ALU.is_gt, fill=0.0, base=0,
                                   pattern=[[1, P]], channel_multiplier=-1).then_inc(made, 1)

            @block.tensor
            def _(pe):
                pe.wait_ge(loaded, 64)
                pe.transpose(pl[:, 3, 0:HM, :].rearrange("p t e -> p (t e)"), b1r[:], K.ident[0:E * HM, 0:E * HM])
                for t in range(TT):
                    for c in range(DC):
                        last = pe.matmul(pl[:, 0, t, :], K.XNT[:, c, t * P:(t + 1) * P], W[:, c, :],
                                         start=c == 0, stop=c == DC - 1)
                last.then_inc(mm, 1)
                pe.wait_ge(counted, 1)
                ch = chosen[:].rearrange("p t e -> p (t e)")
                pe.matmul(pl[:, 1, :, :].rearrange("p t e -> p (t e)"), before[:], ch, start=True, stop=True)
                pe.matmul(pl[:, 2, :, :].rearrange("p t e -> p (t e)"), ones[:], ch, start=True, stop=True).then_inc(mm, 1)
                pe.wait_ge(ask, 2)
                for t in range(TT):
                    last = pe.transpose(pt[:, t // 4, (t % 4) * P:(t % 4 + 1) * P], weights[:, t, :], K.ident[:])
                last.then_inc(turned, 1)
                pe.wait_ge(moved, 1)
                for n in range(TT // 2):
                    if n >= 2:
                        pe.wait_ge(ba, n - 1)
                    for k in range(2):
                        t = 2 * n + k
                        last = pe.matmul(pb[:, n % 2, k * D:(k + 1) * D], wT[:, t * P:(t + 1) * P], b2t[:],
                                         start=True, stop=True)
                    last.then_inc(bd, 1)

            @block.scalar
            def _(act):
                act.wait_ge(ask, 1)
                act.activation(ex[:], lg[:], ACT.Exp).then_inc(ans, 1)
                act.wait_ge(turned, 1)
                act.copy(wT[:], pt[:].rearrange("p a n -> p (a n)")).then_inc(moved, 1)

            @block.vector
            def _(dve):
                link = Link(dve, chain)
                tt, ts = dve.tensor_tensor, dve.tensor_scalar
                dve.wait_ge(mm, 1)
                dve.wait_ge(made, 6)
                link(dve.tensor_copy(R.b1[:].rearrange("p e m -> p (e m)"),
                                     pl[:, 3, 0:HM, :].rearrange("p t e -> p (t e)")))
                link(tt(lg[:], pl[:, 0, :, :], brow[:].rearrange("p (a e) -> p a e", a=1).to_broadcast([P, TT, E]),
                        ALU.add))
                others = lg[:].rearrange("p t (a e) -> p t a e", a=1).to_broadcast([P, TT, E, E])
                mine = lg[:].rearrange("p t (e a) -> p t e a", a=1).to_broadcast([P, TT, E, E])
                link(tt(gr[:], others, mine, ALU.is_gt))
                link(tt(eq[:], others, mine, ALU.is_equal))
                link(tt(eq[:], eq[:], earlier[:].rearrange("p (a e) f -> p a e f", a=1).to_broadcast([P, TT, E, E]),
                        ALU.mult))
                link(tt(gr[:], gr[:], eq[:], ALU.add))
                link(dve.tensor_reduce(rank[:], gr[:], AX.X, ALU.add))
                link(ts(chosen[:], rank[:], float(TOPK), None, ALU.is_lt))
                dve.sem_inc(counted, 1)
                link(dve.tensor_reduce(mx[:], lg[:], AX.X, ALU.max))

                def by_t(x):
                    return x.rearrange("p (t a) -> p t a", a=1).to_broadcast([P, TT, E])
                link(tt(lg[:], lg[:], by_t(mx[:]), ALU.subtract))
                dve.sem_inc(ask, 1)
                dve.wait_ge(mm, 2)
                link(dve.memset(within[:, 0, :], 0.0))
                for t in range(1, TT):
                    link(tt(within[:, t, :], within[:, t - 1, :], pl[:, 2, t - 1, :], ALU.add))
                link(tt(total[:], within[:, TT - 1, :], pl[:, 2, TT - 1, :], ALU.add))
                link(tt(within[:], within[:], pl[:, 1, :, :], ALU.add))
                link(ts(tiles[:], total[:], 1.0 / P, (P - 1.0) / P - 0.5 + 0.5 / P, ALU.mult, ALU.add))
                link(ts(tiles[:], tiles[:], ROUND, ROUND, ALU.add, ALU.subtract))
                link(dve.memset(first[:, 0:1], 0.0))
                for e in range(1, E):
                    link(tt(first[:, e:e + 1], first[:, e - 1:e], tiles[:, e - 1:e], ALU.add))
                link(tt(cmp[:], tid[:].rearrange("p (n a) -> p n a", a=1).to_broadcast([P, NT, E]),
                        first[:].rearrange("p (a e) -> p a e", a=1).to_broadcast([P, NT, E]), ALU.is_ge))
                link(dve.tensor_reduce(ef[:], cmp[:, :, 1:], AX.X, ALU.add))
                link(dve.tensor_copy(R.expert[:], ef[:]))
                link(ts(first[:], first[:], float(P), None, ALU.mult))
                link(tt(within[:], within[:], first[:].rearrange("p (a e) -> p a e", a=1).to_broadcast([P, TT, E]), ALU.add))
                dve.wait_ge(ans, 1)
                link(tt(ex[:], ex[:], chosen[:], ALU.mult))
                link(dve.tensor_reduce(sm[:], ex[:], AX.X, ALU.add))
                link(dve.reciprocal(mx[:], sm[:]))
                link(tt(weights[:], ex[:], by_t(mx[:]), ALU.mult))
                dve.sem_inc(ask, 1)
                for k in range(TOPK):
                    link(ts(chosen[:], rank[:], float(k), None, ALU.is_equal))
                    link(tt(lg[:], chosen[:], within[:], ALU.mult))
                    link(dve.tensor_reduce(posf[:, :, k], lg[:], AX.X, ALU.add))
                    link(dve.tensor_copy(R.pos[:, k, :], posf[:, :, k]))
                    link(tt(lg[:], chosen[:], weights[:], ALU.mult))
                    link(dve.tensor_reduce(R.w[:, k, :], lg[:], AX.X, ALU.add))
                for n in range(TT // 2):
                    dve.wait_ge(bd, n + 1)
                    x = K.X[:, 2 * n:2 * n + 2, :]
                    tt(x, x, pb[:, n % 2, :].rearrange("p (k d) -> p k d", k=2), ALU.add).then_inc(ba, 1)


def experts(nc, K, a, R):
    W1, W2 = a["L1_ffn_W1"], a["L1_ffn_W2"]
    with Stage(nc, "experts") as st:
        w1 = [st.sb(f"w1{x}", [P, E, DC, HID], BF16) for x in "hl"]
        w2 = [st.sb(f"w2{x}", [P, E, HM, D], BF16) for x in "hl"]
        raw = [x.rearrange("p a n -> p (a n)").rearrange("p (s n) -> p s n", s=2) for x in (K.XNT, K.XN)]
        FIRST = 2
        gathered = K.XN
        xs = st.sb("xs", [P, 2, D])
        xh, xl = st.sb("xh", [P, 2, DC, P], BF16), st.sb("xl", [P, 2, DC, P], BF16)
        hf = st.sb("hf", [P, 2, HM, P])
        hh, hl = st.sb("hh", [P, HM, P], BF16), st.sb("hl", [P, HM, P], BF16)
        y = st.sb("y", [P, 2, D])
        px, ph, py = st.ps("px", [P, 2, N]), st.ps("ph", [P, 2, HM, P]), st.ps("py", [P, 2, N])
        wl = [st.sem(f"weights{j}") for j in range(2)]
        xsem, ysem = [st.sem(f"x{j}") for j in range(2)], [st.sem(f"stored{j}") for j in range(2)]
        sent, first_hi, first_loaded = st.sem("sent"), st.sem("first_hi"), [st.sem(f"first{j}") for j in range(2)]
        whi, wready = st.sem("whi"), st.sem("wready")
        turned, xhi, xsplit, h_ready, g_done, hhi, hsplit, y_ready, y_out = (st.sem(x) for x in (
            "turned", "xhi", "xsplit", "h_ready", "g_done", "hhi", "hsplit", "y_ready", "y_out"))
        back, used, links = [st.sem(f"back{j}") for j in range(2)], st.sem("used"), st.sem("links")
        HH = HM // 2
        GT = 4

        def over_tiles(eng, body, ahead):
            loops = (NT - 1 - ahead - (NT - 1 - ahead) % 2) // 2 if ahead else NT // 2
            with eng.Fori(0, loops, 1) as i:
                for j in range(2):
                    body(i * 2 + j, j, 2)
            for n in range(2 * loops, NT):
                body(n, n % 2, NT - 1 - n)

        def fetch(eng, e, s, where, sems):
            w = (W1, W2)[s][e].rearrange("(c p) n -> p c n", p=P)
            eng.dma_start(raw[where][:, s, :].rearrange("p (c n) -> p c n", n=w.shape[2]), w).then_inc(sems[s], 16)

        def parts(e, s):
            return [x[:, e, :, :].rearrange("p c n -> p (c n)") for x in (w1, w2)[s]]

        with st.block() as block:
            @block.gpsimd
            def _(pool):
                pool.wait_ge(K.rows_zeroed, 16)
                for t in range(TT):
                    for k in range(TOPK):
                        pool.indirect_dma_start(R.rows, bass.IndirectOffsetOnAxis(R.pos[:, k, t:t + 1], 0),
                                                K.XN[:, t, :], None).then_inc(sent, 16)
                pool.wait_ge(sent, 16 * TT * TOPK)
                for s in range(2):
                    fetch(pool, FIRST, s, 1, wl)
                pool.wait_ge(wready, 2 * FIRST)
                for e in range(FIRST, E):
                    for s in range(2):
                        h, l = parts(e, s)
                        n = e * 2 + s + 1
                        pool.wait_ge(wl[s], (e + 1 - FIRST) * 16)
                        pool.tensor_copy(h, raw[1][:, s, :]).then_inc(whi, 1)
                        pool.wait_ge(whi, n - 2 * FIRST)
                        pool.tensor_tensor(l, raw[1][:, s, :], h, ALU.subtract).then_inc(wready, 1)
                        if e < E - 1:
                            pool.wait_ge(wready, n)
                            fetch(pool, e + 1, s, 1, wl)
                for j in range(2):
                    pool.wait_ge(ysem[j], 16 + 16 * ((NT + 1 - j) // 2))
                for t in range(TT):
                    g = t // GT
                    if g >= 2 and t % GT == 0:
                        pool.wait_ge(used, g - 1)
                    for k in range(TOPK):
                        pool.indirect_dma_start(gathered[:, (t * TOPK + k) % TT, :], None, R.results,
                                                bass.IndirectOffsetOnAxis(R.pos[:, k, t:t + 1], 0)).then_inc(back[g % 2], 16)

            @block.sync
            def _(sp):
                def load(n, j):
                    sp.dma_start(xs[:, j, :], R.rows[bass.ds(n * P, P), :]).then_inc(xsem[j], 16)

                for c in range(2 * FIRST):
                    if c >= 2:
                        sp.wait_ge(wready, c - 1)
                    fetch(sp, c // 2, c % 2, 0, first_loaded)
                sp.wait_ge(sent, 16 * TT * TOPK)
                for n in range(2):
                    load(n, n)

                def body(n, j, more):
                    if more >= 2:
                        sp.wait_ge(turned, n + 1)
                        load(n + 2, j)
                over_tiles(sp, body, 2)

            @block.tensor
            def _(pe):
                def turn(n, j):
                    pe.wait_ge(xsem[j], (n - j) * 8 + 16)
                    pe.wait_ge(xsplit, n + 1)
                    for c in range(DC):
                        last = pe.transpose(px[:, j, c * P:(c + 1) * P], xs[:, j, c * P:(c + 1) * P], K.ident[:])
                    last.then_inc(turned, 1)

                def expert_of(n):
                    return pe.value_load(R.expert[0:1, bass.ds(n, 1)], min_val=0, max_val=E - 1)

                def up(n, j, e):
                    pe.wait_ge(wready, e * 2 + 1)
                    pe.wait_ge(xsplit, n + 3)
                    for h in range(2):
                        pe.wait_ge(g_done, n * 2 + h + 1)
                        for m in range(h * HH, (h + 1) * HH):
                            prods = [(w, x, c) for c in range(DC) for w, x in ((0, xh), (1, xh), (0, xl))]
                            for q, (w, x, c) in enumerate(prods):
                                last = pe.matmul(ph[:, j, m, :],
                                                 w1[w][:, bass.ds(e, 1), c, m * P:(m + 1) * P].rearrange("p a n -> p (a n)"),
                                                 x[:, j, c, :], start=q == 0, stop=q == len(prods) - 1)
                        last.then_inc(h_ready, 1)

                def down(n, j, e):
                    pe.wait_ge(wready, e * 2 + 2)
                    pe.wait_ge(y_out, n + 1)
                    for m in range(HM):
                        if m % HH == 0:
                            pe.wait_ge(hsplit, n * 2 + m // HH + 1)
                        for q, (x, w) in enumerate(((hh, 0), (hh, 1), (hl, 0))):
                            last = pe.matmul(py[:, j, 0:D], x[:, m, :],
                                             w2[w][:, bass.ds(e, 1), m, :].rearrange("p a n -> p (a n)"),
                                             start=m == 0 and q == 0, stop=m == HM - 1 and q == 2)
                    last.then_inc(y_ready, 1)

                turn(0, 0)
                up(0, 0, expert_of(0))
                turn(1, 1)

                def body(n, j, more):
                    if more >= 1:
                        this, following = expert_of(n), expert_of(n + 1)
                        up(n + 1, 1 - j, following)
                    else:
                        this = expert_of(n)
                    if more >= 2:
                        turn(n + 2, j)
                    down(n, j, this)
                over_tiles(pe, body, 2)

            @block.scalar
            def _(act):
                act.sem_inc(g_done, 4)
                act.sem_inc(y_out, 2)
                for j in range(2):
                    act.sem_inc(ysem[j], 16)

                for c in range(2 * FIRST):
                    act.wait_ge(first_loaded[c % 2], (c // 2 + 1) * 16)
                    act.copy(parts(c // 2, c % 2)[0], raw[0][:, c % 2, :]).then_inc(first_hi, 1)

                def gelu(n, j):
                    e = act.value_load(R.expert[0:1, bass.ds(n, 1)], min_val=0, max_val=E - 1)
                    for h in range(2):
                        act.wait_ge(h_ready, n * 2 + h + 1)
                        for m in range(h * HH, (h + 1) * HH):
                            last = act.activation(hf[:, j, m, :], ph[:, j, m, :], ACT.Gelu_apprx_tanh,
                                                  bias=R.b1[:, bass.ds(e, 1), m])
                        last.then_inc(g_done, 1)

                def body(n, j, more):
                    if more >= 1:
                        gelu(n + 1, 1 - j)
                    act.wait_ge(y_ready, n + 2)
                    act.wait_ge(ysem[j], (n - j) * 8 + 16)
                    act.copy(y[:, j, :], py[:, j, 0:D]).then_inc(y_out, 1)
                    act.wait_ge(y_out, n + 3)
                    act.dma_start(R.results[bass.ds(n * P, P), :], y[:, j, :]).then_inc(ysem[j], 16)
                gelu(0, 0)
                over_tiles(act, body, 2)
                for j in range(2):
                    act.wait_ge(ysem[j], 16 + 16 * ((NT + 1 - j) // 2))

            @block.vector
            def _(dve):
                dve.sem_inc(xsplit, 2)
                dve.sem_inc(y_ready, 1)

                def split_x(n, j):
                    dve.wait_ge(turned, n + 1)
                    src = px[:, j, 0:D].rearrange("p (c n) -> p c n", c=DC)
                    dve.tensor_copy(xh[:, j, :, :], src).then_inc(xhi, 1)
                    dve.wait_ge(xhi, n + 1)
                    dve.tensor_tensor(xl[:, j, :, :], src, xh[:, j, :, :], ALU.subtract).then_inc(xsplit, 1)

                def split_h(n, j):
                    dve.wait_ge(y_ready, n + 1)
                    for h in range(2):
                        ms = slice(h * HH, (h + 1) * HH)
                        dve.wait_ge(g_done, n * 2 + h + 5)
                        dve.tensor_copy(hh[:, ms, :], hf[:, j, ms, :]).then_inc(hhi, 1)
                        dve.wait_ge(hhi, n * 2 + h + 1)
                        dve.tensor_tensor(hl[:, ms, :], hf[:, j, ms, :], hh[:, ms, :], ALU.subtract).then_inc(hsplit, 1)

                for c in range(2 * FIRST):
                    h, l = parts(c // 2, c % 2)
                    dve.wait_ge(first_hi, c + 1)
                    dve.tensor_tensor(l, raw[0][:, c % 2, :], h, ALU.subtract).then_inc(wready, 1)
                split_x(0, 0)

                def body(n, j, more):
                    if more >= 1:
                        split_x(n + 1, 1 - j)
                    split_h(n, j)
                over_tiles(dve, body, 2)
                link = Link(dve, links)
                for g in range(TT // GT):
                    dve.wait_ge(back[g % 2], 16 * GT * TOPK * (g // 2 + 1))
                    for k in range(TOPK):
                        for t in range(g * GT, (g + 1) * GT):
                            last = dve.scalar_tensor_tensor(out=K.X[:, t, :], in0=gathered[:, (t * TOPK + k) % TT, :],
                                                            scalar=R.w[:, k, t:t + 1], in1=K.X[:, t, :],
                                                            op0=ALU.mult, op1=ALU.add)
                        link(last)
                    dve.sem_inc(used, 1)


def finish(nc, K, out, parity=True):
    with Stage(nc, "finish") as st:
        stored = st.sem("stored")
        with st.block() as block:
            @block.sync
            def _(sp):
                n = 0
                for b in range(B):
                    if not parity:
                        sp.dma_start(out[b].rearrange("(t p) d -> p t d", p=P),
                                     K.X[:, b * TB:(b + 1) * TB, :]).then_inc(stored, 16)
                        n += 1
                        continue
                    for x in range(2):
                        sp.dma_start(by_parity(out[b])[:, x, :, :],
                                     K.X[:, b * TB + x * TB // 2:b * TB + (x + 1) * TB // 2, :]).then_inc(stored, 16)
                        n += 1
                sp.wait_ge(stored, 16 * n)


class Shared:
    pass


def decoder(nc, a, out, upto=99):
    Stage.spent = []
    with ExitStack() as ctx:
        def sb(name, shape, dt=F32):
            return ctx.enter_context(nc.sbuf_tensor(name, shape, dt))

        K = Shared()
        K.X = sb("X", [P, TT, D])
        work = sb("work", [P, 2 * TT * D])
        K.XN = work[:, 0:TT * D].rearrange("p (t d) -> p t d", t=TT)
        K.XNT = work[:, TT * D:].rearrange("p (c n) -> p c n", c=DC)
        K.wide = work[:, :].rearrange("p (t d) -> p t d", t=TT)
        K.ident, K.identb = sb("ident", [P, P]), sb("identb", [P, P], BF16)
        K.ones, K.onesb = sb("ones", [P, P]), sb("onesb", [P, P], BF16)
        K.cmask, K.cmaskT = sb("cmask", [P, P], BF16), sb("cmaskT", [P, N // P, N], BF16)
        K.eps = sb("eps", [P, 1])
        K.CT = sb("CT", [CW_P, CW_N, B * CL])
        QS = nc.dram_tensor("q_stacks", [NH, ROWS, B * S], BF16, kind="Internal").ap()
        KS = nc.dram_tensor("k_stacks", [NH, ROWS, B * S], BF16, kind="Internal").ap()
        G = nc.dram_tensor("bias_rows", [NH, 2 * N], F32, kind="Internal").ap()

        def stack_of(src):
            return lambda head: src[bass.ds(head, 1)].rearrange("a r (b n) -> (a r) b n", b=B)

        K.scratch = nc.dram_tensor("tokens", [B, S, D], F32, kind="Internal").ap()
        K.rows = nc.dram_tensor("expert_rows", [NT * P, D], F32, kind="Internal").ap()
        K.rows_zeroed = nc.alloc_semaphore("rows_zeroed")
        K.zeros = sb("zeros", [P, D])
        setup(nc, K, a["x"])
        context(nc, K, a["ctx_768"])

        layernorm(nc, K, "n0", K.X, K.XN, K.XNT)
        with nc.sbuf_tensor("a0_values", [P, TT, D], F32) as V:
            qkv16(nc, K, "a0_qkv", None, K.XNT, QS, KS, V, a["L0_attn_w_attn"], bias=a["L0_attn_b_attn"],
                  lora=(a["L0_attn_la_attn"], a["L0_attn_lb_attn"]),
                  quant=(a["L0_attn_kv_scale"], a["L0_attn_kv_zero_point"]))
            attention(nc, K, "a0", NH, HD ** -0.5, HD, P, TB, True, [(stack_of(QS), ROWS)], [(stack_of(KS), ROWS)],
                      [(0, 0)], lambda b, h: V[:, b * TB:(b + 1) * TB, bass.ds(h * HD, HD)], K.XN, True)
        project(nc, K, "a0_out", K.XN, D, a["L0_attn_w_proj"], a["L0_attn_b_proj"],
                lora=(a["L0_attn_la_proj"], a["L0_attn_lb_proj"]))
        if upto <= 1:
            return finish(nc, K, out, False)
        layernorm(nc, K, "n1", K.X, K.XN, K.XNT)
        cross_attention(nc, K, a)
        if upto <= 2:
            return finish(nc, K, out, False)
        layernorm(nc, K, "n2", K.X, K.XN, K.XNT)
        routed_attention(nc, K, a)
        if upto <= 3:
            return finish(nc, K, out, False)
        layernorm(nc, K, "n3", K.X, K.XN, K.XNT)
        with nc.sbuf_tensor("a1_values", [P, TT, D], F32) as V:
            qkv16(nc, K, "a1_qkv", None, K.XNT, QS, KS, V, [a[f"L1_attn_W{x}"] for x in "qkv"], transposed=True)
            attention(nc, K, "a1", NH, D ** -0.5, HD, P, TB, False, [(stack_of(QS), ROWS)], [(stack_of(KS), ROWS)],
                      [(0, 0)], lambda b, h: V[:, b * TB:(b + 1) * TB, bass.ds(h * HD, HD)], K.XN, True)
            relative_bias(nc, K, V, a["L1_attn_bias_table"], K.XN, G)
        layernorm(nc, K, "a1_norm", K.XN, K.XN, gamma=a["L1_attn_ln_gamma"], beta=a["L1_attn_ln_beta"])
        add_into(nc, K, "a1_add", K.X[:], K.XN)
        if upto <= 4:
            return finish(nc, K, out, False)
        state_space(nc, K, a)
        if upto <= 5:
            return finish(nc, K, out)
        layernorm(nc, K, "n5", K.X, K.XN, K.XNT)
        R = Shared()
        R.rows, R.results = K.rows, nc.dram_tensor("expert_results", [NT * P, D], F32, kind="Internal").ap()
        R.pos, R.w, R.expert = sb("f_pos", [P, TOPK, TT], I32), sb("f_w", [P, TOPK, TT]), sb("f_expert", [P, NT], I32)
        R.b1 = sb("f_b1", [P, E, HM])
        route_tokens(nc, K, a, R)
        experts(nc, K, a, R)
        finish(nc, K, out)


def constants():
    half, blocks = S // 2, S // P // 2
    position, frequency = np.arange(S), np.arange(half)
    angle = np.outer(position, 2 * frequency + 1) % (4 * S) * (2 * np.pi / (4 * S))
    table = np.stack([np.cos(angle), -np.sin(angle)])
    table = table.reshape(2, half, 2, half).transpose(2, 0, 1, 3)

    def bf16(x):
        bits = x.astype(np.float32).view(np.uint32)
        bits = (bits + 0x7fff + (bits >> 16 & 1)) >> 16
        return bits.astype(np.uint16), (bits << 16).view(np.float32)

    def laid_out(x):
        x = x.reshape(2, 2, blocks, P, blocks, P).transpose(4, 3, 0, 1, 2, 5)
        high, value = bf16(x)
        return np.stack([high, bf16(x - value)[0]], axis=2)
    return {"dft_tables": np.stack([laid_out(table), laid_out(table.transpose(0, 1, 3, 2) / S)])}


def kernel(**inputs):
    import concourse.bacc as bacc
    from concourse.bass_utils import run_bass_kernel_spmd

    nc = bacc.Bacc("TRN2", target_bir_lowering=False, num_devices=1)
    arrays = dict(constants())
    for name, value in inputs.items():
        array = np.ascontiguousarray(value)
        arrays[name] = array.view(np.uint8) if array.dtype == bool else array
    a = {name: nc.dram_tensor(name, array.shape, mybir.dt.from_np(array.dtype), kind="ExternalInput").ap()
         for name, array in arrays.items()}
    out = nc.dram_tensor("y", (B, S, D), F32, kind="ExternalOutput").ap()
    decoder(nc, a, out)
    return run_bass_kernel_spmd(nc, [arrays], core_ids=[0]).results[0]["y"]
```

```python
from contextlib import ExitStack

import numpy as np
import concourse.bass as bass
from concourse import mybir

F32 = mybir.dt.float32
BF16 = mybir.dt.bfloat16
I32 = mybir.dt.int32
ALU = mybir.AluOpType
ACT = mybir.ActivationFunctionType
AX = mybir.AxisListType

P = 128
B, S, D = 2, 1024, 256
DC = D // P
TT = B * S // P
TB = S // P
N = 512
NQ = S // N
ROUND = 12582912.0
LN_EPS = 1e-5
NEG = -1.0e30


class Link:

    def __init__(self, eng, sem):
        self.eng, self.sem, self.n = eng, sem, 0

    def __call__(self, ins):
        self.n += 1
        ins.then_inc(self.sem, 1)
        self.eng.wait_ge(self.sem, self.n)


class Stage:

    spent = []
    KEEP = 110

    def __init__(self, nc, name):
        self.nc, self.name, self.ctx, self.sems = nc, name, ExitStack(), []

    def __enter__(self):
        self.ctx.__enter__()
        if len(Stage.spent) > Stage.KEEP:
            self.nc.clear_and_free_semaphores(Stage.spent)
            Stage.spent = []
            self.nc.all_engine_barrier()
        return self

    def __exit__(self, *a):
        Stage.spent += self.sems
        return self.ctx.__exit__(*a)

    def sb(self, name, shape, dt=F32):
        return self.ctx.enter_context(self.nc.sbuf_tensor(f"{self.name}_{name}", shape, dt))

    def ps(self, name, shape, dt=F32):
        return self.ctx.enter_context(self.nc.psum_tensor(f"{self.name}_{name}", shape, dt))

    def sem(self, name):
        self.sems.append(self.nc.alloc_semaphore(f"{self.name}_{name}"))
        return self.sems[-1]

    def block(self):
        return self.nc.Block()


def row(ap, n=P):
    return ap.rearrange("(a n) -> a n", a=1).to_broadcast([n, ap.shape[0]])


def setup(nc, K, x):
    with Stage(nc, "setup") as st:
        loaded, made, zeroed = st.sem("loaded"), st.sem("made"), st.sem("zeroed")
        with st.block() as block:
            @block.sync
            def _(sp):
                for b in range(B):
                    sp.dma_start(K.X[:, b * TB:(b + 1) * TB, :],
                                 x[b].rearrange("(t p) d -> p t d", p=P)).then_inc(loaded, 16)
                sp.wait_ge(zeroed, 1)
                sp.dma_start(K.rows.rearrange("(t p) d -> p t d", p=P),
                             K.zeros[:].rearrange("p (a d) -> p a d", a=1).to_broadcast([P, NT, D])).then_inc(K.rows_zeroed, 16)
                sp.wait_ge(loaded, 16 * B)

            @block.gpsimd
            def _(pool):
                pool.memset(K.zeros[:], 0.0).then_inc(zeroed, 1)
                pool.memset(K.ident[:], 0.0).then_inc(zeroed, 1)
                pool.memset(K.cmask[:], 0.0).then_inc(zeroed, 1)
                pool.memset(K.cmaskT[:], 0.0).then_inc(zeroed, 1)
                pool.memset(K.ones[:], 1.0).then_inc(zeroed, 1)
                pool.wait_ge(zeroed, 5)
                pool.affine_select(out=K.ident[:], in_=K.ident[:], compare_op=ALU.not_equal, fill=1.0,
                                   base=0, pattern=[[-1, P]], channel_multiplier=1).then_inc(made, 1)
                pool.affine_select(out=K.cmask[:], in_=K.cmask[:], compare_op=ALU.is_ge, fill=NEG,
                                   base=0, pattern=[[-1, P]], channel_multiplier=1).then_inc(made, 1)
                pool.affine_select(out=K.cmaskT[:], in_=K.cmaskT[:], compare_op=ALU.is_ge, fill=NEG,
                                   base=0, pattern=[[-P, N // P], [1, N]], channel_multiplier=-1).then_inc(made, 1)

            @block.vector
            def _(dve):
                dve.wait_ge(made, 1)
                dve.tensor_copy(K.identb[:], K.ident[:]).then_inc(zeroed, 1)
                dve.memset(K.eps[:], LN_EPS).then_inc(zeroed, 1)
                dve.memset(K.onesb[:], 1.0).then_inc(zeroed, 1)


def norm_stats(st, block, K, src, mean_rstd, ready):
    stats = st.sb("stats", [P, TT, 6])
    aggr = st.sb("aggr", [P, TT, 2])
    std = st.sb("std", [P, TT])
    stats_done, aggr_done, std_done = st.sem("stats_done"), st.sem("aggr_done"), st.sem("std_done")

    def on_vector(dve):
        for t in range(TT):
            dve.bn_stats(stats[:, t, :], src[:, t, :]).then_inc(stats_done, 1)
        dve.wait_ge(stats_done, TT)
        for t in range(TT):
            dve.bn_aggr(aggr[:, t, :], stats[:, t, :]).then_inc(aggr_done, 1)
        dve.wait_ge(aggr_done, TT)
        dve.tensor_copy(mean_rstd[:, :, 0], aggr[:, :, 0]).then_inc(ready, 1)
        dve.wait_ge(std_done, 1)
        dve.reciprocal(mean_rstd[:, :, 1], std[:]).then_inc(ready, 1)
        dve.wait_ge(ready, 2)

    def on_scalar(act):
        act.wait_ge(aggr_done, TT)
        act.activation(std[:], aggr[:, :, 1], ACT.Sqrt, bias=K.eps[:, 0:1]).then_inc(std_done, 1)

    return on_vector, on_scalar


def transposer(st, src, dst, width, ident, src_ready):
    pt = st.ps("turned", [P, 4, N])
    turned, moved = st.sem("turned"), st.sem("moved")
    jobs = [(g, c) for g in range(TT // 4) for c in range(width // P)]

    def on_tensor(pe):
        for n, (g, c) in enumerate(jobs):
            src_ready(pe, 4 * g + 3)
            if n >= 4:
                pe.wait_ge(moved, n - 3)
            for k in range(4):
                last = pe.transpose(pt[:, n % 4, k * P:(k + 1) * P], src[:, 4 * g + k, c * P:(c + 1) * P], ident[:])
            last.then_inc(turned, 1)

    def on_scalar(act):
        for n, (g, c) in enumerate(jobs):
            act.wait_ge(turned, n + 1)
            act.copy(dst[:, c, g * N:(g + 1) * N], pt[:, n % 4, :]).then_inc(moved, 1)

    return on_tensor, on_scalar, moved


def layernorm(nc, K, name, src, dst, dstT=None, gamma=None, beta=None):
    with Stage(nc, name) as st:
        mr = st.sb("mean_rstd", [P, TT, 2])
        ready, normed, loaded = st.sem("ready"), st.sem("normed"), st.sem("loaded")
        centred, scaled = st.sem("centred"), st.sem("scaled")
        if gamma is not None:
            gb = st.sb("gb", [P, 2, D])
        with st.block() as block:
            stats_v, stats_s = norm_stats(st, block, K, src, mr, ready)
            if dstT is not None:
                turn_t, turn_s, _ = transposer(st, dst, dstT, D, K.ident,
                                               lambda e, t: e.wait_ge(normed, t + 1))

            @block.sync
            def _(sp):
                if gamma is not None:
                    sp.dma_start(gb[:, 0, :], row(gamma)).then_inc(loaded, 16)
                    sp.dma_start(gb[:, 1, :], row(beta)).then_inc(loaded, 16)

            @block.vector
            def _(dve):
                stats_v(dve)
                if gamma is not None:
                    dve.wait_ge(loaded, 32)
                for g in range(TT // 4):
                    ts = slice(4 * g, 4 * g + 4)
                    for t in range(4 * g, 4 * g + 4):
                        dve.tensor_scalar(dst[:, t, :], src[:, t, :], mr[:, t, 0:1], mr[:, t, 1:2],
                                          ALU.subtract, ALU.mult).then_inc(normed if gamma is None else centred, 1)
                    if gamma is not None:
                        dve.wait_ge(centred, 4 * g + 4)
                        dve.tensor_tensor(dst[:, ts, :], dst[:, ts, :], gb[:, 0:1, :].to_broadcast([P, 4, D]),
                                          ALU.mult).then_inc(scaled, 1)

            @block.gpsimd
            def _(pool):
                if gamma is not None:
                    for g in range(TT // 4):
                        ts = slice(4 * g, 4 * g + 4)
                        pool.wait_ge(scaled, g + 1)
                        pool.tensor_tensor(dst[:, ts, :], dst[:, ts, :], gb[:, 1:2, :].to_broadcast([P, 4, D]),
                                           ALU.add).then_inc(normed, 4)

            @block.scalar
            def _(act):
                stats_s(act)
                if dstT is not None:
                    turn_s(act)

            @block.tensor
            def _(pe):
                if dstT is not None:
                    turn_t(pe)


def part_stores(st, src, name):
    return [st.sb(f"{name}_{x}", list(src.shape), BF16) for x in ("hi", "mid", "lo")]


HD = 16
NH = D // HD
QBLOCKS = (0, 1, 2, 0, 1, 0)
KBLOCKS = (0, 0, 0, 1, 1, 2)
ROWS = HD * len(QBLOCKS)


def qkv16(nc, K, name, XNT, QS, KS, V, weights, bias=None, lora=None, quant=None, transposed=False):
    with Stage(nc, name) as st:
        Wt = st.sb("W", [P, DC, 3 * D])
        QF, KF = st.sb("QF", [P, DC, B * S]), st.sb("KF", [P, DC, B * S])
        qparts, kparts = part_stores(st, QF, "q"), part_stores(st, KF, "k")
        pm = st.ps("mm", [P, 6, N])
        pw = st.ps("w", [P, 2, N])
        loaded, wmm, wready = st.sem("loaded"), st.sem("wmm"), st.sem("wready")
        mm, evq, evk, evv = st.sem("mm"), st.sem("evq"), st.sem("evk"), st.sem("evv")
        vlink, stored = st.sem("vlink"), st.sem("stored")
        inv, kfinal = st.sem("inv"), st.sem("kfinal")
        khi, kmid, klo, kr1 = (st.sem("k" + x) for x in ("hi", "mid", "lo", "r1"))
        qhi, qmid, qlo, qr1 = (st.sem("q" + x) for x in ("hi", "mid", "lo", "r1"))
        if transposed:
            Wraw = st.sb("Wraw", [P, 3, DC, D])
        if lora is not None:
            la, lb = st.sb("la", [P, DC, HD]), st.sb("lb", [HD, 3 * D])
            laT = st.sb("laT", [HD, DC, P])
        if bias is not None:
            bqk, bv = st.sb("bqk", [P, 2, DC]), st.sb("bv", [P, D])
        if quant is not None:
            qs = st.sb("quant", [P, 3])
        TN = B * S // N
        nload = (3 if transposed else 1) + (2 if lora is not None else 0) + (2 if bias is not None else 0) \
            + (2 if quant is not None else 0)
        qk = [(w, c, t) for w in (1, 0) for c in range(DC) for t in range(B * S // N)]
        vt = list(range(TT // 2))
        jobs = [("qk", j) for j in qk] + [("v", j) for j in vt]
        evac = {"q": 0, "k": 0, "v": 0}
        seen = []
        for kind, j in jobs:
            k = "v" if kind == "v" else "qk"[j[0]]
            evac[k] += 1
            seen.append((k, evac[k]))
        sem_of = {"q": evq, "k": evk, "v": evv}
        with st.block() as block:
            @block.sync
            def _(sp):
                if transposed:
                    for w in range(3):
                        sp.dma_start(Wraw[:, w, :, :], weights[w].rearrange("(c p) n -> p c n", p=P)).then_inc(loaded, 16)
                else:
                    sp.dma_start(Wt[:], weights.rearrange("(c p) n -> p c n", p=P)).then_inc(loaded, 16)
                if lora is not None:
                    sp.dma_start(la[:], lora[0].rearrange("(c p) n -> p c n", p=P)).then_inc(loaded, 16)
                    sp.dma_start(lb[:], lora[1]).then_inc(loaded, 16)
                if bias is not None:
                    sp.dma_start(bqk[:].rearrange("p w c -> p (w c)"),
                                 bias[0:2 * D].rearrange("(w p) -> p w", p=P),
                                 allow_slow_non_contiguous=True).then_inc(loaded, 16)
                    sp.dma_start(bv[:], row(bias[2 * D:3 * D])).then_inc(loaded, 16)
                if quant is not None:
                    sp.dma_start(qs[:, 0:1], row(quant[0])).then_inc(loaded, 16)
                    sp.dma_start(qs[:, 1:2], row(quant[1])).then_inc(loaded, 16)
                stores = 0
                for part, dones in enumerate(((khi, qhi), (kmid, qmid), (klo, qlo))):
                    for done, parts, blocks, out in zip(dones, (kparts, qparts), (KBLOCKS, QBLOCKS), (KS, QS)):
                        for c in range(DC):
                            sp.wait_ge(done, c + 1)
                            for j, which in enumerate(blocks):
                                if which == part:
                                    sp.dma_start(out[c * P // HD:(c + 1) * P // HD, j * HD:(j + 1) * HD, :],
                                                 parts[part][:, c, :]).then_inc(stored, 16)
                                    stores += 1
                sp.wait_ge(stored, 16 * stores)

            @block.tensor
            def _(pe):
                pe.wait_ge(loaded, 16 * nload)
                n = 0
                if transposed:
                    for w in range(3):
                        if n >= 2:
                            pe.wait_ge(wready, n - 1)
                        for ci in range(DC):
                            for co in range(DC):
                                last = pe.transpose(pw[:, n % 2, ci * D + co * P:ci * D + (co + 1) * P],
                                                    Wraw[:, w, co, ci * P:(ci + 1) * P], K.ident[:])
                        last.then_inc(wmm, 1)
                        n += 1
                if lora is not None:
                    for c in range(DC):
                        last = pe.transpose(pw[0:HD, 0, c * P:(c + 1) * P], la[:, c, :], K.ident[:])
                    last.then_inc(wmm, 1)
                    for c in range(DC):
                        for h in range(2):
                            n += 1
                            pe.wait_ge(wready, n)
                            pe.matmul(pw[:, n % 2, 0:3 * D // 2], laT[:, c, :], lb[:, h * 3 * D // 2:(h + 1) * 3 * D // 2],
                                      start=True, stop=True).then_inc(wmm, 1)
                    n += 1
                pe.wait_ge(wready, n)
                for m, (kind, j) in enumerate(jobs):
                    if m >= 6:
                        pe.wait_ge(sem_of[seen[m - 6][0]], seen[m - 6][1])
                    if kind == "qk":
                        w, c, t = j
                        for ci in range(DC):
                            last = pe.matmul(pm[:, m % 6, :], Wt[:, ci, w * D + c * P:w * D + (c + 1) * P],
                                             XNT[:, ci, t * N:(t + 1) * N], start=ci == 0, stop=ci == DC - 1)
                    else:
                        for k in range(2):
                            for ci in range(DC):
                                last = pe.matmul(pm[:, m % 6, k * D:(k + 1) * D],
                                                 XNT[:, ci, (2 * j + k) * P:(2 * j + k + 1) * P],
                                                 Wt[:, ci, 2 * D:3 * D], start=ci == 0, stop=ci == DC - 1)
                    last.then_inc(mm, 1)

            @block.scalar
            def _(act):
                if lora is not None:
                    act.wait_ge(wmm, 1)
                    act.mul(laT[:], pw[0:HD, 0, 0:D].rearrange("p (c n) -> p c n", c=DC), 2.0).then_inc(wready, 1)
                if bias is not None:
                    act.wait_ge(loaded, 16 * nload)
                at = [m for m, (kind, j) in enumerate(jobs) if kind == "qk" and j[0] == 0]

                def take(m):
                    _, c, t = jobs[m][1]
                    act.wait_ge(mm, m + 1)
                    dst = QF[:, c, t * N:(t + 1) * N]
                    if bias is not None:
                        act.activation(dst, pm[:, m % 6, :], ACT.Identity, bias=bqk[:, 0, c:c + 1]).then_inc(evq, 1)
                    else:
                        act.copy(dst, pm[:, m % 6, :]).then_inc(evq, 1)

                def part(ready, n, src, dst, done, c):
                    act.wait_ge(ready, n)
                    act.copy(dst[:, c, :], src[:, c, :]).then_inc(done, 1)

                for c in range(DC):
                    for m in at[c * TN:(c + 1) * TN]:
                        take(m)
                    part(kfinal, c + 1, KF, kparts[0], khi, c)
                for c in range(DC):
                    part(evq, (c + 1) * TN, QF, qparts[0], qhi, c)
                for c in range(DC):
                    part(kr1, c + 1, KF, kparts[1], kmid, c)
                for c in range(DC):
                    part(qr1, c + 1, QF, qparts[1], qmid, c)

            @block.gpsimd
            def _(pool):
                for c in range(DC):
                    pool.wait_ge(qhi, c + 1)
                    pool.tensor_tensor(QF[:, c, :], QF[:, c, :], qparts[0][:, c, :], ALU.subtract).then_inc(qr1, 1)
                for c in range(DC):
                    pool.wait_ge(qmid, c + 1)
                    pool.tensor_tensor(qparts[2][:, c, :], QF[:, c, :], qparts[1][:, c, :], ALU.subtract).then_inc(qlo, 1)

            @block.vector
            def _(dve):
                if transposed:
                    for w in range(3):
                        dve.wait_ge(wmm, w + 1)
                        dve.tensor_copy(Wt[:, :, w * D:(w + 1) * D],
                                        pw[:, w % 2, :].rearrange("p (c n) -> p c n", c=DC)).then_inc(wready, 1)
                if lora is not None:
                    n = 1
                    for c in range(DC):
                        for h in range(2):
                            cols = slice(h * 3 * D // 2, (h + 1) * 3 * D // 2)
                            dve.wait_ge(wmm, n + 1)
                            dve.tensor_tensor(Wt[:, c, cols], Wt[:, c, cols], pw[:, n % 2, 0:3 * D // 2],
                                              ALU.add).then_inc(wready, 1)
                            n += 1
                if quant is not None:
                    dve.wait_ge(loaded, 16 * nload)
                    dve.reciprocal(qs[:, 2:3], qs[:, 0:1]).then_inc(inv, 1)
                    dve.wait_ge(inv, 1)
                link = Link(dve, vlink)

                def quantize(y):
                    link(dve.tensor_scalar(y, y, qs[:, 2:3], qs[:, 1:2], ALU.mult, ALU.add))
                    link(dve.tensor_scalar(y, y, ROUND, ROUND, ALU.add, ALU.subtract))
                    link(dve.tensor_scalar(y, y, 0.0, 255.0, ALU.max, ALU.min))
                    link(dve.tensor_scalar(y, y, qs[:, 1:2], qs[:, 0:1], ALU.subtract, ALU.mult))

                def take_k(m):
                    _, c, t = jobs[m][1]
                    dve.wait_ge(mm, m + 1)
                    dst = KF[:, c, t * N:(t + 1) * N]
                    if bias is not None:
                        dve.tensor_scalar(dst, pm[:, m % 6, :], bqk[:, 1, c:c + 1], None, ALU.add).then_inc(evk, 1)
                    else:
                        dve.tensor_copy(dst, pm[:, m % 6, :]).then_inc(evk, 1)

                def take_v(some):
                    for j in some:
                        m = len(qk) + j
                        dve.wait_ge(mm, m + 1)
                        dst = V[:, 2 * j:2 * j + 2, :]
                        src = pm[:, m % 6, :].rearrange("p (k n) -> p k n", k=2)
                        if bias is not None:
                            dve.tensor_tensor(dst, src, bv[:].rearrange("p (a n) -> p a n", a=1).to_broadcast([P, 2, D]),
                                              ALU.add).then_inc(evv, 1)
                        else:
                            dve.tensor_copy(dst, src).then_inc(evv, 1)

                for c in range(DC):
                    for t in range(TN):
                        take_k(c * TN + t)
                    dve.wait_ge(evk, (c + 1) * TN)
                    if quant is not None:
                        quantize(KF[:, c, :])
                    dve.sem_inc(kfinal, 1)
                for c in range(DC):
                    dve.wait_ge(khi, c + 1)
                    dve.tensor_tensor(KF[:, c, :], KF[:, c, :], kparts[0][:, c, :], ALU.subtract).then_inc(kr1, 1)
                take_v(vt[:len(vt) // 2])
                for c in range(DC):
                    dve.wait_ge(kmid, c + 1)
                    dve.tensor_tensor(kparts[2][:, c, :], KF[:, c, :], kparts[1][:, c, :], ALU.subtract).then_inc(klo, 1)
                take_v(vt[len(vt) // 2:])
                dve.wait_ge(evv, len(vt))
                if quant is not None:
                    quantize(V[:])


def attention(nc, K, name, heads, scale, dv, kp, kt, causal, qsrc, ksrc, pairs, V, Y, staged):
    nk = kp * kt
    narrow = dv == HD
    vw = 32 if narrow else dv + 1
    chunks = []
    for qt in range(TB):
        end = (qt + 1) * P if causal else nk
        chunks += [(qt, k0, min(N, end - k0)) for k0 in range(0, end, N)]
    nm = len(chunks)
    nb = nm + NQ if staged else nm
    steps = []
    for qh in range(NQ):
        last = (qh + 1) * (N // P) if causal else kt
        steps += [(qh, (a, a + 1)) for a in range(0, last, 2)]
    ns = len(steps)
    early = 2
    per = 2 if kt > 2 else 1
    ng = ns // per
    first_of = [min(n for n, s in enumerate(steps) if s[0] == qh) for qh in range(NQ)]
    last_of = [max(n for n, s in enumerate(steps) if s[0] == qh) for qh in range(NQ)]
    UB = 4
    NI = heads // 2
    nq, nkk = len(qsrc), len(ksrc)
    rough = pairs[:2]
    kr = qsrc[0][1]
    lead = nm * 4 // ns if ns > early else nm
    kx = kr + 2 if staged else kr

    def maxima_by(n):
        return min(nm, lead + (nm - lead) * (n - early + 1) // (ns - 2 - early)) if ns > early else nm

    def hidden(qh, k):
        return N // 2 if causal and k - qh * (N // P) >= N // P // 2 else 0
    with Stage(nc, name) as st:
        if staged:
            Qs = [st.sb(f"Q{j}", [P, UB, S], BF16) for j in range(nq)]
            Ks = [st.sb(f"K{j}", [P, UB, nk], BF16) for j in range(nkk)]

        def operand(staging, source, length, i, u, c0, c1, rows):
            if staged:
                return staging[0:rows, u, c0:c1]
            start = (u % 2) * length
            return source[:, bass.ds(i * 2 + u // 2, 1), start + c0:start + c1].rearrange("p a n -> p (a n)")

        def q_of(j, i, u, c0, c1, rows=kr):
            return operand(Qs[j] if staged else None, qsrc[j][0], S, i, u, c0, c1, rows)

        def k_of(j, i, u, c0, c1, rows=kr):
            return operand(Ks[j] if staged else None, ksrc[j][0], nk, i, u, c0, c1, rows)
        Vs = st.sb("V", [kp, UB, kt, vw])
        Pr = st.sb("P", [kp, 2, 2 * per, N])
        if staged:
            MR = st.sb("MR", [P, 2, TB, 2], BF16)
        else:
            MD = st.sb("MD", [P, 2, S], BF16)
        mxc = st.sb("mxc", [P, TB, 2])
        mneg = st.sb("mneg", [P, TB])
        OT = st.sb("OT", [P, NQ, N])
        rc = st.sb("rc", [P, NQ, N // P])
        sel = st.sb("sel", [P, dv + 1])
        SM, ST = st.ps("SM", [P, 2, N]), st.ps("ST", [P, 2, 2, N])
        OP, OUT = st.ps("OP", [P, N]), st.ps("OUT", [P, N // P, P])
        ld = [st.sem(f"operands{j}") for j in range(2)]
        mx_ready, mx_read, md_ready = st.sem("mx_ready"), st.sem("mx_read"), st.sem("md_ready")
        comb, st_ready, exp_done, pv_done = st.sem("comb"), st.sem("st_ready"), st.sem("exp_done"), st.sem("pv_done")
        ot_done, out_ready, rc_done, y_done = st.sem("ot_done"), st.sem("out_ready"), st.sem("rc_done"), st.sem("y_done")
        v_ready, fixed, sel_done = st.sem("v_ready"), st.sem("fixed"), st.sem("sel_done")
        comb_init, ones_done = st.sem("comb_init"), st.sem("ones_done")
        rows_ready, rows_read = st.sem("rows_ready"), st.sem("rows_read")
        nd = nq + nkk

        def following(i, u):
            return (i, u + 1) if u < UB - 1 else (i + 1, 0)

        with st.block() as block:
            @block.sync
            def _(sp):
                def load(i, hp):
                    head = i * 2 + hp
                    for j in range(nq):
                        sp.dma_start(Qs[j][0:kr, 2 * hp:2 * hp + 2, :], qsrc[j][0](head)).then_inc(ld[hp], 16)
                    for j in range(nkk):
                        sp.dma_start(Ks[j][0:kr, 2 * hp:2 * hp + 2, :], ksrc[j][0](head)).then_inc(ld[hp], 16)

                if not staged:
                    return
                for hp in range(2):
                    load(0, hp)
                with sp.Fori(1, NI, 1) as i:
                    for hp in range(2):
                        sp.wait_ge(st_ready, (i * UB + 2 * hp + 2 - UB) * ns + 1)
                        load(i, hp)

            @block.gpsimd
            def _(pool):
                if staged:
                    pool.memset(Ks[0][kr:kx, :, :], 1.0).then_inc(ones_done, 1)
                    pool.wait_ge(ones_done, 1)
                if narrow:
                    pool.memset(sel[:], 0.0).then_inc(sel_done, 1)
                    pool.wait_ge(sel_done, 1)
                    for j in range(4):
                        pool.affine_select(out=sel[:], in_=sel[:], compare_op=ALU.not_equal, fill=1.0,
                                           base=-32 * j, pattern=[[-1, dv + 1]], channel_multiplier=1).then_inc(sel_done, 1)
                        pool.wait_ge(sel_done, j + 2)
                    pool.memset(Vs[:], 0.0).then_inc(fixed, 1)
                    pool.wait_ge(fixed, 1)
                    pool.memset(Vs[:, :, :, dv:dv + 1], 1.0).then_inc(fixed, 1)
                else:
                    pool.memset(Vs[:, :, :, dv:dv + 1], 1.0).then_inc(fixed, 2)
                    pool.tensor_copy(sel[:], K.ident[:, 0:dv + 1]).then_inc(sel_done, 5)
                pool.wait_ge(fixed, 2)

                def copy_v(i, hp):
                    head = i * 2 + hp
                    for b in range(B):
                        pool.tensor_copy(Vs[:, 2 * hp + b, :, 0:dv], V(b, head)).then_inc(v_ready, 1)

                for hp in range(2):
                    copy_v(0, hp)
                with pool.Fori(1, NI, 1) as i:
                    for hp in range(2):
                        pool.wait_ge(pv_done, (i * UB + 2 * hp + 2 - UB) * ng + 2)
                        copy_v(i, hp)

            @block.tensor
            def _(pe):
                def maxima(i, u, some):
                    U = i * UB + u
                    for c in some:
                        qt, k0, kn = chunks[c]
                        if c == 0 and staged:
                            pe.wait_ge(ld[u // 2], (i + 1) * (16 * nd))
                        if staged and c < 2:
                            pe.wait_ge(rows_read, 2 * U + c + 1)
                        else:
                            pe.wait_ge(mx_read, U * nm + c + 1)
                        diag = causal and k0 + kn == (qt + 1) * P
                        parts = [(0, kn, False)] if not diag else [(0, kn - P, False)] * (kn > P) + [(kn - P, kn, True)]
                        for c0, c1, masked in parts:
                            out = SM[:, (u * nb + c) % 2, c0:c1]
                            for n, (a, b_) in enumerate(rough):
                                last = pe.matmul(out, q_of(a, i, u, qt * P, (qt + 1) * P),
                                                 k_of(b_, i, u, k0 + c0, k0 + c1),
                                                 start=n == 0, stop=n == len(rough) - 1 and not masked)
                            if masked:
                                last = pe.matmul(out, K.identb[:], K.cmask[:], start=False, stop=True)
                        last.then_inc(mx_ready, 1)

                def rows(i, u):
                    U = i * UB + u
                    pe.wait_ge(md_ready, U + 1)
                    for qh in range(NQ):
                        for t in range(N // P):
                            last = pe.matmul(SM[kr:kx, (u * nb + nm + qh) % 2, t * P:(t + 1) * P],
                                             MR[:, u % 2, qh * (N // P) + t, :], K.identb[:], start=True, stop=True)
                        last.then_inc(rows_ready, 1)

                def scores(i, u, n):
                    U = i * UB + u
                    qh, kts = steps[n]
                    if n == 0 and staged:
                        pe.wait_ge(rows_read, 2 * U + 4)
                    elif n == 0:
                        pe.wait_ge(md_ready, U + 1)
                    pe.wait_ge(exp_done, U * ns + n + 1)
                    for j, k in enumerate(kts):
                        groups, jd = [(0, N, False)], k - qh * (N // P)
                        if causal and jd >= 0:
                            c0, end = hidden(qh, k), (jd + 1) * P
                            groups = [(c0, end, True)] + [(end, N, False)] * (end < N)
                        for c0, c1, masked in groups:
                            out = ST[0:kp, (u * ns + n) % 2, j, c0:c1]
                            for m, (a, b_) in enumerate(pairs):
                                last = pe.matmul(out, k_of(b_, i, u, k * kp, (k + 1) * kp, kx),
                                                 q_of(a, i, u, qh * N + c0, qh * N + c1, kx), start=m == 0,
                                                 stop=staged and not masked and m == len(pairs) - 1)
                            if masked:
                                last = pe.matmul(out, K.identb[:], K.cmaskT[:, jd, c0:c1], start=False, stop=staged)
                            if not staged:
                                last = pe.matmul(out, K.onesb[:, 0:kp], MD[:, u % 2, qh * N + c0:qh * N + c1],
                                                 start=False, stop=True)
                    last.then_inc(st_ready, 1)

                def values(i, u, g):
                    U = i * UB + u
                    mine = steps[g * per:(g + 1) * per]
                    qh = mine[0][0]
                    end = (qh + 1) * (N // P) if causal else kt
                    if g == 0:
                        pe.wait_ge(v_ready, U + 1)
                    if g * per == first_of[qh]:
                        pe.wait_ge(ot_done, 2 * U + qh + 1)
                    pe.wait_ge(exp_done, U * ns + (g + 1) * per + 2)
                    for m, (_, kts) in enumerate(mine):
                        for j, k in enumerate(kts):
                            p = Pr[:, (u * ng + g) % 2, 2 * m + j, :]
                            if narrow:
                                c0 = hidden(qh, k)
                                cn = hidden(qh, k + 4) if k + 4 < end else N
                                out = OP[32 * (k % 4):32 * (k % 4) + 32, :]
                                for a, b_, stop in [(c0, cn, True)] * (cn > c0) + [(cn, N, False)] * (cn < N):
                                    last = pe.matmul(out[:, a:b_], Vs[:, u, k, :], p[:, a:b_], start=k < 4, stop=stop)
                            else:
                                last = pe.matmul(OP[0:vw, :], Vs[:, u, k, :], p, start=k == 0, stop=k == end - 1)
                    last.then_inc(pv_done, 1)

                def outputs(i, u, qh):
                    U = i * UB + u
                    rows = P if narrow else vw
                    pe.wait_ge(ot_done, 2 * U + qh + 2)
                    pe.wait_ge(y_done, 2 * U + qh + 1)
                    for t in range(N // P):
                        r = rows // 2 if narrow and qh == 0 and t * P < hidden(0, 2) else rows
                        last = pe.matmul(OUT[:, t, 0:dv + 1], OT[0:r, qh, t * P:(t + 1) * P], sel[0:r, :],
                                         start=True, stop=True)
                    last.then_inc(out_ready, 1)

                def unit(i, u, last, next_last):
                    more = chunks and not last
                    ni, nu = following(i, u)
                    done = lead
                    after = following(ni, nu)
                    more2 = not (last or next_last)
                    for n in range(early, ns):
                        scores(i, u, n)
                        if more:
                            upto = maxima_by(n)
                            maxima(ni, nu, range(done, upto))
                            done = upto
                        if more2 and n == ns - 1:
                            maxima(*after, range(lead // 4))
                        if (n + 1) % per == 0 and n >= per:
                            values(i, u, (n + 1) // per - 2)
                        if n == ns - 2 and more and staged:
                            rows(ni, nu)
                        if n == last_of[0] + 1 + per:
                            outputs(i, u, 0)
                    if more2 and ns == early:
                        maxima(*after, range(lead // 4))
                    if more:
                        scores(ni, nu, 0)
                    if more2:
                        maxima(*after, range(lead // 4, lead // 2))
                    if ns == early:
                        values(i, u, 0)
                    else:
                        values(i, u, ng - 1)
                    if more2:
                        maxima(*after, range(lead // 2, 3 * lead // 4))
                    if ns == early:
                        values(i, u, ng - 1)
                        outputs(i, u, 0)
                    if more:
                        scores(ni, nu, 1)
                    if more2:
                        maxima(*after, range(3 * lead // 4, lead))
                    outputs(i, u, 1)

                pe.sem_inc(st_ready, 1)
                pe.wait_ge(fixed, 2)
                pe.wait_ge(sel_done, 5)
                maxima(0, 0, range(nm))
                if staged:
                    pe.wait_ge(ones_done, 1)
                    rows(0, 0)
                for n in range(early):
                    scores(0, 0, n)
                maxima(0, 1, range(lead))
                with pe.Fori(0, NI - 1, 1) as i:
                    for u in range(UB):
                        unit(i, u, False, False)
                for u in range(UB):
                    unit(NI - 1, u, u == UB - 1, u == UB - 2)

            @block.scalar
            def _(act):
                act.sem_inc(ot_done, 1)
                act.sem_inc(exp_done, 2)
                act.sem_inc(pv_done, 2)
                act.sem_inc(rows_read, 2)

                def rows(i, u):
                    U = i * UB + u
                    for qh in range(NQ):
                        act.wait_ge(rows_ready, 2 * U + qh + 1)
                        act.copy(Qs[0][kr:kx, u, qh * N:(qh + 1) * N],
                                 SM[kr:kx, (u * nb + nm + qh) % 2, :]).then_inc(rows_read, 1)

                def turned(i, u, qh):
                    U = i * UB + u
                    rows = P if narrow else vw
                    act.wait_ge(pv_done, U * ng + (last_of[qh] + 1) // per + 2)
                    act.wait_ge(y_done, 2 * U + 1)
                    cut = hidden(0, 2) if narrow and qh == 0 else 0
                    if cut:
                        act.copy(OT[0:rows // 2, qh, 0:cut], OP[0:rows // 2, 0:cut])
                    act.copy(OT[0:rows, qh, cut:], OP[0:rows, cut:]).then_inc(ot_done, 1)

                def unit(i, u, last):
                    U = i * UB + u
                    for n in range(ns):
                        g = n // per
                        act.wait_ge(st_ready, U * ns + n + 2)
                        act.wait_ge(pv_done, U * ng + g + 1)
                        c0 = hidden(steps[n][0], steps[n][1][0])
                        act.activation(Pr[:, (u * ng + g) % 2, 2 * (n % per):2 * (n % per) + 2, c0:],
                                       ST[0:kp, (u * ns + n) % 2, :, c0:], ACT.Exp, scale=scale).then_inc(exp_done, 1)
                        if n == last_of[0] + per:
                            turned(i, u, 0)
                        if n == ns - 2 and staged and not last:
                            rows(*following(i, u))
                    if last_of[1] < last_of[0] + per:
                        turned(i, u, 0)
                    turned(i, u, 1)

                if staged:
                    rows(0, 0)
                with act.Fori(0, NI - 1, 1) as i:
                    for u in range(UB):
                        unit(i, u, False)
                for u in range(UB):
                    unit(NI - 1, u, u == UB - 1)

            @block.vector
            def _(dve):
                dve.sem_inc(mx_read, 2)
                dve.sem_inc(y_done, 1)

                def maxima(i, u, some):
                    U = i * UB + u
                    for c in some:
                        qt, k0, kn = chunks[c]
                        dve.wait_ge(mx_ready, U * nm + c + 1)
                        dve.tensor_reduce(mxc[:, qt, k0 // N:k0 // N + 1], SM[:, (u * nb + c) % 2, 0:kn],
                                          AX.X, ALU.max).then_inc(mx_read, 1)

                def diagonal(i, u, first=False):
                    U = i * UB + u
                    dve.wait_ge(mx_read, U * nm + nm + 2)
                    if staged:
                        dve.tensor_reduce(mneg[:], mxc[:], AX.X, ALU.max, negate=True).then_inc(comb, 1)
                        dve.wait_ge(comb, 2 * U + 1)
                        dve.tensor_copy(MR[:, u % 2, :, 0], mneg[:]).then_inc(comb, 1)
                        dve.wait_ge(comb, 2 * U + 2)
                        dve.tensor_tensor(MR[:, u % 2, :, 1], mneg[:], MR[:, u % 2, :, 0], ALU.subtract).then_inc(md_ready, 1)
                        return
                    dve.wait_ge(md_ready, U)
                    dve.tensor_reduce(mneg[:], mxc[:], AX.X, ALU.max, negate=True).then_inc(comb, 1)
                    dve.wait_ge(comb, U + 1)
                    if not first:
                        dve.wait_ge(st_ready, (U - 1) * ns + 1)
                    for t in range(TB):
                        last = dve.tensor_scalar(MD[:, u % 2, t * P:(t + 1) * P], K.identb[:], mneg[:, t:t + 1],
                                                 None, ALU.mult)
                    last.then_inc(md_ready, 1)

                def result(i, u, qh):
                    U = i * UB + u
                    head = i * 2 + u // 2
                    dve.wait_ge(out_ready, 2 * U + qh + 1)
                    dve.reciprocal(rc[:, qh, :], OUT[:, :, dv]).then_inc(rc_done, 1)
                    dve.wait_ge(rc_done, 2 * U + qh + 1)
                    t0 = (u % 2) * TB + qh * (N // P)
                    dve.tensor_tensor(Y[:, t0:t0 + N // P, bass.ds(head * dv, dv)], OUT[:, :, 0:dv],
                                      rc[:, qh, :].rearrange("p (t a) -> p t a", a=1).to_broadcast([P, N // P, dv]),
                                      ALU.mult).then_inc(y_done, 1)

                def unit(i, u, last, next_last):
                    ni, nu = following(i, u)
                    split_at = maxima_by(min(last_of[0] + 1 + per, ns - 1))
                    if not last:
                        maxima(ni, nu, range(lead, split_at))
                        if split_at < nm:
                            result(i, u, 0)
                        maxima(ni, nu, range(split_at, nm))
                        if ns > early:
                            diagonal(ni, nu)
                        if split_at == nm and ns > early:
                            result(i, u, 0)
                    elif ns > early:
                        result(i, u, 0)
                    if not (last or next_last):
                        after = following(ni, nu)
                        maxima(*after, range(3 * lead // 4))
                    if ns == early:
                        result(i, u, 0)
                    if not (last or next_last):
                        maxima(*after, range(3 * lead // 4, lead))
                        if ns == early:
                            diagonal(*after)
                    result(i, u, 1)

                dve.memset(mxc[:], -3.0e38).then_inc(comb_init, 1)
                dve.wait_ge(comb_init, 1)
                maxima(0, 0, range(nm))
                diagonal(0, 0, True)
                maxima(0, 1, range(lead))
                if ns == early:
                    diagonal(0, 1, True)
                with dve.Fori(0, NI - 1, 1) as i:
                    for u in range(UB):
                        unit(i, u, False, False)
                for u in range(UB):
                    unit(NI - 1, u, u == UB - 1, u == UB - 2)
                dve.wait_ge(y_done, 2 * UB * NI + 1)




def project(nc, K, name, Y, width, weight, bias, lora=None):
    WC = width // P
    with Stage(nc, name) as st:
        YT = st.sb("YT", [P, WC, B * S])
        Wt = st.sb("W", [P, WC, D])
        brow = st.sb("bias", [P, D])
        pm, pw = st.ps("mm", [P, 3, 2, D]), st.ps("w", [P, D])
        loaded, wmm, wready, biased = st.sem("loaded"), st.sem("wmm"), st.sem("wready"), st.sem("biased")
        mm, added = st.sem("mm"), st.sem("added")
        if lora is not None:
            la, lb, laT = st.sb("la", [P, DC, HD]), st.sb("lb", [HD, D]), st.sb("laT", [HD, D])
        nload = 2 + (2 if lora is not None else 0)
        with st.block() as block:
            turn_t, turn_s, moved = transposer(st, Y, YT, width, K.ident, lambda e, t: None)
            turns = TT // 4 * WC

            @block.sync
            def _(sp):
                sp.dma_start(Wt[:], weight.rearrange("(c p) n -> p c n", p=P)).then_inc(loaded, 16)
                sp.dma_start(brow[:], row(bias)).then_inc(loaded, 16)
                if lora is not None:
                    sp.dma_start(la[:], lora[0].rearrange("(c p) n -> p c n", p=P)).then_inc(loaded, 16)
                    sp.dma_start(lb[:], lora[1]).then_inc(loaded, 16)

            @block.tensor
            def _(pe):
                pe.wait_ge(loaded, 16 * nload)
                if lora is not None:
                    for c in range(DC):
                        last = pe.transpose(pw[0:HD, c * P:(c + 1) * P], la[:, c, :], K.ident[:])
                    last.then_inc(wmm, 1)
                    for c in range(DC):
                        pe.wait_ge(wready, c + 1)
                        pe.matmul(pw[:], laT[:, c * P:(c + 1) * P], lb[:], start=True, stop=True).then_inc(wmm, 1)
                turn_t(pe)
                pe.wait_ge(moved, turns)
                if lora is not None:
                    pe.wait_ge(wready, 1 + DC)
                for j in range(TT // 2):
                    if j >= 3:
                        pe.wait_ge(added, j - 2)
                    for k in range(2):
                        for c in range(WC):
                            t = 2 * j + k
                            last = pe.matmul(pm[:, j % 3, k, :], YT[:, c, t * P:(t + 1) * P], Wt[:, c, :],
                                             start=c == 0, stop=c == WC - 1)
                    last.then_inc(mm, 1)

            @block.scalar
            def _(act):
                if lora is not None:
                    act.wait_ge(wmm, 1)
                    act.mul(laT[:], pw[0:HD, :], 2.0).then_inc(wready, 1)
                turn_s(act)

            @block.vector
            def _(dve):
                dve.wait_ge(loaded, 16 * nload)
                if lora is not None:
                    for c in range(DC):
                        dve.wait_ge(wmm, c + 2)
                        dve.tensor_tensor(Wt[:, c, :], Wt[:, c, :], pw[:], ALU.add).then_inc(wready, 1)
                dve.tensor_tensor(K.X[:], K.X[:], brow[:].rearrange("p (a n) -> p a n", a=1).to_broadcast([P, TT, D]),
                                  ALU.add).then_inc(biased, 1)
                dve.wait_ge(biased, 1)
                for j in range(TT // 2):
                    dve.wait_ge(mm, j + 1)
                    dve.tensor_tensor(K.X[:, 2 * j:2 * j + 2, :], K.X[:, 2 * j:2 * j + 2, :], pm[:, j % 3, :, :],
                                      ALU.add).then_inc(added, 1)


WD = 64
CT_P, CT_N = 77, 2
CL = CT_P * CT_N
CW, CW_P, CW_N = 192, 96, 2


def context(nc, K, ctx):
    with Stage(nc, "context") as st:
        raw = st.sb("raw", [CT_P, B * CT_N, CW])
        pt = st.ps("turned", [CW_P, CW_N, N])
        loaded, turned, moved = st.sem("loaded"), st.sem("turned"), st.sem("moved")
        with st.block() as block:
            @block.sync
            def _(sp):
                sp.dma_start(raw[:], ctx.rearrange("b (t p) w -> p (b t) w", p=CT_P)).then_inc(loaded, 16)

            @block.tensor
            def _(pe):
                pe.wait_ge(loaded, 16)
                for c in range(CW_N):
                    for t in range(B * CT_N):
                        last = pe.transpose(pt[:, c, t * CT_P:(t + 1) * CT_P], raw[:, t, c * CW_P:(c + 1) * CW_P],
                                            K.ident[0:CT_P, 0:CT_P])
                last.then_inc(turned, 1)

            @block.vector
            def _(dve):
                dve.wait_ge(turned, 1)
                dve.tensor_copy(K.CT[:], pt[:, :, 0:B * CL]).then_inc(moved, 1)


def stacks64(nc, K, name, kind, W, kp, src, jobs, out, bias=None):
    H = WD
    w0 = max(n for _, _, n, _, _ in jobs)
    with Stage(nc, name) as st:
        R = st.sb("R", [P, 4, w0])
        pm = st.ps("mm", [P, 4, N])
        mm, ev, done, rdone, q1, q2, repeated = (
            st.sem(x) for x in ("mm", "ev", "done", "rdone", "q1", "q2", "repeated"))
        with st.block() as block:
            @block.tensor
            def _(pe):
                for m, (w, c0, n, dh, d0) in enumerate(jobs):
                    if m >= 4:
                        pe.wait_ge(ev, m - 3)
                    nc_ = W.shape[1]
                    for c in range(nc_):
                        last = pe.matmul(pm[:, m % 4, 0:n], W[0:kp, c, w, :], src[0:kp, c, c0:c0 + n],
                                         start=c == 0, stop=c == nc_ - 1)
                    last.then_inc(mm, 1)

            @block.scalar
            def _(act):
                def repeat_high(m):
                    _, _, n, dh, d0 = jobs[m]
                    o = [x[:, dh, d0:d0 + n] for x in out]
                    act.wait_ge(q1, m + 1)
                    if kind == "q":
                        act.copy(o[1][0:H], o[0][0:H]).then_inc(repeated, 1)
                    else:
                        act.copy(o[2][H:P], o[0][H:P]).then_inc(repeated, 1)

                for m, (w, c0, n, dh, d0) in enumerate(jobs):
                    if m:
                        repeat_high(m - 1)
                    act.wait_ge(mm, m + 1)
                    if m >= 4:
                        act.wait_ge(done, m - 3)
                        act.wait_ge(q2, m - 3)
                    if bias is None:
                        act.copy(R[:, m % 4, 0:n], pm[:, m % 4, 0:n]).then_inc(ev, 1)
                    else:
                        act.activation(R[:, m % 4, 0:n], pm[:, m % 4, 0:n], ACT.Identity,
                                       bias=bias[:, w:w + 1]).then_inc(ev, 1)
                repeat_high(len(jobs) - 1)

            @block.vector
            def _(dve):
                for m, (w, c0, n, dh, d0) in enumerate(jobs):
                    o = [x[:, dh, d0:d0 + n] for x in out]
                    r = R[:, m % 4, 0:n]
                    dve.wait_ge(ev, m + 1)
                    dve.tensor_copy(o[0], r).then_inc(q1, 1)
                    dve.wait_ge(q1, m + 1)
                    dve.tensor_tensor(r, r, o[0], ALU.subtract).then_inc(rdone, 1)
                    dve.wait_ge(rdone, m + 1)
                    if kind == "q":
                        dve.tensor_copy(o[0][H:P], r[H:P]).then_inc(done, 1)
                    else:
                        dve.tensor_copy(o[1], r).then_inc(done, 1)

            @block.gpsimd
            def _(pool):
                for m, (w, c0, n, dh, d0) in enumerate(jobs):
                    o = [x[:, dh, d0:d0 + n] for x in out]
                    r = R[:, m % 4, 0:n]
                    if kind == "q":
                        pool.wait_ge(done, m + 1)
                        pool.tensor_tensor(o[1][H:P], r[H:P], o[0][H:P], ALU.subtract).then_inc(q2, 1)
                    else:
                        pool.wait_ge(done, m + 1)
                        pool.tensor_tensor(o[2][0:H], r[0:H], o[1][0:H], ALU.subtract).then_inc(q2, 1)


def cross_values(nc, K, name, Wv, width, V):
    with Stage(nc, name) as st:
        Wt = st.sb("W", [CW_P, CW_N, width])
        pm = st.ps("mm", [CT_P, 4, N])
        loaded, mm, ev = st.sem("loaded"), st.sem("mm"), st.sem("ev")
        with st.block() as block:
            @block.sync
            def _(sp):
                sp.dma_start(Wt[:], Wv.rearrange("(c p) n -> p c n", p=CW_P)).then_inc(loaded, 16)

            @block.tensor
            def _(pe):
                pe.wait_ge(loaded, 16)
                for t in range(B * CT_N):
                    for c in range(CW_N):
                        last = pe.matmul(pm[:, t, 0:width], K.CT[:, c, t * CT_P:(t + 1) * CT_P], Wt[:, c, :],
                                         start=c == 0, stop=c == CW_N - 1)
                    last.then_inc(mm, 1)

            @block.vector
            def _(dve):
                for t in range(B * CT_N):
                    dve.wait_ge(mm, t + 1)
                    dve.tensor_copy(V[:, t, :], pm[:, t, 0:width]).then_inc(ev, 1)


def load_twice(nc, K, name, pairs):
    with Stage(nc, name) as st:
        loaded = st.sem("loaded")
        with st.block() as block:
            @block.sync
            def _(sp):
                n = 0
                for dst, src, p in pairs:
                    for c in range(dst.shape[1]):
                        for twice in range(2):
                            sp.dma_start(dst[:, c, :, twice * WD:(twice + 1) * WD],
                                         src[c * p:(c + 1) * p, :].rearrange("p (h n) -> p h n", n=WD)).then_inc(loaded, 16)
                            n += 1
                sp.wait_ge(loaded, 16 * n)


def cross_attention(nc, K, a):
    H = 8
    with ExitStack() as ctx:
        def sb(name, shape, dt=F32):
            return ctx.enter_context(nc.sbuf_tensor(name, shape, dt))
        QA, QB = sb("c0_QA", [P, H, B * S], BF16), sb("c0_QB", [P, H, B * S], BF16)
        KK = [sb(f"c0_K{x}", [P, H, B * CL], BF16) for x in "ABC"]
        V = sb("c0_values", [CT_P, B * CT_N, H * WD])
        with nc.sbuf_tensor("c0_Wq", [P, DC, H, P], F32) as Wq, nc.sbuf_tensor("c0_Wk", [CW_P, CW_N, H, P], F32) as Wk:
            load_twice(nc, K, "c0_w", [(Wq, a["L0_xattn_Wq"], P), (Wk, a["L0_xattn_Wk"], CW_P)])
            cross_values(nc, K, "c0_v", a["L0_xattn_Wv"], H * WD, V)
            stacks64(nc, K, "c0_q", "q", Wq, P, K.XNT,
                     [(h, t * N, N, h, t * N) for h in range(H) for t in range(B * S // N)], [QA, QB])
            stacks64(nc, K, "c0_k", "k", Wk, CW_P, K.CT, [(h, 0, B * CL, h, 0) for h in range(H)], KK)
        Y = K.wide

        attention(nc, K, "c0", H, WD ** -0.5, WD, CT_P, CT_N, False, [(QA, P), (QB, P)],
                  [(x, P) for x in KK], [(0, 0), (0, 1), (1, 2)],
                  lambda b, h: V[:, b * CT_N:(b + 1) * CT_N, bass.ds(h * WD, WD)], Y, False)
    project(nc, K, "c0_out", Y, H * WD, a["L0_xattn_Wo"], a["L0_xattn_bo"])


def ranks(link, dve, scores, others, earlier, greater, equal, rank):
    link(dve.tensor_tensor(greater, others, scores, ALU.is_gt))
    link(dve.tensor_tensor(equal, others, scores, ALU.is_equal))
    link(dve.tensor_tensor(equal, equal, earlier, ALU.mult))
    link(dve.tensor_tensor(greater, greater, equal, ALU.add))
    link(dve.tensor_reduce(rank, greater, AX.X, ALU.add))


def choose_heads(nc, K, Wr, br, chosen, active):
    H = Wr.shape[1]
    with Stage(nc, "choose") as st:
        total = st.sb("total", [P, DC, B])
        W, brow = st.sb("W", [P, DC, H]), st.sb("br", [1, H])
        lg, rank, sel = st.sb("logits", [1, B, H]), st.sb("rank", [1, B, H]), st.sb("sel", [1, B, H])
        g, e = st.sb("g", [1, B * H, H]), st.sb("e", [1, B * H, H])
        earlier, place = st.sb("earlier", [1, B * H, H]), st.sb("place", [1, B, H])
        index, idx = st.sb("index", [1, B, H]), st.sb("idx", [1, B, active])
        hit = st.sb("hit", [1, B, H])
        pm = st.ps("mm", [1, B, H])
        loaded, summed, mm, chain, made = (st.sem(x) for x in ("loaded", "summed", "mm", "chain", "made"))
        with st.block() as block:
            @block.sync
            def _(sp):
                sp.dma_start(W[:], Wr.rearrange("(c p) n -> p c n", p=P)).then_inc(loaded, 16)
                sp.dma_start(brow[:], br.rearrange("(a n) -> a n", a=1)).then_inc(loaded, 16)

            @block.gpsimd
            def _(pool):
                pool.memset(earlier[:], 1.0).then_inc(made, 1)
                pool.wait_ge(made, 1)
                for b in range(B):
                    v = earlier[:, b * H:(b + 1) * H, :]
                    pool.affine_select(out=v, in_=v, compare_op=ALU.is_gt, fill=0.0, base=0,
                                       pattern=[[1, H], [-1, H]], channel_multiplier=0).then_inc(made, 1)
                pool.iota(index[:], pattern=[[0, B], [1, H]], base=0, channel_multiplier=0,
                          allow_small_or_imprecise_dtypes=True).then_inc(made, 1)

            @block.vector
            def _(dve):
                dve.tensor_reduce(total[:], K.XNT[:].rearrange("p c (b n) -> p c b n", b=B), AX.X,
                                  ALU.add).then_inc(summed, 1)
                dve.wait_ge(mm, 1)
                dve.wait_ge(made, 2 + B)
                link = Link(dve, chain)
                link(dve.tensor_scalar(lg[:], pm[:], 1.0 / S, None, ALU.mult))
                link(dve.tensor_tensor(lg[:], lg[:], brow[:].rearrange("p (a h) -> p a h", a=1).to_broadcast([1, B, H]),
                                       ALU.add))
                for b in range(B):
                    v = slice(b * H, (b + 1) * H)
                    mine = lg[:, b, :].rearrange("p (h a) -> p h a", a=1).to_broadcast([1, H, H])
                    others = lg[:, b:b + 1, :].to_broadcast([1, H, H])
                    ranks(link, dve, mine, others, earlier[:, v, :], g[:, v, :], e[:, v, :], rank[:, b, :])
                link(dve.tensor_scalar(sel[:], rank[:], float(active), None, ALU.is_lt))
                for b in range(B):
                    v = slice(b * H, (b + 1) * H)
                    link(dve.tensor_tensor(e[:, v, :], sel[:, b:b + 1, :].to_broadcast([1, H, H]), earlier[:, v, :],
                                           ALU.mult))
                    link(dve.tensor_reduce(place[:, b, :], e[:, v, :], AX.X, ALU.add))
                link(dve.tensor_tensor(index[:], index[:], sel[:], ALU.mult))
                for k in range(active):
                    link(dve.tensor_scalar(hit[:], place[:], float(k), None, ALU.is_equal))
                    link(dve.tensor_tensor(hit[:], hit[:], index[:], ALU.mult))
                    link(dve.tensor_reduce(idx[:, :, k], hit[:], AX.X, ALU.add))
                link(dve.tensor_copy(chosen[:], idx[:]))

            @block.tensor
            def _(pe):
                pe.wait_ge(loaded, 32)
                pe.wait_ge(summed, 1)
                for b in range(B):
                    for c in range(DC):
                        last = pe.matmul(pm[0:1, b, :], total[:, c, b:b + 1], W[:, c, :], start=c == 0, stop=c == DC - 1)
                last.then_inc(mm, 1)


def routed_attention(nc, K, a):
    A = 4
    with ExitStack() as ctx:
        def sb(name, shape, dt=F32):
            return ctx.enter_context(nc.sbuf_tensor(name, shape, dt))
        QA, QB = sb("m0_QA", [P, A, B * S], BF16), sb("m0_QB", [P, A, B * S], BF16)
        KK = [sb(f"m0_K{x}", [P, A, B * S], BF16) for x in "ABC"]
        V = sb("m0_values", [P, TT, A * WD])
        chosen = sb("m0_chosen", [1, B, A], I32)
        choose_heads(nc, K, a["L0_ffn_Wr"], a["L0_ffn_br"], chosen, A)
        with Stage(nc, "m0_w") as st:
            W = [st.sb(f"W{x}", [P, DC, B * A, P]) for x in "qk"]
            bias = [st.sb(f"b{x}", [P, B * A]) for x in "qk"]
            Wv, bv = st.sb("Wv", [P, DC, B, A * WD]), st.sb("bv", [P, B, A * WD])
            with Stage(nc, "m0_load") as ld:
                loaded, loaded2, loaded3 = ld.sem("loaded"), ld.sem("loaded2"), ld.sem("loaded3")
                doubled = ld.sem("doubled")
                with ld.block() as block:
                    def fetch(eng, loaded, Wx, bx, wsrc, bsrc, n):
                        for b in range(B):
                            for k in range(A):
                                w = b * A + k
                                h = eng.value_load(chosen[0:1, b, k:k + 1], min_val=0, max_val=15)
                                src = wsrc.rearrange("(c p) n -> p c n", p=P)[:, :, bass.ds(h * WD, WD)]
                                bcol = bsrc[bass.ds(h * WD, WD)].rearrange("(p a) -> p a", a=1)
                                eng.dma_start(Wx[:, :, w, 0:WD], src).then_inc(loaded, 16)
                                eng.dma_start(bx[0:WD, w:w + 1], bcol,
                                              allow_slow_non_contiguous=True).then_inc(loaded, 16)
                                n += 2
                        return n

                    @block.vector
                    def _(dve):
                        for x, sem in ((0, loaded), (1, loaded2)):
                            dve.wait_ge(sem, 16 * 2 * B * A)
                            dve.tensor_copy(W[x][:, :, :, WD:].rearrange("p c w n -> p (c w) n"),
                                            W[x][:, :, :, 0:WD].rearrange("p c w n -> p (c w) n")).then_inc(doubled, 1)
                            dve.tensor_copy(bias[x][WD:P, :], bias[x][0:WD, :]).then_inc(doubled, 1)

                    @block.sync
                    def _(sp):
                        n = fetch(sp, loaded, W[0], bias[0], a["L0_ffn_Wq"], a["L0_ffn_bq"], 0)
                        sp.wait_ge(loaded, 16 * n)

                    @block.scalar
                    def _(act):
                        n = fetch(act, loaded2, W[1], bias[1], a["L0_ffn_Wk"], a["L0_ffn_bk"], 0)
                        act.wait_ge(loaded2, 16 * n)

                    @block.gpsimd
                    def _(pool):
                        n = 0
                        for b in range(B):
                            for k in range(A):
                                h = pool.value_load(chosen[0:1, b, k:k + 1], min_val=0, max_val=15)
                                src = a["L0_ffn_Wv"].rearrange("(c p) n -> p c n", p=P)[:, :, bass.ds(h * WD, WD)]
                                pool.dma_start(Wv[:, :, b, k * WD:(k + 1) * WD], src).then_inc(loaded3, 16)
                                pool.dma_start(bv[:, b, k * WD:(k + 1) * WD],
                                               row(a["L0_ffn_bv"][bass.ds(h * WD, WD)])).then_inc(loaded3, 16)
                                n += 2
                        pool.wait_ge(loaded3, 16 * n)
            jobs = [(b * A + k, b * S + t * N, N, k, b * S + t * N)
                    for b in range(B) for k in range(A) for t in range(S // N)]
            stacks64(nc, K, "m0_q", "q", W[0], P, K.XNT, jobs, [QA, QB], bias=bias[0])
            stacks64(nc, K, "m0_k", "k", W[1], P, K.XNT, jobs, KK, bias=bias[1])
            with Stage(nc, "m0_v") as vs:
                pm = vs.ps("mm", [P, 4, N])
                mm, ev = vs.sem("mm"), vs.sem("ev")
                with vs.block() as block:
                    @block.tensor
                    def _(pe):
                        for t in range(TT):
                            if t >= 4:
                                pe.wait_ge(ev, t - 3)
                            for c in range(DC):
                                last = pe.matmul(pm[:, t % 4, 0:A * WD], K.XNT[:, c, t * P:(t + 1) * P], Wv[:, c, t // TB, :],
                                                 start=c == 0, stop=c == DC - 1)
                            last.then_inc(mm, 1)

                    @block.vector
                    def _(dve):
                        for t in range(TT):
                            dve.wait_ge(mm, t + 1)
                            dve.tensor_tensor(V[:, t, :], pm[:, t % 4, 0:A * WD], bv[:, t // TB, :], ALU.add).then_inc(ev, 1)

        attention(nc, K, "m0", A, WD ** -0.5, WD, P, TB, False, [(QA, P), (QB, P)],
                  [(x, P) for x in KK], [(0, 0), (0, 1), (1, 2)],
                  lambda b, h: V[:, b * TB:(b + 1) * TB, bass.ds(h * WD, WD)], K.XN, False)
    project(nc, K, "m0_out", K.XN, A * WD, a["L0_ffn_Wo"], a["L0_ffn_bo"])


def relative_bias(nc, K, V, table, Y, G):
    R = table.shape[0]
    assert R < N and S - 1 - R >= N and S == 2 * N
    KT = N // P
    U = 2 * N
    HW = N + (KT - 1) * P
    with Stage(nc, "bias") as st:
        tb, gt = st.sb("table", [P, R // P + 1, NH]), st.sb("gt", [NH, U])
        crow = st.sb("crow", [P, NH])
        flip, sel = st.sb("flip", [P, P]), st.sb("sel", [P, 32])
        vr = st.sb("vr", [P, B, KT, D])
        slot, hk = st.sb("slot", [P, 2, KT, B, HD]), st.sb("hankel", [P, 2, HW])
        ot = st.sb("ot", [P, 2, N])
        cs = st.sb("cs", [P, B, D])
        ps_r, ps_s = st.ps("rev", [P, 2, 2, D]), st.ps("sum", [P, B, D])
        ps_t, ps_o, ps_f = st.ps("turn", [NH, N]), st.ps("o", [P, 2, N]), st.ps("f", [P, 2, N])
        loaded, made, turned, gdone, stored = (st.sem(x) for x in ("loaded", "made", "turned", "gdone", "stored"))
        rev, revc, sums, chain = (st.sem(x) for x in ("rev", "revc", "sums", "chain"))
        hl = [st.sem(f"hankel{j}") for j in range(2)]
        vs, od, oc, fd, yd = (st.sem(x) for x in ("vslot", "o", "ocopied", "final", "y"))
        with st.block() as block:
            @block.sync
            def _(sp):
                full = R // P * P
                sp.dma_start(tb[:, 0:R // P, :], table[0:full, :].rearrange("(t p) h -> p t h", p=P)).then_inc(loaded, 16)
                sp.dma_start(tb[0:R - full, R // P, :], table[full:R, :]).then_inc(loaded, 16)
                sp.dma_start(crow[:], row(table[R - 1, :])).then_inc(loaded, 16)
                sp.wait_ge(gdone, 3)
                sp.dma_start(G, gt[:]).then_inc(stored, 16)
                sp.wait_ge(stored, 16)

                def load(i, j):
                    src = bass.AP(G.tensor, (i * 2 + j) * U, [[1, P], [1, HW]])
                    sp.dma_start(hk[:, j, :], src).then_inc(hl[j], 16)

                for j in range(2):
                    load(0, j)
                with sp.Fori(1, NH // 2, 1) as i:
                    for j in range(2):
                        sp.wait_ge(od, i * 2 + j - 1)
                        load(i, j)

            @block.gpsimd
            def _(pool):
                pool.memset(flip[:], 0.0).then_inc(made, 1)
                pool.memset(sel[:], 0.0).then_inc(made, 1)
                pool.wait_ge(made, 2)
                pool.affine_select(out=flip[:], in_=flip[:], compare_op=ALU.not_equal, fill=1.0, base=-(P - 1),
                                   pattern=[[1, P]], channel_multiplier=1).then_inc(made, 1)
                for j in range(4):
                    pool.affine_select(out=sel[:], in_=sel[:], compare_op=ALU.not_equal, fill=1.0, base=-32 * j,
                                       pattern=[[-1, 32]], channel_multiplier=1).then_inc(made, 1)
                    pool.wait_ge(made, 4 + j)
                pool.wait_ge(revc, B * KT // 2)

                def copy_v(i, j):
                    for b in range(B):
                        last = pool.tensor_copy(slot[:, j, :, b, :], vr[:, b, :, bass.ds((i * 2 + j) * HD, HD)])
                    last.then_inc(vs, 1)

                for j in range(2):
                    copy_v(0, j)
                with pool.Fori(1, NH // 2, 1) as i:
                    for j in range(2):
                        pool.wait_ge(od, i * 2 + j - 1)
                        copy_v(i, j)

            @block.tensor
            def _(pe):
                pe.wait_ge(loaded, 48)
                for t in range(R // P + 1):
                    n = min(P, R - t * P)
                    last = pe.transpose(ps_t[:, t * P:t * P + n], tb[0:n, t, :], K.ident[0:n, 0:n])
                last.then_inc(turned, 1)
                for b in range(B):
                    for t in range(TB):
                        last = pe.matmul(ps_s[:, b, :], K.ones[:], V[:, b * TB + t, :], start=t == 0, stop=t == TB - 1)
                last.then_inc(sums, 1)
                pe.wait_ge(made, 7)
                for n in range(B * KT // 2):
                    if n >= 2:
                        pe.wait_ge(revc, n - 1)
                    for k in range(2):
                        b, t = divmod(2 * n + k, KT)
                        last = pe.matmul(ps_r[:, n % 2, k, :], flip[:], V[:, b * TB + N // P + t, :], start=True, stop=True)
                    last.then_inc(rev, 1)

                def products(i, j):
                    h = i * 2 + j
                    pe.wait_ge(hl[j], (i + 1) * 16)
                    pe.wait_ge(vs, h + 1)
                    pe.wait_ge(oc, h + 1)
                    for k in range(KT):
                        last = pe.matmul(ps_o[32 * k:32 * k + 32, j, :], slot[:, j, k, :, :].rearrange("p b d -> p (b d)"),
                                         hk[:, j, (KT - 1 - k) * P:(KT - 1 - k) * P + N], start=True, stop=True)
                    last.then_inc(od, 1)

                def finals(i, j):
                    h = i * 2 + j
                    pe.wait_ge(oc, h + 3)
                    pe.wait_ge(yd, h + 1)
                    for t in range(KT):
                        last = pe.matmul(ps_f[:, j, t * B * HD:(t + 1) * B * HD], ot[:, j, t * P:(t + 1) * P],
                                         sel[:], start=True, stop=True)
                    last.then_inc(fd, 1)

                products(0, 0)
                with pe.Fori(0, NH // 2 - 1, 1) as i:
                    products(i, 1)
                    finals(i, 0)
                    products(i + 1, 0)
                    finals(i, 1)
                products(NH // 2 - 1, 1)
                for j in range(2):
                    finals(NH // 2 - 1, j)

            @block.scalar
            def _(act):
                act.sem_inc(oc, 2)
                for n in range(B * KT // 2):
                    act.wait_ge(rev, n + 1)
                    b, t = divmod(2 * n, KT)
                    act.copy(vr[:, b, t:t + 2, :], ps_r[:, n % 2, :, :]).then_inc(revc, 1)
                with act.Fori(0, NH // 2, 1) as i:
                    for j in range(2):
                        act.wait_ge(od, i * 2 + j + 1)
                        act.wait_ge(fd, i * 2 + j + 1)
                        act.copy(ot[:, j, :], ps_o[:, j, :]).then_inc(oc, 1)

            @block.vector
            def _(dve):
                dve.sem_inc(yd, 2)
                dve.sem_inc(fd, 2)
                dve.memset(gt[:], 0.0).then_inc(gdone, 1)
                dve.wait_ge(turned, 1)
                dve.wait_ge(gdone, 1)
                dve.tensor_copy(gt[:, 0:R], ps_t[:, 0:R]).then_inc(gdone, 1)
                dve.wait_ge(gdone, 2)
                dve.tensor_scalar(gt[:, 0:R], ps_t[:, 0:R], gt[:, R - 1:R], None, ALU.subtract).then_inc(gdone, 1)
                dve.wait_ge(sums, 1)
                dve.wait_ge(loaded, 48)
                link = Link(dve, chain)
                for b in range(B):
                    link(dve.tensor_tensor(cs[:, b, :].rearrange("p (h d) -> p h d", d=HD),
                                           ps_s[:, b, :].rearrange("p (h d) -> p h d", d=HD),
                                           crow[:].rearrange("p (h a) -> p h a", a=1).to_broadcast([P, NH, HD]), ALU.mult))
                    y = Y[:, b * TB:(b + 1) * TB, :]
                    link(dve.tensor_tensor(y, y, cs[:, b:b + 1, :].to_broadcast([P, TB, D]), ALU.add))
                with dve.Fori(0, NH // 2, 1) as i:
                    for j in range(2):
                        h = i * 2 + j
                        dve.wait_ge(fd, h + 3)
                        for b in range(B):
                            y = Y[:, b * TB:b * TB + KT, bass.ds(h * HD, HD)]
                            f = ps_f[:, j, 0:KT * B * HD].rearrange("p (t b d) -> p t b d", t=KT, b=B)
                            last = dve.tensor_tensor(y, y, f[:, :, b, :], ALU.add)
                        last.then_inc(yd, 1)


XH, XD, TOP = 4, 32, 32


def sparse_cross(nc, K, a, text_mask, ctx_mask, CTT):
    Wq, Wk, Wv = (a[f"L1_xattn_W{x}"] for x in "qkv")
    with Stage(nc, "e_att") as st:
        wq, wk = st.sb("wq", [P, DC, P]), st.sb("wk", [CW_P, CW_N, P])
        wv, V = st.sb("wv", [CW_P, CW_N, D]), st.sb("V", [CT_P, B * CT_N, D])
        QT, KT = st.sb("QT", [P, B * S]), st.sb("KT", [P, B * CL])
        AT = st.sb("AT", [CT_P, CT_N, B * S])
        mraw, mrow = st.sb("mraw", [P, B, CL], mybir.dt.uint8), st.sb("mrow", [P, B, CL])
        traw, tmask = st.sb("traw", [P, TT], mybir.dt.uint8), st.sb("tmask", [P, TT])
        sc = st.sb("sc", [P, 2, XH, CL])
        left, ex, mk = st.sb("left", [P, XH, CL]), st.sb("ex", [P, 2, XH, CL]), st.sb("mk", [P, 2, XH, CL])
        top, neg = st.sb("top", [P, XH, TOP // 8, 8]), st.sb("neg", [P, 2, XH])
        den, r, half = st.sb("den", [P, 2, XH]), st.sb("r", [P, 2, XH]), st.sb("half", [P, 2, CL])
        mean = st.sb("mean", [P, 2, CL])
        ps, pt, pc = st.ps("s", [P, 2, 2, N]), st.ps("t", [CT_P, 2, N]), st.ps("c", [P, 2, N])
        loaded, mm, ev = (st.sem(x) for x in ("loaded", "mm", "ev"))
        s_ready, s_read, chain, e_go, e_done = (st.sem(x) for x in ("s_ready", "s_read", "chain", "e_go", "e_done"))
        m_ready, t_ready, t_done, c_ready, c_done = (st.sem(x) for x in ("m_ready", "t_ready", "t_done", "c_ready", "c_done"))
        mk_ready, mx_done, r_ready, pchain = (st.sem(x) for x in ("mk_ready", "mx_done", "r_ready", "pchain"))
        pair_done = st.sem("pair_done")
        nload = 4 + 2 * B

        def scores_of(t):
            return ps[:, t % 2, :, 0:2 * CL].rearrange("p a (h n) -> p a h n", h=2)

        jobs = [("q", 0), ("k", 0)] + [("q", t) for t in range(1, B * S // N)] + [("v", t) for t in range(B * CT_N)]
        NT4 = N // P
        with st.block() as block:
            @block.sync
            def _(sp):
                sp.dma_start(wq[:], Wq.rearrange("(c p) n -> p c n", p=P)).then_inc(loaded, 16)
                sp.dma_start(wk[:], Wk.rearrange("(c p) n -> p c n", p=CW_P)).then_inc(loaded, 16)
                sp.dma_start(wv[:], Wv.rearrange("(c p) n -> p c n", p=CW_P)).then_inc(loaded, 16)
                sp.dma_start(mraw[:].rearrange("p b n -> p (b n)"), row(ctx_mask.rearrange("b n -> (b n)"))).then_inc(loaded, 16)
                for b in range(B):
                    for x in range(2):
                        sp.dma_start(traw[:, b * TB + x * TB // 2:b * TB + (x + 1) * TB // 2],
                                     text_mask[b].rearrange("(m p x) -> p x m", p=P, x=2)[:, x, :],
                                     allow_slow_non_contiguous=True).then_inc(loaded, 16)

            @block.tensor
            def _(pe):
                pe.wait_ge(loaded, 16 * nload)
                def project_job(m):
                    kind, t = jobs[m]
                    if m >= 2:
                        pe.wait_ge(ev, m - 1)
                    out = pc[:, m % 2, :]
                    for c in range(DC):
                        kw = dict(start=c == 0, stop=c == DC - 1)
                        if kind == "q":
                            last = pe.matmul(out, wq[:, c, :], K.XNT[:, c, t * N:(t + 1) * N], **kw)
                        elif kind == "k":
                            last = pe.matmul(out[:, 0:B * CL], wk[:, c, :], K.CT[:, c, :], **kw)
                        else:
                            last = pe.matmul(out[0:CT_P, 0:D], K.CT[:, c, t * CT_P:(t + 1) * CT_P], wv[:, c, :], **kw)
                    last.then_inc(mm, 1)

                def scores(t):
                    b = t // TB
                    if t >= 2:
                        pe.wait_ge(s_read, t - 1)
                    for h in range(XH):
                        if h == 2:
                            pe.wait_ge(pair_done, t + 1)
                        last = pe.matmul(scores_of(t)[:, h % 2, h // 2, :], QT[h * XD:(h + 1) * XD, t * P:(t + 1) * P],
                                         KT[h * XD:(h + 1) * XD, b * CL:(b + 1) * CL], start=True, stop=True)
                        if h == 1:
                            last.then_inc(pair_done, 1)
                    last.then_inc(s_ready, 1)

                def turn(t):
                    pe.wait_ge(m_ready, t + 1)
                    if t >= 2:
                        pe.wait_ge(t_done, t - 1)
                    for j in range(CT_N):
                        last = pe.transpose(pt[:, t % 2, j * P:(j + 1) * P], mean[:, t % 2, j * CT_P:(j + 1) * CT_P],
                                            K.ident[:])
                    last.then_inc(t_ready, 1)

                def sums(block_):
                    b = block_ // (S // N)
                    pe.wait_ge(t_done, NT4 * (block_ + 1))
                    for c in range(DC):
                        m = block_ * DC + c
                        if m >= 2:
                            pe.wait_ge(c_done, m - 1)
                        for j in range(CT_N):
                            last = pe.matmul(pc[:, m % 2, :], V[:, b * CT_N + j, c * P:(c + 1) * P],
                                             AT[:, j, block_ * N:(block_ + 1) * N], start=j == 0, stop=j == CT_N - 1)
                        last.then_inc(c_ready, 1)

                for m in range(2):
                    project_job(m)
                pe.wait_ge(ev, 2)
                for t in range(2):
                    scores(t)
                for m in range(2, len(jobs)):
                    project_job(m)
                pe.wait_ge(ev, len(jobs))
                for t in range(2, TT):
                    scores(t)
                    if t >= 3 and (t - 3) % NT4 == NT4 - 1:
                        sums((t - 3) // NT4)
                    turn(t - 2)
                turn(TT - 2)
                turn(TT - 1)
                sums(TT // NT4 - 1)

            @block.scalar
            def _(act):
                for m, (kind, t) in enumerate(jobs):
                    act.wait_ge(mm, m + 1)
                    src = pc[:, m % 2, :]
                    if kind == "q":
                        act.copy(QT[:, t * N:(t + 1) * N], src).then_inc(ev, 1)
                    elif kind == "k":
                        act.copy(KT[:], src[:, 0:B * CL]).then_inc(ev, 1)
                    else:
                        act.copy(V[:, t, :], src[0:CT_P, 0:D]).then_inc(ev, 1)

                def take_sums(block_):
                    for c in range(DC):
                        m = block_ * DC + c
                        act.wait_ge(c_ready, m + 1)
                        act.copy(CTT[:, c, block_ * N:(block_ + 1) * N], pc[:, m % 2, :]).then_inc(c_done, 1)

                def take_turned(t):
                    act.wait_ge(t_ready, t + 1)
                    act.copy(AT[:, :, t * P:(t + 1) * P],
                             pt[:, t % 2, 0:CT_N * P].rearrange("p (j n) -> p j n", j=CT_N)).then_inc(t_done, 1)

                for t in range(TT):
                    act.wait_ge(e_go, t + 1)
                    if t >= 2:
                        act.wait_ge(mx_done, t - 1)
                    for h in range(XH):
                        last = act.activation(ex[:, t % 2, h, :], sc[:, t % 2, h, :], ACT.Exp, bias=neg[:, t % 2, h:h + 1])
                    last.then_inc(e_done, 1)
                    if t >= 3 and (t - 3) % NT4 == NT4 - 1:
                        take_sums((t - 3) // NT4)
                    if t >= 2:
                        take_turned(t - 2)
                take_turned(TT - 2)
                take_turned(TT - 1)
                take_sums(TT // NT4 - 1)

            @block.vector
            def _(dve):
                link = Link(dve, chain)
                dve.wait_ge(loaded, 16 * nload)
                link(dve.tensor_copy(mrow[:], mraw[:]))
                link(dve.tensor_scalar(mrow[:], mrow[:], 1.0, -NEG, ALU.subtract, ALU.mult))
                link(dve.tensor_copy(tmask[:], traw[:]))
                link(dve.tensor_scalar(tmask[:], tmask[:], 1.0 / XH, None, ALU.mult))

                def denominators(t):
                    dve.wait_ge(mx_done, t + 1)
                    link(dve.tensor_reduce(den[:, t % 2, :], mk[:, t % 2, :, :], AX.X, ALU.add))
                    link(dve.reciprocal(r[:, t % 2, :], den[:, t % 2, :]))
                    dve.tensor_scalar(r[:, t % 2, :], r[:, t % 2, :], tmask[:, t:t + 1], None, ALU.mult).then_inc(r_ready, 1)

                for t in range(TT):
                    b, s2 = t // TB, sc[:, t % 2, :, :]
                    dve.wait_ge(s_ready, t + 1)
                    if t >= 2:
                        dve.wait_ge(e_done, t - 1)
                    for bank in range(2):
                        last = dve.scalar_tensor_tensor(out=s2[:, bank:XH:2, :], in0=scores_of(t)[:, bank, :, :],
                                                        scalar=XD ** -0.5,
                                                        in1=mrow[:, b:b + 1, :].to_broadcast([P, 2, CL]),
                                                        op0=ALU.mult, op1=ALU.add)
                    last.then_inc(s_read, 1)
                    dve.wait_ge(s_read, t + 1)
                    for n in range(TOP // 8):
                        for h in range(XH):
                            last = dve.max(top[:, h, n, :], s2[:, h, :] if n == 0 else left[:, h, :])
                        link(last)
                        if n == 0:
                            dve.tensor_scalar(neg[:, t % 2, :], top[:, :, 0, 0], -1.0, None, ALU.mult).then_inc(e_go, 1)
                        for h in range(XH):
                            last = dve.match_replace(left[:, h, :], top[:, h, n, :], s2[:, h, :] if n == 0 else left[:, h, :],
                                                     -3.0e38)
                        link(last)
                    if t >= 2:
                        dve.wait_ge(m_ready, t - 1)
                    dve.tensor_tensor(mk[:, t % 2, :, :], left[:], s2, ALU.not_equal).then_inc(mk_ready, 1)
                    dve.wait_ge(mk_ready, t + 1)
                    if t:
                        denominators(t - 1)
                denominators(TT - 1)

            @block.gpsimd
            def _(pool):
                link = Link(pool, pchain)

                def mean_of(t):
                    pool.wait_ge(r_ready, t + 1)
                    m = mk[:, t % 2, :, :]
                    link(pool.tensor_tensor(m, m, r[:, t % 2, :].rearrange("p (h a) -> p h a", a=1)
                                            .to_broadcast([P, XH, CL]), ALU.mult))
                    link(pool.tensor_tensor(half[:], m[:, 0:2, :], m[:, 2:4, :], ALU.add))
                    if t >= 2:
                        pool.wait_ge(t_ready, t - 1)
                    pool.tensor_tensor(mean[:, t % 2, :], half[:, 0, :], half[:, 1, :], ALU.add).then_inc(m_ready, 1)
                    pool.wait_ge(m_ready, t + 1)

                for t in range(TT):
                    m = mk[:, t % 2, :, :]
                    pool.wait_ge(mk_ready, t + 1)
                    pool.wait_ge(e_done, t + 1)
                    pool.tensor_tensor(m, m, ex[:, t % 2, :, :], ALU.mult).then_inc(mx_done, 1)
                    if t:
                        mean_of(t - 1)
                mean_of(TT - 1)


def film(nc, K, name, CTT, W, bias, gate, dst):
    with Stage(nc, name) as st:
        Wt, brow, g = st.sb("W", [P, DC, 2 * D]), st.sb("bias", [P, 2 * D]), st.sb("gate", [P, 1])
        f = st.sb("f", [P, 2, 2 * D])
        pm = st.ps("mm", [P, 3, N])
        loaded, mm, fd, d1, d2, d3 = (st.sem(x) for x in ("loaded", "mm", "fd", "d1", "d2", "d3"))
        with st.block() as block:
            @block.sync
            def _(sp):
                sp.dma_start(Wt[:], W.rearrange("(c p) n -> p c n", p=P)).then_inc(loaded, 16)
                sp.dma_start(brow[:], row(bias)).then_inc(loaded, 16)
                sp.dma_start(g[:], row(gate)).then_inc(loaded, 16)

            @block.tensor
            def _(pe):
                pe.wait_ge(loaded, 48)
                for t in range(TT):
                    if t >= 3:
                        pe.wait_ge(fd, t - 2)
                    for c in range(DC):
                        last = pe.matmul(pm[:, t % 3, :], CTT[:, c, t * P:(t + 1) * P], Wt[:, c, :],
                                         start=c == 0, stop=c == DC - 1)
                    last.then_inc(mm, 1)

            @block.vector
            def _(dve):
                dve.wait_ge(loaded, 48)
                for t in range(TT):
                    ft = f[:, t % 2, :]
                    dve.wait_ge(mm, t + 1)
                    if t >= 2:
                        dve.wait_ge(d3, t - 1)
                    dve.tensor_tensor(ft, pm[:, t % 3, :], brow[:], ALU.add).then_inc(fd, 1)
                    dve.wait_ge(fd, t + 1)
                    dve.tensor_scalar(ft, ft, g[:, 0:1], None, ALU.mult).then_inc(d1, 1)
                    dve.wait_ge(d1, t + 1)
                    dve.scalar_tensor_tensor(out=dst[:, t, :], in0=ft[:, 0:D], scalar=1.0, in1=dst[:, t, :],
                                             op0=ALU.add, op1=ALU.mult).then_inc(d2, 1)

            @block.gpsimd
            def _(pool):
                for t in range(TT):
                    pool.wait_ge(d2, t + 1)
                    pool.tensor_tensor(dst[:, t, :], dst[:, t, :], f[:, t % 2, D:], ALU.add).then_inc(d3, 1)


TWO_PI = 6.283185307179586
FACT = [1.0, 1.0, 1 / 2, 1 / 6, 1 / 24, 1 / 120, 1 / 720, 1 / 5040]
LN2_HI, LN2_LO = 0.693359375, -2.12194440e-4
PI2_HI, PI2_LO = 6.28125, 6.283185307179586 - 6.28125
NS = 64
LB = S // P


def accurate_exp(link, eng, out, x, k, r, pw):
    link(eng.tensor_scalar(k, x, 1.4426950408889634, ROUND, ALU.mult, ALU.add))
    link(eng.tensor_scalar(k, k, ROUND, -126.0, ALU.subtract, ALU.max))
    link(eng.tensor_scalar(k, k, 127.0, None, ALU.min))
    link(eng.scalar_tensor_tensor(out=r, in0=k, scalar=-LN2_HI, in1=x, op0=ALU.mult, op1=ALU.add))
    link(eng.scalar_tensor_tensor(out=r, in0=k, scalar=-LN2_LO, in1=r, op0=ALU.mult, op1=ALU.add))
    link(eng.tensor_scalar(k, k, 127.0, 8388608.0, ALU.add, ALU.mult))
    link(eng.tensor_copy(pw, k))
    link(eng.tensor_scalar(out, r, FACT[7], None, ALU.mult))
    for n in range(6, 0, -1):
        link(eng.scalar_tensor_tensor(out=out, in0=out, scalar=FACT[n], in1=r, op0=ALU.add, op1=ALU.mult))
    link(eng.scalar_tensor_tensor(out=out, in0=out, scalar=1.0, in1=pw.bitcast(F32), op0=ALU.add, op1=ALU.mult))


def by_parity(ap):
    return ap.rearrange("(m p x) d -> p x m d", p=P, x=2)


def ssm_kernel(nc, K, a, KN):
    CH, SL = 16, 4
    with Stage(nc, "ssm") as st:
        raw = st.sb("raw", [P, 4, DC, 2, NS])
        V = [st.sb(f"v{n}", [P, D]) for n in range(4)]
        Ar, Ai, Cr, Ci = V
        dt, ar, tw = st.sb("dt", [P, D]), st.sb("ar", [P, D]), st.sb("tw", [P, D])
        T = [st.sb(f"t{n}", [P, D]) for n in range(8)]
        pw = st.sb("pw", [P, D], I32)
        R, Rk = st.sb("R", [P, D, LB]), [st.sb(f"Rk{n}", [P, D, LB]) for n in range(3)]
        posn, blk, odd, start = st.sb("pos", [P, P]), st.sb("blk", [P, LB]), st.sb("odd", [P, LB]), st.sb("start", [P, LB])
        ph = st.sb("ph", [P, 8])
        F, G = st.sb("F", [P, SL, CH, P]), st.sb("G", [P, SL, CH, P])
        W2 = st.sb("W2", [P, CH, P])
        pv, pk = st.ps("turned", [P, 4, N]), st.ps("k", [P, D, LB])
        loaded, chain, turned, made, coef = (st.sem(x) for x in ("loaded", "chain", "turned", "made", "coef"))
        f1, f2, f3, f4, g1, sn, wd, kd = (st.sem(x) for x in ("f1", "f2", "f3", "f4", "g1", "sn", "wd", "kd"))
        e1, ask, ans, kcopied = st.sem("e1"), st.sem("ask"), st.sem("ans"), st.sem("kcopied")
        stored, reloaded = st.sem("stored"), st.sem("reloaded")
        names = ("A_re", "A_im", "C_re", "C_im")
        NCH = D // CH
        def asked(T, Rk):
            return [(T[5][:], T[3][:], 0.5, None, ACT.Sin), (T[6][:], T[3][:], 1.0, None, ACT.Sin),
                    (Rk[0][:], Rk[0][:], -6.283185, 2, ACT.Sin), (Rk[1][:], Rk[1][:], -6.283185, None, ACT.Sin),
                    (Rk[2][:], Rk[2][:], 1.0, None, ACT.Exp)]

        with st.block() as block:
            @block.sync
            def _(sp):
                for j, x in enumerate(names):
                    for twice in range(2):
                        sp.dma_start(raw[:, j, :, twice, :],
                                     a["L1_xattn_" + x].rearrange("(c p) n -> p c n", p=P)).then_inc(loaded, 16)
                sp.dma_start(dt[:], row(a["L1_xattn_log_dt"])).then_inc(loaded, 16)
                for b in range(B):
                    sp.dma_start(K.scratch[b].rearrange("(t p) d -> p t d", p=P),
                                 K.X[:, b * TB:(b + 1) * TB, :]).then_inc(stored, 16)
                sp.wait_ge(stored, 16 * B)
                for b in range(B):
                    for x in range(2):
                        sp.dma_start(K.X[:, b * TB + x * TB // 2:b * TB + (x + 1) * TB // 2, :],
                                     by_parity(K.scratch[b])[:, x, :, :]).then_inc(reloaded, 16)
                sp.wait_ge(reloaded, 16 * B * 2)

            @block.tensor
            def _(pe):
                pe.wait_ge(loaded, 16 * 9)
                for j in range(4):
                    for c in range(DC):
                        last = pe.transpose(pv[:, j, c * P:(c + 1) * P], raw[:, j, c, :, :].rearrange("p t n -> p (t n)"),
                                            K.ident[:])
                last.then_inc(turned, 1)
                pe.wait_ge(coef, 1)

                def slot(i, j):
                    q = i * SL + j
                    pe.wait_ge(wd, q + 1 + SL)
                    for c in range(CH):
                        last = pe.matmul(pk[:, bass.ds(q * CH + c, 1), :].rearrange("p a n -> p (a n)"), F[:, j, c, :],
                                         R[:, bass.ds(q * CH + c, 1), :].rearrange("p a n -> p (a n)"),
                                         start=True, stop=True)
                    last.then_inc(kd, 1)

                with pe.Fori(0, NCH // SL, 1) as i:
                    for j in range(SL):
                        slot(i, j)

            @block.gpsimd
            def _(pool):
                pool.iota(posn[:], pattern=[[2, P]], base=0, channel_multiplier=0,
                          allow_small_or_imprecise_dtypes=True).then_inc(made, 1)
                for x, steps in ((blk, (1, 0)), (odd, (0, 1)), (start, (2 * P, 1))):
                    pool.iota(x[:], pattern=[[steps[1], 2], [steps[0], LB // 2]], base=0, channel_multiplier=0,
                              allow_small_or_imprecise_dtypes=True).then_inc(made, 1)
                pool.wait_ge(coef, 1)

                def growth(q, j):
                    pool.wait_ge(wd, q + 1)
                    pool.tensor_tensor(G[:, j, :, :], ar[:, bass.ds(q * CH, CH)].rearrange("p (c a) -> p c a", a=1)
                                       .to_broadcast([P, CH, P]),
                                       posn[:].rearrange("p (a n) -> p a n", a=1).to_broadcast([P, CH, P]),
                                       ALU.mult).then_inc(g1, 1)

                def pair(i, h, more):
                    for j in (2 * h, 2 * h + 1):
                        if more:
                            growth(i * SL + j + 2, (j + 2) % SL)
                    for j in (2 * h, 2 * h + 1):
                        q = i * SL + j
                        pool.wait_ge(sn, q + 1)
                        pool.wait_ge(e1, q + 1)
                        pool.tensor_tensor(F[:, j, :, :], F[:, j, :, :], G[:, j, :, :], ALU.mult).then_inc(wd, 1)

                for j in range(2):
                    growth(j, j)
                with pool.Fori(0, NCH // SL - 1, 1) as i:
                    for h in range(2):
                        pair(i, h, True)
                for h in range(2):
                    pair(NCH // SL - 1, h, h == 0)

            @block.scalar
            def _(act):
                act.sem_inc(kd, SL)
                act.sem_inc(wd, SL)
                for n, (o, x, s, bcol, fn) in enumerate(asked(T, Rk)):
                    act.wait_ge(ask, n + 1)
                    act.activation(o, x, fn, scale=s, **({} if bcol is None else {"bias": ph[:, bcol:bcol + 1]})).then_inc(ans, 1)
                with act.Fori(0, NCH // SL, 1) as i:
                    for pair in range(0, SL, 2):
                        for j in (pair, pair + 1):
                            q = i * SL + j
                            act.wait_ge(f4, q + 1)
                            act.activation(F[:, j, :, :], F[:, j, :, :], ACT.Sin, scale=-6.283185,
                                           bias=ph[:, 1:2]).then_inc(sn, 1)
                        for j in (pair, pair + 1):
                            q = i * SL + j
                            act.wait_ge(g1, q + 1)
                            act.activation(G[:, j, :, :], G[:, j, :, :], ACT.Exp).then_inc(e1, 1)
                act.wait_ge(kd, NCH + SL)
                for b in range(LB // 2):
                    d = slice(b * D * 2 // LB, (b + 1) * D * 2 // LB)
                    act.copy(KN[:, :, d], pk[:, d, :].rearrange("p c l -> p l c")).then_inc(kcopied, 1)

            @block.vector
            def _(dve):
                link = Link(dve, chain)
                tt, ts, stt = dve.tensor_tensor, dve.tensor_scalar, dve.scalar_tensor_tensor
                top, bot = slice(0, NS), slice(NS, P)
                for rows, phase in ((top, 0.25), (bot, 0.0)):
                    link(dve.memset(ph[rows, 0:1], phase))
                    link(dve.memset(ph[rows, 1:2], phase * TWO_PI))
                    link(dve.memset(ph[rows, 3:4], phase + 0.5 - 1e-7))
                    link(dve.memset(ph[rows, 4:5], phase - 0.5 + 1e-7))
                link(dve.memset(ph[:, 2:3], 0.25 * TWO_PI))
                dve.wait_ge(turned, 1)
                for j in range(4):
                    link(dve.tensor_copy(V[j][:], pv[:, j, 0:D]))
                t = [x[:] for x in T]
                link(dve.tensor_copy(t[7], dt[:]))
                accurate_exp(link, dve, dt[:], t[7], t[0], t[1], pw[:])
                link(tt(ar[:], dt[:], Ar[:], ALU.mult))
                link(tt(t[2], dt[:], Ai[:], ALU.mult))
                link(ts(t[3], t[2], 1 / TWO_PI, ROUND, ALU.mult, ALU.add))
                link(ts(t[4], t[3], ROUND, None, ALU.subtract))
                link(stt(out=t[3], in0=t[4], scalar=-PI2_HI, in1=t[2], op0=ALU.mult, op1=ALU.add))
                link(stt(out=t[3], in0=t[4], scalar=-PI2_LO, in1=t[3], op0=ALU.mult, op1=ALU.add))
                link(ts(t[3], t[3], 3.1415925, -3.1415925, ALU.min, ALU.max))
                link(ts(tw[:], t[3], 1 / TWO_PI, None, ALU.mult))
                dve.sem_inc(ask, 2)
                accurate_exp(link, dve, t[7], ar[:], t[0], t[1], pw[:])
                dve.wait_ge(ans, 2)
                link(tt(t[5], t[5], t[5], ALU.mult))
                link(tt(t[5], t[5], t[7], ALU.mult))
                link(ts(t[0], t[7], 1.0, None, ALU.subtract))
                link(stt(out=t[0], in0=t[5], scalar=-2.0, in1=t[0], op0=ALU.mult, op1=ALU.add))
                link(tt(t[1], t[7], t[6], ALU.mult))
                link(tt(t[2], Ar[:], Ar[:], ALU.mult))
                link(tt(t[4], Ai[:], Ai[:], ALU.mult))
                link(tt(t[2], t[2], t[4], ALU.add))
                link(dve.reciprocal(t[2], t[2]))
                link(tt(t[4], t[0], Ar[:], ALU.mult))
                link(tt(t[5], t[1], Ai[:], ALU.mult))
                link(tt(t[4], t[4], t[5], ALU.add))
                link(tt(t[5], t[1], Ar[:], ALU.mult))
                link(tt(t[6], t[0], Ai[:], ALU.mult))
                link(tt(t[5], t[5], t[6], ALU.subtract))
                link(tt(t[4], t[4], t[2], ALU.mult))
                link(tt(t[5], t[5], t[2], ALU.mult))
                link(tt(t[0], Cr[:], t[4], ALU.mult))
                link(tt(t[6], Ci[:], t[5], ALU.mult))
                link(tt(t[0], t[0], t[6], ALU.subtract))
                link(tt(t[1], Cr[:], t[5], ALU.mult))
                link(tt(t[6], Ci[:], t[4], ALU.mult))
                link(tt(t[1], t[1], t[6], ALU.add))
                link(ts(t[4][top], t[0][top], 2.0, None, ALU.mult))
                link(ts(t[4][bot], t[1][bot], -2.0, None, ALU.mult))
                link(ts(t[5][top], t[1][top], 2.0, None, ALU.mult))
                link(ts(t[5][bot], t[0][bot], 2.0, None, ALU.mult))
                link(ts(t[2], tw[:], 2.0 * P, None, ALU.mult))
                link(ts(t[6], t[2], ROUND, ROUND, ALU.add, ALU.subtract))
                link(tt(t[2], t[2], t[6], ALU.subtract))
                dve.wait_ge(made, 4)

                def by_d(x):
                    return x.rearrange("p (d a) -> p d a", a=1).to_broadcast([P, D, LB])

                def by_block(x):
                    return x[:].rearrange("p (a n) -> p a n", a=1).to_broadcast([P, D, LB])

                link(tt(R[:], by_d(t[2]), by_block(blk), ALU.mult))
                link(tt(Rk[0][:], by_d(tw[:]), by_block(odd), ALU.mult))
                link(tt(R[:], R[:], Rk[0][:], ALU.add))
                for n, phase in ((0, 0.25), (1, 0.0)):
                    link(ts(Rk[n][:], R[:], phase, ROUND, ALU.add, ALU.add))
                    link(stt(out=Rk[n][:], in0=Rk[n][:], scalar=ROUND, in1=R[:], op0=ALU.subtract, op1=ALU.subtract))
                    link(ts(Rk[n][:], Rk[n][:], phase + 0.5 - 1e-7, phase - 0.5 + 1e-7, ALU.min, ALU.max))
                link(tt(Rk[2][:], by_d(ar[:]), by_block(start), ALU.mult))
                dve.sem_inc(ask, 3)
                dve.wait_ge(ans, 5)
                link(tt(Rk[0][:], Rk[0][:], by_d(t[4]), ALU.mult))
                link(tt(Rk[1][:], Rk[1][:], by_d(t[5]), ALU.mult))
                link(tt(Rk[0][:], Rk[0][:], Rk[1][:], ALU.subtract))
                link(tt(R[:], Rk[0][:], Rk[2][:], ALU.mult))
                dve.sem_inc(coef, 1)

                def slot(i, j):
                    q = i * SL + j
                    f, k = F[:, j, :, :], W2[:]
                    dve.wait_ge(kd, q + 1)
                    tt(f, tw[:, bass.ds(q * CH, CH)].rearrange("p (c a) -> p c a", a=1).to_broadcast([P, CH, P]),
                       posn[:].rearrange("p (a n) -> p a n", a=1).to_broadcast([P, CH, P]), ALU.mult).then_inc(f1, 1)
                    dve.wait_ge(f1, q + 1)
                    ts(k, f, ph[:, 0:1], ROUND, ALU.add, ALU.add).then_inc(f2, 1)
                    dve.wait_ge(f2, q + 1)
                    stt(out=f, in0=k, scalar=ROUND, in1=f, op0=ALU.subtract, op1=ALU.subtract).then_inc(f3, 1)
                    dve.wait_ge(f3, q + 1)
                    ts(f, f, ph[:, 3:4], ph[:, 4:5], ALU.min, ALU.max).then_inc(f4, 1)

                with dve.Fori(0, NCH // SL, 1) as i:
                    for j in range(SL):
                        slot(i, j)


def convolution(nc, K, KN, U, Dskip, tables):
    FB = S // P // 2
    W2 = B * D
    with Stage(nc, "conv") as st:
        uh, ul = st.sb("uh", [P, TT, D], BF16), st.sb("ul", [P, TT, D], BF16)
        kh, kl = st.sb("kh", [P, LB, D], BF16), st.sb("kl", [P, LB, D], BF16)
        H, L = st.sb("H", [P, FB, 4, W2], BF16), st.sb("L", [P, FB, 4, W2], BF16)
        tab = st.sb("tab", [P, 2, 2, 2, 2, FB, P], BF16)
        free = K.XNT.rearrange("p c n -> p (c n)")
        es = free[:, 0:4 * W2].rearrange("p (x n) -> p x n", x=4)
        su, di = (free[:, x * W2:(x + 2) * W2].rearrange("p (x n) -> p x n", x=2) for x in (4, 6))
        ks, ksu, kdi = st.sb("ks", [P, 2, 2, D]), st.sb("ksu", [P, 2, D]), st.sb("kdi", [P, 2, D])
        tp, tq, ab = (st.sb(x, [P, 4, W2]) for x in ("tp", "tq", "ab"))
        drow = st.sb("drow", [P, D])
        px, pk, py = st.ps("x", [P, 4, N]), st.ps("k", [P, 2, N]), st.ps("y", [P, 2, N])
        tl = [st.sem(f"table{j}") for j in range(2)]
        loaded, hi, lo, xd, ev, used, pd, qd = (st.sem(x) for x in ("loaded", "hi", "lo", "xd", "ev", "used", "pd", "qd"))
        abd, hd, ld, skipped, bd, ba = (st.sem(x) for x in ("abd", "hd", "ld", "skipped", "bd", "ba"))
        NBK = 6

        def spectrum(x):
            return x.rearrange("p x (b d) -> p x b d", b=1).to_broadcast([P, x.shape[1], B, D])

        def both(x):
            return x.rearrange("p x (b d) -> p x b d", b=B)

        def times(eng, out, x, k, done):
            eng.tensor_tensor(both(out[:, 0:2, :]), both(x), spectrum(k[:]), ALU.mult).then_inc(done, 1)
            for y in range(2):
                eng.tensor_tensor(both(out[:, 2 + y:3 + y, :]), both(x[:, y:y + 1, :]), spectrum(k[:, 1 - y:2 - y, :]),
                                  ALU.mult).then_inc(done, 1)

        with st.block() as block:
            @block.sync
            def _(sp):
                sp.dma_start(drow[:], row(Dskip)).then_inc(loaded, 16)
                for way in range(2):
                    for q in range(FB):
                        if way or q >= 2:
                            sem, per = (bd, 2) if way and q >= 2 else (xd, NBK)
                            sp.wait_ge(sem, per * (q - 1 if q >= 2 else FB - 1 + q))
                        sp.dma_start(tab[:, q % 2].rearrange("p a b c f n -> p (a b c f n)"),
                                     tables[way, q].rearrange("p a b c f n -> p (a b c f n)").bitcast(BF16)).then_inc(tl[q % 2], 16)

            @block.tensor
            def _(pe):
                parts = ((0, 0), (0, 1), (1, 0))
                pe.wait_ge(lo, 2)
                with pe.Fori(0, FB // 2, 1) as i:
                    for j in range(2):
                        q = i * 2 + j
                        pe.wait_ge(tl[j], (i + 1) * 16)
                        for n in range(NBK):
                            pe.wait_ge(ev, q * NBK + n + 1)
                            if n < 4:
                                odd, cs = divmod(n, 2)
                                jobs = [(px[:, n, :], cs, uh[:].rearrange("p (b t) d -> p t b d", b=B),
                                         ul[:].rearrange("p (b t) d -> p t b d", b=B))]
                            else:
                                odd = n - 4
                                jobs = [(pk[:, odd, cs * D:(cs + 1) * D], cs, kh, kl) for cs in range(2)]
                            for out, cs, *ops in jobs:
                                for m in range(FB):
                                    for x, (w, o) in enumerate(parts):
                                        last = pe.matmul(out, tab[:, j, w, odd, cs, m, :], ops[o][:, odd * FB + m],
                                                         start=m == 0 and x == 0, stop=m == FB - 1 and x == 2)
                            last.then_inc(xd, 1)
                pe.wait_ge(ld, FB)
                with pe.Fori(0, FB // 2, 1) as i:
                    for j in range(2):
                        pe.wait_ge(tl[j], (i + 1) * 16 + 16 * (FB // 2))
                        for odd in range(2):
                            pe.wait_ge(ba, (i * 2 + j) * 2 + odd + 1)
                            for f in range(FB):
                                for cs in range(2):
                                    for x, (w, o) in enumerate(parts):
                                        last = pe.matmul(py[:, odd, :], tab[:, j, w, odd, cs, f, :],
                                                         (H, L)[o][:, f, 2 * odd + cs, :], start=f == cs == x == 0,
                                                         stop=f == FB - 1 and cs == 1 and x == 2)
                            last.then_inc(bd, 1)

            @block.scalar
            def _(act):
                act.copy(uh[:], U[:]).then_inc(hi, 1)
                act.copy(kh[:], KN[:]).then_inc(hi, 1)
                act.sem_inc(ev, NBK)
                act.sem_inc(used, 2)

                def high(q):
                    act.wait_ge(abd, 2 * (q + 1))
                    act.copy(H[:, q, :, :], ab[:]).then_inc(hd, 1)

                for q in range(FB):
                    for n in range(NBK):
                        act.wait_ge(xd, q * NBK + n + 1)
                        if n == 0:
                            act.wait_ge(used, 2 * q + 2)
                        if n < 4:
                            act.copy(es[:, n, :], px[:, n, :]).then_inc(ev, 1)
                        else:
                            act.copy(ks[:, n - 4, :, :].rearrange("p x d -> p (x d)"), pk[:, n - 4, :]).then_inc(ev, 1)
                        if q and n == 3:
                            high(q - 1)
                high(FB - 1)

            @block.gpsimd
            def _(pool):
                def step(sem, n):
                    pool.wait_ge(sem, n)

                for q in range(FB):
                    step(ev, (q + 2) * NBK)
                    if q:
                        step(abd, 2 * q)
                    pool.tensor_tensor(di, es[:, 0:2, :], es[:, 2:4, :], ALU.subtract).then_inc(qd, 1)
                    pool.tensor_tensor(kdi[:], ks[:, 0, :, :], ks[:, 1, :, :], ALU.subtract).then_inc(qd, 1)
                    step(qd, 7 * q + 2)
                    pool.sem_inc(used, 1)
                    times(pool, tq, di, kdi, qd)
                    step(qd, 7 * q + 5)
                    pool.tensor_tensor(tq[:, 0, :], tq[:, 0, :], tq[:, 1, :], ALU.subtract).then_inc(qd, 1)
                    pool.tensor_tensor(tq[:, 2, :], tq[:, 2, :], tq[:, 3, :], ALU.add).then_inc(qd, 1)
                pool.wait_ge(loaded, 16)
                pool.wait_ge(lo, 2)
                pool.wait_ge(qd, 7 * FB)
                pool.tensor_tensor(U[:], U[:], drow[:].rearrange("p (a d) -> p a d", a=1).to_broadcast([P, TT, D]),
                                   ALU.mult).then_inc(skipped, 1)

            @block.vector
            def _(dve):
                dve.sem_inc(ba, 2)
                for n, (l, h, x) in enumerate(((ul, uh, U), (kl, kh, KN))):
                    dve.wait_ge(hi, n + 1)
                    dve.tensor_tensor(l[:], x[:], h[:], ALU.subtract).then_inc(lo, 1)
                for q in range(FB):
                    dve.wait_ge(ev, (q + 2) * NBK)
                    dve.tensor_tensor(su, es[:, 0:2, :], es[:, 2:4, :], ALU.add).then_inc(pd, 1)
                    dve.tensor_tensor(ksu[:], ks[:, 0, :, :], ks[:, 1, :, :], ALU.add).then_inc(pd, 1)
                    dve.wait_ge(pd, 7 * q + 2)
                    dve.sem_inc(used, 1)
                    times(dve, tp, su, ksu, pd)
                    dve.wait_ge(pd, 7 * q + 5)
                    dve.tensor_tensor(tp[:, 0, :], tp[:, 0, :], tp[:, 1, :], ALU.subtract).then_inc(pd, 1)
                    dve.tensor_tensor(tp[:, 2, :], tp[:, 2, :], tp[:, 3, :], ALU.add).then_inc(pd, 1)
                    dve.wait_ge(pd, 7 * q + 7)
                    dve.wait_ge(qd, 7 * q + 7)
                    dve.tensor_tensor(ab[:, 0:2, :], tp[:, 0:4:2, :], tq[:, 0:4:2, :], ALU.add).then_inc(abd, 1)
                    dve.tensor_tensor(ab[:, 2:4, :], tp[:, 0:4:2, :], tq[:, 0:4:2, :], ALU.subtract).then_inc(abd, 1)
                    dve.wait_ge(hd, q + 1)
                    dve.tensor_tensor(L[:, q, :, :], ab[:], H[:, q, :, :], ALU.subtract).then_inc(ld, 1)
                dve.wait_ge(skipped, 1)
                for m in range(FB):
                    for odd in range(2):
                        dve.wait_ge(bd, 2 * m + odd + 1)
                        u = U[:].rearrange("p (b t) d -> p b t d", b=B)[:, :, odd * FB + m, :]
                        dve.tensor_tensor(u, u, py[:, odd, :].rearrange("p (b d) -> p b d", b=B), ALU.add).then_inc(ba, 1)


def add_into(nc, K, name, dst, src):
    with Stage(nc, name) as st:
        added = st.sem("added")
        with st.block() as block:
            @block.vector
            def _(dve):
                dve.tensor_tensor(dst, dst, src, ALU.add).then_inc(added, 1)


def feed_forward(nc, K, name, HT, W1, b1, W2, b2, fn, acc):
    width = W1.shape[1]
    PT = width // P
    TC = B * S // N
    TN = N // P
    YP = TN // 2
    with Stage(nc, name) as st:
        w1, w2 = st.sb("w1", [P, DC, width]), st.sb("w2", [P, PT, D])
        b1t, b2t = st.sb("b1", [P, PT]), st.sb("b2", [P, D])
        hg = st.sb("hg", [P, 2, PT, N])
        ph, py = st.ps("h", [P, 4, N]), st.ps("y", [P, 4, N])
        w1_loaded, w2_loaded, b1_loaded, b2_loaded, b2_added = (
            st.sem(x) for x in ("w1_loaded", "w2_loaded", "b1_loaded", "b2_loaded", "b2_added"))
        h_ready, h_done, y_ready, y_done = (st.sem(x) for x in ("h_ready", "h_done", "y_ready", "y_done"))
        with st.block() as block:
            @block.sync
            def _(sp):
                for h in range(2):
                    cols = slice(h * width // 2, (h + 1) * width // 2)
                    sp.dma_start(w1[:, :, cols], W1[:, cols].rearrange("(c p) n -> p c n", p=P)).then_inc(w1_loaded, 16)
                    sp.wait_ge(w1_loaded, 16 * (h + 1))
                sp.dma_start(w2[:], W2.rearrange("(c p) n -> p c n", p=P)).then_inc(w2_loaded, 16)

            @block.gpsimd
            def _(pool):
                pool.dma_start(b1t[:], b1.rearrange("(t p) -> p t", p=P),
                               allow_slow_non_contiguous=True).then_inc(b1_loaded, 16)
                pool.dma_start(b2t[:], row(b2)).then_inc(b2_loaded, 16)

            @block.tensor
            def _(pe):
                def up(t):
                    for m in range(PT):
                        n = t * PT + m
                        if t == 0 and m % (PT // 2) == 0:
                            pe.wait_ge(w1_loaded, 16 * (m // (PT // 2) + 1))
                        if n >= 4:
                            pe.wait_ge(h_done, n - 3)
                        for c in range(DC):
                            last = pe.matmul(ph[:, m % 4, :], w1[:, c, m * P:(m + 1) * P],
                                             HT[:, c, t * N:(t + 1) * N], start=c == 0, stop=c == DC - 1)
                        last.then_inc(h_ready, 1)

                def down(t):
                    pe.wait_ge(h_done, (t + 1) * PT)
                    if t == 0:
                        pe.wait_ge(w2_loaded, 16)
                    for y in range(YP):
                        n = t * YP + y
                        if n >= 4:
                            pe.wait_ge(y_done, n - 3)
                        for k in range(2):
                            c0 = (2 * y + k) * P
                            for m in range(PT):
                                last = pe.matmul(py[:, n % 4, k * D:(k + 1) * D], hg[:, t % 2, m, c0:c0 + P],
                                                 w2[:, m, :], start=m == 0, stop=m == PT - 1)
                        last.then_inc(y_ready, 1)

                up(0)
                for t in range(1, TC):
                    up(t)
                    down(t - 1)
                down(TC - 1)

            @block.scalar
            def _(act):
                act.wait_ge(b1_loaded, 16)
                for t in range(TC):
                    if t >= 2:
                        act.wait_ge(y_ready, (t - 1) * YP)
                    for m in range(PT):
                        act.wait_ge(h_ready, t * PT + m + 1)
                        act.activation(hg[:, t % 2, m, :], ph[:, m % 4, :], fn, bias=b1t[:, m:m + 1]).then_inc(h_done, 1)

            @block.vector
            def _(dve):
                dve.wait_ge(b2_loaded, 16)
                dve.tensor_tensor(acc[:], acc[:], b2t[:].rearrange("p (a d) -> p a d", a=1).to_broadcast([P, TT, D]),
                                  ALU.add).then_inc(b2_added, 1)
                dve.wait_ge(b2_added, 1)
                for n in range(TC * YP):
                    dve.wait_ge(y_ready, n + 1)
                    two = acc[:, 2 * n:2 * n + 2, :]
                    dve.tensor_tensor(two, two, py[:, n % 4, :].rearrange("p (k d) -> p k d", k=2),
                                      ALU.add).then_inc(y_done, 1)


def state_space(nc, K, a):
    g = lambda x: a["L1_xattn_" + x]
    with ExitStack() as ctx:
        def sb(name, shape, dt=F32):
            return ctx.enter_context(nc.sbuf_tensor(name, shape, dt))
        KN = sb("e_KN", [P, LB, D])
        ssm_kernel(nc, K, a, KN)
        layernorm(nc, K, "n4", K.X, K.XN, K.XNT)
        U = sb("e_U", [P, TT, D])
        with nc.sbuf_tensor("e_CTT", [P, DC, B * S], F32) as CTT:
            sparse_cross(nc, K, a, a["mask_BxS_bf1"], a["mask_BxS2_bf1"], CTT)
            layernorm(nc, K, "e_n1", K.XN, U, gamma=g("g_norm_in"), beta=g("b_norm_in"))
            film(nc, K, "e_f1", CTT, g("W_film_in"), g("b_film_in"), g("mod_gate"), U)
            convolution(nc, K, KN, U, g("D_skip"), a["dft_tables"])
            film(nc, K, "e_f2", CTT, g("W_film_out"), g("b_film_out"), g("mod_gate"), U)
        add_into(nc, K, "e_a1", U[:], K.XN)
        layernorm(nc, K, "e_n2", U, K.XN, K.XNT, gamma=g("g_ffn"), beta=g("b_ffn"))
        feed_forward(nc, K, "e_ff", K.XNT, g("W1"), g("b1"), g("W2"), g("b2"), ACT.Gelu, U)
        layernorm(nc, K, "e_n3", U, U, gamma=g("g_norm_out"), beta=g("b_norm_out"))
        add_into(nc, K, "e_a2", K.X[:], U[:])


E, TOPK, HID = 8, 2, 1024
HM = HID // P
NT = B * S * TOPK // P + E - 1


def route_tokens(nc, K, a, R):
    with Stage(nc, "route") as st:
        W, brow, b2t = st.sb("W", [P, DC, E]), st.sb("br", [P, E]), st.sb("b2", [E, D])
        b1r = st.sb("b1r", [E * HM, P])
        lg, rank, ex = (st.sb(x, [P, TT, E]) for x in ("lg", "rank", "ex"))
        weights, chosen, within = (st.sb(x, [P, TT, E]) for x in ("weights", "chosen", "within"))
        gr, eq = st.sb("gr", [P, TT, E, E]), st.sb("eq", [P, TT, E, E])
        earlier, before, ones = st.sb("earlier", [P, E, E]), st.sb("before", [P, P]), st.sb("ones", [P, P])
        mx, sm = st.sb("mx", [P, TT]), st.sb("sm", [P, TT])
        total, first, tiles = (st.sb(x, [P, E]) for x in ("total", "first", "tiles"))
        tid, cmp, ef, posf = st.sb("tid", [P, NT]), st.sb("cmp", [P, NT, E]), st.sb("ef", [P, NT]), st.sb("posf", [P, TT, 2])
        wT = st.sb("wT", [E, B * S])
        pl, pt, pb = st.ps("l", [P, 4, TT, E]), st.ps("t", [E, 4, N]), st.ps("b", [P, 2, N])
        loaded, made, mm, chain, ask, ans, turned, moved, bd, ba = (
            st.sem(x) for x in ("loaded", "made", "mm", "chain", "ask", "ans", "turned", "moved", "bd", "ba"))
        counted = st.sem("counted")
        with st.block() as block:
            @block.sync
            def _(sp):
                sp.dma_start(W[:], a["L1_ffn_Wr"].rearrange("(c p) n -> p c n", p=P)).then_inc(loaded, 16)
                sp.dma_start(brow[:], row(a["L1_ffn_br"])).then_inc(loaded, 16)
                sp.dma_start(b2t[:], a["L1_ffn_b2"]).then_inc(loaded, 16)
                sp.dma_start(b1r[:], a["L1_ffn_b1"].rearrange("e (m p) -> (e m) p", p=P)).then_inc(loaded, 16)

            @block.gpsimd
            def _(pool):
                pool.memset(earlier[:], 1.0).then_inc(made, 1)
                pool.memset(before[:], 1.0).then_inc(made, 1)
                pool.memset(ones[:], 1.0).then_inc(made, 1)
                pool.iota(tid[:], pattern=[[1, NT]], base=0, channel_multiplier=0,
                          allow_small_or_imprecise_dtypes=True).then_inc(made, 1)
                pool.wait_ge(made, 4)
                pool.affine_select(out=earlier[:], in_=earlier[:], compare_op=ALU.is_gt, fill=0.0, base=0,
                                   pattern=[[1, E], [-1, E]], channel_multiplier=0).then_inc(made, 1)
                pool.affine_select(out=before[:], in_=before[:], compare_op=ALU.is_gt, fill=0.0, base=0,
                                   pattern=[[1, P]], channel_multiplier=-1).then_inc(made, 1)

            @block.tensor
            def _(pe):
                pe.wait_ge(loaded, 64)
                pe.transpose(pl[:, 3, 0:HM, :].rearrange("p t e -> p (t e)"), b1r[:], K.ident[0:E * HM, 0:E * HM])
                for t in range(TT):
                    for c in range(DC):
                        last = pe.matmul(pl[:, 0, t, :], K.XNT[:, c, t * P:(t + 1) * P], W[:, c, :],
                                         start=c == 0, stop=c == DC - 1)
                last.then_inc(mm, 1)
                pe.wait_ge(counted, 1)
                ch = chosen[:].rearrange("p t e -> p (t e)")
                pe.matmul(pl[:, 1, :, :].rearrange("p t e -> p (t e)"), before[:], ch, start=True, stop=True)
                pe.matmul(pl[:, 2, :, :].rearrange("p t e -> p (t e)"), ones[:], ch, start=True, stop=True).then_inc(mm, 1)
                pe.wait_ge(ask, 2)
                for t in range(TT):
                    last = pe.transpose(pt[:, t // 4, (t % 4) * P:(t % 4 + 1) * P], weights[:, t, :], K.ident[:])
                last.then_inc(turned, 1)
                pe.wait_ge(moved, 1)
                for n in range(TT // 2):
                    if n >= 2:
                        pe.wait_ge(ba, n - 1)
                    for k in range(2):
                        t = 2 * n + k
                        last = pe.matmul(pb[:, n % 2, k * D:(k + 1) * D], wT[:, t * P:(t + 1) * P], b2t[:],
                                         start=True, stop=True)
                    last.then_inc(bd, 1)

            @block.scalar
            def _(act):
                act.wait_ge(ask, 1)
                act.activation(ex[:], lg[:], ACT.Exp).then_inc(ans, 1)
                act.wait_ge(turned, 1)
                act.copy(wT[:], pt[:].rearrange("p a n -> p (a n)")).then_inc(moved, 1)

            @block.vector
            def _(dve):
                link = Link(dve, chain)
                tt, ts = dve.tensor_tensor, dve.tensor_scalar
                dve.wait_ge(mm, 1)
                dve.wait_ge(made, 6)
                link(dve.tensor_copy(R.b1[:].rearrange("p e m -> p (e m)"),
                                     pl[:, 3, 0:HM, :].rearrange("p t e -> p (t e)")))
                link(tt(lg[:], pl[:, 0, :, :], brow[:].rearrange("p (a e) -> p a e", a=1).to_broadcast([P, TT, E]),
                        ALU.add))
                others = lg[:].rearrange("p t (a e) -> p t a e", a=1).to_broadcast([P, TT, E, E])
                mine = lg[:].rearrange("p t (e a) -> p t e a", a=1).to_broadcast([P, TT, E, E])
                link(tt(gr[:], others, mine, ALU.is_gt))
                link(tt(eq[:], others, mine, ALU.is_equal))
                link(tt(eq[:], eq[:], earlier[:].rearrange("p (a e) f -> p a e f", a=1).to_broadcast([P, TT, E, E]),
                        ALU.mult))
                link(tt(gr[:], gr[:], eq[:], ALU.add))
                link(dve.tensor_reduce(rank[:], gr[:], AX.X, ALU.add))
                link(ts(chosen[:], rank[:], float(TOPK), None, ALU.is_lt))
                dve.sem_inc(counted, 1)
                link(dve.tensor_reduce(mx[:], lg[:], AX.X, ALU.max))

                def by_t(x):
                    return x.rearrange("p (t a) -> p t a", a=1).to_broadcast([P, TT, E])
                link(tt(lg[:], lg[:], by_t(mx[:]), ALU.subtract))
                dve.sem_inc(ask, 1)
                dve.wait_ge(mm, 2)
                link(dve.memset(within[:, 0, :], 0.0))
                for t in range(1, TT):
                    link(tt(within[:, t, :], within[:, t - 1, :], pl[:, 2, t - 1, :], ALU.add))
                link(tt(total[:], within[:, TT - 1, :], pl[:, 2, TT - 1, :], ALU.add))
                link(tt(within[:], within[:], pl[:, 1, :, :], ALU.add))
                link(ts(tiles[:], total[:], 1.0 / P, (P - 1.0) / P - 0.5 + 0.5 / P, ALU.mult, ALU.add))
                link(ts(tiles[:], tiles[:], ROUND, ROUND, ALU.add, ALU.subtract))
                link(dve.memset(first[:, 0:1], 0.0))
                for e in range(1, E):
                    link(tt(first[:, e:e + 1], first[:, e - 1:e], tiles[:, e - 1:e], ALU.add))
                link(tt(cmp[:], tid[:].rearrange("p (n a) -> p n a", a=1).to_broadcast([P, NT, E]),
                        first[:].rearrange("p (a e) -> p a e", a=1).to_broadcast([P, NT, E]), ALU.is_ge))
                link(dve.tensor_reduce(ef[:], cmp[:, :, 1:], AX.X, ALU.add))
                link(dve.tensor_copy(R.expert[:], ef[:]))
                link(ts(first[:], first[:], float(P), None, ALU.mult))
                link(tt(within[:], within[:], first[:].rearrange("p (a e) -> p a e", a=1).to_broadcast([P, TT, E]), ALU.add))
                dve.wait_ge(ans, 1)
                link(tt(ex[:], ex[:], chosen[:], ALU.mult))
                link(dve.tensor_reduce(sm[:], ex[:], AX.X, ALU.add))
                link(dve.reciprocal(mx[:], sm[:]))
                link(tt(weights[:], ex[:], by_t(mx[:]), ALU.mult))
                dve.sem_inc(ask, 1)
                for k in range(TOPK):
                    link(ts(chosen[:], rank[:], float(k), None, ALU.is_equal))
                    link(tt(lg[:], chosen[:], within[:], ALU.mult))
                    link(dve.tensor_reduce(posf[:, :, k], lg[:], AX.X, ALU.add))
                    link(dve.tensor_copy(R.pos[:, k, :], posf[:, :, k]))
                    link(tt(lg[:], chosen[:], weights[:], ALU.mult))
                    link(dve.tensor_reduce(R.w[:, k, :], lg[:], AX.X, ALU.add))
                for n in range(TT // 2):
                    dve.wait_ge(bd, n + 1)
                    x = K.X[:, 2 * n:2 * n + 2, :]
                    tt(x, x, pb[:, n % 2, :].rearrange("p (k d) -> p k d", k=2), ALU.add).then_inc(ba, 1)


def experts(nc, K, a, R):
    W1, W2 = a["L1_ffn_W1"], a["L1_ffn_W2"]
    with Stage(nc, "experts") as st:
        w1 = [st.sb(f"w1{x}", [P, E, DC, HID], BF16) for x in "hl"]
        w2 = [st.sb(f"w2{x}", [P, E, HM, D], BF16) for x in "hl"]
        raw = [x.rearrange("p a n -> p (a n)").rearrange("p (s n) -> p s n", s=2) for x in (K.XNT, K.XN)]
        FIRST = 2
        gathered = K.XN
        xs = st.sb("xs", [P, 2, D])
        xh, xl = st.sb("xh", [P, 2, DC, P], BF16), st.sb("xl", [P, 2, DC, P], BF16)
        hf = st.sb("hf", [P, 2, HM, P])
        hh, hl = st.sb("hh", [P, HM, P], BF16), st.sb("hl", [P, HM, P], BF16)
        y = st.sb("y", [P, 2, D])
        px, ph, py = st.ps("px", [P, 2, N]), st.ps("ph", [P, 2, HM, P]), st.ps("py", [P, 2, N])
        wl = [st.sem(f"weights{j}") for j in range(2)]
        xsem, ysem = [st.sem(f"x{j}") for j in range(2)], [st.sem(f"stored{j}") for j in range(2)]
        sent, first_hi, first_loaded = st.sem("sent"), st.sem("first_hi"), [st.sem(f"first{j}") for j in range(2)]
        whi, wready = st.sem("whi"), st.sem("wready")
        turned, xhi, xsplit, h_ready, g_done, hhi, hsplit, y_ready, y_out = (st.sem(x) for x in (
            "turned", "xhi", "xsplit", "h_ready", "g_done", "hhi", "hsplit", "y_ready", "y_out"))
        back, used, links = [st.sem(f"back{j}") for j in range(2)], st.sem("used"), st.sem("links")
        HH = HM // 2
        GT = 4

        def over_tiles(eng, body, ahead):
            loops = (NT - 1 - ahead - (NT - 1 - ahead) % 2) // 2 if ahead else NT // 2
            with eng.Fori(0, loops, 1) as i:
                for j in range(2):
                    body(i * 2 + j, j, 2)
            for n in range(2 * loops, NT):
                body(n, n % 2, NT - 1 - n)

        def fetch(eng, e, s, where, sems):
            w = (W1, W2)[s][e].rearrange("(c p) n -> p c n", p=P)
            eng.dma_start(raw[where][:, s, :].rearrange("p (c n) -> p c n", n=w.shape[2]), w).then_inc(sems[s], 16)

        def parts(e, s):
            return [x[:, e, :, :].rearrange("p c n -> p (c n)") for x in (w1, w2)[s]]

        with st.block() as block:
            @block.gpsimd
            def _(pool):
                pool.wait_ge(K.rows_zeroed, 16)
                for t in range(TT):
                    for k in range(TOPK):
                        pool.indirect_dma_start(R.rows, bass.IndirectOffsetOnAxis(R.pos[:, k, t:t + 1], 0),
                                                K.XN[:, t, :], None).then_inc(sent, 16)
                pool.wait_ge(sent, 16 * TT * TOPK)
                for s in range(2):
                    fetch(pool, FIRST, s, 1, wl)
                pool.wait_ge(wready, 2 * FIRST)
                for e in range(FIRST, E):
                    for s in range(2):
                        h, l = parts(e, s)
                        n = e * 2 + s + 1
                        pool.wait_ge(wl[s], (e + 1 - FIRST) * 16)
                        pool.tensor_copy(h, raw[1][:, s, :]).then_inc(whi, 1)
                        pool.wait_ge(whi, n - 2 * FIRST)
                        pool.tensor_tensor(l, raw[1][:, s, :], h, ALU.subtract).then_inc(wready, 1)
                        if e < E - 1:
                            pool.wait_ge(wready, n)
                            fetch(pool, e + 1, s, 1, wl)
                for j in range(2):
                    pool.wait_ge(ysem[j], 16 + 16 * ((NT + 1 - j) // 2))
                for t in range(TT):
                    g = t // GT
                    if g >= 2 and t % GT == 0:
                        pool.wait_ge(used, g - 1)
                    for k in range(TOPK):
                        pool.indirect_dma_start(gathered[:, (t * TOPK + k) % TT, :], None, R.results,
                                                bass.IndirectOffsetOnAxis(R.pos[:, k, t:t + 1], 0)).then_inc(back[g % 2], 16)

            @block.sync
            def _(sp):
                def load(n, j):
                    sp.dma_start(xs[:, j, :], R.rows[bass.ds(n * P, P), :]).then_inc(xsem[j], 16)

                for c in range(2 * FIRST):
                    if c >= 2:
                        sp.wait_ge(wready, c - 1)
                    fetch(sp, c // 2, c % 2, 0, first_loaded)
                sp.wait_ge(sent, 16 * TT * TOPK)
                for n in range(2):
                    load(n, n)

                def body(n, j, more):
                    if more >= 2:
                        sp.wait_ge(turned, n + 1)
                        load(n + 2, j)
                over_tiles(sp, body, 2)

            @block.tensor
            def _(pe):
                def turn(n, j):
                    pe.wait_ge(xsem[j], (n - j) * 8 + 16)
                    pe.wait_ge(xsplit, n + 1)
                    for c in range(DC):
                        last = pe.transpose(px[:, j, c * P:(c + 1) * P], xs[:, j, c * P:(c + 1) * P], K.ident[:])
                    last.then_inc(turned, 1)

                def expert_of(n):
                    return pe.value_load(R.expert[0:1, bass.ds(n, 1)], min_val=0, max_val=E - 1)

                def up(n, j, e):
                    pe.wait_ge(wready, e * 2 + 1)
                    pe.wait_ge(xsplit, n + 3)
                    for h in range(2):
                        pe.wait_ge(g_done, n * 2 + h + 1)
                        for m in range(h * HH, (h + 1) * HH):
                            prods = [(w, x, c) for c in range(DC) for w, x in ((0, xh), (1, xh), (0, xl))]
                            for q, (w, x, c) in enumerate(prods):
                                last = pe.matmul(ph[:, j, m, :],
                                                 w1[w][:, bass.ds(e, 1), c, m * P:(m + 1) * P].rearrange("p a n -> p (a n)"),
                                                 x[:, j, c, :], start=q == 0, stop=q == len(prods) - 1)
                        last.then_inc(h_ready, 1)

                def down(n, j, e):
                    pe.wait_ge(wready, e * 2 + 2)
                    pe.wait_ge(y_out, n + 1)
                    for m in range(HM):
                        if m % HH == 0:
                            pe.wait_ge(hsplit, n * 2 + m // HH + 1)
                        for q, (x, w) in enumerate(((hh, 0), (hh, 1), (hl, 0))):
                            last = pe.matmul(py[:, j, 0:D], x[:, m, :],
                                             w2[w][:, bass.ds(e, 1), m, :].rearrange("p a n -> p (a n)"),
                                             start=m == 0 and q == 0, stop=m == HM - 1 and q == 2)
                    last.then_inc(y_ready, 1)

                turn(0, 0)
                up(0, 0, expert_of(0))
                turn(1, 1)

                def body(n, j, more):
                    if more >= 1:
                        this, following = expert_of(n), expert_of(n + 1)
                        up(n + 1, 1 - j, following)
                    else:
                        this = expert_of(n)
                    if more >= 2:
                        turn(n + 2, j)
                    down(n, j, this)
                over_tiles(pe, body, 2)

            @block.scalar
            def _(act):
                act.sem_inc(g_done, 4)
                act.sem_inc(y_out, 2)
                for j in range(2):
                    act.sem_inc(ysem[j], 16)

                for c in range(2 * FIRST):
                    act.wait_ge(first_loaded[c % 2], (c // 2 + 1) * 16)
                    act.copy(parts(c // 2, c % 2)[0], raw[0][:, c % 2, :]).then_inc(first_hi, 1)

                def gelu(n, j):
                    e = act.value_load(R.expert[0:1, bass.ds(n, 1)], min_val=0, max_val=E - 1)
                    for h in range(2):
                        act.wait_ge(h_ready, n * 2 + h + 1)
                        for m in range(h * HH, (h + 1) * HH):
                            last = act.activation(hf[:, j, m, :], ph[:, j, m, :], ACT.Gelu_apprx_tanh,
                                                  bias=R.b1[:, bass.ds(e, 1), m])
                        last.then_inc(g_done, 1)

                def body(n, j, more):
                    if more >= 1:
                        gelu(n + 1, 1 - j)
                    act.wait_ge(y_ready, n + 2)
                    act.wait_ge(ysem[j], (n - j) * 8 + 16)
                    act.copy(y[:, j, :], py[:, j, 0:D]).then_inc(y_out, 1)
                    act.wait_ge(y_out, n + 3)
                    act.dma_start(R.results[bass.ds(n * P, P), :], y[:, j, :]).then_inc(ysem[j], 16)
                gelu(0, 0)
                over_tiles(act, body, 2)
                for j in range(2):
                    act.wait_ge(ysem[j], 16 + 16 * ((NT + 1 - j) // 2))

            @block.vector
            def _(dve):
                dve.sem_inc(xsplit, 2)
                dve.sem_inc(y_ready, 1)

                def split_x(n, j):
                    dve.wait_ge(turned, n + 1)
                    src = px[:, j, 0:D].rearrange("p (c n) -> p c n", c=DC)
                    dve.tensor_copy(xh[:, j, :, :], src).then_inc(xhi, 1)
                    dve.wait_ge(xhi, n + 1)
                    dve.tensor_tensor(xl[:, j, :, :], src, xh[:, j, :, :], ALU.subtract).then_inc(xsplit, 1)

                def split_h(n, j):
                    dve.wait_ge(y_ready, n + 1)
                    for h in range(2):
                        ms = slice(h * HH, (h + 1) * HH)
                        dve.wait_ge(g_done, n * 2 + h + 5)
                        dve.tensor_copy(hh[:, ms, :], hf[:, j, ms, :]).then_inc(hhi, 1)
                        dve.wait_ge(hhi, n * 2 + h + 1)
                        dve.tensor_tensor(hl[:, ms, :], hf[:, j, ms, :], hh[:, ms, :], ALU.subtract).then_inc(hsplit, 1)

                for c in range(2 * FIRST):
                    h, l = parts(c // 2, c % 2)
                    dve.wait_ge(first_hi, c + 1)
                    dve.tensor_tensor(l, raw[0][:, c % 2, :], h, ALU.subtract).then_inc(wready, 1)
                split_x(0, 0)

                def body(n, j, more):
                    if more >= 1:
                        split_x(n + 1, 1 - j)
                    split_h(n, j)
                over_tiles(dve, body, 2)
                link = Link(dve, links)
                for g in range(TT // GT):
                    dve.wait_ge(back[g % 2], 16 * GT * TOPK * (g // 2 + 1))
                    for k in range(TOPK):
                        for t in range(g * GT, (g + 1) * GT):
                            last = dve.scalar_tensor_tensor(out=K.X[:, t, :], in0=gathered[:, (t * TOPK + k) % TT, :],
                                                            scalar=R.w[:, k, t:t + 1], in1=K.X[:, t, :],
                                                            op0=ALU.mult, op1=ALU.add)
                        link(last)
                    dve.sem_inc(used, 1)


def finish(nc, K, out, parity=True):
    with Stage(nc, "finish") as st:
        stored = st.sem("stored")
        with st.block() as block:
            @block.sync
            def _(sp):
                n = 0
                for b in range(B):
                    if not parity:
                        sp.dma_start(out[b].rearrange("(t p) d -> p t d", p=P),
                                     K.X[:, b * TB:(b + 1) * TB, :]).then_inc(stored, 16)
                        n += 1
                        continue
                    for x in range(2):
                        sp.dma_start(by_parity(out[b])[:, x, :, :],
                                     K.X[:, b * TB + x * TB // 2:b * TB + (x + 1) * TB // 2, :]).then_inc(stored, 16)
                        n += 1
                sp.wait_ge(stored, 16 * n)


class Shared:
    pass


def decoder(nc, a, out, upto=99):
    Stage.spent = []
    with ExitStack() as ctx:
        def sb(name, shape, dt=F32):
            return ctx.enter_context(nc.sbuf_tensor(name, shape, dt))

        K = Shared()
        K.X = sb("X", [P, TT, D])
        work = sb("work", [P, 2 * TT * D])
        K.XN = work[:, 0:TT * D].rearrange("p (t d) -> p t d", t=TT)
        K.XNT = work[:, TT * D:].rearrange("p (c n) -> p c n", c=DC)
        K.wide = work[:, :].rearrange("p (t d) -> p t d", t=TT)
        K.ident, K.identb = sb("ident", [P, P]), sb("identb", [P, P], BF16)
        K.ones, K.onesb = sb("ones", [P, P]), sb("onesb", [P, P], BF16)
        K.cmask, K.cmaskT = sb("cmask", [P, P], BF16), sb("cmaskT", [P, N // P, N], BF16)
        K.eps = sb("eps", [P, 1])
        K.CT = sb("CT", [CW_P, CW_N, B * CL])
        QS = nc.dram_tensor("q_stacks", [NH, ROWS, B * S], BF16, kind="Internal").ap()
        KS = nc.dram_tensor("k_stacks", [NH, ROWS, B * S], BF16, kind="Internal").ap()
        G = nc.dram_tensor("bias_rows", [NH, 2 * N], F32, kind="Internal").ap()

        def stack_of(src):
            return lambda head: src[bass.ds(head, 1)].rearrange("a r (b n) -> (a r) b n", b=B)

        K.scratch = nc.dram_tensor("tokens", [B, S, D], F32, kind="Internal").ap()
        K.rows = nc.dram_tensor("expert_rows", [NT * P, D], F32, kind="Internal").ap()
        K.rows_zeroed = nc.alloc_semaphore("rows_zeroed")
        K.zeros = sb("zeros", [P, D])
        setup(nc, K, a["x"])
        context(nc, K, a["ctx_768"])

        layernorm(nc, K, "n0", K.X, K.XN, K.XNT)
        with nc.sbuf_tensor("a0_values", [P, TT, D], F32) as V:
            qkv16(nc, K, "a0_qkv", K.XNT, QS, KS, V, a["L0_attn_w_attn"], bias=a["L0_attn_b_attn"],
                  lora=(a["L0_attn_la_attn"], a["L0_attn_lb_attn"]),
                  quant=(a["L0_attn_kv_scale"], a["L0_attn_kv_zero_point"]))
            attention(nc, K, "a0", NH, HD ** -0.5, HD, P, TB, True, [(stack_of(QS), ROWS)], [(stack_of(KS), ROWS)],
                      [(0, 0)], lambda b, h: V[:, b * TB:(b + 1) * TB, bass.ds(h * HD, HD)], K.XN, True)
        project(nc, K, "a0_out", K.XN, D, a["L0_attn_w_proj"], a["L0_attn_b_proj"],
                lora=(a["L0_attn_la_proj"], a["L0_attn_lb_proj"]))
        if upto <= 1:
            return finish(nc, K, out, False)
        layernorm(nc, K, "n1", K.X, K.XN, K.XNT)
        cross_attention(nc, K, a)
        if upto <= 2:
            return finish(nc, K, out, False)
        layernorm(nc, K, "n2", K.X, K.XN, K.XNT)
        routed_attention(nc, K, a)
        if upto <= 3:
            return finish(nc, K, out, False)
        layernorm(nc, K, "n3", K.X, K.XN, K.XNT)
        with nc.sbuf_tensor("a1_values", [P, TT, D], F32) as V:
            qkv16(nc, K, "a1_qkv", K.XNT, QS, KS, V, [a[f"L1_attn_W{x}"] for x in "qkv"], transposed=True)
            attention(nc, K, "a1", NH, D ** -0.5, HD, P, TB, False, [(stack_of(QS), ROWS)], [(stack_of(KS), ROWS)],
                      [(0, 0)], lambda b, h: V[:, b * TB:(b + 1) * TB, bass.ds(h * HD, HD)], K.XN, True)
            relative_bias(nc, K, V, a["L1_attn_bias_table"], K.XN, G)
        layernorm(nc, K, "a1_norm", K.XN, K.XN, gamma=a["L1_attn_ln_gamma"], beta=a["L1_attn_ln_beta"])
        add_into(nc, K, "a1_add", K.X[:], K.XN)
        if upto <= 4:
            return finish(nc, K, out, False)
        state_space(nc, K, a)
        if upto <= 5:
            return finish(nc, K, out)
        layernorm(nc, K, "n5", K.X, K.XN, K.XNT)
        R = Shared()
        R.rows, R.results = K.rows, nc.dram_tensor("expert_results", [NT * P, D], F32, kind="Internal").ap()
        R.pos, R.w, R.expert = sb("f_pos", [P, TOPK, TT], I32), sb("f_w", [P, TOPK, TT]), sb("f_expert", [P, NT], I32)
        R.b1 = sb("f_b1", [P, E, HM])
        route_tokens(nc, K, a, R)
        experts(nc, K, a, R)
        finish(nc, K, out)


def constants():
    half, blocks = S // 2, S // P // 2
    position, frequency = np.arange(S), np.arange(half)
    angle = np.outer(position, 2 * frequency + 1) % (4 * S) * (2 * np.pi / (4 * S))
    table = np.stack([np.cos(angle), -np.sin(angle)])
    table = table.reshape(2, half, 2, half).transpose(2, 0, 1, 3)

    def bf16(x):
        bits = x.astype(np.float32).view(np.uint32)
        bits = (bits + 0x7fff + (bits >> 16 & 1)) >> 16
        return bits.astype(np.uint16), (bits << 16).view(np.float32)

    def laid_out(x):
        x = x.reshape(2, 2, blocks, P, blocks, P).transpose(4, 3, 0, 1, 2, 5)
        high, value = bf16(x)
        return np.stack([high, bf16(x - value)[0]], axis=2)
    return {"dft_tables": np.stack([laid_out(table), laid_out(table.transpose(0, 1, 3, 2) / S)])}


def kernel(**inputs):
    import concourse.bacc as bacc
    from concourse.bass_utils import run_bass_kernel_spmd

    nc = bacc.Bacc("TRN2", target_bir_lowering=False, num_devices=1)
    arrays = dict(constants())
    for name, value in inputs.items():
        array = np.ascontiguousarray(value)
        arrays[name] = array.view(np.uint8) if array.dtype == bool else array
    a = {name: nc.dram_tensor(name, array.shape, mybir.dt.from_np(array.dtype), kind="ExternalInput").ap()
         for name, array in arrays.items()}
    out = nc.dram_tensor("y", (B, S, D), F32, kind="ExternalOutput").ap()
    decoder(nc, a, out)
    return run_bass_kernel_spmd(nc, [arrays], core_ids=[0]).results[0]["y"]
```
